# Optimizing a Trainium2 kernel written in Bass

```python
import numpy as np
import jax
import jax.numpy as jnp

def _softmax(x, axis=-1):
    return jax.nn.softmax(x, axis=axis)

def _gelu(x):
    return jax.nn.gelu(x, approximate=True)

def _silu(x):
    return jax.nn.silu(x)

def _sigmoid(x):
    return jax.nn.sigmoid(x)

def _layernorm(x, axis=-1, eps=1e-05):
    m = jnp.mean(x, axis=axis, keepdims=True)
    v = jnp.var(x, axis=axis, keepdims=True)
    return (x - m) / jnp.sqrt(v + eps)

def _scatter_add(tgt, idx, src, axis=0):
    return tgt.at[idx].add(src)

def _segment_sum(src, seg, n):
    return jax.ops.segment_sum(src, seg, n)
kernel_name = 'mk_hybrid_d4_jaxref_r8_f7e7f6'

def setup_inputs(seed: int=0):
    np.random.seed(seed)
    _w = jnp.asarray

    def _L0_attn_a_setup():
        import jax, jax.numpy as jnp
        import numpy as np
        DIM = 128
        DEPTH = 6
        HEADS = 8
        FF_MULT = 4
        LN_EPS = 1e-05
        LEAKY_SLOPE = 0.01

        def _layernorm(x, w, b):
            m = jnp.mean(x, axis=-1, keepdims=True)
            v = jnp.mean(jnp.square(x - m), axis=-1, keepdims=True)
            return (x - m) * jax.lax.rsqrt(v + LN_EPS) * w + b

        def _linear_attn(q, k, v):
            q = jax.nn.softmax(q, axis=-1)
            k = jax.nn.softmax(k, axis=-2)
            context = jnp.einsum('bhnd,bhne->bhde', k, v)
            return jnp.einsum('bhnd,bhde->bhne', q, context)
        key = jax.random.key(seed)
        ks = jax.random.split(key, 12)
        b, t = (2, 512)
        s = 0.02
        return {'x': jax.random.normal(ks[0], (b, t, DIM), dtype=jnp.float32), 'ln1_w': jnp.ones((DEPTH, DIM), jnp.float32), 'ln1_b': jnp.zeros((DEPTH, DIM), jnp.float32), 'wq': jax.random.normal(ks[1], (DEPTH, DIM, DIM), jnp.float32) * s, 'wk': jax.random.normal(ks[2], (DEPTH, DIM, DIM), jnp.float32) * s, 'wv': jax.random.normal(ks[3], (DEPTH, DIM, DIM), jnp.float32) * s, 'wo': jax.random.normal(ks[4], (DEPTH, DIM, DIM), jnp.float32) * s, 'bo': jnp.zeros((DEPTH, DIM), jnp.float32), 'ln2_w': jnp.ones((DEPTH, DIM), jnp.float32), 'ln2_b': jnp.zeros((DEPTH, DIM), jnp.float32), 'w1': jax.random.normal(ks[5], (DEPTH, DIM, FF_MULT * DIM), jnp.float32) * s, 'w2': jax.random.normal(ks[6], (DEPTH, FF_MULT * DIM, DIM), jnp.float32) * s}
    _L0_attn_a_in = _L0_attn_a_setup()

    def _L0_attn_b_setup():
        import jax, jax.numpy as jnp
        import numpy as np
        B, S, DIM, HDIM = (8, 128, 128, 128)
        H = DIM // HDIM
        GN_EPS = 0.001

        def group_norm(y, gamma, beta, groups, eps=GN_EPS):
            b, s, c = y.shape
            g = y.reshape(b, s, groups, c // groups)
            mean = g.mean(axis=(1, 3), keepdims=True)
            var = g.var(axis=(1, 3), keepdims=True)
            g = (g - mean) * jax.lax.rsqrt(var + eps)
            return g.reshape(b, s, c) * gamma + beta
        key = jax.random.key(seed)
        ks = jax.random.split(key, 7)
        x = jax.random.normal(ks[0], (B, S, DIM), dtype=jnp.float32)
        sc_h = 1.0 / np.sqrt(HDIM).astype(np.float32)
        sc_d = 1.0 / np.sqrt(DIM).astype(np.float32)
        Wq = jax.random.normal(ks[1], (H, HDIM, HDIM), dtype=jnp.float32) * sc_h
        Wk = jax.random.normal(ks[2], (H, HDIM, HDIM), dtype=jnp.float32) * sc_h
        Wv = jax.random.normal(ks[3], (H, HDIM, HDIM), dtype=jnp.float32) * sc_h
        Wg = jax.random.normal(ks[4], (DIM, DIM), dtype=jnp.float32) * sc_d
        Wo = jax.random.normal(ks[5], (DIM, DIM), dtype=jnp.float32) * sc_d
        gn_gamma = jnp.ones((DIM,), dtype=jnp.float32)
        gn_beta = jnp.zeros((DIM,), dtype=jnp.float32)
        return {'x': x, 'Wq': Wq, 'Wk': Wk, 'Wv': Wv, 'Wg': Wg, 'Wo': Wo, 'gn_gamma': gn_gamma, 'gn_beta': gn_beta}
    _L0_attn_b_in = _L0_attn_b_setup()

    def _L0_ffn_setup():
        import jax, jax.numpy as jnp
        import numpy as np
        DIM = 128
        DEPTH = 2
        HEADS = 8
        DIM_HEAD = 64
        WINDOW = 64
        INNER = HEADS * DIM_HEAD
        HID = int(DIM * 4 * 2 / 3)
        B, N = (2, 1024)
        QK_SCALE = 8.0

        def shift_token(t):
            t1, t2 = jnp.split(t, 2, axis=-1)
            t2 = jnp.pad(t2, ((0, 0), (1, 0), (0, 0)))[:, :-1]
            return jnp.concatenate([t1, t2], axis=-1)

        def l2norm(t):
            return t / jnp.clip(jnp.linalg.norm(t, axis=-1, keepdims=True), 1e-12)

        def rotate_half(x):
            x1, x2 = jnp.split(x, 2, axis=-1)
            return jnp.concatenate([-x2, x1], axis=-1)

        def rotary_xpos(q, k):
            n = q.shape[-2]
            half_idx = jnp.arange(0, DIM_HEAD, 2, dtype=jnp.float32)
            inv_freq = 1.0 / 10000.0 ** (half_idx / DIM_HEAD)
            t = jnp.arange(n, dtype=jnp.float32)
            freqs = t[:, None] * inv_freq[None, :]
            freqs = jnp.concatenate([freqs, freqs], axis=-1)
            base = (half_idx + 0.4 * DIM_HEAD) / (1.4 * DIM_HEAD)
            power = (t - n // 2) / float(WINDOW // 2)
            scale = base[None, :] ** power[:, None]
            scale = jnp.concatenate([scale, scale], axis=-1)
            cos, sin = (jnp.cos(freqs), jnp.sin(freqs))
            q = q * cos * scale + rotate_half(q) * sin * scale
            k = k * cos / scale + rotate_half(k) * sin / scale
            return (q, k)

        def local_attention(q, k, v):
            b, h, n, d = q.shape
            w = n // WINDOW
            bq = q.reshape(b, h, w, WINDOW, d) * QK_SCALE
            bk = k.reshape(b, h, w, WINDOW, d)
            bv = v.reshape(b, h, w, WINDOW, d)

            def look_around(t):
                p = jnp.pad(t, ((0, 0), (0, 0), (1, 0), (0, 0), (0, 0)))
                return jnp.concatenate([p[:, :, :w], p[:, :, 1:]], axis=3)
            bk, bv = (look_around(bk), look_around(bv))
            bt = jnp.arange(n).reshape(w, WINDOW)
            btp = jnp.pad(bt, ((1, 0), (0, 0)), constant_values=-1)
            btk = jnp.concatenate([btp[:w], btp[1:]], axis=1)
            sim = jnp.einsum('bhwid,bhwjd->bhwij', bq, bk)
            i = bt[:, :, None]
            j = btk[:, None, :]
            mask = (i < j) | (i > j + WINDOW) | (j == -1)
            sim = jnp.where(mask, -jnp.finfo(sim.dtype).max, sim)
            attn = jax.nn.softmax(sim, axis=-1)
            out = jnp.einsum('bhwij,bhwjd->bhwid', attn, bv)
            return out.reshape(b, h, n, d)

        def _layer(x, wqkv, qs, ksc, wo, lg, lb, w1, b1, w2, b2):
            b, n, _ = x.shape
            h = shift_token(x)
            qkv = h @ wqkv
            q, k, v = jnp.split(qkv, 3, axis=-1)
            to_heads = lambda t: t.reshape(b, n, HEADS, DIM_HEAD).transpose(0, 2, 1, 3)
            q, k, v = (to_heads(q), to_heads(k), to_heads(v))
            q = l2norm(q) * qs
            k = l2norm(k) * ksc
            q, k = rotary_xpos(q, k)
            o = local_attention(q, k, v)
            o = o.transpose(0, 2, 1, 3).reshape(b, n, INNER)
            x = x + o @ wo
            h = shift_token(x)
            mu = h.mean(-1, keepdims=True)
            var = h.var(-1, keepdims=True)
            h = (h - mu) / jnp.sqrt(var + 1e-05) * lg + lb
            h = h @ w1 + b1
            a, g = jnp.split(h, 2, axis=-1)
            h = a * jax.nn.gelu(g, approximate=False)
            x = x + h @ w2 + b2
            return x
        key = jax.random.key(seed)
        ks = jax.random.split(key, 6)
        return {'x': jax.random.normal(ks[0], (B, N, DIM), jnp.float32), 'wqkv': jax.random.normal(ks[1], (DEPTH, DIM, 3 * INNER), jnp.float32) * 0.02, 'q_scale': jnp.ones((DEPTH, DIM_HEAD), jnp.float32), 'k_scale': jnp.ones((DEPTH, DIM_HEAD), jnp.float32), 'wo': jax.random.normal(ks[2], (DEPTH, INNER, DIM), jnp.float32) * 0.02, 'ln_g': jnp.ones((DEPTH, DIM), jnp.float32), 'ln_b': jnp.zeros((DEPTH, DIM), jnp.float32), 'w1': jax.random.normal(ks[3], (DEPTH, DIM, 2 * HID), jnp.float32) * 0.02, 'b1': jnp.zeros((DEPTH, 2 * HID), jnp.float32), 'w2': jax.random.normal(ks[4], (DEPTH, HID, DIM), jnp.float32) * 0.02, 'b2': jnp.zeros((DEPTH, DIM), jnp.float32)}
    _L0_ffn_in = _L0_ffn_setup()

    def _L1_attn_a_setup():
        import jax, jax.numpy as jnp
        import numpy as np
        B, T, D = (4, 256, 128)
        H, Kd = (4, 32)
        Vd = 64
        KEY_DIM, VAL_DIM = (H * Kd, H * Vd)
        CONV = 4
        EPS = 1e-06
        LN_EPS = 1e-05

        def _layernorm(x, g, b):
            m = jnp.mean(x, -1, keepdims=True)
            v = jnp.mean((x - m) ** 2, -1, keepdims=True)
            return (x - m) * jax.lax.rsqrt(v + LN_EPS) * g + b

        def _rmsnorm(x, w):
            return x * jax.lax.rsqrt(jnp.mean(x * x, -1, keepdims=True) + EPS) * w

        def _l2norm(x):
            return x * jax.lax.rsqrt(jnp.sum(x * x, -1, keepdims=True) + EPS)

        def _causal_conv_silu(x, w):
            t = x.shape[1]
            xp = jnp.pad(x, ((0, 0), (CONV - 1, 0), (0, 0)))
            y = xp[:, 0:t, :] * w[:, 0]
            for i in range(1, CONV):
                y = y + xp[:, i:i + t, :] * w[:, i]
            return jax.nn.silu(y)

        def _gated_delta_rule(q, k, v, g, beta):
            qT = jnp.moveaxis(q, 1, 0)
            kT = jnp.moveaxis(k, 1, 0)
            vT = jnp.moveaxis(v, 1, 0)
            gT = jnp.moveaxis(g, 1, 0)
            bT = jnp.moveaxis(beta, 1, 0)
            S0 = jnp.zeros((q.shape[0], H, Kd, Vd), q.dtype)

            def step(S, inp):
                q_t, k_t, v_t, g_t, b_t = inp
                S = S * jnp.exp(g_t)[..., None, None]
                kv = jnp.einsum('bhk,bhkv->bhv', k_t, S)
                delta = (v_t - kv) * b_t[..., None]
                S = S + k_t[..., :, None] * delta[..., None, :]
                o = jnp.einsum('bhk,bhkv->bhv', q_t, S)
                return (S, o)
            _, o = jax.lax.scan(step, S0, (qT, kT, vT, gT, bT))
            return jnp.moveaxis(o, 0, 1)

        def _forward(x, ln1_g, ln1_b, ln2_g, ln2_b, rms_in_w, Wq, Wk, Wv, conv_q_w, conv_k_w, conv_v_w, Wa, dt_bias, A_log, Wb, Wg, o_norm_w, Wo, W2, b2):
            b, t, _ = x.shape
            h = _layernorm(x, ln1_g, ln1_b)
            h = _rmsnorm(h, rms_in_w)
            q = _causal_conv_silu(h @ Wq, conv_q_w).reshape(b, t, H, Kd)
            k = _causal_conv_silu(h @ Wk, conv_k_w).reshape(b, t, H, Kd)
            v = _causal_conv_silu(h @ Wv, conv_v_w).reshape(b, t, H, Vd)
            q = _l2norm(q) * Kd ** (-0.5)
            k = _l2norm(k)
            g = -jnp.exp(A_log) * jax.nn.softplus(h @ Wa + dt_bias)
            beta = jax.nn.sigmoid(h @ Wb)
            o = _gated_delta_rule(q, k, v, g, beta)
            gate = (h @ Wg).reshape(b, t, H, Vd)
            o = _rmsnorm(o, o_norm_w) * jax.nn.silu(gate)
            enc = o.reshape(b, t, VAL_DIM) @ Wo
            x = x + enc
            h2 = _layernorm(x, ln2_g, ln2_b)
            x_out = jax.nn.gelu(h2 @ W2 + b2, approximate=False) + x
            return x_out
        key = jax.random.key(seed)
        ks = jax.random.split(key, 16)
        r = lambda k, shp, s=0.02: jax.random.normal(k, shp, dtype=jnp.float32) * s
        return {'x': jax.random.normal(ks[0], (B, T, D), dtype=jnp.float32), 'ln1_g': jnp.ones((D,), jnp.float32), 'ln1_b': jnp.zeros((D,), jnp.float32), 'ln2_g': jnp.ones((D,), jnp.float32), 'ln2_b': jnp.zeros((D,), jnp.float32), 'rms_in_w': jnp.ones((D,), jnp.float32), 'Wq': r(ks[1], (D, KEY_DIM)), 'Wk': r(ks[2], (D, KEY_DIM)), 'Wv': r(ks[3], (D, VAL_DIM)), 'conv_q_w': r(ks[4], (KEY_DIM, CONV), 0.3), 'conv_k_w': r(ks[5], (KEY_DIM, CONV), 0.3), 'conv_v_w': r(ks[6], (VAL_DIM, CONV), 0.3), 'Wa': r(ks[7], (D, H)), 'dt_bias': r(ks[8], (H,), 0.5), 'A_log': jnp.log(jax.random.uniform(ks[9], (H,), minval=1.0, maxval=16.0)), 'Wb': r(ks[10], (D, H)), 'Wg': r(ks[11], (D, VAL_DIM)), 'o_norm_w': jnp.ones((Vd,), jnp.float32), 'Wo': r(ks[12], (VAL_DIM, D)), 'W2': r(ks[13], (D, D)), 'b2': jnp.zeros((D,), jnp.float32)}
    _L1_attn_a_in = _L1_attn_a_setup()

    def _L1_attn_b_setup():
        import jax, jax.numpy as jnp
        import numpy as np
        import math
        INPUT_SIZE = 128
        HIDDEN = 128
        SEQ_LEN = 32
        BATCH = 128

        def _lstm(input_seq, w, u, bias):
            H = u.shape[0]
            B = input_seq.shape[1]
            x_proj = jnp.einsum('sbi,ih->sbh', input_seq, w) + bias

            def step(carry, xp_t):
                h_prev, c_prev = carry
                g = xp_t + h_prev @ u
                gates = jax.nn.sigmoid(g[:, :3 * H])
                c_cand = jnp.tanh(g[:, 3 * H:])
                ig, fg, og = (gates[:, :H], gates[:, H:2 * H], gates[:, 2 * H:])
                c = fg * c_prev + ig * c_cand
                h = og * jnp.tanh(c)
                return ((h, c), h)
            init = (jnp.zeros((B, H), dtype=input_seq.dtype), jnp.zeros((B, H), dtype=input_seq.dtype))
            _, hs = jax.lax.scan(step, init, x_proj)
            return hs
        key = jax.random.key(seed)
        k1, k2, k3, k4 = jax.random.split(key, 4)
        stddev = 1.0 / math.sqrt(HIDDEN)
        input_seq = jax.random.normal(k1, (SEQ_LEN, BATCH, INPUT_SIZE), dtype=jnp.float32)
        w = jax.random.uniform(k2, (INPUT_SIZE, 4 * HIDDEN), minval=-stddev, maxval=stddev, dtype=jnp.float32)
        u = jax.random.uniform(k3, (HIDDEN, 4 * HIDDEN), minval=-stddev, maxval=stddev, dtype=jnp.float32)
        bias = jax.random.uniform(k4, (4 * HIDDEN,), minval=-stddev, maxval=stddev, dtype=jnp.float32)
        return {'input_seq': input_seq, 'w': w, 'u': u, 'bias': bias}
    _L1_attn_b_in = _L1_attn_b_setup()

    def _L1_ffn_setup():
        import jax, jax.numpy as jnp
        import numpy as np
        ALPHA = 1.0
        key = jax.random.key(seed)
        ks = jax.random.split(key, 7)
        B, S, IN, OUT = (8, 1024, 128, 128)
        RANK, DDIM, UDIM = (4, 100, 50)
        return {'hidden_states': jax.random.normal(ks[0], (B, S, IN), dtype=jnp.float32), 'W': jax.random.normal(ks[1], (OUT, IN), dtype=jnp.float32) * 0.02, 'b': jax.random.normal(ks[2], (OUT,), dtype=jnp.float32) * 0.02, 'lora_down': jax.random.normal(ks[3], (RANK, DDIM), dtype=jnp.float32) * 0.1, 'lora_up': jax.random.normal(ks[4], (UDIM, RANK), dtype=jnp.float32) * 0.1, 'down_aux': jax.random.normal(ks[5], (DDIM, IN), dtype=jnp.float32) * 0.03, 'up_aux': jax.random.normal(ks[6], (OUT, UDIM), dtype=jnp.float32) * 0.03}
    _L1_ffn_in = _L1_ffn_setup()

    def _L2_attn_a_setup():
        import jax, jax.numpy as jnp
        import numpy as np
        B, S, D_IN = (4, 512, 128)
        D_HID = 256
        D_INNER = D_HID // 2
        NB = 8
        LOG_A_SCALE = -8.0
        R_MIN, R_MAX = (0.9, 0.999)

        def _bdl(x, w, b):
            Bb, Ss, d = x.shape
            nb, bin_, bout = w.shape
            xb = x.reshape(Bb, Ss, nb, bin_)
            y = jnp.einsum('bsni,nio->bsno', xb, w) + b.reshape(nb, bout)
            return y.reshape(Bb, Ss, nb * bout)

        def _reference_tuple_inner(x, w_in, b_in, w_gx, b_gx, w_ga, b_ga, a_real_param, a_imag_param, w_out, b_out):
            xh = x @ w_in + b_in
            gate_x = jax.nn.sigmoid(_bdl(xh, w_gx, b_gx))
            gate_a = jax.nn.sigmoid(_bdl(xh, w_ga, b_ga))
            log_a = LOG_A_SCALE * gate_a * jax.nn.softplus(a_real_param)
            log_a_imag = a_imag_param * gate_a
            a = jnp.exp(jax.lax.complex(log_a, log_a_imag))
            xc = jax.lax.complex(xh[..., :D_INNER], xh[..., D_INNER:])
            xc = gate_x * xc
            norm = jnp.sqrt(jnp.maximum(1.0 - jnp.exp(2.0 * log_a), 1e-06))
            xc = norm * xc

            def combine(l, r):
                return (r[0] * l[0], r[0] * l[1] + r[1])
            _, h = jax.lax.associative_scan(combine, (a, xc), axis=1)
            h_m = jnp.concatenate([h.real, h.imag], axis=-1)
            y = h_m @ w_out + b_out
            h_last = h_m[:, -1]
            return (y, h_last)
        key = jax.random.key(seed)
        ks = jax.random.split(key, 10)
        x = jax.random.normal(ks[0], (B, S, D_IN), dtype=jnp.float32)
        w_in = jax.random.normal(ks[1], (D_IN, D_HID), dtype=jnp.float32) / np.sqrt(D_IN)
        b_in = jnp.zeros((D_HID,), jnp.float32)
        bin_, bout = (D_HID // NB, D_INNER // NB)
        w_gx = jax.random.normal(ks[2], (NB, bin_, bout), dtype=jnp.float32) / np.sqrt(bin_)
        b_gx = jnp.zeros((D_INNER,), jnp.float32)
        w_ga = jax.random.normal(ks[3], (NB, bin_, bout), dtype=jnp.float32) / np.sqrt(bin_)
        b_ga = jnp.zeros((D_INNER,), jnp.float32)
        u = jax.random.uniform(ks[4], (D_INNER,))
        a_real = 0.5 * jnp.log(u * (R_MAX ** 2 - R_MIN ** 2) + R_MIN ** 2 + 1e-08)
        a_real_param = jnp.log(jnp.exp(-a_real) - 1.0)
        a_imag_param = jnp.pi * 0.1 * jax.random.uniform(ks[5], (D_INNER,))
        w_out = jax.random.normal(ks[6], (D_HID, D_IN), dtype=jnp.float32) / np.sqrt(D_HID)
        b_out = jnp.zeros((D_IN,), jnp.float32)
        return dict(x=x, w_in=w_in, b_in=b_in, w_gx=w_gx, b_gx=b_gx, w_ga=w_ga, b_ga=b_ga, a_real_param=a_real_param, a_imag_param=a_imag_param, w_out=w_out, b_out=b_out)
    _L2_attn_a_in = _L2_attn_a_setup()

    def _L2_attn_b_setup():
        import jax, jax.numpy as jnp
        import numpy as np
        import math
        DIM = 128
        ATTN_DIM = 128
        B, S = (2, 512)
        key = jax.random.key(seed)
        k1, k2, k3 = jax.random.split(key, 3)
        x = jax.random.normal(k1, (B, S, DIM), dtype=jnp.float32)
        W_qkv = jax.random.normal(k2, (3 * ATTN_DIM, DIM), dtype=jnp.float32) * (1.0 / math.sqrt(DIM))
        b_qkv = jax.random.normal(k3, (3 * ATTN_DIM,), dtype=jnp.float32) * 0.01
        return {'x': x, 'W_qkv': W_qkv, 'b_qkv': b_qkv}
    _L2_attn_b_in = _L2_attn_b_setup()

    def _L2_ffn_setup():
        import jax, jax.numpy as jnp
        import numpy as np
        DIM = 128

        def _reference_tuple_inner(x, W_r, W_k, W_v, mu_r, mu_k):
            B, T, C = x.shape
            x_prev = jnp.concatenate([jnp.zeros((B, 1, C), x.dtype), x[:, :-1, :]], axis=1)
            xr = mu_r * x + (1.0 - mu_r) * x_prev
            xk = mu_k * x + (1.0 - mu_k) * x_prev
            r = jax.nn.sigmoid(jnp.einsum('btc,dc->btd', xr, W_r))
            k = jnp.einsum('btc,dc->btd', xk, W_k)
            k_act = jnp.square(jax.nn.relu(k))
            out = r * jnp.einsum('btc,dc->btd', k_act, W_v)
            new_state = x[:, -1, :]
            return (out, new_state)
        key = jax.random.key(seed)
        ks = jax.random.split(key, 6)
        B, T, C = (8, 256, DIM)
        x = jax.random.normal(ks[0], (B, T, C), dtype=jnp.float32)
        s = 1.0 / np.sqrt(C)
        W_r = jax.random.uniform(ks[1], (C, C), jnp.float32, -s, s)
        W_k = jax.random.uniform(ks[2], (C, C), jnp.float32, -s, s)
        W_v = jax.random.uniform(ks[3], (C, C), jnp.float32, -s, s)
        mu_r = jax.random.uniform(ks[4], (C,), jnp.float32)
        mu_k = jax.random.uniform(ks[5], (C,), jnp.float32)
        return {'x': x, 'W_r': W_r, 'W_k': W_k, 'W_v': W_v, 'mu_r': mu_r, 'mu_k': mu_k}
    _L2_ffn_in = _L2_ffn_setup()

    def _L3_attn_a_setup():
        import jax, jax.numpy as jnp
        import numpy as np
        from jax import lax
        D_MODEL = 128
        D_STATE = 16
        D_CONV = 4
        EXPAND = 2
        D_INNER = D_MODEL * EXPAND
        DT_RANK = 64
        BATCH = 2
        SEQ = 512
        DT_MIN, DT_MAX = (0.001, 0.1)
        key = jax.random.key(seed)
        ks = jax.random.split(key, 12)
        xavier = lambda k, shape: jax.random.normal(k, shape, jnp.float32) * np.float32(np.sqrt(2.0 / (shape[0] + shape[1])))
        x = jax.random.normal(ks[0], (BATCH, SEQ, D_MODEL), jnp.float32)
        in_proj_w = xavier(ks[1], (2 * D_INNER, D_MODEL))
        in_proj_b = jnp.zeros((2 * D_INNER,), jnp.float32)
        conv_w = jax.random.normal(ks[2], (D_INNER, D_CONV), jnp.float32) * 0.02
        conv_b = jnp.zeros((D_INNER,), jnp.float32)
        A_log = jnp.log(jnp.tile(jnp.arange(1, D_STATE + 1, dtype=jnp.float32)[:, None], (1, D_INNER)))
        D = jnp.ones((D_INNER,), jnp.float32)
        x_proj_w = xavier(ks[3], (DT_RANK + 2 * D_STATE, D_INNER))
        dt_proj_w = jax.random.normal(ks[4], (D_INNER, DT_RANK), jnp.float32) * np.float32(DT_RANK ** (-0.5))
        dt = jnp.exp(jax.random.uniform(ks[5], (D_INNER,), jnp.float32) * np.float32(np.log(DT_MAX) - np.log(DT_MIN)) + np.float32(np.log(DT_MIN)))
        dt_proj_b = dt + jnp.log(-jnp.expm1(-dt))
        out_proj_w = xavier(ks[6], (D_MODEL, D_INNER))
        out_proj_b = jnp.zeros((D_MODEL,), jnp.float32)
        return {'x': x, 'in_proj_w': in_proj_w, 'in_proj_b': in_proj_b, 'conv_w': conv_w, 'conv_b': conv_b, 'A_log': A_log, 'D': D, 'x_proj_w': x_proj_w, 'dt_proj_w': dt_proj_w, 'dt_proj_b': dt_proj_b, 'out_proj_w': out_proj_w, 'out_proj_b': out_proj_b}
    _L3_attn_a_in = _L3_attn_a_setup()

    def _L3_attn_b_setup():
        import jax, jax.numpy as jnp
        import numpy as np
        B, T, D, H = (2, 256, 128, 16)
        DH = D // H
        ROPE_BASE = 10000.0

        def _rope(Xh, cos, sin):
            x0 = Xh[..., 0::2]
            x1 = Xh[..., 1::2]
            r0 = cos * x0 - sin * x1
            r1 = sin * x0 + cos * x1
            return jnp.stack((r0, r1), axis=-1).reshape(Xh.shape)
        key = jax.random.key(seed)
        ks = jax.random.split(key, 5)
        s = 1.0 / np.sqrt(D)
        return {'X': jax.random.normal(ks[0], (B, T, D), dtype=jnp.float32), 'W_q': jax.random.normal(ks[1], (D, D), dtype=jnp.float32) * s, 'W_k': jax.random.normal(ks[2], (D, D), dtype=jnp.float32) * s, 'W_v': jax.random.normal(ks[3], (D, D), dtype=jnp.float32) * s, 'W_o': jax.random.normal(ks[4], (D, D), dtype=jnp.float32) * s}
    _L3_attn_b_in = _L3_attn_b_setup()

    def _L3_ffn_setup():
        import jax, jax.numpy as jnp
        import numpy as np
        DM, NEXPERTS, SETS, ESIZE = (128, 32, 4, 32)
        B, S = (2, 1024)
        key = jax.random.key(seed)
        ks = jax.random.split(key, 7)
        sc = 0.02
        return {'x': jax.random.normal(ks[0], (B, S, DM), jnp.float32), 'Wc': jax.random.normal(ks[1], (DM, NEXPERTS, SETS), jnp.float32) * sc, 'bc': jax.random.normal(ks[2], (NEXPERTS, SETS), jnp.float32) * sc, 'W1': jax.random.normal(ks[3], (NEXPERTS, SETS, DM, ESIZE), jnp.float32) * sc, 'b1': jax.random.normal(ks[4], (NEXPERTS, SETS, ESIZE), jnp.float32) * sc, 'W2': jax.random.normal(ks[5], (NEXPERTS, SETS, DM, ESIZE), jnp.float32) * sc, 'b2': jax.random.normal(ks[6], (NEXPERTS, SETS, DM), jnp.float32) * sc}
    _L3_ffn_in = _L3_ffn_setup()
    _d = {'L0_attn_a_x': _L0_attn_a_in['x'], 'L0_attn_a_ln1_w': _L0_attn_a_in['ln1_w'], 'L0_attn_a_ln1_b': _L0_attn_a_in['ln1_b'], 'L0_attn_a_wq': _L0_attn_a_in['wq'], 'L0_attn_a_wk': _L0_attn_a_in['wk'], 'L0_attn_a_wv': _L0_attn_a_in['wv'], 'L0_attn_a_wo': _L0_attn_a_in['wo'], 'L0_attn_a_bo': _L0_attn_a_in['bo'], 'L0_attn_a_ln2_w': _L0_attn_a_in['ln2_w'], 'L0_attn_a_ln2_b': _L0_attn_a_in['ln2_b'], 'L0_attn_a_w1': _L0_attn_a_in['w1'], 'L0_attn_a_w2': _L0_attn_a_in['w2'], 'L0_attn_b_Wq': _L0_attn_b_in['Wq'], 'L0_attn_b_Wk': _L0_attn_b_in['Wk'], 'L0_attn_b_Wv': _L0_attn_b_in['Wv'], 'L0_attn_b_Wg': _L0_attn_b_in['Wg'], 'L0_attn_b_Wo': _L0_attn_b_in['Wo'], 'L0_attn_b_gn_gamma': _L0_attn_b_in['gn_gamma'], 'L0_attn_b_gn_beta': _L0_attn_b_in['gn_beta'], 'L0_ffn_wqkv': _L0_ffn_in['wqkv'], 'L0_ffn_q_scale': _L0_ffn_in['q_scale'], 'L0_ffn_k_scale': _L0_ffn_in['k_scale'], 'L0_ffn_wo': _L0_ffn_in['wo'], 'L0_ffn_ln_g': _L0_ffn_in['ln_g'], 'L0_ffn_ln_b': _L0_ffn_in['ln_b'], 'L0_ffn_w1': _L0_ffn_in['w1'], 'L0_ffn_b1': _L0_ffn_in['b1'], 'L0_ffn_w2': _L0_ffn_in['w2'], 'L0_ffn_b2': _L0_ffn_in['b2'], 'L1_attn_a_ln1_g': _L1_attn_a_in['ln1_g'], 'L1_attn_a_ln1_b': _L1_attn_a_in['ln1_b'], 'L1_attn_a_ln2_g': _L1_attn_a_in['ln2_g'], 'L1_attn_a_ln2_b': _L1_attn_a_in['ln2_b'], 'L1_attn_a_rms_in_w': _L1_attn_a_in['rms_in_w'], 'L1_attn_a_Wq': _L1_attn_a_in['Wq'], 'L1_attn_a_Wk': _L1_attn_a_in['Wk'], 'L1_attn_a_Wv': _L1_attn_a_in['Wv'], 'L1_attn_a_conv_q_w': _L1_attn_a_in['conv_q_w'], 'L1_attn_a_conv_k_w': _L1_attn_a_in['conv_k_w'], 'L1_attn_a_conv_v_w': _L1_attn_a_in['conv_v_w'], 'L1_attn_a_Wa': _L1_attn_a_in['Wa'], 'L1_attn_a_dt_bias': _L1_attn_a_in['dt_bias'], 'L1_attn_a_A_log': _L1_attn_a_in['A_log'], 'L1_attn_a_Wb': _L1_attn_a_in['Wb'], 'L1_attn_a_Wg': _L1_attn_a_in['Wg'], 'L1_attn_a_o_norm_w': _L1_attn_a_in['o_norm_w'], 'L1_attn_a_Wo': _L1_attn_a_in['Wo'], 'L1_attn_a_W2': _L1_attn_a_in['W2'], 'L1_attn_a_b2': _L1_attn_a_in['b2'], 'L1_attn_b_w': _L1_attn_b_in['w'], 'L1_attn_b_u': _L1_attn_b_in['u'], 'L1_attn_b_bias': _L1_attn_b_in['bias'], 'L1_ffn_W': _L1_ffn_in['W'], 'L1_ffn_b': _L1_ffn_in['b'], 'L1_ffn_lora_down': _L1_ffn_in['lora_down'], 'L1_ffn_lora_up': _L1_ffn_in['lora_up'], 'L1_ffn_down_aux': _L1_ffn_in['down_aux'], 'L1_ffn_up_aux': _L1_ffn_in['up_aux'], 'L2_attn_a_w_in': _L2_attn_a_in['w_in'], 'L2_attn_a_b_in': _L2_attn_a_in['b_in'], 'L2_attn_a_w_gx': _L2_attn_a_in['w_gx'], 'L2_attn_a_b_gx': _L2_attn_a_in['b_gx'], 'L2_attn_a_w_ga': _L2_attn_a_in['w_ga'], 'L2_attn_a_b_ga': _L2_attn_a_in['b_ga'], 'L2_attn_a_a_real_param': _L2_attn_a_in['a_real_param'], 'L2_attn_a_a_imag_param': _L2_attn_a_in['a_imag_param'], 'L2_attn_a_w_out': _L2_attn_a_in['w_out'], 'L2_attn_a_b_out': _L2_attn_a_in['b_out'], 'L2_attn_b_W_qkv': _L2_attn_b_in['W_qkv'], 'L2_attn_b_b_qkv': _L2_attn_b_in['b_qkv'], 'L2_ffn_W_r': _L2_ffn_in['W_r'], 'L2_ffn_W_k': _L2_ffn_in['W_k'], 'L2_ffn_W_v': _L2_ffn_in['W_v'], 'L2_ffn_mu_r': _L2_ffn_in['mu_r'], 'L2_ffn_mu_k': _L2_ffn_in['mu_k'], 'L3_attn_a_in_proj_w': _L3_attn_a_in['in_proj_w'], 'L3_attn_a_in_proj_b': _L3_attn_a_in['in_proj_b'], 'L3_attn_a_conv_w': _L3_attn_a_in['conv_w'], 'L3_attn_a_conv_b': _L3_attn_a_in['conv_b'], 'L3_attn_a_A_log': _L3_attn_a_in['A_log'], 'L3_attn_a_D': _L3_attn_a_in['D'], 'L3_attn_a_x_proj_w': _L3_attn_a_in['x_proj_w'], 'L3_attn_a_dt_proj_w': _L3_attn_a_in['dt_proj_w'], 'L3_attn_a_dt_proj_b': _L3_attn_a_in['dt_proj_b'], 'L3_attn_a_out_proj_w': _L3_attn_a_in['out_proj_w'], 'L3_attn_a_out_proj_b': _L3_attn_a_in['out_proj_b'], 'L3_attn_b_W_q': _L3_attn_b_in['W_q'], 'L3_attn_b_W_k': _L3_attn_b_in['W_k'], 'L3_attn_b_W_v': _L3_attn_b_in['W_v'], 'L3_attn_b_W_o': _L3_attn_b_in['W_o'], 'L3_ffn_Wc': _L3_ffn_in['Wc'], 'L3_ffn_bc': _L3_ffn_in['bc'], 'L3_ffn_W1': _L3_ffn_in['W1'], 'L3_ffn_b1': _L3_ffn_in['b1'], 'L3_ffn_W2': _L3_ffn_in['W2'], 'L3_ffn_b2': _L3_ffn_in['b2']}
    _x0 = _d['L0_attn_a_x']
    _d['L0_attn_a_x'] = jax.random.normal(jax.random.fold_in(jax.random.key(seed), 1), (8, 256, 128), dtype=_x0.dtype)
    del _x0
    return _d

def reference(L0_attn_a_x, L0_attn_a_ln1_w, L0_attn_a_ln1_b, L0_attn_a_wq, L0_attn_a_wk, L0_attn_a_wv, L0_attn_a_wo, L0_attn_a_bo, L0_attn_a_ln2_w, L0_attn_a_ln2_b, L0_attn_a_w1, L0_attn_a_w2, L0_attn_b_Wq, L0_attn_b_Wk, L0_attn_b_Wv, L0_attn_b_Wg, L0_attn_b_Wo, L0_attn_b_gn_gamma, L0_attn_b_gn_beta, L0_ffn_wqkv, L0_ffn_q_scale, L0_ffn_k_scale, L0_ffn_wo, L0_ffn_ln_g, L0_ffn_ln_b, L0_ffn_w1, L0_ffn_b1, L0_ffn_w2, L0_ffn_b2, L1_attn_a_ln1_g, L1_attn_a_ln1_b, L1_attn_a_ln2_g, L1_attn_a_ln2_b, L1_attn_a_rms_in_w, L1_attn_a_Wq, L1_attn_a_Wk, L1_attn_a_Wv, L1_attn_a_conv_q_w, L1_attn_a_conv_k_w, L1_attn_a_conv_v_w, L1_attn_a_Wa, L1_attn_a_dt_bias, L1_attn_a_A_log, L1_attn_a_Wb, L1_attn_a_Wg, L1_attn_a_o_norm_w, L1_attn_a_Wo, L1_attn_a_W2, L1_attn_a_b2, L1_attn_b_w, L1_attn_b_u, L1_attn_b_bias, L1_ffn_W, L1_ffn_b, L1_ffn_lora_down, L1_ffn_lora_up, L1_ffn_down_aux, L1_ffn_up_aux, L2_attn_a_w_in, L2_attn_a_b_in, L2_attn_a_w_gx, L2_attn_a_b_gx, L2_attn_a_w_ga, L2_attn_a_b_ga, L2_attn_a_a_real_param, L2_attn_a_a_imag_param, L2_attn_a_w_out, L2_attn_a_b_out, L2_attn_b_W_qkv, L2_attn_b_b_qkv, L2_ffn_W_r, L2_ffn_W_k, L2_ffn_W_v, L2_ffn_mu_r, L2_ffn_mu_k, L3_attn_a_in_proj_w, L3_attn_a_in_proj_b, L3_attn_a_conv_w, L3_attn_a_conv_b, L3_attn_a_A_log, L3_attn_a_D, L3_attn_a_x_proj_w, L3_attn_a_dt_proj_w, L3_attn_a_dt_proj_b, L3_attn_a_out_proj_w, L3_attn_a_out_proj_b, L3_attn_b_W_q, L3_attn_b_W_k, L3_attn_b_W_v, L3_attn_b_W_o, L3_ffn_Wc, L3_ffn_bc, L3_ffn_W1, L3_ffn_b1, L3_ffn_W2, L3_ffn_b2):

    def _L0_attn_a_ref(x, ln1_w, ln1_b, wq, wk, wv, wo, bo, ln2_w, ln2_b, w1, w2):
        import jax, jax.numpy as jnp
        import numpy as np
        DIM = 128
        DEPTH = 6
        HEADS = 8
        FF_MULT = 4
        LN_EPS = 1e-05
        LEAKY_SLOPE = 0.01

        def _layernorm(x, w, b):
            m = jnp.mean(x, axis=-1, keepdims=True)
            v = jnp.mean(jnp.square(x - m), axis=-1, keepdims=True)
            return (x - m) * jax.lax.rsqrt(v + LN_EPS) * w + b

        def _linear_attn(q, k, v):
            q = jax.nn.softmax(q, axis=-1)
            k = jax.nn.softmax(k, axis=-2)
            context = jnp.einsum('bhnd,bhne->bhde', k, v)
            return jnp.einsum('bhnd,bhde->bhne', q, context)
        b, t, e = x.shape
        h, dh = (HEADS, e // HEADS)
        for i in range(DEPTH):
            xn = _layernorm(x, ln1_w[i], ln1_b[i])
            q = (xn @ wq[i]).reshape(b, t, h, dh).transpose(0, 2, 1, 3)
            k = (xn @ wk[i]).reshape(b, t, h, dh).transpose(0, 2, 1, 3)
            v = (xn @ wv[i]).reshape(b, t, h, dh).transpose(0, 2, 1, 3)
            attn = _linear_attn(q, k, v)
            attn = attn.transpose(0, 2, 1, 3).reshape(b, t, e)
            x = attn @ wo[i] + bo[i] + x
            xn = _layernorm(x, ln2_w[i], ln2_b[i])
            hdn = xn @ w1[i]
            hdn = jnp.where(hdn >= 0, hdn, LEAKY_SLOPE * hdn)
            x = hdn @ w2[i] + x
        return x

    def _L0_attn_b_ref(x, Wq, Wk, Wv, Wg, Wo, gn_gamma, gn_beta):
        import jax, jax.numpy as jnp
        import numpy as np
        B, S, DIM, HDIM = (8, 128, 128, 128)
        H = DIM // HDIM
        GN_EPS = 0.001

        def group_norm(y, gamma, beta, groups, eps=GN_EPS):
            b, s, c = y.shape
            g = y.reshape(b, s, groups, c // groups)
            mean = g.mean(axis=(1, 3), keepdims=True)
            var = g.var(axis=(1, 3), keepdims=True)
            g = (g - mean) * jax.lax.rsqrt(var + eps)
            return g.reshape(b, s, c) * gamma + beta
        b, s, c = x.shape
        h, hd = (Wq.shape[0], Wq.shape[1])
        Wgate = jax.nn.relu(jnp.einsum('bsc,cd->bsd', x, Wg))
        xh = x.reshape(b, s, h, hd)
        Q = jnp.einsum('bshd,hde->bhse', xh, Wq)
        K = jnp.einsum('bshd,hde->bhse', xh, Wk)
        V = jnp.einsum('bshd,hde->bhse', xh, Wv)
        idx = jnp.arange(s, dtype=jnp.float32)
        gammas = 1.0 - 2.0 ** (-5.0 - jnp.arange(h, dtype=jnp.float32))
        decay = gammas[:, None, None] ** (idx[None, :, None] - idx[None, None, :])
        scores = jnp.einsum('bhsd,bhtd->bhst', Q, K) * decay[None]
        ret = jnp.einsum('bhst,bhtd->bhsd', scores, V)
        y = ret.transpose(0, 2, 1, 3).reshape(b, s, c)
        Y = group_norm(y, gn_gamma, gn_beta, groups=hd)
        return jnp.einsum('bsc,cd->bsd', Wgate * Y, Wo)

    def _L0_ffn_ref(x, wqkv, q_scale, k_scale, wo, ln_g, ln_b, w1, b1, w2, b2):
        import jax, jax.numpy as jnp
        import numpy as np
        DIM = 128
        DEPTH = 2
        HEADS = 8
        DIM_HEAD = 64
        WINDOW = 64
        INNER = HEADS * DIM_HEAD
        HID = int(DIM * 4 * 2 / 3)
        B, N = (2, 1024)
        QK_SCALE = 8.0

        def shift_token(t):
            t1, t2 = jnp.split(t, 2, axis=-1)
            t2 = jnp.pad(t2, ((0, 0), (1, 0), (0, 0)))[:, :-1]
            return jnp.concatenate([t1, t2], axis=-1)

        def l2norm(t):
            return t / jnp.clip(jnp.linalg.norm(t, axis=-1, keepdims=True), 1e-12)

        def rotate_half(x):
            x1, x2 = jnp.split(x, 2, axis=-1)
            return jnp.concatenate([-x2, x1], axis=-1)

        def rotary_xpos(q, k):
            n = q.shape[-2]
            half_idx = jnp.arange(0, DIM_HEAD, 2, dtype=jnp.float32)
            inv_freq = 1.0 / 10000.0 ** (half_idx / DIM_HEAD)
            t = jnp.arange(n, dtype=jnp.float32)
            freqs = t[:, None] * inv_freq[None, :]
            freqs = jnp.concatenate([freqs, freqs], axis=-1)
            base = (half_idx + 0.4 * DIM_HEAD) / (1.4 * DIM_HEAD)
            power = (t - n // 2) / float(WINDOW // 2)
            scale = base[None, :] ** power[:, None]
            scale = jnp.concatenate([scale, scale], axis=-1)
            cos, sin = (jnp.cos(freqs), jnp.sin(freqs))
            q = q * cos * scale + rotate_half(q) * sin * scale
            k = k * cos / scale + rotate_half(k) * sin / scale
            return (q, k)

        def local_attention(q, k, v):
            b, h, n, d = q.shape
            w = n // WINDOW
            bq = q.reshape(b, h, w, WINDOW, d) * QK_SCALE
            bk = k.reshape(b, h, w, WINDOW, d)
            bv = v.reshape(b, h, w, WINDOW, d)

            def look_around(t):
                p = jnp.pad(t, ((0, 0), (0, 0), (1, 0), (0, 0), (0, 0)))
                return jnp.concatenate([p[:, :, :w], p[:, :, 1:]], axis=3)
            bk, bv = (look_around(bk), look_around(bv))
            bt = jnp.arange(n).reshape(w, WINDOW)
            btp = jnp.pad(bt, ((1, 0), (0, 0)), constant_values=-1)
            btk = jnp.concatenate([btp[:w], btp[1:]], axis=1)
            sim = jnp.einsum('bhwid,bhwjd->bhwij', bq, bk)
            i = bt[:, :, None]
            j = btk[:, None, :]
            mask = (i < j) | (i > j + WINDOW) | (j == -1)
            sim = jnp.where(mask, -jnp.finfo(sim.dtype).max, sim)
            attn = jax.nn.softmax(sim, axis=-1)
            out = jnp.einsum('bhwij,bhwjd->bhwid', attn, bv)
            return out.reshape(b, h, n, d)

        def _layer(x, wqkv, qs, ksc, wo, lg, lb, w1, b1, w2, b2):
            b, n, _ = x.shape
            h = shift_token(x)
            qkv = h @ wqkv
            q, k, v = jnp.split(qkv, 3, axis=-1)
            to_heads = lambda t: t.reshape(b, n, HEADS, DIM_HEAD).transpose(0, 2, 1, 3)
            q, k, v = (to_heads(q), to_heads(k), to_heads(v))
            q = l2norm(q) * qs
            k = l2norm(k) * ksc
            q, k = rotary_xpos(q, k)
            o = local_attention(q, k, v)
            o = o.transpose(0, 2, 1, 3).reshape(b, n, INNER)
            x = x + o @ wo
            h = shift_token(x)
            mu = h.mean(-1, keepdims=True)
            var = h.var(-1, keepdims=True)
            h = (h - mu) / jnp.sqrt(var + 1e-05) * lg + lb
            h = h @ w1 + b1
            a, g = jnp.split(h, 2, axis=-1)
            h = a * jax.nn.gelu(g, approximate=False)
            x = x + h @ w2 + b2
            return x
        for l in range(DEPTH):
            x = _layer(x, wqkv[l], q_scale[l], k_scale[l], wo[l], ln_g[l], ln_b[l], w1[l], b1[l], w2[l], b2[l])
        return x

    def _L1_attn_a_ref(x, ln1_g, ln1_b, ln2_g, ln2_b, rms_in_w, Wq, Wk, Wv, conv_q_w, conv_k_w, conv_v_w, Wa, dt_bias, A_log, Wb, Wg, o_norm_w, Wo, W2, b2):
        import jax, jax.numpy as jnp
        import numpy as np
        B, T, D = (4, 256, 128)
        H, Kd = (4, 32)
        Vd = 64
        KEY_DIM, VAL_DIM = (H * Kd, H * Vd)
        CONV = 4
        EPS = 1e-06
        LN_EPS = 1e-05

        def _layernorm(x, g, b):
            m = jnp.mean(x, -1, keepdims=True)
            v = jnp.mean((x - m) ** 2, -1, keepdims=True)
            return (x - m) * jax.lax.rsqrt(v + LN_EPS) * g + b

        def _rmsnorm(x, w):
            return x * jax.lax.rsqrt(jnp.mean(x * x, -1, keepdims=True) + EPS) * w

        def _l2norm(x):
            return x * jax.lax.rsqrt(jnp.sum(x * x, -1, keepdims=True) + EPS)

        def _causal_conv_silu(x, w):
            t = x.shape[1]
            xp = jnp.pad(x, ((0, 0), (CONV - 1, 0), (0, 0)))
            y = xp[:, 0:t, :] * w[:, 0]
            for i in range(1, CONV):
                y = y + xp[:, i:i + t, :] * w[:, i]
            return jax.nn.silu(y)

        def _gated_delta_rule(q, k, v, g, beta):
            qT = jnp.moveaxis(q, 1, 0)
            kT = jnp.moveaxis(k, 1, 0)
            vT = jnp.moveaxis(v, 1, 0)
            gT = jnp.moveaxis(g, 1, 0)
            bT = jnp.moveaxis(beta, 1, 0)
            S0 = jnp.zeros((q.shape[0], H, Kd, Vd), q.dtype)

            def step(S, inp):
                q_t, k_t, v_t, g_t, b_t = inp
                S = S * jnp.exp(g_t)[..., None, None]
                kv = jnp.einsum('bhk,bhkv->bhv', k_t, S)
                delta = (v_t - kv) * b_t[..., None]
                S = S + k_t[..., :, None] * delta[..., None, :]
                o = jnp.einsum('bhk,bhkv->bhv', q_t, S)
                return (S, o)
            _, o = jax.lax.scan(step, S0, (qT, kT, vT, gT, bT))
            return jnp.moveaxis(o, 0, 1)

        def _forward(x, ln1_g, ln1_b, ln2_g, ln2_b, rms_in_w, Wq, Wk, Wv, conv_q_w, conv_k_w, conv_v_w, Wa, dt_bias, A_log, Wb, Wg, o_norm_w, Wo, W2, b2):
            b, t, _ = x.shape
            h = _layernorm(x, ln1_g, ln1_b)
            h = _rmsnorm(h, rms_in_w)
            q = _causal_conv_silu(h @ Wq, conv_q_w).reshape(b, t, H, Kd)
            k = _causal_conv_silu(h @ Wk, conv_k_w).reshape(b, t, H, Kd)
            v = _causal_conv_silu(h @ Wv, conv_v_w).reshape(b, t, H, Vd)
            q = _l2norm(q) * Kd ** (-0.5)
            k = _l2norm(k)
            g = -jnp.exp(A_log) * jax.nn.softplus(h @ Wa + dt_bias)
            beta = jax.nn.sigmoid(h @ Wb)
            o = _gated_delta_rule(q, k, v, g, beta)
            gate = (h @ Wg).reshape(b, t, H, Vd)
            o = _rmsnorm(o, o_norm_w) * jax.nn.silu(gate)
            enc = o.reshape(b, t, VAL_DIM) @ Wo
            x = x + enc
            h2 = _layernorm(x, ln2_g, ln2_b)
            x_out = jax.nn.gelu(h2 @ W2 + b2, approximate=False) + x
            return x_out
        return _forward(x, ln1_g, ln1_b, ln2_g, ln2_b, rms_in_w, Wq, Wk, Wv, conv_q_w, conv_k_w, conv_v_w, Wa, dt_bias, A_log, Wb, Wg, o_norm_w, Wo, W2, b2)

    def _L1_attn_b_ref(input_seq, w, u, bias):
        import jax, jax.numpy as jnp
        import numpy as np
        import math
        INPUT_SIZE = 128
        HIDDEN = 128
        SEQ_LEN = 32
        BATCH = 128

        def _lstm(input_seq, w, u, bias):
            H = u.shape[0]
            B = input_seq.shape[1]
            x_proj = jnp.einsum('sbi,ih->sbh', input_seq, w) + bias

            def step(carry, xp_t):
                h_prev, c_prev = carry
                g = xp_t + h_prev @ u
                gates = jax.nn.sigmoid(g[:, :3 * H])
                c_cand = jnp.tanh(g[:, 3 * H:])
                ig, fg, og = (gates[:, :H], gates[:, H:2 * H], gates[:, 2 * H:])
                c = fg * c_prev + ig * c_cand
                h = og * jnp.tanh(c)
                return ((h, c), h)
            init = (jnp.zeros((B, H), dtype=input_seq.dtype), jnp.zeros((B, H), dtype=input_seq.dtype))
            _, hs = jax.lax.scan(step, init, x_proj)
            return hs
        return _lstm(input_seq, w, u, bias)

    def _L1_ffn_ref(hidden_states, W, b, lora_down, lora_up, down_aux, up_aux):
        import jax, jax.numpy as jnp
        import numpy as np
        ALPHA = 1.0
        lilora_weight = up_aux @ (lora_up @ (lora_down @ down_aux))
        base = jnp.einsum('bsi,oi->bso', hidden_states, W) + b
        delta = jnp.einsum('bsi,oi->bso', hidden_states, lilora_weight)
        return base + ALPHA * delta

    def _L2_attn_a_ref(x, w_in, b_in, w_gx, b_gx, w_ga, b_ga, a_real_param, a_imag_param, w_out, b_out):
        import jax, jax.numpy as jnp
        import numpy as np
        B, S, D_IN = (4, 512, 128)
        D_HID = 256
        D_INNER = D_HID // 2
        NB = 8
        LOG_A_SCALE = -8.0
        R_MIN, R_MAX = (0.9, 0.999)

        def _bdl(x, w, b):
            Bb, Ss, d = x.shape
            nb, bin_, bout = w.shape
            xb = x.reshape(Bb, Ss, nb, bin_)
            y = jnp.einsum('bsni,nio->bsno', xb, w) + b.reshape(nb, bout)
            return y.reshape(Bb, Ss, nb * bout)

        def _reference_tuple_inner(x, w_in, b_in, w_gx, b_gx, w_ga, b_ga, a_real_param, a_imag_param, w_out, b_out):
            xh = x @ w_in + b_in
            gate_x = jax.nn.sigmoid(_bdl(xh, w_gx, b_gx))
            gate_a = jax.nn.sigmoid(_bdl(xh, w_ga, b_ga))
            log_a = LOG_A_SCALE * gate_a * jax.nn.softplus(a_real_param)
            log_a_imag = a_imag_param * gate_a
            a = jnp.exp(jax.lax.complex(log_a, log_a_imag))
            xc = jax.lax.complex(xh[..., :D_INNER], xh[..., D_INNER:])
            xc = gate_x * xc
            norm = jnp.sqrt(jnp.maximum(1.0 - jnp.exp(2.0 * log_a), 1e-06))
            xc = norm * xc

            def combine(l, r):
                return (r[0] * l[0], r[0] * l[1] + r[1])
            _, h = jax.lax.associative_scan(combine, (a, xc), axis=1)
            h_m = jnp.concatenate([h.real, h.imag], axis=-1)
            y = h_m @ w_out + b_out
            h_last = h_m[:, -1]
            return (y, h_last)
        return _reference_tuple_inner(x, w_in, b_in, w_gx, b_gx, w_ga, b_ga, a_real_param, a_imag_param, w_out, b_out)[0]

    def _L2_attn_b_ref(x, W_qkv, b_qkv):
        import jax, jax.numpy as jnp
        import numpy as np
        import math
        DIM = 128
        ATTN_DIM = 128
        B, S = (2, 512)
        b, s, d = x.shape
        qkv = jnp.einsum('bsd,ed->bse', x, W_qkv) + b_qkv
        q, k, v = jnp.split(qkv, 3, axis=-1)
        score = jnp.einsum('bqd,bkd->bqk', q, k)
        causal = jnp.tril(jnp.ones((s, s), dtype=bool))
        score = jnp.where(causal, score, -jnp.inf)
        attn = jax.nn.softmax(score / math.sqrt(ATTN_DIM), axis=-1)
        y = jnp.einsum('bqk,bkd->bqd', attn, v)
        return y

    def _L2_ffn_ref(x, W_r, W_k, W_v, mu_r, mu_k):
        import jax, jax.numpy as jnp
        import numpy as np
        DIM = 128

        def _reference_tuple_inner(x, W_r, W_k, W_v, mu_r, mu_k):
            B, T, C = x.shape
            x_prev = jnp.concatenate([jnp.zeros((B, 1, C), x.dtype), x[:, :-1, :]], axis=1)
            xr = mu_r * x + (1.0 - mu_r) * x_prev
            xk = mu_k * x + (1.0 - mu_k) * x_prev
            r = jax.nn.sigmoid(jnp.einsum('btc,dc->btd', xr, W_r))
            k = jnp.einsum('btc,dc->btd', xk, W_k)
            k_act = jnp.square(jax.nn.relu(k))
            out = r * jnp.einsum('btc,dc->btd', k_act, W_v)
            new_state = x[:, -1, :]
            return (out, new_state)
        return _reference_tuple_inner(x, W_r, W_k, W_v, mu_r, mu_k)[0]

    def _L3_attn_a_ref(x, in_proj_w, in_proj_b, conv_w, conv_b, A_log, D, x_proj_w, dt_proj_w, dt_proj_b, out_proj_w, out_proj_b):
        import jax, jax.numpy as jnp
        import numpy as np
        from jax import lax
        D_MODEL = 128
        D_STATE = 16
        D_CONV = 4
        EXPAND = 2
        D_INNER = D_MODEL * EXPAND
        DT_RANK = 64
        BATCH = 2
        SEQ = 512
        DT_MIN, DT_MAX = (0.001, 0.1)
        b, L, _ = x.shape
        xz = x @ in_proj_w.T + in_proj_b
        x_in, z = jnp.split(xz, 2, axis=-1)
        x_pad = jnp.pad(x_in, ((0, 0), (D_CONV - 1, 0), (0, 0)))
        x_conv = conv_b
        x_conv = sum((x_pad[:, k:k + L, :] * conv_w[None, None, :, k] for k in range(D_CONV))) + conv_b
        x_conv = jax.nn.silu(x_conv)
        x_dbl = x_conv @ x_proj_w.T
        dt_low = x_dbl[..., :DT_RANK]
        Bm = x_dbl[..., DT_RANK:DT_RANK + D_STATE]
        Cm = x_dbl[..., DT_RANK + D_STATE:]
        dt = jax.nn.softplus(dt_low @ dt_proj_w.T + dt_proj_b)
        A = -jnp.exp(A_log).T
        safe_A = jnp.where(jnp.abs(A) < 1e-06, jnp.ones_like(A), A)

        def step(h, inp):
            xt, dtt, Bt, Ct = inp
            A_bar = jnp.exp(dtt[..., None] * A)
            B_bar = (A_bar - 1.0) / safe_A * Bt[:, None, :]
            h = A_bar * h + B_bar * xt[..., None]
            y = jnp.einsum('bds,bs->bd', h, Ct) + D * xt
            return (h, y)
        xs = (jnp.swapaxes(x_conv, 0, 1), jnp.swapaxes(dt, 0, 1), jnp.swapaxes(Bm, 0, 1), jnp.swapaxes(Cm, 0, 1))
        h0 = jnp.zeros((b, D_INNER, D_STATE), x.dtype)
        _, ys = lax.scan(step, h0, xs)
        y = jnp.swapaxes(ys, 0, 1) * jax.nn.silu(z)
        return y @ out_proj_w.T + out_proj_b

    def _L3_attn_b_ref(X, W_q, W_k, W_v, W_o):
        import jax, jax.numpy as jnp
        import numpy as np
        B, T, D, H = (2, 256, 128, 16)
        DH = D // H
        ROPE_BASE = 10000.0

        def _rope(Xh, cos, sin):
            x0 = Xh[..., 0::2]
            x1 = Xh[..., 1::2]
            r0 = cos * x0 - sin * x1
            r1 = sin * x0 + cos * x1
            return jnp.stack((r0, r1), axis=-1).reshape(Xh.shape)
        b, t, d = X.shape
        Q = X @ W_q.T
        K = X @ W_k.T
        V = X @ W_v.T
        Qh = Q.reshape(b, t, H, DH).transpose(0, 2, 1, 3)
        Kh = K.reshape(b, t, H, DH).transpose(0, 2, 1, 3)
        Vh = V.reshape(b, t, H, DH).transpose(0, 2, 1, 3)
        theta = ROPE_BASE ** (-2.0 * jnp.arange(DH // 2, dtype=jnp.float32) / DH)
        pos = jnp.arange(t, dtype=jnp.float32)
        angles = pos[:, None] * theta[None, :]
        cos = jnp.cos(angles).astype(Qh.dtype)
        sin = jnp.sin(angles).astype(Qh.dtype)
        Qr = _rope(Qh, cos, sin)
        Kr = _rope(Kh, cos, sin)
        scores = jnp.einsum('bhqd,bhkd->bhqk', Qr, Kr) * DH ** (-0.5)
        causal = jnp.triu(jnp.ones((t, t), dtype=bool), 1)
        neg = jnp.finfo(scores.dtype).min
        scores = jnp.where(causal[None, None], neg, scores)
        pattern = jax.nn.softmax(scores, axis=-1)
        heads = jnp.einsum('bhqk,bhkd->bhqd', pattern, Vh)
        out = heads.transpose(0, 2, 1, 3).reshape(b, t, d)
        return out @ W_o.T

    def _L3_ffn_ref(x, Wc, bc, W1, b1, W2, b2):
        import jax, jax.numpy as jnp
        import numpy as np
        DM, NEXPERTS, SETS, ESIZE = (128, 32, 4, 32)
        B, S = (2, 1024)
        b, s, d = x.shape
        g = Wc.shape[1]
        grouped = x.reshape(b, s // g, g, d)
        logits = jnp.einsum('bntd,des->bntes', grouped, Wc) + bc
        tie = jnp.linspace(0.0, 1e-06, g, dtype=x.dtype).reshape(-1, 1, 1)
        logits = logits + tie
        perm = (logits == jnp.max(logits, axis=-3, keepdims=True)).astype(x.dtype)
        permuted = jnp.einsum('bntd,bntes->bnesd', grouped, perm)
        inner = jax.nn.relu(jnp.einsum('bnesd,esdf->bnesf', permuted, W1) + b1)
        result_permuted = jnp.einsum('bnesf,esdf->bnesd', inner, W2) + b2
        result = jnp.einsum('bnesd,bntes->bntd', result_permuted, perm)
        return result.reshape(b, s, d)
    x = L0_attn_a_x
    x = x + _L0_attn_a_ref(_layernorm(x, axis=-1), L0_attn_a_ln1_w, L0_attn_a_ln1_b, L0_attn_a_wq, L0_attn_a_wk, L0_attn_a_wv, L0_attn_a_wo, L0_attn_a_bo, L0_attn_a_ln2_w, L0_attn_a_ln2_b, L0_attn_a_w1, L0_attn_a_w2)
    x = x + _L0_ffn_ref(_layernorm(x, axis=-1), L0_ffn_wqkv, L0_ffn_q_scale, L0_ffn_k_scale, L0_ffn_wo, L0_ffn_ln_g, L0_ffn_ln_b, L0_ffn_w1, L0_ffn_b1, L0_ffn_w2, L0_ffn_b2)
    x = x + _L0_attn_b_ref(_layernorm(x, axis=-1), L0_attn_b_Wq, L0_attn_b_Wk, L0_attn_b_Wv, L0_attn_b_Wg, L0_attn_b_Wo, L0_attn_b_gn_gamma, L0_attn_b_gn_beta)
    x = x + _L0_ffn_ref(_layernorm(x, axis=-1), L0_ffn_wqkv, L0_ffn_q_scale, L0_ffn_k_scale, L0_ffn_wo, L0_ffn_ln_g, L0_ffn_ln_b, L0_ffn_w1, L0_ffn_b1, L0_ffn_w2, L0_ffn_b2)
    x = x + _L1_attn_a_ref(_layernorm(x, axis=-1), L1_attn_a_ln1_g, L1_attn_a_ln1_b, L1_attn_a_ln2_g, L1_attn_a_ln2_b, L1_attn_a_rms_in_w, L1_attn_a_Wq, L1_attn_a_Wk, L1_attn_a_Wv, L1_attn_a_conv_q_w, L1_attn_a_conv_k_w, L1_attn_a_conv_v_w, L1_attn_a_Wa, L1_attn_a_dt_bias, L1_attn_a_A_log, L1_attn_a_Wb, L1_attn_a_Wg, L1_attn_a_o_norm_w, L1_attn_a_Wo, L1_attn_a_W2, L1_attn_a_b2)
    x = x + _L1_ffn_ref(_layernorm(x, axis=-1), L1_ffn_W, L1_ffn_b, L1_ffn_lora_down, L1_ffn_lora_up, L1_ffn_down_aux, L1_ffn_up_aux)
    x = x + _L1_attn_b_ref(_layernorm(x, axis=-1), L1_attn_b_w, L1_attn_b_u, L1_attn_b_bias)
    x = x + _L1_ffn_ref(_layernorm(x, axis=-1), L1_ffn_W, L1_ffn_b, L1_ffn_lora_down, L1_ffn_lora_up, L1_ffn_down_aux, L1_ffn_up_aux)
    x = x + _L2_attn_a_ref(_layernorm(x, axis=-1), L2_attn_a_w_in, L2_attn_a_b_in, L2_attn_a_w_gx, L2_attn_a_b_gx, L2_attn_a_w_ga, L2_attn_a_b_ga, L2_attn_a_a_real_param, L2_attn_a_a_imag_param, L2_attn_a_w_out, L2_attn_a_b_out)
    x = x + _L2_ffn_ref(_layernorm(x, axis=-1), L2_ffn_W_r, L2_ffn_W_k, L2_ffn_W_v, L2_ffn_mu_r, L2_ffn_mu_k)
    x = x + _L2_attn_b_ref(_layernorm(x, axis=-1), L2_attn_b_W_qkv, L2_attn_b_b_qkv)
    x = x + _L2_ffn_ref(_layernorm(x, axis=-1), L2_ffn_W_r, L2_ffn_W_k, L2_ffn_W_v, L2_ffn_mu_r, L2_ffn_mu_k)
    x = x + _L3_attn_a_ref(_layernorm(x, axis=-1), L3_attn_a_in_proj_w, L3_attn_a_in_proj_b, L3_attn_a_conv_w, L3_attn_a_conv_b, L3_attn_a_A_log, L3_attn_a_D, L3_attn_a_x_proj_w, L3_attn_a_dt_proj_w, L3_attn_a_dt_proj_b, L3_attn_a_out_proj_w, L3_attn_a_out_proj_b)
    x = x + _L3_ffn_ref(_layernorm(x, axis=-1), L3_ffn_Wc, L3_ffn_bc, L3_ffn_W1, L3_ffn_b1, L3_ffn_W2, L3_ffn_b2)
    x = x + _L3_attn_b_ref(_layernorm(x, axis=-1), L3_attn_b_W_q, L3_attn_b_W_k, L3_attn_b_W_v, L3_attn_b_W_o)
    x = x + _L3_ffn_ref(_layernorm(x, axis=-1), L3_ffn_Wc, L3_ffn_bc, L3_ffn_W1, L3_ffn_b1, L3_ffn_W2, L3_ffn_b2)
    return x

_drawn_inputs = setup_inputs


def setup_inputs(seed=0):
    import zlib

    import numpy as np

    out = dict(_drawn_inputs(seed))
    spreads = {'L0_attn_a_ln1_w': (1.0, 0.6),
     'L0_attn_a_ln1_b': (0.0, 0.8),
     'L0_attn_a_bo': (0.0, 0.1),
     'L0_attn_a_ln2_w': (1.0, 0.6),
     'L0_attn_a_ln2_b': (0.0, 0.8),
     'L0_attn_b_gn_gamma': (1.0, 0.2),
     'L0_attn_b_gn_beta': (0.0, 0.319),
     'L0_ffn_q_scale': (1.0, 0.6),
     'L0_ffn_k_scale': (1.0, 0.6),
     'L0_ffn_ln_g': (1.0, 0.6),
     'L0_ffn_ln_b': (0.0, 0.8),
     'L0_ffn_b1': (0.0, 0.8),
     'L0_ffn_b2': (0.0, 0.1),
     'L1_attn_a_ln1_g': (1.0, 0.6),
     'L1_attn_a_ln1_b': (0.0, 0.8),
     'L1_attn_a_ln2_g': (1.0, 0.6),
     'L1_attn_a_ln2_b': (0.0, 0.8),
     'L1_attn_a_rms_in_w': (1.0, 0.6),
     'L1_attn_a_o_norm_w': (1.0, 0.6),
     'L1_attn_a_b2': (0.0, 0.772),
     'L2_attn_a_b_in': (0.0, 0.601),
     'L2_attn_a_b_gx': (0.0, 2.0),
     'L2_attn_a_b_ga': (0.0, 2.0),
     'L2_attn_a_b_out': (0.0, 1.073),
     'L3_attn_a_in_proj_b': (0.0, 0.8),
     'L3_attn_a_conv_b': (0.0, 0.8),
     'L3_attn_a_D': (1.0, 0.6),
     'L3_attn_a_out_proj_b': (0.0, 2.0)}
    factors = {'L0_attn_a_wq': 8.0,
     'L0_attn_a_wk': 8.0,
     'L0_attn_a_wv': 3.503,
     'L0_attn_a_wo': 3.079,
     'L0_ffn_w1': 5.272,
     'L0_ffn_w2': 5.204,
     'L1_attn_a_Wq': 8.0,
     'L1_attn_a_Wk': 8.0,
     'L1_attn_a_Wv': 8.0,
     'L1_attn_a_conv_q_w': 8.0,
     'L1_attn_a_conv_k_w': 8.0,
     'L1_attn_a_conv_v_w': 8.0,
     'L1_attn_a_Wa': 8.0,
     'L1_attn_a_dt_bias': 8.0,
     'L1_attn_a_A_log': 8.0,
     'L1_attn_a_Wb': 8.0,
     'L1_attn_a_Wg': 8.0,
     'L1_attn_a_Wo': 8.0,
     'L1_attn_b_u': 8.0,
     'L1_attn_b_bias': 8.0,
     'L1_ffn_b': 6.559,
     'L1_ffn_lora_down': 8.0,
     'L1_ffn_lora_up': 8.0,
     'L1_ffn_down_aux': 8.0,
     'L1_ffn_up_aux': 8.0,
     'L2_attn_b_b_qkv': 64.0,
     'L2_ffn_W_r': 7.859,
     'L2_ffn_mu_r': 8.0,
     'L2_ffn_mu_k': 3.061,
     'L3_attn_a_in_proj_w': 8.0,
     'L3_attn_a_conv_w': 8.0,
     'L3_attn_a_A_log': 8.0,
     'L3_attn_a_x_proj_w': 8.0,
     'L3_attn_a_dt_proj_w': 8.0,
     'L3_attn_a_dt_proj_b': 8.0,
     'L3_attn_a_out_proj_w': 8.0,
     'L3_ffn_Wc': 22.528,
     'L3_ffn_W1': 39.992,
     'L3_ffn_b1': 200.0,
     'L3_ffn_W2': 32.976,
     'L3_ffn_b2': 200.0,
     'L3_attn_b_W_q': 8.0,
     'L3_attn_b_W_k': 8.0,
     'L3_attn_b_W_v': 8.0,
     'L3_attn_b_W_o': 8.0}
    for name, (base, spread) in spreads.items():
        noise = np.random.default_rng([zlib.crc32(name.encode()), seed]).standard_normal(out[name].shape)
        drawn = base * np.exp(spread * noise) if base else spread * noise
        out[name] = jnp.asarray(drawn.astype(out[name].dtype))
    for name, factor in factors.items():
        out[name] = (out[name] * factor).astype(out[name].dtype)
    return out
```

```python
from contextlib import ExitStack

import numpy as np

import concourse.bass as bass
from concourse import mybir

F32 = mybir.dt.float32
ALU = mybir.AluOpType
ACT = mybir.ActivationFunctionType
AX = mybir.AxisListType.X

P = 128
SEQS = 8
LEN = 256
TOK = SEQS * LEN
W = 512
NJ = TOK // W
SPW = W // LEN
TPW = W // P
LN_EPS = 1e-5


class Stage:

    def __init__(self, nc, name):
        self.nc, self.name = nc, name
        self.stack = ExitStack()
        self.sems = []

    def signals(self, names, prefix=""):
        sems = [self.nc.alloc_semaphore(f"{self.name}_{prefix}{s}") for s in names.split()]
        self.sems += sems
        return sems

    def sb(self, name, shape):
        return self.stack.enter_context(self.nc.sbuf_tensor(f"{self.name}_{name}", shape, F32))

    def end(self):
        self.stack.close()
        self.nc.clear_and_free_semaphores(self.sems)
        self.nc.all_engine_barrier()


def at(k, j, n=NJ):
    return k * n + j + 1


def toks(j, w=W):
    return slice(j * w, (j + 1) * w)


class LayerNorm:

    def __init__(self, K, st, prefix, affine=False):
        self.K, self.affine = K, affine
        (self.mean_ready, self.centered, self.square_ready, self.var_ready, self.log_ready, self.rstd_ready,
         self.scaled, self.norm_ready) = st.signals(
            "mean_ready centered square_ready var_ready log_ready rstd_ready scaled norm_ready", prefix)
        self.xc, self.sq = K.ln_xc, K.ln_sq

    def pe(self, pe, k, src, wait_src, wait_var_bank=None):
        nc, K = self.K.nc, self.K
        for j in range(NJ):
            wait_src(j)
            nc.tensor.matmul(K.ps[:, j, :], K.mean_mat, src[:, toks(j)], start=True, stop=True)\
                .then_inc(self.mean_ready, 1)
        for j in range(NJ):
            pe.wait_ge(self.square_ready, at(k, j))
            if wait_var_bank is not None:
                wait_var_bank(j)
            nc.tensor.matmul(K.ps[:, 4 + j, :], K.mean_mat, self.sq[:, toks(j)], start=True, stop=True)\
                .then_inc(self.var_ready, 1)

    def act(self, act, k, out=None, weight=None, bias=None):
        nc = self.K.nc
        for j in range(NJ):
            act.wait_ge(self.centered, at(k, j))
            nc.scalar.activation(self.sq[:, toks(j)], self.xc[:, toks(j)], ACT.Square).then_inc(self.square_ready, 1)
        for j in range(NJ + 2):
            if j < NJ:
                act.wait_ge(self.var_ready, at(k, j))
                nc.scalar.activation(self.sq[:, toks(j)], self.K.ps[:, 4 + j, :], ACT.Ln, bias=self.K.eps_ln)\
                    .then_inc(self.log_ready, 1)
            if 1 <= j <= NJ:
                act.wait_ge(self.log_ready, at(k, j - 1))
                nc.scalar.activation(self.sq[:, toks(j - 1)], self.sq[:, toks(j - 1)], ACT.Exp, scale=-0.5)\
                    .then_inc(self.rstd_ready, 1)
            if self.affine and j >= 2:
                act.wait_ge(self.scaled, at(k, j - 2))
                nc.scalar.activation(out[:, toks(j - 2)], self.xc[:, toks(j - 2)], ACT.Identity, bias=bias,
                                     scale=weight).then_inc(self.norm_ready, 1)

    def dve(self, dve, k, src, out=None):
        nc = self.K.nc
        for j in range(NJ):
            dve.wait_ge(self.mean_ready, at(k, j))
            nc.vector.tensor_tensor(self.xc[:, toks(j)], src[:, toks(j)], self.K.ps[:, j, :], ALU.subtract)\
                .then_inc(self.centered, 1)
        for j in range(NJ):
            dve.wait_ge(self.rstd_ready, at(k, j))
            dst = self.xc if self.affine else out
            nc.vector.tensor_tensor(dst[:, toks(j)], self.xc[:, toks(j)], self.sq[:, toks(j)], ALU.mult)\
                .then_inc(self.scaled if self.affine else self.norm_ready, 1)


def _log1p_series(degree=5):
    top = 1.0 / 9
    nodes = top / 2 * (1 + np.cos(np.pi * (np.arange(degree + 1) + 0.5) / (degree + 1)))
    s = np.sqrt(nodes)
    return [float(c) for c in np.polyfit(nodes, 2 * np.arctanh(s) / s, degree)]


ATANH = _log1p_series()
PI_IN = float(np.nextafter(np.float32(np.pi), np.float32(0)))


class Attention:

    def __init__(self, K, st, groups, heads, dv, scale, prefix="att_"):
        self.K, self.groups, self.G, self.dv, self.scale = K, groups, heads, dv, scale
        (self.sim_ready, self.masked, self.max_ready, self.p_ready, self.pt_ready, self.pt_copied, self.o_ready,
         self.recip, self.o_copied) = st.signals(
            "sim_ready masked max_ready p_ready pt_ready pt_copied o_ready recip o_copied", prefix)
        self.s = st.sb(prefix + "s", [P, 3, heads, LEN])
        self.pt = st.sb(prefix + "pt", [P, 2, heads * 2 * P])
        self.stat = st.sb(prefix + "stat", [P, 4, 3, heads])
        self.n = len(groups)

    def sim(self, g):
        flat = self.K.ps[:, 2 * (g % 2):2 * (g % 2) + 2, :].rearrange("p b n -> p (b n)")
        return flat[:, 0:self.G * LEN].rearrange("p (h n) -> p h n", n=LEN)

    def moved(self, g):
        return self.K.ps[:, 4:6, :].rearrange("p b n -> p (b n)")[:, 0:self.G * self.groups[g][1] * P]

    def pe(self, pe, base, wait_in):
        nc, K = self.K.nc, self.K

        def scores(g):
            wait_in(g)
            if g >= 2:
                pe.wait_ge(self.masked, base + (g - 1))
            qk, tiles = self.groups[g][0:2]
            for h in range(self.G):
                mm = nc.tensor.matmul(self.sim(g)[:, h, 0:tiles * P], qk[h][0], qk[h][1], start=True, stop=True)
            mm.then_inc(self.sim_ready, 1)

        def turn(g):
            pe.wait_ge(self.p_ready, base + (g + 1))
            tiles = self.groups[g][1]
            for h in range(self.G):
                for kt in range(tiles):
                    mm = nc.tensor.transpose(self.moved(g)[:, toks(h * tiles + kt, P)],
                                             self.s[:, g % 3, h, toks(kt, P)], K.ident)
            mm.then_inc(self.pt_ready, 1)

        def values(g):
            pe.wait_ge(self.pt_copied, base + (g + 1))
            if g >= 2:
                pe.wait_ge(self.o_copied, base + (g - 1))
            tiles, v = self.groups[g][1], self.groups[g][3]
            for h in range(self.G):
                for kt in range(tiles):
                    mm = nc.tensor.matmul(K.ps[:, 6 + g % 2, h * self.dv:(h + 1) * self.dv],
                                          self.pt[:, g % 2, toks(h * tiles + kt, P)], v[h][kt],
                                          start=(kt == 0), stop=(kt == tiles - 1))
            mm.then_inc(self.o_ready, 1)

        for g in range(min(3, self.n)):
            scores(g)
        for g in range(self.n):
            turn(g)
            if g + 3 < self.n:
                scores(g + 3)
            values(g)

    def act(self, act, base):
        nc = self.K.nc

        def exps(g):
            act.wait_ge(self.max_ready, base + (g + 1))
            n = self.groups[g][1] * P
            for h in range(self.G):
                a = nc.scalar.activation(self.s[:, g % 3, h, 0:n], self.s[:, g % 3, h, 0:n], ACT.Exp,
                                         bias=self.stat[:, g % 4, 0, h:h + 1], accum_out=self.stat[:, g % 4, 1, h:h + 1])
            a.then_inc(self.p_ready, 1)

        exps(0)
        if self.n > 1:
            exps(1)
        for g in range(self.n):
            act.wait_ge(self.pt_ready, base + (g + 1))
            if g >= 2:
                act.wait_ge(self.o_ready, base + (g - 1))
            m = self.moved(g)
            nc.scalar.activation(self.pt[:, g % 2, 0:m.shape[1]], m, ACT.Copy).then_inc(self.pt_copied, 1)
            if g + 2 < self.n:
                exps(g + 2)

    def dve(self, dve, base):
        nc = self.K.nc

        def mask_and_max(g):
            dve.wait_ge(self.sim_ready, base + (g + 1))
            if g >= 3:
                dve.wait_ge(self.pt_ready, base + (g - 2))
            n = self.groups[g][1] * P
            mask = self.groups[g][2].unsqueeze(1).to_broadcast([P, self.G, n])
            nc.vector.scalar_tensor_tensor(self.s[:, g % 3, :, 0:n], self.sim(g)[:, :, 0:n], self.scale, mask,
                                           ALU.mult, ALU.add).then_inc(self.masked, 1)
            dve.wait_ge(self.masked, base + (g + 1))
            nc.vector.tensor_reduce(self.stat[:, g % 4, 0, :], self.s[:, g % 3, :, 0:n], AX, ALU.max, negate=True)\
                .then_inc(self.max_ready, 1)

        for g in range(min(3, self.n)):
            mask_and_max(g)
        for g in range(self.n):
            if g + 3 < self.n:
                mask_and_max(g + 3)
            dve.wait_ge(self.p_ready, base + (g + 1))
            nc.vector.reciprocal(self.stat[:, g % 4, 2, :], self.stat[:, g % 4, 1, :]).then_inc(self.recip, 1)
            dve.wait_ge(self.recip, base + (g + 1))
            dve.wait_ge(self.o_ready, base + (g + 1))
            o = self.K.ps[:, 6 + g % 2, 0:self.G * self.dv].rearrange("p (h d) -> p h d", d=self.dv)
            nc.vector.tensor_tensor(self.groups[g][4], o,
                                    self.stat[:, g % 4, 2, :].unsqueeze(2).to_broadcast([P, self.G, self.dv]),
                                    ALU.mult).then_inc(self.o_copied, 1)


def linear_attention_stage(K, depth=6):
    nc = K.nc
    HD, HEADS, CH = 16, 8, 4
    st = Stage(nc, "linattn")
    (st.wa_ready, st.wb_ready, st.q_ready, st.q_max, st.q_shift, st.q_exp, st.q_sum, st.q_rsum, st.q_soft,
     st.q_moved, st.k_ready, st.k_max, st.k_exp, st.k_rsum, st.k_moved, st.k_copied, st.v_ready,
     st.v_copied, st.q_copied, st.ctx_ready, st.ctx_masked, st.attn_ready, st.attn_copied,
     st.proj_ready, st.y_attn, st.hid_ready, st.hid_leak, st.hid_act, st.mlp_ready, st.y_ready,
     st.x_done) = st.signals(
        "wa_ready wb_ready q_ready q_max q_shift q_exp q_sum q_rsum q_soft q_moved k_ready k_max k_exp k_rsum "
        "k_moved k_copied v_ready v_copied q_copied ctx_ready ctx_masked attn_ready attn_copied "
        "proj_ready y_attn hid_ready hid_leak hid_act mlp_ready y_ready x_done")
    outer = LayerNorm(K, st, "outer_")
    inner = LayerNorm(K, st, "inner_", affine=True)
    wa = st.sb("wa", [P, K.d["linattn_wa"].shape[2]])
    wb = st.sb("wb", [P, K.d["linattn_wb"].shape[2]])
    wq, wk, wv, wo = (wa[:, toks(i, P)] for i in range(4))
    ln1w, ln1b, bo = (wa[:, 512 + i:513 + i] for i in range(3))
    w1 = [wb[:, toks(c, P)] for c in range(CH)]
    w2 = [wb[:, toks(CH + c, P)] for c in range(CH)]
    ln2w, ln2b = (wb[:, 2 * CH * P + i:2 * CH * P + i + 1] for i in range(2))
    y, h = K.y, K.h
    qs = st.sb("qs", [P, TOK])
    qst = st.sb("qst", [P, NJ, 64])
    ke = st.sb("ke", [P, TOK])
    kst = st.sb("kst", [P, NJ, 3, SPW])
    kt = st.sb("kt", [P, TOK])
    vt = st.sb("vt", [P, TOK])
    qt = st.sb("qt", [P, TOK])
    ctx = st.sb("ctx", [P, NJ, SPW, P])
    at_ = st.sb("at", [P, TOK])
    hid = st.sb("hid", [P, CH, TOK])
    leak = st.sb("leak", [P, TOK])
    heads = TPW * HEADS

    def grouped(ap):
        return ap.rearrange("p (g f) -> p g f", f=HD)

    with nc.Block() as block:
        @block.sync
        def _(sp):
            def load(what, to, l, done):
                sp.dma_start(to[:, :], K.d[what][bass.ds(l, 1), :, :].rearrange("a p n -> (a p) n")).then_inc(done, 16)

            load("linattn_wa", wa, 0, st.wa_ready)
            load("linattn_wb", wb, 0, st.wb_ready)
            with sp.Fori(0, depth - 1) as l:
                sp.wait_ge(st.y_attn, (l + 1) * NJ)
                load("linattn_wa", wa, l + 1, st.wa_ready)
                sp.wait_ge(st.y_ready, (l + 2) * NJ)
                load("linattn_wb", wb, l + 1, st.wb_ready)

        @block.tensor
        def _(pe):
            outer.pe(pe, 0, K.x, lambda j: None)
            with pe.Fori(0, depth) as l:
                inner.pe(pe, 2 * l, y, lambda j: pe.wait_ge(st.y_ready, at(l, j)))
                pe.wait_ge(st.wa_ready, 16 * l + 16)
                for j in range(NJ):
                    pe.wait_ge(inner.norm_ready, at(2 * l, j))
                    for t in range(TPW):
                        mm = nc.tensor.matmul(K.ps[:, j, toks(t, P)], h[:, toks(TPW * j + t, P)], wq,
                                              start=True, stop=True)
                    mm.then_inc(st.q_ready, 1)
                for j in range(NJ):
                    nc.tensor.matmul(K.ps[:, 4 + j, :], wk, h[:, toks(j)], start=True, stop=True)\
                        .then_inc(st.k_ready, 1)
                for j in range(NJ):
                    pe.wait_ge(st.q_shift, at(l, j))
                    for t in range(TPW):
                        mm = nc.tensor.matmul(K.ps[:, j, toks(t, P)], h[:, toks(TPW * j + t, P)], wv,
                                              start=True, stop=True)
                    mm.then_inc(st.v_ready, 1)
                for j in range(NJ):
                    pe.wait_ge(st.k_exp, at(l, j))
                    for t in range(TPW):
                        mm = nc.tensor.transpose(K.ps[:, 4 + j, toks(t, P)], ke[:, toks(TPW * j + t, P)], K.ident)
                    mm.then_inc(st.k_moved, 1)
                for j in range(NJ):
                    pe.wait_ge(st.q_soft, at(l, j))
                    pe.wait_ge(st.v_copied, at(l, j))
                    for t in range(TPW):
                        mm = nc.tensor.transpose(K.ps[:, j, toks(t, P)], qs[:, toks(TPW * j + t, P)], K.ident)
                    mm.then_inc(st.q_moved, 1)
                for j in range(NJ):
                    pe.wait_ge(st.k_copied, at(l, j))
                    for s in range(SPW):
                        for t in range(2):
                            tile = toks(TPW * j + 2 * s + t, P)
                            mm = nc.tensor.matmul(K.ps[:, 4 + j, toks(s, P)], kt[:, tile], vt[:, tile],
                                                  start=(t == 0), stop=(t == 1))
                    mm.then_inc(st.ctx_ready, 1)
                for j in range(NJ):
                    pe.wait_ge(st.ctx_masked, at(l, j))
                    pe.wait_ge(st.q_copied, at(l, j))
                    for s in range(SPW):
                        mm = nc.tensor.matmul(K.ps[:, j, toks(s, LEN)], ctx[:, j, s, :],
                                              qt[:, toks(SPW * j + s, LEN)], start=True, stop=True)
                    mm.then_inc(st.attn_ready, 1)
                for j in range(NJ):
                    pe.wait_ge(st.attn_copied, at(l, j))
                    nc.tensor.matmul(K.ps[:, 4 + j, :], wo, at_[:, toks(j)], start=True, stop=True)\
                        .then_inc(st.proj_ready, 1)
                inner.pe(pe, 2 * l + 1, y, lambda j: pe.wait_ge(st.y_attn, at(l, j)))
                pe.wait_ge(st.wb_ready, 16 * l + 16)
                for c in range(CH + 1):
                    for j in range(NJ):
                        if c < CH:
                            if c == 0:
                                pe.wait_ge(inner.norm_ready, at(2 * l + 1, j))
                            else:
                                pe.wait_ge(st.hid_act, at(CH * l + c - 1, j))
                            nc.tensor.matmul(K.ps[:, j, :], w1[c], h[:, toks(j)], start=True, stop=True)\
                                .then_inc(st.hid_ready, 1)
                        if c > 0:
                            if c == CH:
                                pe.wait_ge(st.hid_act, at(CH * l + c - 1, j))
                            mm = nc.tensor.matmul(K.ps[:, 4 + j, :], w2[c - 1], hid[:, c - 1, toks(j)],
                                                  start=(c == 1), stop=(c == CH))
                            if c == CH:
                                mm.then_inc(st.mlp_ready, 1)

        @block.scalar
        def _(act):
            nc.scalar.preload_act_table_set("natural_log_exp_and_others")
            outer.act(act, 0)
            with act.Fori(0, depth) as l:
                act.wait_ge(st.wa_ready, 16 * l + 16)
                inner.act(act, 2 * l, h, ln1w, ln1b)
                for j in range(NJ):
                    act.wait_ge(st.k_max, at(l, j))
                    for s in range(SPW):
                        a = nc.scalar.activation(ke[:, toks(SPW * j + s, LEN)], K.ps[:, 4 + j, toks(s, LEN)], ACT.Exp,
                                                 bias=kst[:, j, 0, s:s + 1], accum_out=kst[:, j, 1, s:s + 1])
                    a.then_inc(st.k_exp, 1)
                    act.wait_ge(st.q_shift, at(l, j))
                    nc.scalar.activation(qs[:, toks(j)], qs[:, toks(j)], ACT.Exp).then_inc(st.q_exp, 1)
                for j in range(NJ):
                    act.wait_ge(st.v_ready, at(l, j))
                    nc.scalar.activation(vt[:, toks(j)], K.ps[:, j, :], ACT.Copy).then_inc(st.v_copied, 1)
                for j in range(NJ):
                    act.wait_ge(st.q_moved, at(l, j))
                    nc.scalar.activation(qt[:, toks(j)], K.ps[:, j, :], ACT.Copy).then_inc(st.q_copied, 1)
                for j in range(NJ):
                    act.wait_ge(st.attn_ready, at(l, j))
                    nc.scalar.activation(at_[:, toks(j)], K.ps[:, j, :], ACT.Copy).then_inc(st.attn_copied, 1)
                act.wait_ge(st.wb_ready, 16 * l + 16)
                inner.act(act, 2 * l + 1, h, ln2w, ln2b)
                for c in range(CH):
                    for j in range(NJ):
                        act.wait_ge(st.hid_ready, at(CH * l + c, j))
                        nc.scalar.activation(leak[:, toks(j)], K.ps[:, j, :], ACT.Copy, scale=0.01)\
                            .then_inc(st.hid_leak, 1)

        @block.vector
        def _(dve):
            outer.dve(dve, 0, K.x, y)
            dve.wait_ge(outer.norm_ready, NJ)
            dve.sem_inc(st.y_ready, NJ)
            with dve.Fori(0, depth) as l:
                inner.dve(dve, 2 * l, y)
                dve.wait_ge(st.wa_ready, 16 * l + 16)
                for j in range(NJ):
                    dve.wait_ge(st.q_ready, at(l, j))
                    nc.vector.tensor_reduce(qst[:, j, 0:heads], grouped(K.ps[:, j, :]), AX, ALU.max)\
                        .then_inc(st.q_max, 1)
                    dve.wait_ge(st.q_max, at(l, j))
                    nc.vector.tensor_tensor(grouped(qs[:, toks(j)]), grouped(K.ps[:, j, :]),
                                            qst[:, j, 0:heads].unsqueeze(2).to_broadcast([P, heads, HD]),
                                            ALU.subtract).then_inc(st.q_shift, 1)
                for j in range(NJ):
                    dve.wait_ge(st.k_ready, at(l, j))
                    nc.vector.tensor_reduce(kst[:, j, 0, :], K.ps[:, 4 + j, :].rearrange("p (s n) -> p s n", n=LEN),
                                            AX, ALU.max, negate=True).then_inc(st.k_max, 1)
                for j in range(NJ):
                    dve.wait_ge(st.q_exp, at(l, j))
                    nc.vector.tensor_reduce(qst[:, j, 32:32 + heads], grouped(qs[:, toks(j)]), AX, ALU.add)\
                        .then_inc(st.q_sum, 1)
                for j in range(NJ):
                    dve.wait_ge(st.q_sum, at(l, j))
                    nc.vector.reciprocal(qst[:, j, 0:heads], qst[:, j, 32:32 + heads]).then_inc(st.q_rsum, 1)
                for j in range(NJ):
                    dve.wait_ge(st.q_rsum, at(l, j))
                    nc.vector.tensor_tensor(grouped(qs[:, toks(j)]), grouped(qs[:, toks(j)]),
                                            qst[:, j, 0:heads].unsqueeze(2).to_broadcast([P, heads, HD]),
                                            ALU.mult).then_inc(st.q_soft, 1)
                for j in range(NJ):
                    dve.wait_ge(st.k_exp, at(l, j))
                    nc.vector.reciprocal(kst[:, j, 2, :], kst[:, j, 1, :]).then_inc(st.k_rsum, 1)
                for j in range(NJ):
                    dve.wait_ge(st.k_moved, at(l, j))
                    nc.vector.tensor_copy(kt[:, toks(j)], K.ps[:, 4 + j, :]).then_inc(st.k_copied, 1)
                for j in range(NJ):
                    dve.wait_ge(st.ctx_ready, at(l, j))
                    dve.wait_ge(st.k_rsum, at(l, j))
                    for s in range(SPW):
                        v = nc.vector.scalar_tensor_tensor(ctx[:, j, s, :], K.ps[:, 4 + j, toks(s, P)],
                                                           kst[:, j, 2, s:s + 1], K.head_mask16,
                                                           ALU.mult, ALU.mult)
                    v.then_inc(st.ctx_masked, 1)
                for j in range(NJ):
                    dve.wait_ge(st.proj_ready, at(l, j))
                    nc.vector.scalar_tensor_tensor(y[:, toks(j)], K.ps[:, 4 + j, :], bo, y[:, toks(j)],
                                                   ALU.add, ALU.add).then_inc(st.y_attn, 1)
                inner.dve(dve, 2 * l + 1, y)
                for c in range(CH):
                    for j in range(NJ):
                        dve.wait_ge(st.hid_leak, at(CH * l + c, j))
                        nc.vector.tensor_tensor(hid[:, c, toks(j)], K.ps[:, j, :], leak[:, toks(j)], ALU.max)\
                            .then_inc(st.hid_act, 1)
                for j in range(NJ):
                    dve.wait_ge(st.mlp_ready, at(l, j))
                    nc.vector.tensor_tensor(y[:, toks(j)], K.ps[:, 4 + j, :], y[:, toks(j)], ALU.add)\
                        .then_inc(st.y_ready, 1)
            for j in range(NJ):
                dve.wait_ge(st.y_ready, at(depth, j))
                nc.vector.tensor_tensor(K.x[:, toks(j)], K.x[:, toks(j)], y[:, toks(j)], ALU.add)\
                    .then_inc(st.x_done, 1)
    st.end()


def window_attention_stage(K, tag):
    nc = K.nc
    DEPTH, DH, GH, QC = 2, 64, 4, 4
    NB = 4
    LAG = 2
    HID = 341
    HC = [(0, 128), (128, 128), (256, HID - 256)]
    st = Stage(nc, f"window{tag}")
    (st.tabs_ready, st.wa_ready, st.wb_ready, st.tab_ready, st.edge, st.y_ready, st.sh_low, st.sh_high,
     st.lin_ready, st.sq_ready, st.lin_read, st.rot_read, st.ss_ready, st.ss_safe, st.ss_log, st.rn_ready,
     st.turned, st.qk_done, st.v_ready, st.v_copied, st.o_turned, st.o_moved, st.proj_ready, st.y_attn,
     st.sh2_low, st.sh2_high, st.hid_a, st.hid_g, st.gelu_done, st.hid_done, st.mlp_ready, st.x_done) = st.signals(
        "tabs_ready wa_ready wb_ready tab_ready edge y_ready sh_low sh_high lin_ready sq_ready "
        "lin_read rot_read ss_ready ss_safe ss_log rn_ready turned qk_done v_ready v_copied "
        "o_turned o_moved proj_ready y_attn sh2_low sh2_high hid_a hid_g gelu_done hid_done "
        "mlp_ready x_done")
    outer = LayerNorm(K, st, "outer_")
    inner = LayerNorm(K, st, "inner_", affine=True)
    wa = st.sb("wa", [P, K.d["window_wa"].shape[2]])
    wb = st.sb("wb", [P, K.d["window_wb"].shape[2]])
    tabs = st.sb("tabs", [P, 4, LEN])
    wqk = []
    for i in range(2 * QC):
        wqk.append((wa[:, toks(2 * i, P)], wa[:, toks(2 * i + 1, P)]))
    o = 4 * QC * P
    wv = wa[:, o:o + 512]
    o += 512
    wo = [wa[:, o + c * P:o + (c + 1) * P] for c in range(QC)]
    o += 512
    scales = [wa[:, o + i:o + i + 1] for i in range(4)]
    w1a = [wb[:, a:a + n] for a, n in HC]
    w1g = [wb[:, HID + a:HID + a + n] for a, n in HC]
    o = 2 * HID
    w2 = [wb[0:n, o + c * P:o + (c + 1) * P] for c, (a, n) in enumerate(HC)]
    o += 3 * P
    ln_w, ln_b, b2 = (wb[:, o + i:o + i + 1] for i in range(3))
    b1a = [wb[0:n, o + 3 + c:o + 4 + c] for c, (a, n) in enumerate(HC)]
    b1g = [wb[0:n, o + 6 + c:o + 7 + c] for c, (a, n) in enumerate(HC)]

    y = K.y
    sh = st.sb("sh", [P, W])
    tab = st.sb("tab", [P, 4, LEN])
    sq = st.sb("sq", [P, NB, W])
    part = st.sb("part", [P, NB, 2, W])
    qk = st.sb("qk", [P, 2 * QC, W])
    vt = st.sb("vt", [P, TPW, W])
    ot = st.sb("ot", [P, TPW, W])
    of = st.sb("of", [P, QC, W])
    ya = K.h
    sh2 = st.sb("sh2", [P, TOK])
    hn = K.ln_xc
    gl = st.sb("gl", [P, 3, W])
    hid = st.sb("hid", [P, 2, 3, W])
    seqs = lambda ap: ap.rearrange("p (s n) -> p s n", n=LEN)

    groups = []
    for s in range(SPW):
        for t in range(2):
            for hg in range(2):
                ops, vs = [], []
                for h in range(hg, 2 * GH, 2):
                    rows = slice(DH * (h % 2), DH * (h % 2) + DH)
                    ops.append((qk[rows, h // 2, s * LEN + t * P:s * LEN + (t + 1) * P],
                                qk[rows, QC + h // 2, s * LEN:s * LEN + (t + 1) * P]))
                    vs.append([vt[:, 2 * s + kt, DH * h:DH * (h + 1)] for kt in range(t + 1)])
                groups.append((ops, t + 1, K.banded[:, LEN * t:LEN * t + (t + 1) * P], vs,
                               ot[:, 2 * s + t, :].rearrange("p (h a d) -> p a h d", a=2, d=DH)[:, hg]))
    att = Attention(K, st, groups, GH, DH, 8.0)
    N = att.n

    with nc.Block() as block:
        @block.sync
        def _(sp):
            def load(what, to, l, done):
                sp.dma_start(to[:, :], K.d[what][bass.ds(l, 1), :, :].rearrange("a p n -> (a p) n")).then_inc(done, 16)

            load("window_wa", wa, 0, st.wa_ready)
            sp.dma_start(tabs[:, :, :].rearrange("p a n -> p (a n)"), K.d["window_tabs"]).then_inc(st.tabs_ready, 16)
            load("window_wb", wb, 0, st.wb_ready)
            with sp.Fori(0, DEPTH - 1) as l:
                sp.wait_ge(st.tab_ready, l + 1)
                sp.wait_ge(st.proj_ready, (l + 1) * NJ)
                load("window_wa", wa, l + 1, st.wa_ready)
                sp.wait_ge(st.y_ready, (l + 2) * NJ)
                load("window_wb", wb, l + 1, st.wb_ready)

        @block.tensor
        def _(pe):
            outer.pe(pe, 0, K.x, lambda j: None)
            with pe.Fori(0, DEPTH) as l:
                with pe.Fori(0, NJ) as n:
                    k = l * NJ + n
                    pe.wait_ge(st.wa_ready, 16 * l + 16)
                    pe.wait_ge(st.y_ready, (l + 1) * NJ)
                    pe.wait_ge(st.sh_low, k + 1)
                    pe.wait_ge(st.sh_high, k + 1)

                    def norm(i):
                        pe.wait_ge(st.sq_ready, k * 8 + (i + 1))
                        if i >= 2:
                            pe.wait_ge(st.ss_safe, k * 8 + (i - 1))
                        nc.tensor.matmul(K.ps[:, 4 + i % 2, :], K.half_ones, sq[:, i % NB, :], start=True, stop=True)\
                            .then_inc(st.ss_ready, 1)

                    for i in range(2 * QC):
                        b = 2 * (i % 2)
                        if i >= 2:
                            pe.wait_ge(st.lin_read, k * 8 + (i - 1))
                            pe.wait_ge(st.rot_read, k * 8 + (i - 1))
                        for a in range(2):
                            mm = nc.tensor.matmul(K.ps[:, b + a, :], wqk[i][a], sh[:, :], start=True, stop=True)
                        mm.then_inc(st.lin_ready, 1)
                        if i >= 1:
                            norm(i - 1)
                    norm(2 * QC - 1)
                    for t in range(TPW):
                        b = (6, 7, 0, 1)[t]
                        if b == 0:
                            pe.wait_ge(st.rot_read, k * 8 + 7)
                            pe.wait_ge(st.lin_read, k * 8 + 7)
                        nc.tensor.matmul(K.ps[:, b, :], sh[:, toks(t, P)], wv, start=True, stop=True)\
                            .then_inc(st.v_ready, 1)
                    pe.wait_ge(st.qk_done, k * 8 + 8)
                    pe.wait_ge(st.v_copied, k * 4 + 4)
                    att.pe(pe, k * N, lambda g: None)
                    pe.wait_ge(att.o_copied, k * N + N)
                    for c in range(QC):
                        for t in range(TPW):
                            mm = nc.tensor.transpose(K.ps[:, c, toks(t, P)], ot[:, t, toks(c, P)], K.ident)
                        mm.then_inc(st.o_turned, 1)
                    for c in range(QC):
                        pe.wait_ge(st.o_moved, k * 4 + (c + 1))
                        mm = nc.tensor.matmul(K.ps[:, 7, :], wo[c], of[:, c, :], start=(c == 0), stop=(c == QC - 1))
                    mm.then_inc(st.proj_ready, 1)
                inner.pe(pe, l, sh2, lambda j: (pe.wait_ge(st.sh2_low, at(l, j)), pe.wait_ge(st.sh2_high, at(l, j))))
                pe.wait_ge(st.wb_ready, 16 * l + 16)
                for j in range(NJ + 1):
                    k = l * NJ + j
                    if j < NJ:
                        pe.wait_ge(inner.norm_ready, at(l, j))
                        for c, (a, m) in enumerate(HC):
                            if j >= 1:
                                pe.wait_ge(st.hid_done, k * 3 + (c - 2))
                            nc.tensor.matmul(K.ps[0:m, c, :], w1g[c], hn[:, toks(j)], start=True, stop=True)\
                                .then_inc(st.hid_g, 1)
                            nc.tensor.matmul(K.ps[0:m, 3 + c, :], w1a[c], hn[:, toks(j)], start=True, stop=True)\
                                .then_inc(st.hid_a, 1)
                    if j >= 1:
                        if j >= 3:
                            pe.wait_ge(st.y_ready, (l + 1) * NJ + j - 2)
                        for c, (a, m) in enumerate(HC):
                            pe.wait_ge(st.hid_done, k * 3 + (c - 2))
                            mm = nc.tensor.matmul(K.ps[:, 6 + (j - 1) % 2, :], w2[c], hid[0:m, (j - 1) % 2, c, :],
                                                  start=(c == 0), stop=(c == 2))
                        mm.then_inc(st.mlp_ready, 1)

        @block.scalar
        def _(act):
            nc.scalar.preload_act_table_set("natural_log_exp_and_others")
            outer.act(act, 0)
            with act.Fori(0, DEPTH) as l:
                nc.scalar.preload_act_table_set("natural_log_exp_and_others")
                with act.Fori(0, NJ) as n:
                    k = l * NJ + n
                    act.wait_ge(st.y_ready, k + 1)
                    nc.scalar.activation(sh[0:64, :], y[0:64, bass.ds(n * W, W)], ACT.Copy).then_inc(st.sh_low, 1)
                    for i in range(2 * QC + LAG):
                        if i < 2 * QC:
                            act.wait_ge(st.lin_ready, k * 8 + (i + 1))
                            if i >= NB:
                                act.wait_ge(st.qk_done, k * 8 + (i + 1 - NB))
                            nc.scalar.activation(sq[:, i % NB, :], K.ps[:, 2 * (i % 2), :], ACT.Square)\
                                .then_inc(st.sq_ready, 1)
                        if i >= LAG:
                            act.wait_ge(st.ss_safe, k * 8 + (i + 1 - LAG))
                            s = sq[:, (i - LAG) % NB, :]
                            nc.scalar.activation(s, s, ACT.Ln, scale=float(2 ** 20)).then_inc(st.ss_log, 1)
                            act.wait_ge(st.ss_log, k * 8 + (i + 1 - LAG))
                            nc.scalar.activation(s, s, ACT.Exp, scale=-0.5, bias=K.ln_shift).then_inc(st.rn_ready, 1)
                    for t in range(TPW):
                        act.wait_ge(st.v_ready, k * 4 + (t + 1))
                        nc.scalar.activation(vt[:, t, :], K.ps[:, (6, 7, 0, 1)[t], :], ACT.Copy)\
                            .then_inc(st.v_copied, 1)
                    att.act(act, k * N)
                    for c in range(QC):
                        act.wait_ge(st.o_turned, k * 4 + (c + 1))
                        nc.scalar.activation(of[:, c, :], K.ps[:, c, :], ACT.Copy).then_inc(st.o_moved, 1)
                    act.wait_ge(st.y_attn, k + 1)
                    nc.scalar.activation(sh2[0:64, bass.ds(n * W, W)], ya[0:64, bass.ds(n * W, W)], ACT.Copy)\
                        .then_inc(st.sh2_low, 1)
                act.wait_ge(st.wb_ready, 16 * l + 16)
                inner.act(act, l, hn, ln_w, ln_b)
                for j in range(NJ):
                    for c, (a, m) in enumerate(HC):
                        act.wait_ge(st.hid_g, (l * NJ + j) * 3 + (c + 1))
                        if j >= 1:
                            act.wait_ge(st.hid_done, (l * NJ + j) * 3 + (c - 2))
                        nc.scalar.activation(gl[0:m, c, :], K.ps[0:m, c, :], ACT.Gelu, bias=b1g[c])\
                            .then_inc(st.gelu_done, 1)

        @block.gpsimd
        def _(pool):
            nc.gpsimd.memset(sh[64:128, :], 0.0)
            nc.gpsimd.memset(sh2[64:128, :], 0.0).then_inc(st.edge, 1)
            with pool.Fori(0, DEPTH * NJ) as k:
                for i in range(2 * QC + LAG):
                    if i < 2 * QC:
                        a = part[:, i % NB, 0, :]
                        pool.wait_ge(st.lin_read, k * 8 + (i + 1))
                        nc.gpsimd.tensor_tensor(a, a, part[:, i % NB, 1, :], ALU.add).then_inc(st.turned, 1)
                    if i >= LAG:
                        c = i - LAG
                        pool.wait_ge(st.turned, k * 8 + (c + 1))
                        pool.wait_ge(st.rn_ready, k * 8 + (c + 1))
                        nc.gpsimd.tensor_tensor(qk[:, c, :], part[:, c % NB, 0, :], sq[:, c % NB, :], ALU.mult)\
                            .then_inc(st.qk_done, 1)

        @block.vector
        def _(dve):
            outer.dve(dve, 0, K.x, y)
            dve.wait_ge(outer.norm_ready, NJ)
            dve.sem_inc(st.y_ready, NJ)
            dve.wait_ge(st.edge, 1)
            dve.wait_ge(st.tabs_ready, 16)
            with dve.Fori(0, DEPTH) as l:
                dve.wait_ge(st.wa_ready, 16 * l + 16)
                for i in range(4):
                    v = nc.vector.tensor_scalar(tab[:, i, :], tabs[:, i, :], scales[i], None, ALU.mult)
                v.then_inc(st.tab_ready, 1)
                with dve.Fori(0, NJ) as n:
                    k = l * NJ + n

                    dve.wait_ge(st.y_ready, k + 1)
                    for s in range(SPW):
                        v = nc.vector.tensor_copy(sh[64:128, s * LEN + 1:(s + 1) * LEN],
                                                  y[64:128, bass.ds(n * W + s * LEN, LEN - 1)])
                    v.then_inc(st.sh_high, 1)
                    for i in range(2 * QC + 1):
                        if i < 2 * QC:
                            b, kind = 2 * (i % 2), 2 * (i // QC)
                            table = lambda a: tab[:, kind + a, :].unsqueeze(1).to_broadcast([P, SPW, LEN])
                            dve.wait_ge(st.tab_ready, l + 1)
                            dve.wait_ge(st.lin_ready, k * 8 + (i + 1))
                            if i >= NB:
                                dve.wait_ge(st.qk_done, k * 8 + (i + 1 - NB))
                            nc.vector.tensor_tensor(seqs(part[:, i % NB, 1, :]), seqs(K.ps[:, b + 1, :]), table(1),
                                                    ALU.mult).then_inc(st.rot_read, 1)
                            dve.wait_ge(st.sq_ready, k * 8 + (i + 1))
                            nc.vector.tensor_tensor(seqs(part[:, i % NB, 0, :]), seqs(K.ps[:, b, :]), table(0),
                                                    ALU.mult).then_inc(st.lin_read, 1)
                        if i >= 1:
                            dve.wait_ge(st.ss_ready, k * 8 + i)
                            nc.vector.tensor_scalar(sq[:, (i - 1) % NB, :], K.ps[:, 4 + (i - 1) % 2, :], 1e-24, None,
                                                    ALU.max).then_inc(st.ss_safe, 1)
                    att.dve(dve, k * N)
                    dve.wait_ge(st.proj_ready, k + 1)
                    nc.vector.tensor_tensor(ya[:, bass.ds(n * W, W)], K.ps[:, 7, :], y[:, bass.ds(n * W, W)], ALU.add)\
                        .then_inc(st.y_attn, 1)
                    dve.wait_ge(st.y_attn, k + 1)
                    for s in range(SPW):
                        v = nc.vector.tensor_copy(sh2[64:128, bass.ds(n * W + (s * LEN + 1), LEN - 1)],
                                                  ya[64:128, bass.ds(n * W + s * LEN, LEN - 1)])
                    v.then_inc(st.sh2_high, 1)
                dve.wait_ge(st.wb_ready, 16 * l + 16)
                inner.dve(dve, l, sh2)
                for j in range(NJ + 1):
                    k = l * NJ + j
                    if j < NJ:
                        for c, (a, m) in enumerate(HC):
                            dve.wait_ge(st.gelu_done, k * 3 + (c + 1))
                            dve.wait_ge(st.hid_a, k * 3 + (c + 1))
                            if j >= 2:
                                dve.wait_ge(st.mlp_ready, k - 1)
                            nc.vector.scalar_tensor_tensor(hid[0:m, j % 2, c, :], K.ps[0:m, 3 + c, :], b1a[c],
                                                           gl[0:m, c, :], ALU.add, ALU.mult).then_inc(st.hid_done, 1)
                    if j >= 1:
                        dve.wait_ge(st.mlp_ready, k)
                        nc.vector.scalar_tensor_tensor(y[:, toks(j - 1)], K.ps[:, 6 + (j - 1) % 2, :], b2,
                                                       ya[:, toks(j - 1)], ALU.add, ALU.add).then_inc(st.y_ready, 1)
            for j in range(NJ):
                dve.wait_ge(st.y_ready, NJ * DEPTH + at(0, j))
                nc.vector.tensor_tensor(K.x[:, toks(j)], K.x[:, toks(j)], y[:, toks(j)], ALU.add)\
                    .then_inc(st.x_done, 1)
    st.end()


def window_attention_first(K):
    window_attention_stage(K, 0)


def window_attention_second(K):
    window_attention_stage(K, 1)


def retention_stage(K):
    nc = K.nc
    st = Stage(nc, "retention")
    (st.w_ready, st.k_ready, st.k_decayed, st.v_ready, st.v_copied, st.q_ready, st.q_copied,
     st.ctx_ready, st.ctx_copied, st.ret_ready, st.ret_decayed, st.stats, st.mean_var, st.gn_log,
     st.gn_rstd, st.shift_a, st.shift_b, st.gate_ready, st.gate_done, st.gn_done, st.gated,
     st.out_ready, st.x_done) = st.signals(
        "w_ready k_ready k_decayed v_ready v_copied q_ready q_copied ctx_ready ctx_copied ret_ready "
        "ret_decayed stats mean_var gn_log gn_rstd shift_a shift_b gate_ready gate_done gn_done "
        "gated out_ready x_done")
    outer = LayerNorm(K, st, "outer_")
    wt = st.sb("wt", [P, K.d["retention_w"].shape[1]])
    wq, wk, wv, wg, wo = (wt[:, toks(i, P)] for i in range(5))
    gn_g, gn_b = wt[:, 640:641], wt[:, 641:642]
    kt, vt, qf, gate, ret = (st.sb(n, [P, TOK]) for n in ("kt", "vt", "qf", "gate", "ret"))
    ctx = st.sb("ctx", [P, SEQS, P])
    bn = st.sb("bn", [P, SEQS, 6])
    mv = st.sb("mv", [P, SEQS, 2])
    co = st.sb("co", [P, 3, SEQS])
    with nc.Block() as block:
        @block.sync
        def _(sp):
            sp.dma_start(wt[:, :], K.d["retention_w"]).then_inc(st.w_ready, 16)

        @block.tensor
        def _(pe):
            outer.pe(pe, 0, K.x, lambda j: None)
            pe.wait_ge(st.w_ready, 16)
            for j in range(NJ):
                pe.wait_ge(outer.norm_ready, at(0, j))
                for t in range(TPW):
                    mm = nc.tensor.matmul(K.ps[:, j, toks(t, P)], K.h[:, toks(TPW * j + t, P)], wk,
                                          start=True, stop=True)
                mm.then_inc(st.k_ready, 1)
            for j in range(NJ):
                for t in range(TPW):
                    mm = nc.tensor.matmul(K.ps[:, 4 + j, toks(t, P)], K.h[:, toks(TPW * j + t, P)], wv,
                                          start=True, stop=True)
                mm.then_inc(st.v_ready, 1)
            for j in range(NJ):
                pe.wait_ge(st.k_decayed, j + 1)
                nc.tensor.matmul(K.ps[:, j, :], wq, K.h[:, toks(j)], start=True, stop=True).then_inc(st.q_ready, 1)
            for j in range(NJ):
                pe.wait_ge(st.v_copied, j + 1)
                for s in range(SPW):
                    for t in range(2):
                        tile = toks(TPW * j + 2 * s + t, P)
                        mm = nc.tensor.matmul(K.ps[:, 4 + j, toks(s, P)], kt[:, tile], vt[:, tile],
                                              start=(t == 0), stop=(t == 1))
                mm.then_inc(st.ctx_ready, 1)
            for j in range(NJ):
                pe.wait_ge(st.q_copied, j + 1)
                pe.wait_ge(st.ctx_copied, j + 1)
                for s in range(SPW):
                    mm = nc.tensor.matmul(K.ps[:, j, toks(s, LEN)], ctx[:, SPW * j + s, :],
                                          qf[:, toks(SPW * j + s, LEN)], start=True, stop=True)
                mm.then_inc(st.ret_ready, 1)
            for j in range(NJ):
                nc.tensor.matmul(K.ps[:, 4 + j, :], wg, K.h[:, toks(j)], start=True, stop=True)\
                    .then_inc(st.gate_ready, 1)
            for j in range(NJ):
                pe.wait_ge(st.gated, j + 1)
                nc.tensor.matmul(K.ps[:, j, :], wo, ret[:, toks(j)], start=True, stop=True).then_inc(st.out_ready, 1)

        @block.scalar
        def _(act):
            nc.scalar.preload_act_table_set("natural_log_exp_and_others")
            outer.act(act, 0)
            for j in range(NJ):
                act.wait_ge(st.v_ready, j + 1)
                nc.scalar.activation(vt[:, toks(j)], K.ps[:, 4 + j, :], ACT.Copy).then_inc(st.v_copied, 1)
            for j in range(NJ):
                act.wait_ge(st.q_ready, j + 1)
                nc.scalar.activation(qf[:, toks(j)], K.ps[:, j, :], ACT.Copy).then_inc(st.q_copied, 1)
            for j in range(NJ):
                act.wait_ge(st.gate_ready, j + 1)
                nc.scalar.activation(gate[:, toks(j)], K.ps[:, 4 + j, :], ACT.Relu).then_inc(st.gate_done, 1)
            act.wait_ge(st.mean_var, SEQS)
            nc.scalar.activation(co[:, 0, :], mv[:, :, 1], ACT.Ln, bias=K.eps_gn).then_inc(st.gn_log, 1)
            act.wait_ge(st.gn_log, 1)
            nc.scalar.activation(co[:, 0, :], co[:, 0, :], ACT.Exp, scale=-0.5).then_inc(st.gn_rstd, 1)
            act.wait_ge(st.shift_b, 2)
            for s in range(SEQS):
                act.wait_ge(st.gate_done, s // SPW + 1)
                seq = toks(s, LEN)
                nc.scalar.activation(ret[:, seq], ret[:, seq], ACT.Identity, scale=co[:, 1, s:s + 1],
                                     bias=co[:, 2, s:s + 1]).then_inc(st.gn_done, 1)

        @block.vector
        def _(dve):
            outer.dve(dve, 0, K.x, K.h)
            for j in range(NJ):
                dve.wait_ge(st.k_ready, j + 1)
                for t in range(TPW):
                    v = nc.vector.tensor_scalar(kt[:, toks(TPW * j + t, P)], K.ps[:, j, toks(t, P)],
                                                K.gamma_col[:, t % 2:t % 2 + 1], None, ALU.mult)
                v.then_inc(st.k_decayed, 1)
            for j in range(NJ):
                dve.wait_ge(st.ctx_ready, j + 1)
                nc.vector.tensor_copy(ctx[:, SPW * j:SPW * (j + 1), :].rearrange("p s n -> p (s n)"),
                                      K.ps[:, 4 + j, 0:SPW * P]).then_inc(st.ctx_copied, 1)
            for j in range(NJ):
                dve.wait_ge(st.ret_ready, j + 1)
                seqs = lambda ap: ap.rearrange("p (s n) -> p s n", n=LEN)
                nc.vector.tensor_tensor(seqs(ret[:, toks(j)]), seqs(K.ps[:, j, :]),
                                        K.gamma_row.unsqueeze(1).to_broadcast([P, SPW, LEN]), ALU.mult)\
                    .then_inc(st.ret_decayed, 1)
            for s in range(SEQS):
                dve.wait_ge(st.ret_decayed, s // SPW + 1)
                nc.vector.bn_stats(bn[:, s, :], ret[:, toks(s, LEN)]).then_inc(st.stats, 1)
            for s in range(SEQS):
                dve.wait_ge(st.stats, s + 1)
                nc.vector.bn_aggr(mv[:, s, :], bn[:, s, :]).then_inc(st.mean_var, 1)
            dve.wait_ge(st.w_ready, 16)
            dve.wait_ge(st.gn_rstd, 1)
            nc.vector.tensor_scalar(co[:, 1, :], co[:, 0, :], gn_g, None, ALU.mult).then_inc(st.shift_a, 1)
            dve.wait_ge(st.shift_a, 1)
            dve.wait_ge(st.mean_var, SEQS)
            nc.vector.tensor_tensor(co[:, 2, :], mv[:, :, 0], co[:, 1, :], ALU.mult).then_inc(st.shift_b, 1)
            dve.wait_ge(st.shift_b, 1)
            nc.vector.tensor_scalar(co[:, 2, :], co[:, 2, :], -1.0, gn_b, ALU.mult, ALU.add).then_inc(st.shift_b, 1)
            for j in range(NJ):
                dve.wait_ge(st.gn_done, SPW * (j + 1))
                nc.vector.tensor_tensor(ret[:, toks(j)], ret[:, toks(j)], gate[:, toks(j)], ALU.mult)\
                    .then_inc(st.gated, 1)
            for j in range(NJ):
                dve.wait_ge(st.out_ready, j + 1)
                nc.vector.tensor_tensor(K.x[:, toks(j)], K.x[:, toks(j)], K.ps[:, j, :], ALU.add)\
                    .then_inc(st.x_done, 1)
    st.end()


def gated_delta_stage(K):
    nc = K.nc
    H, KD, VD, CC, PAD = 4, 32, 64, 2, 3
    NT = TOK // P
    NH = NT * H
    LEVELS = 7
    st = Stage(nc, "delta")
    (st.w_ready, st.c_ready, st.rms_sq, st.rms_ready, st.rms_log, st.rms_rstd, st.h_ready,
     st.in_ready, st.x_in, st.edge, st.conv, st.conved, st.silu_done, st.l2_sq, st.l2_ready,
     st.l2_log, st.l2_rstd, st.l2_done, st.ab_ready, st.ab_copied, st.sp_in, st.sp_n, st.sp_abs,
     st.sp_e, st.sp_d, st.sp_r, st.sp_s, st.sp_z, st.sp_h, st.sp_done, st.ea, st.beta_done,
     st.g_done, st.csum_ready, st.decay_exp, st.beta_decay, st.v_turned, st.v_done, st.k_turned,
     st.k_done, st.rep_done, st.bb_ready, st.kb_done, st.gb_ready, st.gb_exp, st.qg_done,
     st.copies, st.small, st.gl_done, st.lg_ready, st.kk_ready, st.gam_exp, st.gam_masked,
     st.nt_done, st.pt_done, st.bm_done, st.y_ready, st.y_copied, st.xx_ready, st.x_new,
     st.xt_ready, st.xt_new, st.d_ready, st.d_copied, st.s_ready, st.s_done, st.ks_ready,
     st.ks_decay, st.r_done, st.o_ready, st.o_copied, st.on_sq, st.on_ready, st.on_log,
     st.on_rstd, st.on_done, st.gate_ready, st.gate_done, st.gated, st.enc_ready, st.y_enc,
     st.w2_ready, st.gelu, st.x_sum, st.x_done) = st.signals(
        "w_ready c_ready rms_sq rms_ready rms_log rms_rstd h_ready in_ready x_in edge conv conved "
        "silu_done l2_sq l2_ready l2_log l2_rstd l2_done ab_ready ab_copied sp_in sp_n sp_abs sp_e "
        "sp_d sp_r sp_s sp_z sp_h sp_done ea beta_done g_done csum_ready decay_exp beta_decay "
        "v_turned v_done k_turned k_done rep_done bb_ready kb_done gb_ready gb_exp qg_done copies "
        "small gl_done lg_ready kk_ready gam_exp gam_masked nt_done pt_done bm_done y_ready "
        "y_copied xx_ready x_new xt_ready xt_new d_ready d_copied s_ready s_done ks_ready ks_decay "
        "r_done o_ready o_copied on_sq on_ready on_log on_rstd on_done gate_ready gate_done gated "
        "enc_ready y_enc w2_ready gelu x_sum x_done")
    outer = LayerNorm(K, st, "outer_")
    inner = LayerNorm(K, st, "inner_", affine=True)
    wt = st.sb("wt", [P, K.d["delta_w"].shape[1]])
    ct = st.sb("ct", [P, K.d["delta_c"].shape[1]])
    w_in = [wt[:, toks(i, P)] for i in range(4)]
    wg = [wt[:, toks(4 + i, P)] for i in range(2)]
    wo = [wt[:, toks(6 + i, P)] for i in range(2)]
    w2 = wt[:, toks(8, P)]
    o = 9 * P
    wab, dtb, alog = wt[:, o:o + 8], wt[:, o + 8:o + 12], wt[:, o + 12:o + 16]
    o += 16
    conv_w = [[wt[:, o + 4 * c + k:o + 4 * c + k + 1] for k in range(4)] for c in range(4)]
    o += 16
    ln1g, ln1b, ln2g, ln2b, rms_w, b2, onw = (wt[:, o + i:o + i + 1] for i in range(7))
    upto, after = ct[:, 0:P], ct[:, P:2 * P]
    level_mask = [ct[:, toks(2 + i, P)] for i in range(LEVELS)]
    head32 = ct[:, toks(9, P)]
    s_mask = ct[:, 10 * P:12 * P]

    y, h = K.y, K.h
    qf, kf, kb, qg = (st.sb(n, [P, TOK]) for n in ("qf", "kf", "kb", "qg"))
    xi = [st.sb(f"xi{i}", [P, SEQS, LEN + PAD]) for i in range(2)]
    o_f = st.sb("o_f", [P, CC, TOK])
    v_tm = st.sb("v_tm", [P, NT, H * VD])
    k_tm = st.sb("k_tm", [P, NT, P])
    sm = st.sb("sm", [P, 12, NH])
    ea = st.sb("ea", [P, H])
    z_, n_, e_, d_, s_, hh, g, beta, eg, er, bg, _ = (sm[:, i, :] for i in range(12))
    ab2 = st.sb("ab2", [P, NT, 8])
    rep_b, rep_g = K.ln_xc, K.ln_sq
    ks, kbs, qs = (st.sb(n, [P, LEN]) for n in ("ks", "kbs", "qs"))
    kts = st.sb("kts", [P, P])
    small = st.sb("small", [P, 2, 2, H])
    gl = st.sb("gl", [P, 2, H, P])
    gam, nt, pt, xm, xt, ym = (st.sb(n, [P, 2, H, P]) for n in ("gam", "nt", "pt", "xm", "xt", "ym"))
    bm = st.sb("bm", [P, 2, 2, H, P])
    dl = st.sb("dl", [P, 2, H * VD])
    state = st.sb("state", [P, H * VD])
    ksd, rr = st.sb("ksd", [P, H * VD]), st.sb("rr", [P, H * VD])
    seqs = lambda ap: ap.rearrange("p (s n) -> p s n", n=LEN)
    heads = lambda ap: ap.unsqueeze(1).to_broadcast([P, H, P])
    hv = lambda ap: ap.rearrange("p (h v) -> p h v", h=H)
    bank4 = lambda ap: ap.rearrange("p (h n) -> p h n", h=H)
    tile_h = lambda ap: ap.rearrange("p (n h) -> p n h", h=H)
    cv = [qf[:, :], kf[:, :], o_f[:, 0, :], o_f[:, 1, :]]

    with nc.Block() as block:
        @block.sync
        def _(sp):
            sp.dma_start(wt[:, :], K.d["delta_w"]).then_inc(st.w_ready, 16)
            sp.dma_start(ct[:, :], K.d["delta_c"]).then_inc(st.c_ready, 16)

        @block.tensor
        def _(pe):
            outer.pe(pe, 0, K.x, lambda j: None)
            inner.pe(pe, 0, y, lambda j: pe.wait_ge(outer.norm_ready, at(0, j)))
            for j in range(NJ):
                pe.wait_ge(st.rms_sq, j + 1)
                nc.tensor.matmul(K.ps[:, j, :], K.mean_mat, K.ln_sq[:, toks(j)], start=True, stop=True)\
                    .then_inc(st.rms_ready, 1)
            pe.wait_ge(st.w_ready, 16)
            pe.wait_ge(st.c_ready, 16)
            for i in range(4):
                for j in range(NJ):
                    if i == 0:
                        pe.wait_ge(st.h_ready, j + 1)
                    if i >= 2:
                        pe.wait_ge(st.x_in, at(i - 2, j))
                    if i == 1:
                        pe.wait_ge(st.rms_log, NJ)
                    nc.tensor.matmul(K.ps[:, 4 * ((i + 1) % 2) + j, :], w_in[i], h[:, toks(j)], start=True, stop=True)\
                        .then_inc(st.in_ready, 1)
            pe.wait_ge(st.x_in, 4 * NJ)
            for n in range(NT):
                mm = nc.tensor.matmul(K.ps[:, 7, 8 * n:8 * n + 8], h[:, toks(n, P)], wab, start=True, stop=True)
            mm.then_inc(st.ab_ready, 1)
            for i in range(2):
                for j in range(NJ):
                    pe.wait_ge(st.l2_sq, at(i, j))
                    if i == 1:
                        pe.wait_ge(st.l2_log, j + 1)
                    nc.tensor.matmul(K.ps[:, j, :], head32, (K.ln_xc, K.ln_sq)[i][:, toks(j)], start=True, stop=True)\
                        .then_inc(st.l2_ready, 1)
            pe.wait_ge(st.g_done, 1)
            nc.tensor.matmul(K.ps[:, 4, 0:NH], upto, g, start=True, stop=True)
            nc.tensor.matmul(K.ps[:, 4, NH:2 * NH], after, g, start=True, stop=True).then_inc(st.csum_ready, 1)
            for m in range(NT // 2):
                pe.wait_ge(st.silu_done, 4)
                if m >= 2:
                    pe.wait_ge(st.v_done, m - 1)
                for n in range(2 * m, 2 * m + 2):
                    for c in range(CC):
                        mm = nc.tensor.transpose(K.ps[:, 5 + m % 2, toks(2 * (n % 2) + c, P)], o_f[:, c, toks(n, P)],
                                                 K.ident)
                mm.then_inc(st.v_turned, 1)
            for j in range(NJ):
                pe.wait_ge(st.l2_done, at(1, j))
                pe.wait_ge(st.l2_log, 2 * NJ)
                for t in range(TPW):
                    mm = nc.tensor.transpose(K.ps[:, j, toks(t, P)], kf[:, toks(TPW * j + t, P)], K.ident)
                mm.then_inc(st.k_turned, 1)
            for j in range(NJ):
                pe.wait_ge(st.rep_done, 2)
                pe.wait_ge(st.k_done, j + 1)
                for t in range(TPW):
                    mm = nc.tensor.transpose(K.ps[:, j, toks(t, P)], rep_b[:, toks(TPW * j + t, P)], K.ident)
                mm.then_inc(st.bb_ready, 1)
            for j in range(NJ):
                pe.wait_ge(st.decay_exp, 1)
                pe.wait_ge(st.v_done, NT // 2)
                for t in range(TPW):
                    mm = nc.tensor.matmul(K.ps[:, 4 + j, toks(t, P)], rep_g[:, toks(TPW * j + t, P)], upto,
                                          start=True, stop=True)
                mm.then_inc(st.gb_ready, 1)
            pe.wait_ge(st.gb_exp, NJ)
            pe.wait_ge(st.kb_done, NJ)
            pe.wait_ge(st.qg_done, NJ)
            with pe.Fori(0, SEQS) as b:
                for u in range(2):
                    pe.wait_ge(st.gl_done, b * 2 + (u + 1))
                    for i in range(H):
                        mm = nc.tensor.matmul(K.ps[:, u, toks(i, P)], gl[:, u, i, :], upto, start=True, stop=True)
                    mm.then_inc(st.lg_ready, 1)
                pe.wait_ge(st.copies, b + 1)
                for u in range(2):
                    for a in range(2):
                        for i in range(H):
                            rows = slice(KD * i, KD * i + KD)
                            mm = nc.tensor.matmul(K.ps[:, 4 + i, toks(2 * u + a, P)], ks[rows, toks(u, P)],
                                                  (kbs, qs)[a][rows, toks(u, P)], start=True, stop=True)
                            if u == 1 and a == 1:
                                mm.then_inc(st.kk_ready, 1)
                for lv in range(LEVELS):
                    for u in range(2):
                        pe.wait_ge(st.bm_done, b * (2 * LEVELS) + (2 * lv + u + 1))
                        if lv == 0:
                            pe.wait_ge(st.gam_exp, b * 2 + (u + 1))
                        else:
                            pe.wait_ge(st.x_new, b * (2 * LEVELS - 2) + (2 * (lv - 1) + u + 1))
                        for i in range(H):
                            mm = nc.tensor.matmul(K.ps[:, u, toks(i, P)], bm[:, lv % 2, u, i, :],
                                                  K.ident if lv == 0 else xm[:, u, i, :], start=True, stop=True)
                        mm.then_inc(st.y_ready, 1)
                    if lv == 0:
                        continue
                    for u in range(2):
                        pe.wait_ge(st.y_copied, b * (2 * LEVELS - 2) + (2 * (lv - 1) + u + 1))
                        pe.wait_ge(st.xt_new, b * (2 * LEVELS) + (2 * (lv - 1) + u + 1))
                        if lv == 1:
                            pe.wait_ge(st.pt_done, b * 2 + 2)
                        for i in range(H):
                            mm = nc.tensor.matmul(K.ps[:, 4 + u, toks(i, P)], ym[:, u, i, :], xt[:, u, i, :],
                                                  start=True, stop=True)
                        mm.then_inc(st.xt_ready, 1)
                        if lv < LEVELS - 1:
                            for i in range(H):
                                mm = nc.tensor.matmul(K.ps[:, 2 + u, toks(i, P)], xt[:, u, i, :], ym[:, u, i, :],
                                                      start=True, stop=True)
                            mm.then_inc(st.xx_ready, 1)
                pe.wait_ge(st.xt_new, b * (2 * LEVELS) + 2 * LEVELS)
                for i in range(H):
                    mm = nc.tensor.matmul(K.ps[:, 6, i * VD:(i + 1) * VD], xt[:, 0, i, :],
                                          v_tm[:, bass.ds(b * 2, 1), i * VD:(i + 1) * VD].rearrange("p a v -> p (a v)"),
                                          start=True, stop=True)
                mm.then_inc(st.d_ready, 1)
                pe.wait_ge(st.d_copied, b * 2 + 1)
                nc.tensor.matmul(K.ps[:, 7, 0:H * VD], kts[:, :], dl[:, 0, :], start=True, stop=True)\
                    .then_inc(st.s_ready, 1)
                for i in range(H):
                    mm = nc.tensor.matmul(K.ps[VD * (i % 2):VD * (i % 2) + VD, 2, toks(i // 2, P)],
                                          dl[:, 0, i * VD:(i + 1) * VD], pt[:, 0, i, :], start=True, stop=True)
                mm.then_inc(st.o_ready, 1)
                pe.wait_ge(st.s_done, b + 1)
                nc.tensor.matmul(K.ps[:, 0, 0:H * VD], ks[:, P:2 * P], state[:, :], start=True, stop=True)\
                    .then_inc(st.ks_ready, 1)
                pe.wait_ge(st.r_done, b + 1)
                for i in range(H):
                    mm = nc.tensor.matmul(K.ps[:, 1, i * VD:(i + 1) * VD], xt[:, 1, i, :], rr[:, i * VD:(i + 1) * VD],
                                          start=True, stop=True)
                mm.then_inc(st.d_ready, 1)
                pe.wait_ge(st.d_copied, b * 2 + 2)
                for c in range(CC):
                    nc.tensor.matmul(K.ps[:, 3, toks(c, P)], state[:, toks(c, P)], qg[:, bass.ds(b * LEN + P, P)],
                                     start=True, stop=False)
                    for i in (2 * c, 2 * c + 1):
                        mm = nc.tensor.matmul(K.ps[VD * (i % 2):VD * (i % 2) + VD, 3, toks(c, P)],
                                              dl[:, 1, i * VD:(i + 1) * VD], pt[:, 1, i, :], start=False, stop=True)
                mm.then_inc(st.o_ready, 1)
            pe.wait_ge(st.o_copied, 2 * SEQS)
            for c in range(CC):
                for j in range(NJ):
                    pe.wait_ge(st.on_sq, at(c, j))
                    nc.tensor.matmul(K.ps[:, 4 * c + j, :], K.half_ones, (K.ln_xc, K.ln_sq)[c][:, toks(j)],
                                     start=True, stop=True).then_inc(st.on_ready, 1)
            for c in range(CC):
                for j in range(NJ):
                    pe.wait_ge(st.on_log, at(c, j))
                    nc.tensor.matmul(K.ps[:, 4 * c + j, :], wg[c], h[:, toks(j)], start=True, stop=True)\
                        .then_inc(st.gate_ready, 1)
            for j in range(NJ):
                pe.wait_ge(st.gated, at(1, j))
                pe.wait_ge(st.gate_done, 2 * NJ)
                for c in range(CC):
                    mm = nc.tensor.matmul(K.ps[:, j, :], wo[c], o_f[:, c, toks(j)], start=(c == 0), stop=(c == 1))
                mm.then_inc(st.enc_ready, 1)
            inner.pe(pe, 1, y, lambda j: pe.wait_ge(st.y_enc, j + 1))
            for j in range(NJ):
                pe.wait_ge(inner.norm_ready, at(1, j))
                nc.tensor.matmul(K.ps[:, j, :], w2, h[:, toks(j)], start=True, stop=True).then_inc(st.w2_ready, 1)

        @block.scalar
        def _(act):
            nc.scalar.preload_act_table_set("natural_log_exp_and_others")
            outer.act(act, 0)
            act.wait_ge(st.w_ready, 16)
            inner.act(act, 0, h, ln1g, ln1b)
            for j in range(NJ):
                act.wait_ge(inner.norm_ready, at(0, j))
                nc.scalar.activation(K.ln_sq[:, toks(j)], h[:, toks(j)], ACT.Square).then_inc(st.rms_sq, 1)
            for j in range(NJ):
                act.wait_ge(st.rms_ready, j + 1)
                nc.scalar.activation(K.ln_sq[:, toks(j)], K.ps[:, j, :], ACT.Ln, bias=K.eps_rms).then_inc(st.rms_log, 1)
            for j in range(NJ):
                act.wait_ge(st.rms_log, j + 1)
                nc.scalar.activation(K.ln_sq[:, toks(j)], K.ln_sq[:, toks(j)], ACT.Exp, scale=-0.5)\
                    .then_inc(st.rms_rstd, 1)
            nc.scalar.activation(ea[:, :], alog, ACT.Exp).then_inc(st.ea, 1)
            act.wait_ge(st.edge, 1)
            for i in range(4):
                for j in range(NJ):
                    act.wait_ge(st.in_ready, at(i, j))
                    if i >= 2:
                        act.wait_ge(st.conved, i - 1)
                    nc.scalar.activation(xi[i % 2][:, SPW * j:SPW * (j + 1), PAD:],
                                         seqs(K.ps[:, 4 * ((i + 1) % 2) + j, :]), ACT.Copy).then_inc(st.x_in, 1)
            for i in range(4):
                act.wait_ge(st.conved, i + 1)
                nc.scalar.activation(cv[i], cv[i], ACT.Silu).then_inc(st.silu_done, 1)
            act.wait_ge(st.ab_copied, 1)
            nc.scalar.activation(tile_h(beta), ab2[:, :, 4:8], ACT.Sigmoid).then_inc(st.beta_done, 1)
            act.wait_ge(st.h_ready, NJ)
            for i in range(2):
                for j in range(NJ):
                    act.wait_ge(st.silu_done, i + 1)
                    nc.scalar.activation((K.ln_xc, K.ln_sq)[i][:, toks(j)], cv[i][:, toks(j)], ACT.Square)\
                        .then_inc(st.l2_sq, 1)
            for i in range(2):
                for j in range(NJ):
                    act.wait_ge(st.l2_ready, at(i, j))
                    nc.scalar.activation((K.ln_xc, K.ln_sq)[i][:, toks(j)], K.ps[:, j, :], ACT.Ln, bias=K.eps_rms)\
                        .then_inc(st.l2_log, 1)
            for i in range(2):
                for j in range(NJ):
                    act.wait_ge(st.l2_log, at(i, j))
                    r = (K.ln_xc, K.ln_sq)[i][:, toks(j)]
                    nc.scalar.activation(r, r, ACT.Exp, scale=-0.5).then_inc(st.l2_rstd, 1)
            act.wait_ge(st.sp_abs, 1)
            nc.scalar.activation(e_, e_, ACT.Exp, scale=-1.0).then_inc(st.sp_e, 1)
            act.wait_ge(st.csum_ready, 1)
            nc.scalar.activation(sm[:, 8:10, :].rearrange("p a n -> p (a n)"), K.ps[:, 4, 0:2 * NH], ACT.Exp)\
                .then_inc(st.decay_exp, 1)
            for j in range(NJ):
                act.wait_ge(st.gb_ready, j + 1)
                nc.scalar.activation(qg[:, toks(j)], K.ps[:, 4 + j, :], ACT.Exp).then_inc(st.gb_exp, 1)
            act.wait_ge(st.kb_done, NJ)
            act.wait_ge(st.k_done, NJ)
            act.wait_ge(st.l2_done, 2 * NJ)
            with act.Fori(0, SEQS) as b:
                seq = bass.ds(b * LEN, LEN)
                nc.scalar.activation(ks[:, :], kf[:, seq], ACT.Copy)
                nc.scalar.activation(kbs[:, :], kb[:, seq], ACT.Copy)
                nc.scalar.activation(qs[:, :], qf[:, seq], ACT.Copy)
                nc.scalar.activation(kts[:, :], k_tm[:, bass.ds(b * 2, 1), :].rearrange("p a n -> p (a n)"), ACT.Copy)\
                    .then_inc(st.copies, 1)
                for u in range(2):
                    act.wait_ge(st.lg_ready, b * 2 + (u + 1))
                    nc.scalar.activation(gam[:, u], bank4(K.ps[:, u, :]), ACT.Exp).then_inc(st.gam_exp, 1)
                for lv in range(1, LEVELS):
                    for u in range(2):
                        act.wait_ge(st.y_ready, b * (2 * LEVELS) + (2 * lv + u + 1))
                        nc.scalar.activation(ym[:, u], bank4(K.ps[:, u, :]), ACT.Copy).then_inc(st.y_copied, 1)
                for u in range(2):
                    act.wait_ge(st.d_ready, b * 2 + (u + 1))
                    nc.scalar.activation(dl[:, u, :], K.ps[:, (6, 1)[u], 0:H * VD], ACT.Copy).then_inc(st.d_copied, 1)
                for u in range(2):
                    act.wait_ge(st.o_ready, b * 2 + (u + 1))
                    nc.scalar.activation(o_f[:, :, bass.ds(b * LEN + u * P, P)],
                                         K.ps[:, 2 + u, 0:CC * P].rearrange("p (c n) -> p c n", c=CC), ACT.Copy)\
                        .then_inc(st.o_copied, 1)
            act.wait_ge(st.o_copied, 2 * SEQS)
            for c in range(CC):
                for j in range(NJ):
                    nc.scalar.activation((K.ln_xc, K.ln_sq)[c][:, toks(j)], o_f[:, c, toks(j)], ACT.Square)\
                        .then_inc(st.on_sq, 1)
            for c in range(CC):
                for j in range(NJ):
                    act.wait_ge(st.on_ready, at(c, j))
                    nc.scalar.activation((K.ln_xc, K.ln_sq)[c][:, toks(j)], K.ps[:, 4 * c + j, :], ACT.Ln,
                                         scale=1.0 / VD, bias=K.eps_rms).then_inc(st.on_log, 1)
            for c in range(CC):
                for j in range(NJ):
                    act.wait_ge(st.on_log, at(c, j))
                    r = (K.ln_xc, K.ln_sq)[c][:, toks(j)]
                    nc.scalar.activation(r, r, ACT.Exp, scale=-0.5).then_inc(st.on_rstd, 1)
            for c in range(CC):
                for j in range(NJ):
                    act.wait_ge(st.gate_ready, at(c, j))
                    nc.scalar.activation((kb, qg)[c][:, toks(j)], K.ps[:, 4 * c + j, :], ACT.Silu)\
                        .then_inc(st.gate_done, 1)
            act.wait_ge(st.on_done, 2 * NJ)
            inner.act(act, 1, h, ln2g, ln2b)
            for j in range(NJ):
                act.wait_ge(st.w2_ready, j + 1)
                nc.scalar.activation(kf[:, toks(j)], K.ps[:, j, :], ACT.Gelu, bias=b2).then_inc(st.gelu, 1)

        @block.gpsimd
        def _(pool):
            for i in range(2):
                p = nc.gpsimd.memset(xi[i][:, :, 0:PAD], 0.0)
            p.then_inc(st.edge, 1)
            pool.wait_ge(st.c_ready, 16)
            with pool.Fori(0, SEQS) as b:
                for u in range(2):
                    pool.wait_ge(st.small, b + 1)
                    nc.gpsimd.tensor_tensor(gl[:, u], heads(after), small[:, 0, u, :].unsqueeze(2).to_broadcast([P, H, P]),
                                            ALU.mult).then_inc(st.gl_done, 1)
                for u in range(2):
                    pool.wait_ge(st.gam_exp, b * 2 + (u + 1))
                    nc.gpsimd.tensor_tensor(gam[:, u], gam[:, u], heads(upto), ALU.mult).then_inc(st.gam_masked, 1)
                for lv in range(LEVELS):
                    for u in range(2):
                        pool.wait_ge(st.nt_done, b * 2 + (u + 1))
                        if lv >= 2:
                            pool.wait_ge(st.y_ready, b * (2 * LEVELS) + (2 * (lv - 2) + u + 1))
                        if lv == 2:
                            pool.wait_ge(st.xt_new, b * (2 * LEVELS) + (u + 1))
                        nc.gpsimd.tensor_tensor(bm[:, lv % 2, u], nt[:, u], heads(level_mask[lv]), ALU.mult)\
                            .then_inc(st.bm_done, 1)

        @block.vector
        def _(dve):
            outer.dve(dve, 0, K.x, y)
            for j in range(NJ):
                dve.wait_ge(outer.norm_ready, at(0, j))
            inner.dve(dve, 0, y)
            dve.wait_ge(st.w_ready, 16)
            for j in range(NJ):
                dve.wait_ge(st.rms_rstd, j + 1)
                nc.vector.scalar_tensor_tensor(h[:, toks(j)], h[:, toks(j)], rms_w, K.ln_sq[:, toks(j)],
                                               ALU.mult, ALU.mult).then_inc(st.h_ready, 1)
            for i in range(4):
                dve.wait_ge(st.x_in, at(i, NJ - 1))
                dve.wait_ge(st.edge, 1)
                nc.vector.tensor_scalar(seqs(cv[i]), xi[i % 2][:, :, 3:3 + LEN], conv_w[i][3], None, ALU.mult)\
                    .then_inc(st.conv, 1)
                for k in (2, 1, 0):
                    dve.wait_ge(st.conv, 3 * i + 3 - k)
                    nc.vector.scalar_tensor_tensor(seqs(cv[i]), xi[i % 2][:, :, k:k + LEN], conv_w[i][k], seqs(cv[i]),
                                                   ALU.mult, ALU.add).then_inc(st.conved if k == 0 else st.conv, 1)
            dve.wait_ge(st.ab_ready, 1)
            nc.vector.tensor_copy(ab2[:, :, :], K.ps[:, 7, 0:8 * NT].rearrange("p (n a) -> p n a", a=8))\
                .then_inc(st.ab_copied, 1)
            dve.wait_ge(st.ab_copied, 1)
            nc.vector.tensor_tensor(tile_h(z_), ab2[:, :, 0:4], dtb.unsqueeze(1).to_broadcast([P, NT, H]), ALU.add)\
                .then_inc(st.sp_in, 1)
            dve.wait_ge(st.sp_in, 1)
            nc.vector.tensor_scalar(n_, z_, -1.0, None, ALU.mult).then_inc(st.sp_n, 1)
            dve.wait_ge(st.sp_n, 1)
            nc.vector.tensor_tensor(e_, z_, n_, ALU.max).then_inc(st.sp_abs, 1)
            dve.wait_ge(st.sp_e, 1)
            nc.vector.tensor_scalar(d_, e_, 2.0, None, ALU.add).then_inc(st.sp_d, 1)
            dve.wait_ge(st.sp_d, 1)
            nc.vector.reciprocal(d_, d_).then_inc(st.sp_r, 1)
            dve.wait_ge(st.sp_r, 1)
            nc.vector.tensor_tensor(s_, e_, d_, ALU.mult).then_inc(st.sp_s, 1)
            dve.wait_ge(st.sp_s, 1)
            nc.vector.tensor_tensor(d_, s_, s_, ALU.mult).then_inc(st.sp_z, 1)
            dve.wait_ge(st.sp_z, 1)
            nc.vector.tensor_scalar(hh, d_, ATANH[0], None, ALU.mult).then_inc(st.sp_h, 1)
            for n, cf in enumerate(ATANH[1:-1]):
                dve.wait_ge(st.sp_h, n + 1)
                nc.vector.scalar_tensor_tensor(hh, hh, cf, d_, ALU.add, ALU.mult).then_inc(st.sp_h, 1)
            n = len(ATANH) - 1
            dve.wait_ge(st.sp_h, n)
            nc.vector.scalar_tensor_tensor(hh, hh, ATANH[-1], s_, ALU.add, ALU.mult).then_inc(st.sp_h, 1)
            dve.wait_ge(st.sp_h, n + 1)
            nc.vector.scalar_tensor_tensor(z_, z_, 0.0, hh, ALU.max, ALU.add).then_inc(st.sp_done, 1)
            dve.wait_ge(st.sp_done, 1)
            dve.wait_ge(st.ea, 1)
            nc.vector.scalar_tensor_tensor(tile_h(g), tile_h(z_), -1.0, ea[:, :].unsqueeze(1).to_broadcast([P, NT, H]),
                                           ALU.mult, ALU.mult).then_inc(st.g_done, 1)
            for i in range(2):
                for j in range(NJ):
                    dve.wait_ge(st.l2_rstd, at(i, j))
                    nc.vector.scalar_tensor_tensor(cv[i][:, toks(j)], cv[i][:, toks(j)], (KD ** -0.5, 1.0)[i],
                                                   (K.ln_xc, K.ln_sq)[i][:, toks(j)], ALU.mult, ALU.mult)\
                        .then_inc(st.l2_done, 1)
            dve.wait_ge(st.decay_exp, 1)
            dve.wait_ge(st.beta_done, 1)
            nc.vector.tensor_tensor(bg, beta, eg, ALU.mult).then_inc(st.beta_decay, 1)
            for m in range(NT // 2):
                dve.wait_ge(st.v_turned, m + 1)
                nc.vector.tensor_tensor(v_tm[:, 2 * m:2 * m + 2, :].rearrange("p n (h v) -> p (n h) v", v=VD),
                                        K.ps[:, 5 + m % 2, :].rearrange("p (n v) -> p n v", v=VD),
                                        beta[:, 2 * H * m:2 * H * (m + 1)].unsqueeze(2).to_broadcast([P, 2 * H, VD]),
                                        ALU.mult).then_inc(st.v_done, 1)
            for j in range(NJ):
                dve.wait_ge(st.k_turned, j + 1)
                nc.vector.tensor_tensor(k_tm[:, TPW * j:TPW * (j + 1), :].rearrange("p n (h k) -> p (n h) k", k=KD),
                                        K.ps[:, j, :].rearrange("p (n k) -> p n k", k=KD),
                                        er[:, 16 * j:16 * (j + 1)].unsqueeze(2).to_broadcast([P, 16, KD]),
                                        ALU.mult).then_inc(st.k_done, 1)
            dve.wait_ge(st.l2_done, 2 * NJ)
            for rep, src in ((rep_b, beta), (rep_g, g)):
                nc.vector.tensor_copy(rep[:, :].rearrange("p (n k) -> p n k", k=KD),
                                      src.unsqueeze(2).to_broadcast([P, NH, KD])).then_inc(st.rep_done, 1)
            for j in range(NJ):
                dve.wait_ge(st.bb_ready, j + 1)
                nc.vector.tensor_tensor(kb[:, toks(j)], kf[:, toks(j)], K.ps[:, j, :], ALU.mult).then_inc(st.kb_done, 1)
            for j in range(NJ):
                dve.wait_ge(st.gb_exp, j + 1)
                nc.vector.tensor_tensor(qg[:, toks(j)], qg[:, toks(j)], qf[:, toks(j)], ALU.mult)\
                    .then_inc(st.qg_done, 1)
            dve.wait_ge(st.beta_decay, 1)
            dve.wait_ge(st.v_done, NT // 2)
            with dve.Fori(0, SEQS) as b:
                nc.vector.tensor_copy(small[:, 0].rearrange("p u h -> p (u h)"), g[:, bass.ds(b * (2 * H), 2 * H)])
                nc.vector.tensor_copy(small[:, 1].rearrange("p u h -> p (u h)"), bg[:, bass.ds(b * (2 * H), 2 * H)])\
                    .then_inc(st.small, 1)
                for u in range(2):
                    dve.wait_ge(st.kk_ready, b * H + H)
                    dve.wait_ge(st.gam_masked, b * 2 + (u + 1))
                    for a, dst, done in ((0, nt, st.nt_done), (1, pt, st.pt_done)):
                        nc.vector.tensor_tensor(dst[:, u], K.ps[:, 4:8, toks(2 * u + a, P)], gam[:, u], ALU.mult)\
                            .then_inc(done, 1)
                for u in range(2):
                    dve.wait_ge(st.bm_done, b * (2 * LEVELS) + (u + 1))
                    nc.vector.tensor_tensor(xt[:, u], heads(K.ident), bm[:, 0, u], ALU.subtract).then_inc(st.xt_new, 1)
                    dve.wait_ge(st.y_ready, b * (2 * LEVELS) + (u + 1))
                    nc.vector.tensor_tensor(xm[:, u], heads(K.ident), bank4(K.ps[:, u, :]), ALU.subtract)\
                        .then_inc(st.x_new, 1)
                for lv in range(1, LEVELS):
                    for u in range(2):
                        dve.wait_ge(st.xt_ready, b * (2 * LEVELS - 2) + (2 * (lv - 1) + u + 1))
                        dve.wait_ge(st.xt_new, b * (2 * LEVELS) + (2 * (lv - 1) + u + 1))
                        if lv < LEVELS - 1:
                            dve.wait_ge(st.xx_ready, b * (2 * LEVELS - 4) + (2 * (lv - 1) + u + 1))
                        nc.vector.tensor_tensor(xt[:, u], xt[:, u], bank4(K.ps[:, 4 + u, :]), ALU.subtract)\
                            .then_inc(st.xt_new, 1)
                        if lv < LEVELS - 1:
                            dve.wait_ge(st.x_new, b * (2 * LEVELS - 2) + (2 * (lv - 1) + u + 1))
                            nc.vector.tensor_tensor(xm[:, u], xm[:, u], bank4(K.ps[:, 2 + u, :]), ALU.subtract)\
                                .then_inc(st.x_new, 1)
                dve.wait_ge(st.s_ready, b + 1)
                nc.vector.tensor_tensor(state[:, :], K.ps[:, 7, 0:H * VD], s_mask, ALU.mult).then_inc(st.s_done, 1)
                dve.wait_ge(st.small, b + 1)
                dve.wait_ge(st.ks_ready, b + 1)
                nc.vector.tensor_tensor(hv(ksd[:, :]), hv(K.ps[:, 0, 0:H * VD]),
                                        small[:, 1, 1, :].unsqueeze(2).to_broadcast([P, H, VD]), ALU.mult)\
                    .then_inc(st.ks_decay, 1)
                dve.wait_ge(st.ks_decay, b + 1)
                nc.vector.tensor_tensor(rr[:, :], v_tm[:, bass.ds(b * 2 + 1, 1), :].rearrange("p a v -> p (a v)"),
                                        ksd[:, :], ALU.subtract).then_inc(st.r_done, 1)
            for c in range(CC):
                for j in range(NJ):
                    dve.wait_ge(st.on_rstd, at(c, j))
                    nc.vector.scalar_tensor_tensor(o_f[:, c, toks(j)], o_f[:, c, toks(j)], onw,
                                                   (K.ln_xc, K.ln_sq)[c][:, toks(j)], ALU.mult, ALU.mult)\
                        .then_inc(st.on_done, 1)
            for c in range(CC):
                for j in range(NJ):
                    dve.wait_ge(st.gate_done, at(c, j))
                    dve.wait_ge(st.on_done, at(c, j))
                    nc.vector.tensor_tensor(o_f[:, c, toks(j)], o_f[:, c, toks(j)], (kb, qg)[c][:, toks(j)], ALU.mult)\
                        .then_inc(st.gated, 1)
            for j in range(NJ):
                dve.wait_ge(st.enc_ready, j + 1)
                nc.vector.tensor_tensor(y[:, toks(j)], y[:, toks(j)], K.ps[:, j, :], ALU.add).then_inc(st.y_enc, 1)
            for j in range(NJ):
                dve.wait_ge(st.y_enc, j + 1)
                nc.vector.tensor_tensor(K.x[:, toks(j)], K.x[:, toks(j)], y[:, toks(j)], ALU.add).then_inc(st.x_sum, 1)
            inner.dve(dve, 1, y)
            for j in range(NJ):
                dve.wait_ge(st.gelu, j + 1)
                dve.wait_ge(st.x_sum, j + 1)
                nc.vector.tensor_tensor(K.x[:, toks(j)], K.x[:, toks(j)], kf[:, toks(j)], ALU.add)\
                    .then_inc(st.x_done, 1)
    st.end()


def lora_linear_stage(K, tag):
    nc = K.nc
    st = Stage(nc, f"lora{tag}")
    (st.w_ready, st.t1_ready, st.t1_copied, st.t2_ready, st.t2_copied, st.delta_ready,
     st.weff_ready, st.out_ready, st.x_done) = st.signals(
        "w_ready t1_ready t1_copied t2_ready t2_copied delta_ready weff_ready out_ready x_done")
    outer = LayerNorm(K, st, "outer_")
    wt = st.sb("wt", [P, K.d["lora_w"].shape[1]])
    w_t, down_t, down_aux, up_t, upaux_t, bias = (
        wt[:, 0:128], wt[0:100, 128:132], wt[0:100, 132:260], wt[0:4, 260:310], wt[0:50, 310:438], wt[:, 438:439])
    t1 = st.sb("t1", [4, P])
    t2 = st.sb("t2", [50, P])
    weff = st.sb("weff", [P, P])
    with nc.Block() as block:
        @block.sync
        def _(sp):
            sp.dma_start(wt[:, :], K.d["lora_w"]).then_inc(st.w_ready, 16)

        @block.tensor
        def _(pe):
            pe.wait_ge(st.w_ready, 16)
            outer.pe(pe, 0, K.x, lambda j: None)
            pe.wait_ge(outer.centered, at(0, NJ - 1))
            nc.tensor.matmul(K.ps[0:4, 0, 0:128], down_t, down_aux, start=True, stop=True).then_inc(st.t1_ready, 1)
            pe.wait_ge(st.t1_copied, 1)
            nc.tensor.matmul(K.ps[0:50, 1, 0:128], up_t, t1[:, :], start=True, stop=True).then_inc(st.t2_ready, 1)
            pe.wait_ge(st.t2_copied, 1)
            nc.tensor.matmul(K.ps[:, 2, 0:128], t2[:, :], upaux_t, start=True, stop=True).then_inc(st.delta_ready, 1)
            pe.wait_ge(st.weff_ready, 1)
            for j in range(NJ):
                pe.wait_ge(outer.norm_ready, at(0, j))
                nc.tensor.matmul(K.ps[:, j, :], weff[:, :], K.h[:, toks(j)], start=True, stop=True)\
                    .then_inc(st.out_ready, 1)

        @block.scalar
        def _(act):
            nc.scalar.preload_act_table_set("natural_log_exp_and_others")
            outer.act(act, 0)

        @block.vector
        def _(dve):
            outer.dve(dve, 0, K.x, K.h)
            dve.wait_ge(st.t1_ready, 1)
            nc.vector.tensor_copy(t1[:, :], K.ps[0:4, 0, 0:128]).then_inc(st.t1_copied, 1)
            dve.wait_ge(st.t2_ready, 1)
            nc.vector.tensor_copy(t2[:, :], K.ps[0:50, 1, 0:128]).then_inc(st.t2_copied, 1)
            dve.wait_ge(st.w_ready, 16)
            dve.wait_ge(st.delta_ready, 1)
            nc.vector.tensor_tensor(weff[:, :], K.ps[:, 2, 0:128], w_t, ALU.add).then_inc(st.weff_ready, 1)
            for j in range(NJ):
                dve.wait_ge(st.out_ready, j + 1)
                nc.vector.scalar_tensor_tensor(K.x[:, toks(j)], K.ps[:, j, :], bias, K.x[:, toks(j)],
                                               ALU.add, ALU.add).then_inc(st.x_done, 1)
    st.end()


def lora_linear_first(K):
    lora_linear_stage(K, 0)


def lora_linear_second(K):
    lora_linear_stage(K, 1)


def lstm_stage(K):
    nc = K.nc
    st = Stage(nc, "lstm")
    (st.w_ready, st.gates_ready, st.gates_done, st.tanh_done, st.c_part, st.c_new, st.c_tanh,
     st.h_ready) = st.signals(
        "w_ready gates_ready gates_done tanh_done c_part c_new c_tanh h_ready")
    outer = LayerNorm(K, st, "outer_")
    wt = st.sb("wt", [P, K.d["lstm_w"].shape[1]])
    w = [wt[:, toks(g, P)] for g in range(4)]
    u = [wt[:, 512 + P * g:512 + P * (g + 1)] for g in range(4)]
    bias = [wt[:, 1024 + g:1025 + g] for g in range(4)]
    gate = st.sb("gate", [P, 4, LEN])
    part = st.sb("part", [P, LEN])
    c = st.sb("c", [P, LEN])
    tc = st.sb("tc", [P, LEN])
    hs = st.sb("hs", [P, SEQS, LEN])
    with nc.Block() as block:
        @block.sync
        def _(sp):
            sp.dma_start(wt[:, :], K.d["lstm_w"]).then_inc(st.w_ready, 16)

        @block.tensor
        def _(pe):
            pe.wait_ge(st.w_ready, 16)
            outer.pe(pe, 0, K.x, lambda j: None)
            for s in range(SEQS):
                if s < 2:
                    pe.wait_ge(outer.log_ready, at(0, NJ - 1))
                else:
                    pe.wait_ge(st.gates_done, 4 * (s - 1))
                pe.wait_ge(outer.norm_ready, at(0, s // SPW))
                for g in range(4):
                    mm = nc.tensor.matmul(K.ps[:, 4 * (s % 2) + g, 0:LEN], w[g], K.h[:, toks(s, LEN)],
                                          start=True, stop=(s == 0))
                    if s == 0:
                        mm.then_inc(st.gates_ready, 1)
                if s > 0:
                    pe.wait_ge(st.h_ready, s)
                    for g in range(4):
                        nc.tensor.matmul(K.ps[:, 4 * (s % 2) + g, 0:LEN], u[g], hs[:, s - 1, :],
                                         start=False, stop=True).then_inc(st.gates_ready, 1)

        @block.scalar
        def _(act):
            nc.scalar.preload_act_table_set("natural_log_exp_and_others")
            outer.act(act, 0)
            act.wait_ge(st.w_ready, 16)
            for s in range(SEQS):
                for g, f in ((0, ACT.Sigmoid), (1, ACT.Sigmoid), (2, ACT.Sigmoid), (3, ACT.Tanh)):
                    act.wait_ge(st.gates_ready, 4 * s + g + 1)
                    if g == 0 and s > 0:
                        act.wait_ge(st.h_ready, s)
                    nc.scalar.activation(gate[:, g, :], K.ps[:, 4 * (s % 2) + g, 0:LEN], f, bias=bias[g])\
                        .then_inc(st.gates_done, 1)
                act.wait_ge(st.c_new, s + 1)
                nc.scalar.activation(tc[:, :], c[:, :], ACT.Tanh).then_inc(st.c_tanh, 1)

        @block.vector
        def _(dve):
            outer.dve(dve, 0, K.x, K.h)
            for s in range(SEQS):
                dve.wait_ge(st.gates_done, 4 * s + 4)
                if s == 0:
                    nc.vector.tensor_tensor(c[:, :], gate[:, 0, :], gate[:, 3, :], ALU.mult).then_inc(st.c_new, 1)
                else:
                    nc.vector.tensor_tensor(part[:, :], gate[:, 0, :], gate[:, 3, :], ALU.mult)\
                        .then_inc(st.c_part, 1)
                    nc.vector.tensor_tensor(c[:, :], gate[:, 1, :], c[:, :], ALU.mult).then_inc(st.c_part, 1)
                    dve.wait_ge(st.c_part, 2 * s)
                    nc.vector.tensor_tensor(c[:, :], c[:, :], part[:, :], ALU.add).then_inc(st.c_new, 1)
                dve.wait_ge(st.c_tanh, s + 1)
                nc.vector.tensor_tensor(hs[:, s, :], gate[:, 2, :], tc[:, :], ALU.mult).then_inc(st.h_ready, 1)
            dve.wait_ge(st.h_ready, SEQS)
            nc.vector.tensor_tensor(K.x[:, :], K.x[:, :], hs[:, :, :].rearrange("p s n -> p (s n)"), ALU.add)
    st.end()


TWO_PI_HI = float(np.float32(6.28125))
TWO_PI_LO = float(np.float32(2 * np.pi - 6.28125))
ROUND = float(1.5 * 2 ** 23)


def lru_stage(K):
    nc = K.nc
    st = Stage(nc, "lru")
    (st.w_ready, st.sp_e, st.sp_d, st.sp_r, st.sp_s, st.sp_z, st.sp_h, st.decay_col, st.xh_ready,
     st.xh_done, st.gate_ready, st.gate_done, st.xg, st.logr_done, st.r_done, st.e2, st.om,
     st.norm_log, st.norm_done, st.masked, st.theta, st.phi, st.turn0, st.turn1, st.turn2,
     st.turn3, st.half, st.sin_done, st.cos_sq, st.cos_done, st.xn, st.rot_a, st.rot_b, st.rot_c,
     st.rot_d, st.rotated, st.scanned, st.out_ready, st.x_done, st.hrot_done) = st.signals(
        "w_ready sp_e sp_d sp_r sp_s sp_z sp_h decay_col xh_ready xh_done gate_ready gate_done xg "
        "logr_done r_done e2 om norm_log norm_done masked theta phi turn0 turn1 turn2 turn3 half "
        "sin_done cos_sq cos_done xn rot_a rot_b rot_c rot_d rotated scanned out_ready x_done "
        "hrot_done")
    outer = LayerNorm(K, st, "outer_")
    wt = st.sb("wt", [P, K.d["lru_w"].shape[1]])
    win = [wt[:, 0:128], wt[:, 128:256]]
    gates_w = [[wt[:, 256 + 128 * (2 * g + c):384 + 128 * (2 * g + c)] for c in range(2)] for g in range(2)]
    wout = [wt[:, 768:896], wt[:, 896:1024]]
    b_in = [wt[:, 1024:1025], wt[:, 1025:1026]]
    b_gate = [wt[:, 1026:1027], wt[:, 1027:1028]]
    a_real, a_imag, b_out = wt[:, 1028:1029], wt[:, 1029:1030], wt[:, 1030:1031]
    col = st.sb("col", [P, 12])
    xh = st.sb("xh", [P, 2, TOK])
    gx = st.sb("gx", [P, TOK])
    ga = st.sb("ga", [P, TOK])
    r = st.sb("r", [P, TOK])
    nrm = st.sb("nrm", [P, TOK])
    ph = st.sb("ph", [P, TOK])
    tn = st.sb("tn", [P, TOK])
    sn = st.sb("sn", [P, TOK])
    cs = st.sb("cs", [P, TOK])
    seq = lambda ap: ap.rearrange("p (s n) -> p s n", n=LEN)
    e, d2, rc, s_, z, hh, sp_, decay, decay2 = (col[:, i:i + 1] for i in range(9))
    ta, tb = K.ln_xc, K.ln_sq
    with nc.Block() as block:
        @block.sync
        def _(sp):
            sp.dma_start(wt[:, :], K.d["lru_w"]).then_inc(st.w_ready, 16)

        @block.tensor
        def _(pe):
            outer.pe(pe, 0, K.x, lambda j: None)
            pe.wait_ge(st.w_ready, 16)
            for j in range(NJ):
                pe.wait_ge(outer.norm_ready, at(0, j))
                for c in range(2):
                    nc.tensor.matmul(K.ps[:, 4 * c + j, :], win[c], K.h[:, toks(j)], start=True, stop=True)\
                        .then_inc(st.xh_ready, 1)
            for j in range(NJ):
                pe.wait_ge(st.xh_done, 2 * j + 2)
                for g in range(2):
                    for c in range(2):
                        mm = nc.tensor.matmul(K.ps[:, 4 * g + j, :], gates_w[g][c], xh[:, c, toks(j)],
                                              start=(c == 0), stop=(c == 1))
                    mm.then_inc(st.gate_ready, 1)
            for j in range(NJ):
                pe.wait_ge(st.gate_done, 2 * j + 2)
                pe.wait_ge(st.hrot_done, 2)
                for c in range(2):
                    mm = nc.tensor.matmul(K.ps[:, j, :], wout[c], xh[:, c, toks(j)], start=(c == 0), stop=(c == 1))
                mm.then_inc(st.out_ready, 1)

        @block.scalar
        def _(act):
            nc.scalar.preload_act_table_set("natural_log_exp_and_others")
            outer.act(act, 0)
            act.wait_ge(st.w_ready, 16)
            act.wait_ge(st.sp_z, 1)
            nc.scalar.activation(e, z, ACT.Exp, scale=-1.0).then_inc(st.sp_e, 1)
            for j in range(NJ):
                for c in range(2):
                    act.wait_ge(st.xh_ready, 2 * j + c + 1)
                    nc.scalar.activation(xh[:, c, toks(j)], K.ps[:, 4 * c + j, :], ACT.Identity, bias=b_in[c])\
                        .then_inc(st.xh_done, 1)
            for j in range(NJ):
                for g in range(2):
                    act.wait_ge(st.gate_ready, 2 * j + g + 1)
                    nc.scalar.activation((gx, ga)[g][:, toks(j)], K.ps[:, 4 * g + j, :], ACT.Sigmoid, bias=b_gate[g])\
                        .then_inc(st.gate_done, 1)
            act.wait_ge(st.gate_done, 2 * NJ)
            act.wait_ge(st.decay_col, 2)
            nc.scalar.activation(r[:, :], ga[:, :], ACT.Exp, scale=decay).then_inc(st.r_done, 1)
            nc.scalar.activation(nrm[:, :], ga[:, :], ACT.Exp, scale=decay2).then_inc(st.e2, 1)
            act.wait_ge(st.om, 2)
            nc.scalar.activation(nrm[:, :], nrm[:, :], ACT.Ln).then_inc(st.norm_log, 1)
            act.wait_ge(st.norm_log, 1)
            nc.scalar.activation(nrm[:, :], nrm[:, :], ACT.Exp, scale=0.5).then_inc(st.norm_done, 1)
            act.wait_ge(st.turn3, 1)
            nc.scalar.activation(cs[:, :], ph[:, :], ACT.Sin, scale=0.5).then_inc(st.half, 1)
            nc.scalar.activation(sn[:, :], ph[:, :], ACT.Sin).then_inc(st.sin_done, 1)
            act.wait_ge(st.half, 1)
            nc.scalar.activation(cs[:, :], cs[:, :], ACT.Square).then_inc(st.cos_sq, 1)

        @block.vector
        def _(dve):
            dve.wait_ge(st.w_ready, 16)
            nc.vector.tensor_scalar(s_, a_real, -1.0, None, ALU.mult).then_inc(st.sp_s, 1)
            dve.wait_ge(st.sp_s, 1)
            nc.vector.tensor_tensor(z, a_real, s_, ALU.max).then_inc(st.sp_z, 1)
            outer.dve(dve, 0, K.x, K.h)
            dve.wait_ge(st.sp_e, 1)
            nc.vector.tensor_scalar(d2, e, 2.0, None, ALU.add).then_inc(st.sp_d, 1)
            dve.wait_ge(st.sp_d, 1)
            nc.vector.reciprocal(rc, d2).then_inc(st.sp_r, 1)
            dve.wait_ge(st.sp_r, 1)
            nc.vector.tensor_tensor(s_, e, rc, ALU.mult).then_inc(st.sp_s, 1)
            dve.wait_ge(st.sp_s, 2)
            nc.vector.tensor_tensor(z, s_, s_, ALU.mult).then_inc(st.sp_z, 1)
            dve.wait_ge(st.sp_z, 2)
            nc.vector.tensor_scalar(hh, z, ATANH[0], None, ALU.mult).then_inc(st.sp_h, 1)
            for n, cf in enumerate(ATANH[1:-1]):
                dve.wait_ge(st.sp_h, n + 1)
                nc.vector.scalar_tensor_tensor(hh, hh, cf, z, ALU.add, ALU.mult).then_inc(st.sp_h, 1)
            n = len(ATANH) - 1
            dve.wait_ge(st.sp_h, n)
            nc.vector.scalar_tensor_tensor(hh, hh, ATANH[-1], s_, ALU.add, ALU.mult).then_inc(st.sp_h, 1)
            dve.wait_ge(st.sp_h, n + 1)
            nc.vector.scalar_tensor_tensor(sp_, a_real, 0.0, hh, ALU.max, ALU.add).then_inc(st.sp_h, 1)
            dve.wait_ge(st.sp_h, n + 2)
            nc.vector.tensor_scalar(decay, sp_, -8.0, None, ALU.mult).then_inc(st.decay_col, 1)
            nc.vector.tensor_scalar(decay2, sp_, -16.0, None, ALU.mult).then_inc(st.decay_col, 1)
            dve.wait_ge(st.gate_done, 2 * NJ)
            nc.vector.tensor_scalar(tn[:, :], ga[:, :], a_imag, None, ALU.mult).then_inc(st.theta, 1)
            dve.wait_ge(st.theta, 1)
            for s in range(SEQS):
                nc.vector.tensor_tensor_scan(ph[:, toks(s, LEN)], K.one.to_broadcast([P, LEN]),
                                             tn[:, toks(s, LEN)], 0.0, ALU.mult, ALU.add).then_inc(st.phi, 1)
            dve.wait_ge(st.phi, SEQS)
            nc.vector.tensor_scalar(tn[:, :], ph[:, :], 1.0 / (2 * np.pi), ROUND, ALU.mult, ALU.add)\
                .then_inc(st.turn0, 1)
            dve.wait_ge(st.turn0, 1)
            nc.vector.tensor_scalar(tn[:, :], tn[:, :], ROUND, None, ALU.subtract).then_inc(st.turn1, 1)
            dve.wait_ge(st.turn1, 1)
            nc.vector.scalar_tensor_tensor(ph[:, :], tn[:, :], -TWO_PI_HI, ph[:, :], ALU.mult, ALU.add)\
                .then_inc(st.turn2, 1)
            dve.wait_ge(st.turn2, 1)
            nc.vector.scalar_tensor_tensor(ph[:, :], tn[:, :], -TWO_PI_LO, ph[:, :], ALU.mult, ALU.add)\
                .then_inc(st.turn2, 1)
            dve.wait_ge(st.turn2, 2)
            nc.vector.tensor_scalar(ph[:, :], ph[:, :], PI_IN, -PI_IN, ALU.min, ALU.max).then_inc(st.turn3, 1)
            dve.wait_ge(st.e2, 1)
            nc.vector.tensor_scalar(nrm[:, :], nrm[:, :], -1.0, 1.0, ALU.mult, ALU.add).then_inc(st.om, 1)
            dve.wait_ge(st.om, 1)
            nc.vector.tensor_scalar(nrm[:, :], nrm[:, :], 1e-6, None, ALU.max).then_inc(st.om, 1)
            dve.wait_ge(st.r_done, 1)
            nc.vector.memset(seq(r[:, :])[:, :, 0:1], 0.0).then_inc(st.masked, 1)
            dve.wait_ge(st.norm_done, 1)
            nc.vector.tensor_tensor(gx[:, :], gx[:, :], nrm[:, :], ALU.mult).then_inc(st.xg, 1)
            dve.wait_ge(st.xg, 1)
            for c in range(2):
                nc.vector.tensor_tensor(xh[:, c, :], xh[:, c, :], gx[:, :], ALU.mult).then_inc(st.xn, 1)
            dve.wait_ge(st.cos_sq, 1)
            nc.vector.tensor_scalar(cs[:, :], cs[:, :], -2.0, 1.0, ALU.mult, ALU.add).then_inc(st.cos_done, 1)
            dve.wait_ge(st.cos_done, 1)
            dve.wait_ge(st.sin_done, 1)
            dve.wait_ge(st.xn, 2)
            dve.wait_ge(outer.norm_ready, NJ)
            nc.vector.tensor_tensor(ta[:, :], cs[:, :], xh[:, 0, :], ALU.mult).then_inc(st.rot_a, 1)
            nc.vector.tensor_tensor(tb[:, :], sn[:, :], xh[:, 1, :], ALU.mult).then_inc(st.rot_b, 1)
            nc.vector.tensor_tensor(gx[:, :], cs[:, :], xh[:, 1, :], ALU.mult).then_inc(st.rot_c, 1)
            nc.vector.tensor_tensor(tn[:, :], sn[:, :], xh[:, 0, :], ALU.mult).then_inc(st.rot_d, 1)
            dve.wait_ge(st.rot_b, 1)
            nc.vector.tensor_tensor(nrm[:, :], ta[:, :], tb[:, :], ALU.add).then_inc(st.rotated, 1)
            dve.wait_ge(st.rot_d, 1)
            nc.vector.tensor_tensor(gx[:, :], gx[:, :], tn[:, :], ALU.subtract).then_inc(st.rotated, 1)
            dve.wait_ge(st.rotated, 2)
            dve.wait_ge(st.masked, 1)
            nc.vector.tensor_tensor_scan(ta[:, :], r[:, :], nrm[:, :], 0.0, ALU.mult, ALU.add).then_inc(st.scanned, 1)
            nc.vector.tensor_tensor_scan(tb[:, :], r[:, :], gx[:, :], 0.0, ALU.mult, ALU.add).then_inc(st.scanned, 1)
            dve.wait_ge(st.scanned, 2)
            nc.vector.tensor_tensor(nrm[:, :], cs[:, :], ta[:, :], ALU.mult).then_inc(st.rot_a, 1)
            nc.vector.tensor_tensor(gx[:, :], sn[:, :], tb[:, :], ALU.mult).then_inc(st.rot_b, 1)
            nc.vector.tensor_tensor(tn[:, :], sn[:, :], ta[:, :], ALU.mult).then_inc(st.rot_c, 1)
            nc.vector.tensor_tensor(ph[:, :], cs[:, :], tb[:, :], ALU.mult).then_inc(st.rot_d, 1)
            dve.wait_ge(st.rot_b, 2)
            nc.vector.tensor_tensor(xh[:, 0, :], nrm[:, :], gx[:, :], ALU.subtract).then_inc(st.hrot_done, 1)
            dve.wait_ge(st.rot_d, 2)
            nc.vector.tensor_tensor(xh[:, 1, :], tn[:, :], ph[:, :], ALU.add).then_inc(st.hrot_done, 1)
            for j in range(NJ):
                dve.wait_ge(st.out_ready, j + 1)
                nc.vector.scalar_tensor_tensor(K.x[:, toks(j)], K.ps[:, j, :], b_out, K.x[:, toks(j)],
                                               ALU.add, ALU.add).then_inc(st.x_done, 1)
    st.end()


def channel_mix_stage(K, tag):
    nc = K.nc
    st = Stage(nc, f"chmix{tag}")
    (st.w_ready, st.omm_ready, st.prev_ready, st.prev_edge, st.mixed, st.r_ready, st.r_gate,
     st.k_ready, st.k_relu, st.k_sq, st.v_ready, st.out_gated, st.x_done) = st.signals(
        "w_ready omm_ready prev_ready prev_edge mixed r_ready r_gate k_ready k_relu k_sq v_ready "
        "out_gated x_done")
    outer = LayerNorm(K, st, "outer_")
    wt = st.sb("wt", [P, K.d["chmix_w"].shape[1]])
    wr, wk, wv = (wt[:, toks(i, P)] for i in range(3))
    mu = [wt[:, 384:385], wt[:, 385:386]]
    omm = st.sb("omm", [P, 2])
    prev = st.sb("prev", [P, 2, TOK])
    mix = st.sb("mix", [P, 2, TOK])
    r = st.sb("r", [P, TOK])
    ka = st.sb("ka", [P, TOK])
    h = K.h
    with nc.Block() as block:
        @block.sync
        def _(sp):
            sp.dma_start(wt[:, :], K.d["chmix_w"]).then_inc(st.w_ready, 16)

        @block.tensor
        def _(pe):
            outer.pe(pe, 0, K.x, lambda j: None)
            pe.wait_ge(st.w_ready, 16)
            for j in range(NJ):
                pe.wait_ge(st.mixed, 2 * j + 1)
                nc.tensor.matmul(K.ps[:, j, :], wr, mix[:, 0, toks(j)], start=True, stop=True).then_inc(st.r_ready, 1)
                pe.wait_ge(st.mixed, 2 * j + 2)
                nc.tensor.matmul(K.ps[:, 4 + j, :], wk, mix[:, 1, toks(j)], start=True, stop=True)\
                    .then_inc(st.k_ready, 1)
            for j in range(NJ):
                pe.wait_ge(st.k_sq, j + 1)
                nc.tensor.matmul(K.ps[:, 4 + j, :], wv, ka[:, toks(j)], start=True, stop=True).then_inc(st.v_ready, 1)

        @block.scalar
        def _(act):
            nc.scalar.preload_act_table_set("natural_log_exp_and_others")
            outer.act(act, 0)
            act.wait_ge(st.omm_ready, 1)
            for j in range(NJ):
                for i in range(2):
                    act.wait_ge(outer.norm_ready, at(0, j))
                    seqs = h[:, toks(j)].rearrange("p (s n) -> p s n", n=LEN)
                    dst = prev[:, i, toks(j)].rearrange("p (s n) -> p s n", n=LEN)
                    act.wait_ge(st.prev_edge, 1)
                    nc.scalar.activation(dst[:, :, 1:LEN], seqs[:, :, 0:LEN - 1], ACT.Copy, scale=omm[:, i:i + 1])\
                        .then_inc(st.prev_ready, 1)
            for j in range(NJ):
                act.wait_ge(st.k_ready, j + 1)
                nc.scalar.activation(ka[:, toks(j)], K.ps[:, 4 + j, :], ACT.Relu).then_inc(st.k_relu, 1)
            for j in range(NJ):
                act.wait_ge(st.k_relu, j + 1)
                nc.scalar.activation(ka[:, toks(j)], ka[:, toks(j)], ACT.Square).then_inc(st.k_sq, 1)
            for j in range(NJ):
                act.wait_ge(st.r_ready, j + 1)
                nc.scalar.activation(r[:, toks(j)], K.ps[:, j, :], ACT.Sigmoid).then_inc(st.r_gate, 1)

        @block.vector
        def _(dve):
            nc.vector.memset(prev[:, :, :].rearrange("p i (s n) -> p (i s) n", n=LEN)[:, :, 0:1], 0.0)\
                .then_inc(st.prev_edge, 1)
            dve.wait_ge(st.w_ready, 16)
            nc.vector.tensor_scalar(omm[:, :], wt[:, 384:386], -1.0, 1.0, ALU.mult, ALU.add).then_inc(st.omm_ready, 1)
            outer.dve(dve, 0, K.x, h)
            dve.wait_ge(st.prev_edge, 1)
            for j in range(NJ):
                dve.wait_ge(outer.norm_ready, at(0, j))
                for i in range(2):
                    dve.wait_ge(st.prev_ready, 2 * j + i + 1)
                    nc.vector.scalar_tensor_tensor(mix[:, i, toks(j)], h[:, toks(j)], mu[i], prev[:, i, toks(j)],
                                                   ALU.mult, ALU.add).then_inc(st.mixed, 1)
            for j in range(NJ):
                dve.wait_ge(st.v_ready, j + 1)
                dve.wait_ge(st.r_gate, j + 1)
                nc.vector.tensor_tensor(r[:, toks(j)], K.ps[:, 4 + j, :], r[:, toks(j)], ALU.mult)\
                    .then_inc(st.out_gated, 1)
            for j in range(NJ):
                dve.wait_ge(st.out_gated, j + 1)
                nc.vector.tensor_tensor(K.x[:, toks(j)], K.x[:, toks(j)], r[:, toks(j)], ALU.add)\
                    .then_inc(st.x_done, 1)
    st.end()


def channel_mix_first(K):
    channel_mix_stage(K, 0)


def channel_mix_second(K):
    channel_mix_stage(K, 1)


def causal_attention_stage(K):
    nc = K.nc
    st = Stage(nc, "causal")
    (st.w_ready, st.qk_ready, st.qk_done, st.v_ready, st.v_copied, st.o_turned, st.x_done) = st.signals(
        "w_ready qk_ready qk_done v_ready v_copied o_turned x_done")
    outer = LayerNorm(K, st, "outer_")
    wt = st.sb("wt", [P, K.d["causal_w"].shape[1]])
    wq, wk, wv = (wt[:, toks(i, P)] for i in range(3))
    bias = [wt[:, 384 + i:385 + i] for i in range(3)]
    qk = st.sb("qk", [P, 2, TOK])
    vt = st.sb("vt", [P, TOK])
    o = st.sb("o", [P, TOK])
    groups = []
    for s in range(SEQS):
        for t in range(2):
            q = qk[:, 0, s * LEN + t * P:s * LEN + (t + 1) * P]
            k = qk[:, 1, s * LEN:s * LEN + (t + 1) * P]
            v = [[vt[:, toks(2 * s + kt, P)] for kt in range(t + 1)]]
            groups.append(([(q, k)], t + 1, K.causal[:, LEN * t:LEN * t + (t + 1) * P], v,
                           o[:, toks(2 * s + t, P)].unsqueeze(1)))
    att = Attention(K, st, groups, 1, P, float(P) ** -0.5)
    with nc.Block() as block:
        @block.sync
        def _(sp):
            sp.dma_start(wt[:, :], K.d["causal_w"]).then_inc(st.w_ready, 16)

        @block.tensor
        def _(pe):
            outer.pe(pe, 0, K.x, lambda j: None)
            pe.wait_ge(st.w_ready, 16)
            for i, w in enumerate((wq, wk)):
                for j in range(NJ):
                    pe.wait_ge(outer.norm_ready, at(0, j))
                    nc.tensor.matmul(K.ps[:, 4 * i + j, :], w, K.h[:, toks(j)], start=True, stop=True)\
                        .then_inc(st.qk_ready, 1)
            for j in range(NJ):
                pe.wait_ge(st.qk_done, at(0, j))
                for t in range(TPW):
                    mm = nc.tensor.matmul(K.ps[:, j, toks(t, P)], K.h[:, toks(TPW * j + t, P)], wv,
                                          start=True, stop=True)
                mm.then_inc(st.v_ready, 1)
            pe.wait_ge(st.qk_done, 2 * NJ)
            pe.wait_ge(st.v_copied, NJ)
            att.pe(pe, 0, lambda g: None)
            pe.wait_ge(att.o_copied, att.n)
            for j in range(NJ):
                for t in range(TPW):
                    mm = nc.tensor.transpose(K.ps[:, j, toks(t, P)], o[:, toks(TPW * j + t, P)], K.ident)
                mm.then_inc(st.o_turned, 1)

        @block.scalar
        def _(act):
            nc.scalar.preload_act_table_set("natural_log_exp_and_others")
            outer.act(act, 0)
            act.wait_ge(st.w_ready, 16)
            for i in range(2):
                for j in range(NJ):
                    act.wait_ge(st.qk_ready, at(i, j))
                    nc.scalar.activation(qk[:, i, toks(j)], K.ps[:, 4 * i + j, :], ACT.Identity, bias=bias[i])\
                        .then_inc(st.qk_done, 1)
            for j in range(NJ):
                act.wait_ge(st.v_ready, j + 1)
                nc.scalar.activation(vt[:, toks(j)], K.ps[:, j, :], ACT.Copy).then_inc(st.v_copied, 1)
            att.act(act, 0)

        @block.vector
        def _(dve):
            outer.dve(dve, 0, K.x, K.h)
            att.dve(dve, 0)
            dve.wait_ge(st.w_ready, 16)
            for j in range(NJ):
                dve.wait_ge(st.o_turned, j + 1)
                nc.vector.scalar_tensor_tensor(K.x[:, toks(j)], K.ps[:, j, :], bias[2], K.x[:, toks(j)],
                                               ALU.add, ALU.add).then_inc(st.x_done, 1)
    st.end()


def mamba_stage(K):
    nc = K.nc
    NS, DTR, CC, PAD = 16, 64, 2, 3
    st = Stage(nc, "mamba")
    (st.w_ready, st.in_ready, st.x_in, st.edge, st.z_done, st.conv, st.conved, st.silu_done,
     st.xdbl_ready, st.xdbl_copied, st.dt_ready, st.dt_biased, st.dt_abs, st.dt_exp, st.sp_w,
     st.sp_rest, st.sp_most, st.sp_log, st.dt_done, st.a_exp, st.a_neg, st.a_tiny, st.a_keep,
     st.a_safe, st.a_inv, st.picked, st.bc_ready, st.abar_done, st.bx_done, st.b_used, st.cut,
     st.scanned, st.c_used, st.summed, st.y_d, st.y_gated, st.out_ready, st.x_done, st.zeroed) = st.signals(
        "w_ready in_ready x_in edge z_done conv conved silu_done xdbl_ready xdbl_copied dt_ready "
        "dt_biased dt_abs dt_exp sp_w sp_rest sp_most sp_log dt_done a_exp a_neg a_tiny a_keep a_safe "
        "a_inv picked bc_ready abar_done bx_done b_used cut scanned c_used summed y_d y_gated "
        "out_ready x_done zeroed")
    outer = LayerNorm(K, st, "outer_")
    wt = st.sb("wt", [P, K.d["mamba_w"].shape[1]])
    o = 0
    win = [wt[:, toks(i, P)] for i in range(4)]
    o += 512
    wx = [wt[:, o + 96 * c:o + 96 * (c + 1)] for c in range(CC)]
    o += 192
    wdt = [wt[0:DTR, o + P * c:o + P * (c + 1)] for c in range(CC)]
    o += 256
    wo = [wt[:, o + P * c:o + P * (c + 1)] for c in range(CC)]
    o += 256
    a_log = wt[:, o:o + CC * NS]
    o += CC * NS
    conv_w = [[wt[:, o + 4 * c + k:o + 4 * c + k + 1] for k in range(4)] for c in range(CC)]
    o += 8
    in_b = [wt[:, o + i:o + i + 1] for i in range(4)]
    conv_b, d_skip, dt_b = ([wt[:, o + 4 + 2 * i + c:o + 5 + 2 * i + c] for c in range(CC)] for i in range(3))
    out_b = wt[:, o + 10:o + 11]
    xi = st.sb("xi", [P, CC, SEQS, LEN + PAD])
    xc = st.sb("xc", [P, CC, TOK])
    xd = st.sb("xd", [96, TOK])
    dt = st.sb("dt", [P, CC, TOK])
    ab = st.sb("ab", [P, CC, TOK])
    bx = st.sb("bx", [P, CC, TOK])
    yy = st.sb("yy", [P, CC, TOK])
    a2 = st.sb("a2", [P, 3, CC, NS])
    acol = st.sb("acol", [P, 2, 2, CC])
    selb = st.sb("selb", [96, 2, 2, P])
    z = [K.y, st.sb("z1", [P, TOK])]
    hs = [K.ln_xc, K.ln_sq]
    flat = lambda ap: ap.rearrange("p c n -> p (c n)")
    seqs = lambda ap: ap.rearrange("p (s n) -> p s n", n=LEN)
    t1, t2 = flat(ab[:, :, :]), flat(bx[:, :, :])
    dtf = flat(dt[:, :, :])
    with nc.Block() as block:
        @block.sync
        def _(sp):
            sp.dma_start(wt[:, :], K.d["mamba_w"]).then_inc(st.w_ready, 16)

        @block.tensor
        def _(pe):
            outer.pe(pe, 0, K.x, lambda j: None)
            pe.wait_ge(st.w_ready, 16)
            pe.wait_ge(outer.log_ready, NJ)
            for j in range(NJ):
                pe.wait_ge(outer.norm_ready, at(0, j))
                for i in range(4):
                    b = 4 * (j % 2) + i
                    if j >= 2:
                        pe.wait_ge(st.x_in, 2 * (j - 1))
                        pe.wait_ge(st.z_done, 2 * (j - 1))
                    nc.tensor.matmul(K.ps[:, b, :], win[i], K.h[:, toks(j)], start=True, stop=True)\
                        .then_inc(st.in_ready, 1)
            pe.wait_ge(st.x_in, 2 * NJ)
            pe.wait_ge(st.z_done, 2 * NJ)
            pe.wait_ge(st.silu_done, 2)
            for j in range(NJ):
                for c in range(CC):
                    mm = nc.tensor.matmul(K.ps[0:96, j, :], wx[c], xc[:, c, toks(j)], start=(c == 0), stop=(c == 1))
                mm.then_inc(st.xdbl_ready, 1)
            for j in range(NJ):
                pe.wait_ge(st.xdbl_copied, j + 1)
                for c in range(CC):
                    b = 4 + (2 * j + c) % 4
                    if j >= 2:
                        pe.wait_ge(st.dt_biased, 2 * j + c - 3)
                    nc.tensor.matmul(K.ps[:, b, :], wdt[c], xd[0:DTR, toks(j)], start=True, stop=True)\
                        .then_inc(st.dt_ready, 1)
            pe.wait_ge(st.dt_biased, 2 * NJ)
            with pe.Fori(0, NS // 2) as m:
                for u in range(2):
                    k = m * 2 + u
                    pe.wait_ge(st.picked, k + 1)
                    for i in range(2):
                        pe.wait_ge((st.b_used, st.c_used)[i], k * CC + CC)
                        for j in range(NJ):
                            mm = nc.tensor.matmul(K.ps[:, 4 * i + j, :], selb[:, u, i, :], xd[:, toks(j)],
                                                  start=True, stop=True)
                        mm.then_inc(st.bc_ready, 1)
            for j in range(NJ):
                pe.wait_ge(st.y_gated, CC)
                for c in range(CC):
                    mm = nc.tensor.matmul(K.ps[:, j, :], wo[c], yy[:, c, toks(j)], start=(c == 0), stop=(c == 1))
                mm.then_inc(st.out_ready, 1)

        @block.scalar
        def _(act):
            nc.scalar.preload_act_table_set("natural_log_exp_and_others")
            outer.act(act, 0)
            act.wait_ge(st.w_ready, 16)
            nc.scalar.activation(flat(a2[:, 0]), a_log, ACT.Exp).then_inc(st.a_exp, 1)
            act.wait_ge(outer.norm_ready, NJ)
            for j in range(NJ):
                for c in range(CC):
                    act.wait_ge(st.in_ready, 4 * j + 3 + c)
                    nc.scalar.activation(z[c][:, toks(j)], K.ps[:, 4 * (j % 2) + 2 + c, :], ACT.Silu,
                                         bias=in_b[2 + c]).then_inc(st.z_done, 1)
            for c in range(CC):
                act.wait_ge(st.conved, c + 1)
                nc.scalar.activation(xc[:, c, :], xc[:, c, :], ACT.Silu).then_inc(st.silu_done, 1)
            for j in range(NJ):
                act.wait_ge(st.xdbl_ready, j + 1)
                nc.scalar.activation(xd[:, toks(j)], K.ps[0:96, j, :], ACT.Copy).then_inc(st.xdbl_copied, 1)
            for j in range(NJ):
                for c in range(CC):
                    act.wait_ge(st.dt_ready, 2 * j + c + 1)
                    nc.scalar.activation(dt[:, c, toks(j)], K.ps[:, 4 + (2 * j + c) % 4, :], ACT.Identity,
                                         bias=dt_b[c]).then_inc(st.dt_biased, 1)
            nc.scalar.preload_act_table_set("natural_log_exp_and_others")
            act.wait_ge(st.dt_biased, 2 * NJ)
            nc.scalar.activation(t1, dtf, ACT.Abs).then_inc(st.dt_abs, 1)
            act.wait_ge(st.dt_abs, 1)
            nc.scalar.activation(t1, t1, ACT.Exp, scale=-1.0).then_inc(st.dt_exp, 1)
            act.wait_ge(st.sp_rest, 1)
            nc.scalar.activation(t2, t2, ACT.Ln).then_inc(st.sp_log, 1)
            act.wait_ge(st.dt_done, 1)
            with act.Fori(0, NS // 2) as m:
                for u in range(2):
                    k = m * 2 + u
                    for c in range(CC):
                        act.wait_ge(st.picked, k + 1)
                        act.wait_ge(st.scanned, k * CC + c + 1)
                        nc.scalar.activation(ab[:, c, :], dt[:, c, :], ACT.Exp, scale=acol[:, u, 0, c:c + 1])\
                            .then_inc(st.abar_done, 1)

        @block.gpsimd
        def _(pool):
            nc.gpsimd.memset(xi[:, :, :, 0:PAD], 0.0).then_inc(st.edge, 1)
            pool.wait_ge(st.a_inv, 1)
            pool.wait_ge(st.dt_done, 1)
            pool.wait_ge(st.zeroed, 1)

            def pick(k, u):
                for i in range(2):
                    nc.gpsimd.tensor_copy(selb[:, u, i, :],
                                          K.ident[0:96, bass.ds(k + (DTR + NS * i), 1)].to_broadcast([96, P]))
                    p = nc.gpsimd.tensor_copy(acol[:, u, i, :].unsqueeze(2), a2[:, 2 * i, :, bass.ds(k, 1)])
                p.then_inc(st.picked, 1)

            def add_to_y(k):
                for c in range(CC):
                    pool.wait_ge(st.c_used, k * CC + CC + (c + 1))
                    nc.gpsimd.tensor_tensor(yy[:, c, :], yy[:, c, :], hs[c][:, :], ALU.add).then_inc(st.summed, 1)

            pick(0, 0)
            with pool.Fori(0, NS // 2 - 1) as m:
                pick(m * 2 + 1, 1)
                add_to_y(m * 2)
                pick(m * 2 + 2, 0)
                add_to_y(m * 2 + 1)
            pick(NS - 1, 1)
            add_to_y(NS - 2)
            add_to_y(NS - 1)

        @block.vector
        def _(dve):
            outer.dve(dve, 0, K.x, K.h)
            dve.wait_ge(st.w_ready, 16)
            dve.wait_ge(st.a_exp, 1)
            nc.vector.tensor_scalar(flat(a2[:, 0]), flat(a2[:, 0]), -1.0, None, ALU.mult).then_inc(st.a_neg, 1)
            dve.wait_ge(st.a_neg, 1)
            nc.vector.tensor_scalar(flat(a2[:, 1]), flat(a2[:, 0]), -1e-6, None, ALU.is_gt).then_inc(st.a_tiny, 1)
            dve.wait_ge(st.a_tiny, 1)
            nc.vector.tensor_scalar(flat(a2[:, 2]), flat(a2[:, 1]), -1.0, 1.0, ALU.mult, ALU.add).then_inc(st.a_keep, 1)
            dve.wait_ge(st.a_keep, 1)
            nc.vector.tensor_tensor(flat(a2[:, 2]), flat(a2[:, 2]), flat(a2[:, 0]), ALU.mult).then_inc(st.a_keep, 1)
            dve.wait_ge(st.a_keep, 2)
            nc.vector.tensor_tensor(flat(a2[:, 2]), flat(a2[:, 2]), flat(a2[:, 1]), ALU.add).then_inc(st.a_safe, 1)
            dve.wait_ge(st.a_safe, 1)
            nc.vector.reciprocal(flat(a2[:, 2]), flat(a2[:, 2])).then_inc(st.a_inv, 1)
            dve.wait_ge(outer.norm_ready, NJ)
            for j in range(NJ):
                for c in range(CC):
                    dve.wait_ge(st.in_ready, 4 * j + c + 1)
                    nc.vector.tensor_scalar(xi[:, c, SPW * j:SPW * (j + 1), PAD:], seqs(K.ps[:, 4 * (j % 2) + c, :]),
                                            in_b[c], None, ALU.add).then_inc(st.x_in, 1)
            dve.wait_ge(st.x_in, 2 * NJ)
            dve.wait_ge(st.edge, 1)
            for c in range(CC):
                nc.vector.tensor_scalar(seqs(xc[:, c, :]), xi[:, c, :, 3:3 + LEN], conv_w[c][3], conv_b[c],
                                        ALU.mult, ALU.add).then_inc(st.conv, 1)
            for k in (2, 1, 0):
                for c in range(CC):
                    dve.wait_ge(st.conv, 2 * (3 - k) + c - 1)
                    v = nc.vector.scalar_tensor_tensor(seqs(xc[:, c, :]), xi[:, c, :, k:k + LEN], conv_w[c][k],
                                                       seqs(xc[:, c, :]), ALU.mult, ALU.add)
                    v.then_inc(st.conved if k == 0 else st.conv, 1)
            dve.wait_ge(st.dt_exp, 1)
            nc.vector.tensor_scalar(t2, t1, 1.0, None, ALU.add).then_inc(st.sp_w, 1)
            dve.wait_ge(st.sp_w, 1)
            nc.vector.scalar_tensor_tensor(t1, t2, 1.0, t1, ALU.subtract, ALU.subtract).then_inc(st.sp_rest, 1)
            dve.wait_ge(st.sp_rest, 1)
            nc.vector.scalar_tensor_tensor(dtf, dtf, 0.0, t1, ALU.max, ALU.subtract).then_inc(st.sp_most, 1)
            dve.wait_ge(st.sp_most, 1)
            dve.wait_ge(st.sp_log, 1)
            nc.vector.tensor_tensor(dtf, dtf, t2, ALU.add).then_inc(st.dt_done, 1)
            dve.wait_ge(st.dt_done, 1)
            for c in range(CC):
                nc.vector.tensor_scalar(yy[:, c, :], xc[:, c, :], d_skip[c], None, ALU.mult).then_inc(st.scanned, 1)
            dve.wait_ge(st.scanned, CC)
            dve.sem_inc(st.zeroed, 1)
            dve.sem_inc(st.b_used, CC)
            dve.sem_inc(st.c_used, CC)
            dve.sem_inc(st.summed, CC)
            with dve.Fori(0, NS // 2) as m:
                for u in range(2):
                    k = m * 2 + u
                    for c in range(CC):
                        dve.wait_ge(st.bc_ready, k * 2 + 1)
                        dve.wait_ge(st.picked, k + 1)
                        nc.vector.scalar_tensor_tensor(bx[:, c, :], K.ps[:, 0:4, :].rearrange("p b n -> p (b n)"),
                                                       acol[:, u, 1, c:c + 1], xc[:, c, :], ALU.mult, ALU.mult)\
                            .then_inc(st.b_used, 1)
                    for c in range(CC):
                        dve.wait_ge(st.b_used, k * CC + CC + (c + 1))
                        dve.wait_ge(st.abar_done, k * CC + (c + 1))
                        nc.vector.scalar_tensor_tensor(bx[:, c, :], ab[:, c, :], 1.0, bx[:, c, :],
                                                       ALU.subtract, ALU.mult).then_inc(st.bx_done, 1)
                        dve.wait_ge(st.bx_done, k * CC + (c + 1))
                        nc.vector.memset(seqs(ab[:, c, :])[:, :, 0:1], 0.0).then_inc(st.cut, 1)
                    for c in range(CC):
                        dve.wait_ge(st.cut, k * CC + (c + 1))
                        dve.wait_ge(st.summed, k * CC + (c + 1))
                        nc.vector.tensor_tensor_scan(hs[c][:, :], ab[:, c, :], bx[:, c, :], 0.0, ALU.mult, ALU.add)\
                            .then_inc(st.scanned, 1)
                    for c in range(CC):
                        dve.wait_ge(st.bc_ready, k * 2 + 2)
                        dve.wait_ge(st.scanned, k * CC + CC + (c + 1))
                        nc.vector.tensor_tensor(hs[c][:, :], hs[c][:, :], K.ps[:, 4:8, :].rearrange("p b n -> p (b n)"),
                                                ALU.mult).then_inc(st.c_used, 1)
            for c in range(CC):
                dve.wait_ge(st.summed, CC * NS + CC)
                dve.wait_ge(st.z_done, CC * NJ)
                nc.vector.tensor_tensor(yy[:, c, :], yy[:, c, :], z[c][:, :], ALU.mult).then_inc(st.y_gated, 1)
            for j in range(NJ):
                dve.wait_ge(st.out_ready, j + 1)
                nc.vector.scalar_tensor_tensor(K.x[:, toks(j)], K.ps[:, j, :], out_b, K.x[:, toks(j)],
                                               ALU.add, ALU.add).then_inc(st.x_done, 1)
    st.end()


def rope_attention_stage(K):
    nc = K.nc
    HEADS, DH, GH = 16, 8, 4
    st = Stage(nc, "rope")
    (st.w_ready, st.lin_ready, st.rot_cos, st.rot_sin, st.rotated, st.v_ready, st.v_copied,
     st.q_copied, st.q_head, st.o_turned, st.o_moved, st.proj_ready, st.x_done, st.heads_read) = st.signals(
        "w_ready lin_ready rot_cos rot_sin rotated v_ready v_copied q_copied q_head o_turned "
        "o_moved proj_ready x_done heads_read")
    outer = LayerNorm(K, st, "outer_")
    wt = st.sb("wt", [P, K.d["rope_w"].shape[1]])
    wqk = [[wt[:, toks(i, P)] for i in (0, 1)], [wt[:, toks(i, P)] for i in (2, 3)]]
    wv, wo = wt[:, 512:640], wt[:, 640:768]
    cos, sin = wt[:, 768:1024], wt[:, 1024:1280]
    sel = wt[:, 1280:1296]
    qk = st.sb("qk", [P, 2, TOK])
    part = st.sb("part", [P, 2, W])
    vt = st.sb("vt", [P, TOK])
    qm = st.sb("qm", [P, 2, HEADS, LEN])
    o = st.sb("o", [P, TOK])
    ot = K.h
    qst, kst, vst, ost = (st.sb(n, [P, 2, LEN]) for n in ("qs", "ks", "vs", "os"))
    groups = []
    for s in range(2):
        for t in range(2):
            for hg in range(HEADS // GH):
                heads = range(GH * hg, GH * (hg + 1))
                groups.append(([(qm[:, s, h, toks(t, P)], kst[:, s, 0:(t + 1) * P]) for h in heads], t + 1,
                               K.causal[:, LEN * t:LEN * t + (t + 1) * P],
                               [[vst[:, s, P * kt + DH * h:P * kt + DH * (h + 1)] for kt in range(t + 1)]
                                for h in heads],
                               ost[:, s, P * t + DH * GH * hg:P * t + DH * GH * (hg + 1)].rearrange("p (h d) -> p h d", d=DH)))
    att = Attention(K, st, groups, GH, DH, float(DH) ** -0.5)
    N = att.n
    with nc.Block() as block:
        @block.sync
        def _(sp):
            sp.dma_start(wt[:, :], K.d["rope_w"]).then_inc(st.w_ready, 16)

        @block.tensor
        def _(pe):
            outer.pe(pe, 0, K.x, lambda j: None)
            pe.wait_ge(st.w_ready, 16)
            for i in range(2):
                for j in range(NJ):
                    pe.wait_ge(outer.norm_ready, at(0, j))
                    b = (NJ * i + j) % 2
                    if NJ * i + j >= 2:
                        pe.wait_ge(st.rot_sin, at(i, j) - 2)
                    for a in range(2):
                        mm = nc.tensor.matmul(K.ps[:, 2 * b + a, :], wqk[i][a], K.h[:, toks(j)], start=True, stop=True)
                    mm.then_inc(st.lin_ready, 1)
            for j in range(NJ):
                for t in range(TPW):
                    mm = nc.tensor.matmul(K.ps[:, 4 + j, toks(t, P)], K.h[:, toks(TPW * j + t, P)], wv,
                                          start=True, stop=True)
                mm.then_inc(st.v_ready, 1)
            pe.wait_ge(st.rot_sin, 2 * NJ)
            pe.wait_ge(st.v_copied, NJ)
            with pe.Fori(0, NJ) as m:
                att.pe(pe, m * N, lambda g: pe.wait_ge(st.q_head, m * 2 + (g // (N // 2) + 1)))
            for j in range(NJ):
                pe.wait_ge(st.heads_read, 2 * j + 2)
                for t in range(TPW):
                    mm = nc.tensor.transpose(K.ps[:, j, toks(t, P)], o[:, toks(TPW * j + t, P)], K.ident)
                mm.then_inc(st.o_turned, 1)
            for j in range(NJ):
                pe.wait_ge(st.o_moved, j + 1)
                nc.tensor.matmul(K.ps[:, 4 + j, :], wo, ot[:, toks(j)], start=True, stop=True)\
                    .then_inc(st.proj_ready, 1)

        @block.scalar
        def _(act):
            nc.scalar.preload_act_table_set("natural_log_exp_and_others")
            outer.act(act, 0)
            for j in range(NJ):
                act.wait_ge(st.v_ready, j + 1)
                nc.scalar.activation(vt[:, toks(j)], K.ps[:, 4 + j, :], ACT.Copy).then_inc(st.v_copied, 1)
            with act.Fori(0, NJ) as m:
                att.act(act, m * N)
            for j in range(NJ):
                act.wait_ge(st.o_turned, j + 1)
                nc.scalar.activation(ot[:, toks(j)], K.ps[:, j, :], ACT.Copy).then_inc(st.o_moved, 1)

        @block.gpsimd
        def _(pool):
            pool.wait_ge(st.w_ready, 16)
            pool.wait_ge(st.rotated, 2 * NJ)
            pool.wait_ge(st.v_copied, NJ)

            def queries(m, s):
                seq = bass.ds(m * (2 * LEN) + s * LEN, LEN)
                nc.gpsimd.tensor_copy(qst[:, s, :], qk[:, 0, seq]).then_inc(st.q_copied, 1)
                pool.wait_ge(st.q_copied, m * 2 + (s + 1))
                nc.gpsimd.tensor_copy(kst[:, s, :], qk[:, 1, seq])
                for h in range(HEADS):
                    nc.gpsimd.tensor_scalar(qm[:, s, h, :], qst[:, s, :], sel[:, h:h + 1], None, ALU.mult)

            def values(m, s):
                seq = bass.ds(m * (2 * LEN) + s * LEN, LEN)
                nc.gpsimd.tensor_copy(vst[:, s, :], vt[:, seq]).then_inc(st.q_head, 1)

            def take(m, s):
                pool.wait_ge(att.o_copied, m * N + N // 2 * (s + 1))
                seq = bass.ds(m * (2 * LEN) + s * LEN, LEN)
                nc.gpsimd.tensor_copy(o[:, seq], ost[:, s, :]).then_inc(st.heads_read, 1)

            for s in range(2):
                queries(0, s)
                values(0, s)
            with pool.Fori(0, NJ - 1) as m:
                for s in range(2):
                    pool.wait_ge(att.sim_ready, m * N + N // 2 * (s + 1))
                    queries(m + 1, s)
                    take(m, s)
                    values(m + 1, s)
            for s in range(2):
                take(NJ - 1, s)

        @block.vector
        def _(dve):
            outer.dve(dve, 0, K.x, K.h)
            dve.wait_ge(st.w_ready, 16)
            for i in range(2):
                for j in range(NJ):
                    b = (NJ * i + j) % 2
                    n = NJ * i + j
                    seqs = lambda ap: ap.rearrange("p (s n) -> p s n", n=LEN)
                    both = lambda ap: ap.unsqueeze(1).to_broadcast([P, SPW, LEN])
                    dve.wait_ge(st.lin_ready, n + 1)
                    if n:
                        dve.wait_ge(st.rotated, n)
                    nc.vector.tensor_tensor(seqs(part[:, 0, :]), seqs(K.ps[:, 2 * b, :]), both(cos), ALU.mult)\
                        .then_inc(st.rot_cos, 1)
                    nc.vector.tensor_tensor(seqs(part[:, 1, :]), seqs(K.ps[:, 2 * b + 1, :]), both(sin), ALU.mult)\
                        .then_inc(st.rot_sin, 1)
                    dve.wait_ge(st.rot_sin, n + 1)
                    nc.vector.tensor_tensor(qk[:, i, toks(j)], part[:, 0, :], part[:, 1, :], ALU.add)\
                        .then_inc(st.rotated, 1)
            with dve.Fori(0, NJ) as m:
                att.dve(dve, m * N)
            for j in range(NJ):
                dve.wait_ge(st.proj_ready, j + 1)
                nc.vector.tensor_tensor(K.x[:, toks(j)], K.x[:, toks(j)], K.ps[:, 4 + j, :], ALU.add)\
                    .then_inc(st.x_done, 1)
    st.end()


def switch_stage(K, tag):
    nc = K.nc
    GT = 32
    NG = TOK // GT
    ES = P
    NQ = ES // 4
    NT = TOK // P
    st = Stage(nc, f"switch{tag}")
    (st.w_ready, st.w2_ready, st.logit_ready, st.biased, st.logits, st.maxima, st.chosen,
     st.chosen_tm, st.chosen_copied, st.x_tm, st.x_copied, st.picked, st.picked_copied,
     st.h1_ready, st.h1_biased, st.h1_done, st.h2_ready, st.h2_copied, st.turned, st.result_ready,
     st.y_ready, st.x_done) = st.signals(
        "w_ready w2_ready logit_ready biased logits maxima chosen chosen_tm chosen_copied x_tm "
        "x_copied picked picked_copied h1_ready h1_biased h1_done h2_ready h2_copied turned "
        "result_ready y_ready x_done")
    outer = LayerNorm(K, st, "outer_")
    wt = st.sb("wt", [P, K.d["switch_w"].shape[1]])
    w1 = st.sb("w1", [P, ES, GT])
    w2 = st.sb("w2", [P, NQ, P])
    wc, b2, b1, bc, tie = wt[:, 0:128], wt[:, 128:256], wt[:, 256:288], wt[:, 288:289], wt[:, 289:321]
    h = K.h
    logit = K.y
    top = st.sb("top", [P, NG])
    perm = st.sb("perm", [P, TOK])
    perm_tm = K.ln_xc
    h_tm = K.ln_sq
    z = st.sb("z", [P, ES, NG])
    hid = st.sb("hid", [P, NQ, NG])
    res = z
    resm = st.sb("resm", [P, NG, P])
    with nc.Block() as block:
        scalar_copy, vector_copy = nc.scalar.activation, nc.vector.tensor_copy

        def picked_copy(copy, eng, n):
            eng.wait_ge(st.picked, n + 1)
            if n:
                eng.wait_ge(st.picked_copied, n)
            j, g = n // 4, n % 4
            dst = z[:, :, :].rearrange("p e (j t g) -> p j g t e", j=NJ, g=4)[:, j, g]
            src = K.ps[:, (4 + n) % 8, :].rearrange("p (g e) -> p g e", e=P)
            args = (ACT.Copy,) if copy is scalar_copy else ()
            copy(dst, src, *args).then_inc(st.picked_copied, 1)

        def result_copy(copy, eng, n):
            eng.wait_ge(st.h2_ready, n + 1)
            if n:
                eng.wait_ge(st.h2_copied, n)
            args = (ACT.Copy,) if copy is scalar_copy else ()
            copy(res[:, :, :].rearrange("p (c q r) g -> p c r q g", c=4, r=4)[:, n // 4, n % 4],
                 K.ps[:, (4 + n) % 8, :].rearrange("p (q g) -> p q g", g=NG), *args)\
                .then_inc(st.h2_copied, 1)

        @block.sync
        def _(sp):
            sp.dma_start(wt[:, :], K.d["switch_w"]).then_inc(st.w_ready, 16)
            sp.dma_start(w1[:, :, :].rearrange("p a b -> p (a b)"), K.d["switch_w1"]).then_inc(st.w2_ready, 16)
            sp.dma_start(w2[:, :, :].rearrange("p a b -> p (a b)"), K.d["switch_w2"]).then_inc(st.w2_ready, 16)

        @block.tensor
        def _(pe):
            outer.pe(pe, 0, K.x, lambda j: None)
            pe.wait_ge(st.w_ready, 16)
            for j in range(NJ):
                pe.wait_ge(outer.norm_ready, at(0, j))
                nc.tensor.matmul(K.ps[:, j, :], wc, h[:, toks(j)], start=True, stop=True).then_inc(st.logit_ready, 1)
            for j in range(NJ):
                for t in range(TPW):
                    mm = nc.tensor.transpose(K.ps[:, 4 + j, toks(t, P)], h[:, toks(TPW * j + t, P)], K.ident)
                mm.then_inc(st.x_tm, 1)
            for j in range(NJ):
                pe.wait_ge(st.chosen, j + 1)
                for t in range(TPW):
                    mm = nc.tensor.transpose(K.ps[:, j, toks(t, P)], perm[:, toks(TPW * j + t, P)], K.ident)
                mm.then_inc(st.chosen_tm, 1)
            for j in range(NJ):
                pe.wait_ge(st.chosen_copied, j + 1 if j == 0 else NJ)
                pe.wait_ge(st.x_copied, NJ)
                if j >= 2:
                    pe.wait_ge(st.picked_copied, 4 * (j - 1))
                for t in range(TPW):
                    for g in range(4):
                        rows, tile = slice(32 * g, 32 * g + 32), toks(TPW * j + t, P)
                        mm = nc.tensor.matmul(K.ps[:, (4 * (j + 1) + g) % 8, toks(t, P)], h_tm[rows, tile],
                                              perm_tm[rows, tile], start=True, stop=True)
                        if t == TPW - 1:
                            mm.then_inc(st.picked, 1)
            pe.wait_ge(st.w2_ready, 32)
            pe.wait_ge(st.picked_copied, NT)
            for q in range(NQ):
                for r in range(4):
                    mm = nc.tensor.matmul(K.ps[32 * r:32 * r + 32, q // 8, toks(q % 8, NG)], w1[:, 4 * q + r, :],
                                          z[:, 4 * q + r, :], start=True, stop=True)
                if q % 8 == 7:
                    mm.then_inc(st.h1_ready, 1)
            for c in range(4):
                pe.wait_ge(st.h1_done, c + 1 if c == 0 else 4)
                if c >= 2:
                    pe.wait_ge(st.h2_copied, 4 * (c - 1))
                for q in range(8):
                    for r in range(4):
                        rows = slice(32 * r, 32 * r + 32)
                        mm = nc.tensor.matmul(K.ps[:, (4 * (c + 1) + r) % 8, toks(q, NG)], w2[rows, 8 * c + q, :],
                                              hid[rows, 8 * c + q, :], start=True, stop=True)
                        if q == 7:
                            mm.then_inc(st.h2_ready, 1)
            for n in range(NT):
                b = (4 + n) % 8
                pe.wait_ge(st.h2_copied, ES // 8)
                if n >= 8:
                    pe.wait_ge(st.result_ready, n - 7)
                for g in range(4 * n, 4 * n + 4):
                    mm = nc.tensor.transpose(K.ps[:, b, toks(g % 4, P)], res[:, :, g], K.ident)
                mm.then_inc(st.turned, 1)
            for j in range(NJ):
                pe.wait_ge(st.result_ready, min(4 * j + 4 + 8, NT))
                for g in range(16 * j, 16 * j + 16):
                    mm = nc.tensor.matmul(K.ps[:, 4 + j, toks(g % 16, GT)], resm[:, g, :], perm[:, toks(g, GT)],
                                          start=True, stop=True)
                mm.then_inc(st.y_ready, 1)

        @block.scalar
        def _(act):
            nc.scalar.preload_act_table_set("natural_log_exp_and_others")
            outer.act(act, 0)
            act.wait_ge(st.w_ready, 16)
            for j in range(NJ):
                act.wait_ge(st.logit_ready, j + 1)
                nc.scalar.activation(logit[:, toks(j)], K.ps[:, j, :], ACT.Identity, bias=bc).then_inc(st.biased, 1)
            act.wait_ge(outer.norm_ready, NJ)
            for j in range(NJ):
                act.wait_ge(st.x_tm, j + 1)
                nc.scalar.activation(h_tm[:, toks(j)], K.ps[:, 4 + j, :], ACT.Copy).then_inc(st.x_copied, 1)
            for n in range(0, NT, 2):
                picked_copy(scalar_copy, act, n)
            for n in range(0, ES // 8, 2):
                result_copy(scalar_copy, act, n)

        @block.vector
        def _(dve):
            outer.dve(dve, 0, K.x, h)
            dve.wait_ge(st.w_ready, 16)
            grouped = lambda ap: ap.rearrange("p (g t) -> p g t", t=GT)
            for j in range(NJ):
                gs = slice(16 * j, 16 * j + 16)
                dve.wait_ge(st.biased, j + 1)
                nc.vector.tensor_tensor(grouped(logit[:, toks(j)]), grouped(logit[:, toks(j)]),
                                        tie.unsqueeze(1).to_broadcast([P, 16, GT]), ALU.add).then_inc(st.logits, 1)
                dve.wait_ge(st.logits, j + 1)
                nc.vector.tensor_reduce(top[:, gs], grouped(logit[:, toks(j)]), AX, ALU.max).then_inc(st.maxima, 1)
                dve.wait_ge(st.maxima, j + 1)
                nc.vector.tensor_tensor(grouped(perm[:, toks(j)]), grouped(logit[:, toks(j)]),
                                        top[:, gs].unsqueeze(2).to_broadcast([P, 16, GT]), ALU.is_equal)\
                    .then_inc(st.chosen, 1)
            dve.wait_ge(outer.norm_ready, NJ)
            for j in range(NJ):
                dve.wait_ge(st.chosen_tm, j + 1)
                nc.vector.tensor_copy(perm_tm[:, toks(j)], K.ps[:, j, :]).then_inc(st.chosen_copied, 1)
            for n in range(1, NT, 2):
                picked_copy(vector_copy, dve, n)
            for c in range(4):
                part = hid[:, 8 * c:8 * c + 8, :]
                dve.wait_ge(st.h1_ready, c + 1)
                nc.vector.tensor_tensor(part, K.ps[:, c, :].rearrange("p (q g) -> p q g", g=NG),
                                        b1[:, 8 * c:8 * c + 8].unsqueeze(2).to_broadcast([P, 8, NG]), ALU.add)\
                    .then_inc(st.h1_biased, 1)
                dve.wait_ge(st.h1_biased, c + 1)
                nc.vector.tensor_scalar(part, part, 0.0, None, ALU.max).then_inc(st.h1_done, 1)
            for n in range(1, ES // 8, 2):
                result_copy(vector_copy, dve, n)
            for n in range(NT):
                dve.wait_ge(st.turned, n + 1)
                nc.vector.tensor_tensor(resm[:, 4 * n:4 * n + 4, :],
                                        K.ps[:, (4 + n) % 8, :].rearrange("p (g d) -> p g d", d=P),
                                        b2.unsqueeze(1).to_broadcast([P, 4, P]), ALU.add).then_inc(st.result_ready, 1)
            for j in range(NJ):
                dve.wait_ge(st.y_ready, j + 1)
                nc.vector.tensor_tensor(K.x[:, toks(j)], K.x[:, toks(j)], K.ps[:, 4 + j, :], ALU.add)\
                    .then_inc(st.x_done, 1)
    st.end()


def switch_first(K):
    switch_stage(K, 0)


def switch_second(K):
    switch_stage(K, 1)


class Kernel:
    pass


def build(nc, d, out):
    K = Kernel()
    K.nc, K.d = nc, d
    stored = nc.alloc_semaphore("output_stored")
    with ExitStack() as ctx:
        def sb(name, shape):
            return ctx.enter_context(nc.sbuf_tensor(name, shape, F32))

        K.ps = ctx.enter_context(nc.psum_tensor("ps", [P, 8, W], F32))
        K.x = sb("x", [P, TOK])
        K.y = sb("y", [P, TOK])
        K.h = sb("h", [P, TOK])
        K.ln_xc = sb("ln_xc", [P, TOK])
        K.ln_sq = sb("ln_sq", [P, TOK])
        consts = sb("consts", [P, d["consts"].shape[1]])
        K.mean_mat = consts[:, 0:128]
        K.ident = consts[:, 128:256]
        K.head_mask16 = consts[:, 256:384]
        K.half_ones = consts[:, 384:512]
        K.causal = consts[:, 512:1024]
        K.banded = consts[:, 1024:1536]
        K.gamma_row = consts[:, 1536:1792]
        K.gamma_col = consts[:, 1792:1794]
        K.eps_ln = consts[:, 1794:1795]
        K.eps_gn = consts[:, 1795:1796]
        K.eps_rms = consts[:, 1796:1797]
        K.ln_shift = consts[:, 1797:1798]
        K.half_pi = consts[:, 1798:1799]
        K.one = consts[:, 1799:1800]

        st = Stage(nc, "load")
        (st.loaded, st.moved, st.copied) = st.signals(
            "loaded moved copied")
        with nc.Block() as block:
            tm = K.y

            @block.sync
            def _(sp):
                sp.dma_start(consts[:, :], d["consts"]).then_inc(st.loaded, 16)
                sp.dma_start(tm[:, :].rearrange("p (t f) -> p t f", f=P),
                             d["x"].rearrange("(t p) f -> p t f", p=P)).then_inc(st.loaded, 16)

            @block.tensor
            def _(pe):
                pe.wait_ge(st.loaded, 32)
                for j in range(NJ):
                    for t in range(TPW):
                        mm = nc.tensor.transpose(K.ps[:, j, toks(t, P)], tm[:, toks(TPW * j + t, P)], K.ident)
                    mm.then_inc(st.moved, 1)

            @block.vector
            def _(dve):
                for j in range(NJ):
                    dve.wait_ge(st.moved, j + 1)
                    nc.vector.tensor_copy(K.x[:, toks(j)], K.ps[:, j, :]).then_inc(st.copied, 1)
        st.end()

        for stage in STAGES:
            stage(K)

        st = Stage(nc, "store")
        (st.moved, st.copied) = st.signals(
            "moved copied")
        with nc.Block() as block:
            tm = K.y

            @block.tensor
            def _(pe):
                for j in range(NJ):
                    for t in range(TPW):
                        mm = nc.tensor.transpose(K.ps[:, j, toks(t, P)], K.x[:, toks(TPW * j + t, P)], K.ident)
                    mm.then_inc(st.moved, 1)

            @block.vector
            def _(dve):
                for j in range(NJ):
                    dve.wait_ge(st.moved, j + 1)
                    nc.vector.tensor_copy(tm[:, toks(j)], K.ps[:, j, :]).then_inc(st.copied, 1)

            @block.sync
            def _(sp):
                for j in range(NJ):
                    sp.wait_ge(st.copied, j + 1)
                    sp.dma_start(out.rearrange("b (t p) f -> p (b t) f", p=P)[:, TPW * j:TPW * (j + 1), :],
                                 tm[:, toks(j)].rearrange("p (t f) -> p t f", f=P)).then_inc(stored, 16)
                sp.wait_ge(stored, 16 * NJ)
        st.end()


STAGES = [
    linear_attention_stage,
    window_attention_first,
    retention_stage,
    window_attention_second,
    gated_delta_stage,
    lora_linear_first,
    lstm_stage,
    lora_linear_second,
    lru_stage,
    channel_mix_first,
    causal_attention_stage,
    channel_mix_second,
    mamba_stage,
    switch_first,
    rope_attention_stage,
    switch_second,
]


def _constants():
    ar = np.arange(P)
    cols = [
        np.full((P, P), 1.0 / P),
        np.eye(P),
        (ar[:, None] // 16 == ar[None, :] // 16),
        (ar[:, None] // 64 == ar[None, :] // 64),
    ]
    key = np.arange(LEN)
    for t in range(2):
        cols.append(np.where(key[None, :] <= (ar + P * t)[:, None], 0.0, -1e30))
    for t in range(2):
        back = (ar + P * t)[:, None] - key[None, :]
        cols.append(np.where((back >= 0) & (back <= 64), 0.0, -1e30))
    gamma = 1.0 - 2.0 ** -5.0
    cols.append(np.broadcast_to(gamma ** np.arange(LEN, dtype=np.float64), (P, LEN)))
    cols.append(np.stack([gamma ** -(ar + P * t).astype(np.float64) for t in range(2)], 1))
    for v in (LN_EPS, 1e-3, 1e-6, 10 * np.log(2.0), np.pi / 2, 1.0):
        cols.append(np.full((P, 1), v))
    return np.ascontiguousarray(np.concatenate(cols, 1).astype(np.float32))


def _columns(*vectors):
    return np.concatenate([v.reshape(-1, P).T for v in vectors], 1)


def _chunks(w):
    return np.concatenate(list(w.reshape(-1, P, w.shape[1])), 1)


def _block_diagonal(blocks):
    n, a, b = blocks.shape
    full = np.zeros((n * a, n * b), blocks.dtype)
    for i in range(n):
        full[i * a:(i + 1) * a, i * b:(i + 1) * b] = blocks[i]
    return full


def _pad_rows(w, n):
    return np.concatenate([w, np.zeros((n - len(w),) + w.shape[1:], w.dtype)])


def _xpos_tables():
    f32 = np.float32
    half = np.arange(0, 64, 2, dtype=f32)
    inv = f32(1.0) / (f32(10000.0) ** (half / f32(64))).astype(f32)
    t = np.arange(LEN, dtype=f32)
    angle = (t[:, None] * inv[None, :]).astype(f32)
    base = (half + f32(25.6)) / f32(89.6)
    scale = (base[None, :] ** ((t - f32(LEN // 2)) / f32(32))[:, None]).astype(f32)
    angle, scale = (np.tile(z, (1, 4)).T for z in (angle, scale))
    sign = np.where(np.arange(P) % 64 < 32, -1.0, 1.0)[:, None]
    cos, sin = np.cos(angle), sign * np.sin(angle)
    return np.concatenate([cos * scale, sin * scale, cos / scale, sin / scale], 1).astype(f32)


def _delta_constants():
    r, c = np.arange(P)[:, None], np.arange(P)[None, :]
    cols = [r <= c, r > c]
    for m in (1, 2, 4, 8, 16, 32, 64):
        cols.append((r // (2 * m) == c // (2 * m)) & (r % (2 * m) < m) & (c % (2 * m) >= m))
    cols.append(r // 32 == c // 32)
    cols.append(r // 32 == np.arange(256)[None, :] // 64)
    return np.concatenate(cols, 1).astype(np.float32)


def _rope_tables():
    dh = 8
    f = np.arange(P)
    theta = (np.float32(10000.0) ** (np.float32(-2.0) * np.arange(dh // 2, dtype=np.float32) / np.float32(dh)))
    angle = np.arange(LEN, dtype=np.float32)[None, :] * theta.astype(np.float32)[(f % dh) // 2][:, None]
    sign = np.where(f % 2 == 0, -1.0, 1.0)[:, None]
    heads = f[:, None] // dh == np.arange(P // dh)[None, :]
    return np.concatenate([np.cos(angle), sign * np.sin(angle), heads], 1).astype(np.float32)


def _arrays(v):
    a = {"consts": _constants(), "x": v["L0_attn_a_x"].reshape(TOK, P)}
    g = lambda n: v["L0_attn_a_" + n]
    a["linattn_wa"] = np.stack([
        np.concatenate([g("wq")[l], g("wk")[l], g("wv")[l], g("wo")[l],
                        _columns(g("ln1_w")[l], g("ln1_b")[l], g("bo")[l])], 1) for l in range(6)])
    a["linattn_wb"] = np.stack([
        np.concatenate([g("w1")[l], _chunks(g("w2")[l]), _columns(g("ln2_w")[l], g("ln2_b")[l])], 1)
        for l in range(6)])
    g = lambda n: v["L0_ffn_" + n]
    half = np.arange(512) ^ 32
    a["window_tabs"] = _xpos_tables()
    layers, mlps = [], []
    for l in range(2):
        wqkv = g("wqkv")[l]
        cols = []
        for i in range(2):
            w = wqkv[:, 512 * i:512 * (i + 1)]
            for c in range(4):
                cols += [w[:, toks(c, P)], w[:, half][:, toks(c, P)]]
        cols += [wqkv[:, 1024:1536], _chunks(g("wo")[l])]
        for name in ("q_scale", "k_scale"):
            scale = np.tile(g(name)[l], 8)
            cols += [_columns(scale[:P]), _columns(scale[half][:P])]
        layers.append(np.concatenate(cols, 1))
        cols = [g("w1")[l], _chunks(_pad_rows(g("w2")[l], 384)), _columns(g("ln_g")[l], g("ln_b")[l], g("b2")[l])]
        for part in (g("b1")[l][:341], g("b1")[l][341:]):
            cols += [_pad_rows(part[:, None], 384).reshape(3, P).T]
        mlps.append(np.concatenate(cols, 1))
    a["window_wa"], a["window_wb"] = np.stack(layers), np.stack(mlps)
    g = lambda n: v["L0_attn_b_" + n]
    a["retention_w"] = np.concatenate([g("Wq")[0], g("Wk")[0], g("Wv")[0], g("Wg"), g("Wo"),
                                       _columns(g("gn_gamma"), g("gn_beta"))], 1)
    g = lambda n: v["L1_attn_a_" + n]
    rows = lambda w: np.broadcast_to(w[None, :], (P, len(w)))
    a["delta_w"] = np.concatenate([
        g("Wq"), g("Wk"), g("Wv"), g("Wg"), _chunks(g("Wo")), g("W2"), g("Wa"), g("Wb"), rows(g("dt_bias")),
        rows(g("A_log")), g("conv_q_w"), g("conv_k_w"), _chunks(g("conv_v_w")),
        _columns(g("ln1_g"), g("ln1_b"), g("ln2_g"), g("ln2_b"), g("rms_in_w"), g("b2")),
        np.tile(g("o_norm_w"), 2)[:, None]], 1)
    a["delta_c"] = _delta_constants()
    g = lambda n: v["L1_ffn_" + n]
    lora = np.zeros((P, 439), np.float32)
    lora[:, 0:128] = g("W").T
    lora[:100, 128:132] = g("lora_down").T
    lora[:100, 132:260] = g("down_aux")
    lora[:4, 260:310] = g("lora_up").T
    lora[:50, 310:438] = g("up_aux").T
    lora[:, 438] = g("b")
    a["lora_w"] = lora
    g = lambda n: v["L1_attn_b_" + n]
    a["lstm_w"] = np.concatenate([g("w"), g("u"), _columns(g("bias"))], 1)
    g = lambda n: v["L2_ffn_" + n]
    a["chmix_w"] = np.concatenate([g("W_r").T, g("W_k").T, g("W_v").T, _columns(g("mu_r"), g("mu_k"))], 1)
    g = lambda n: v["L2_attn_a_" + n]
    a["lru_w"] = np.concatenate([
        g("w_in"), _chunks(_block_diagonal(g("w_gx"))), _chunks(_block_diagonal(g("w_ga"))), _chunks(g("w_out")),
        _columns(g("b_in"), g("b_gx"), g("b_ga"), g("a_real_param"), g("a_imag_param"), g("b_out"))], 1)
    g = lambda n: v["L2_attn_b_" + n]
    a["causal_w"] = np.concatenate([g("W_qkv").T, _columns(g("b_qkv"))], 1)
    g = lambda n: v["L3_attn_b_" + n]
    swap = np.arange(P) ^ 1
    a["rope_w"] = np.concatenate([g("W_q").T, g("W_q").T[:, swap], g("W_k").T, g("W_k").T[:, swap],
                                  g("W_v").T, g("W_o").T, _rope_tables()], 1)
    g = lambda n: v["L3_attn_a_" + n]
    a["mamba_w"] = np.concatenate([
        g("in_proj_w").T, _chunks(g("x_proj_w").T), _pad_rows(g("dt_proj_w").T, P), _chunks(g("out_proj_w").T),
        _chunks(g("A_log").T), _chunks(g("conv_w")),
        _columns(g("in_proj_b"), g("conv_b"), g("D"), g("dt_proj_b"), g("out_proj_b"))], 1)
    g = lambda n: v["L3_ffn_" + n]
    b1 = g("b1").reshape(32, 4, 32).transpose(1, 2, 0).reshape(P, 32)
    tie = np.broadcast_to(np.linspace(0.0, 1e-6, 32, dtype=np.float32), (P, 32))
    a["switch_w"] = np.concatenate([g("Wc").reshape(P, P), g("b2").reshape(P, P), b1, _columns(g("bc").reshape(P)), tie],
                                   1)
    a["switch_w1"] = g("W1").transpose(2, 0, 1, 3).reshape(P, -1)
    a["switch_w2"] = g("W2").reshape(32, 4, P, 32).transpose(1, 3, 0, 2).reshape(P, -1)
    return {n: np.ascontiguousarray(x) for n, x in a.items()}


def kernel(**inputs):
    import concourse.bacc as _bacc
    from concourse.bass_utils import run_bass_kernel_spmd as _run

    nc = _bacc.Bacc("TRN2", target_bir_lowering=False, num_devices=1)
    arrays = _arrays({n: np.asarray(a) for n, a in inputs.items()})
    d = {n: nc.dram_tensor(f"in_{n}", a.shape, mybir.dt.from_np(a.dtype), kind="ExternalInput").ap()
         for n, a in arrays.items()}
    out = nc.dram_tensor("out", (SEQS, LEN, P), F32, kind="ExternalOutput").ap()
    build(nc, d, out)
    r = _run(nc, [{f"in_{n}": a for n, a in arrays.items()}], core_ids=[0])
    return r.results[0]["out"]
```

```python
from contextlib import ExitStack

import numpy as np

import concourse.bass as bass
from concourse import mybir

F32 = mybir.dt.float32
ALU = mybir.AluOpType
ACT = mybir.ActivationFunctionType
AX = mybir.AxisListType.X

P = 128
SEQS = 8
LEN = 256
TOK = SEQS * LEN
W = 512
NJ = TOK // W
SPW = W // LEN
TPW = W // P
LN_EPS = 1e-5


class Stage:

    def __init__(self, nc, name):
        self.nc, self.name = nc, name
        self.stack = ExitStack()
        self.sems = []

    def signals(self, names, prefix=""):
        sems = [self.nc.alloc_semaphore(f"{self.name}_{prefix}{s}") for s in names.split()]
        self.sems += sems
        return sems

    def sb(self, name, shape):
        return self.stack.enter_context(self.nc.sbuf_tensor(f"{self.name}_{name}", shape, F32))

    def end(self):
        self.stack.close()
        self.nc.clear_and_free_semaphores(self.sems)
        self.nc.all_engine_barrier()


def at(k, j, n=NJ):
    return k * n + j + 1


def toks(j, w=W):
    return slice(j * w, (j + 1) * w)


class LayerNorm:

    def __init__(self, K, st, prefix, affine=False):
        self.K, self.affine = K, affine
        (self.mean_ready, self.centered, self.square_ready, self.var_ready, self.log_ready, self.rstd_ready,
         self.scaled, self.norm_ready) = st.signals(
            "mean_ready centered square_ready var_ready log_ready rstd_ready scaled norm_ready", prefix)
        self.xc, self.sq = K.ln_xc, K.ln_sq

    def pe(self, pe, k, src, wait_src, wait_var_bank=None):
        nc, K = self.K.nc, self.K
        for j in range(NJ):
            wait_src(j)
            nc.tensor.matmul(K.ps[:, j, :], K.mean_mat, src[:, toks(j)], start=True, stop=True)\
                .then_inc(self.mean_ready, 1)
        for j in range(NJ):
            pe.wait_ge(self.square_ready, at(k, j))
            if wait_var_bank is not None:
                wait_var_bank(j)
            nc.tensor.matmul(K.ps[:, 4 + j, :], K.mean_mat, self.sq[:, toks(j)], start=True, stop=True)\
                .then_inc(self.var_ready, 1)

    def act(self, act, k):
        nc = self.K.nc
        for j in range(NJ):
            act.wait_ge(self.centered, at(k, j))
            nc.scalar.activation(self.sq[:, toks(j)], self.xc[:, toks(j)], ACT.Square).then_inc(self.square_ready, 1)
        for j in range(NJ + 1):
            if j < NJ:
                act.wait_ge(self.var_ready, at(k, j))
                nc.scalar.activation(self.sq[:, toks(j)], self.K.ps[:, 4 + j, :], ACT.Ln, bias=self.K.eps_ln)\
                    .then_inc(self.log_ready, 1)
            if j >= 1:
                act.wait_ge(self.log_ready, at(k, j - 1))
                nc.scalar.activation(self.sq[:, toks(j - 1)], self.sq[:, toks(j - 1)], ACT.Exp, scale=-0.5)\
                    .then_inc(self.rstd_ready, 1)

    def dve(self, dve, k, src, out, weight=None, bias=None):
        nc = self.K.nc
        for j in range(NJ):
            dve.wait_ge(self.mean_ready, at(k, j))
            nc.vector.tensor_tensor(self.xc[:, toks(j)], src[:, toks(j)], self.K.ps[:, j, :], ALU.subtract)\
                .then_inc(self.centered, 1)
        for j in range(NJ):
            dve.wait_ge(self.rstd_ready, at(k, j))
            dst = self.xc if self.affine else out
            nc.vector.tensor_tensor(dst[:, toks(j)], self.xc[:, toks(j)], self.sq[:, toks(j)], ALU.mult)\
                .then_inc(self.scaled if self.affine else self.norm_ready, 1)
            if self.affine:
                dve.wait_ge(self.scaled, at(k, j))
                nc.vector.tensor_scalar(out[:, toks(j)], self.xc[:, toks(j)], weight, bias, ALU.mult, ALU.add)\
                    .then_inc(self.norm_ready, 1)


def _log1p_series(degree=5):
    top = 1.0 / 9
    nodes = top / 2 * (1 + np.cos(np.pi * (np.arange(degree + 1) + 0.5) / (degree + 1)))
    s = np.sqrt(nodes)
    return [float(c) for c in np.polyfit(nodes, 2 * np.arctanh(s) / s, degree)]


ATANH = _log1p_series()
PI_IN = float(np.nextafter(np.float32(np.pi), np.float32(0)))


class Attention:

    def __init__(self, K, st, groups, heads, dv, scale, prefix="att_", sim_banks=lambda g: 2 * (g % 2),
                 moved_banks=4, o_bank=lambda g: 6 + g % 2):
        self.K, self.groups, self.G, self.dv, self.scale = K, groups, heads, dv, scale
        self.sim_banks, self.moved_banks, self.o_bank = sim_banks, moved_banks, o_bank
        (self.sim_ready, self.masked, self.max_ready, self.p_ready, self.pt_ready, self.pt_copied, self.o_ready,
         self.recip, self.o_copied) = st.signals(
            "sim_ready masked max_ready p_ready pt_ready pt_copied o_ready recip o_copied", prefix)
        self.s = st.sb(prefix + "s", [P, 3, heads, LEN])
        self.pt = st.sb(prefix + "pt", [P, 2, heads * 2 * P])
        self.stat = st.sb(prefix + "stat", [P, 4, 3, heads])
        self.n = len(groups)

    def sim(self, g):
        b = self.sim_banks(g)
        flat = self.K.ps[:, b:b + 2, :].rearrange("p b n -> p (b n)")
        return flat[:, 0:self.G * LEN].rearrange("p (h n) -> p h n", n=LEN)

    def moved(self, g):
        b = self.moved_banks
        return self.K.ps[:, b:b + 2, :].rearrange("p b n -> p (b n)")[:, 0:self.G * self.groups[g][1] * P]

    def scores(self, pe, base, g):
        for h in range(self.G):
            qk, tiles = self.groups[g][0][h], self.groups[g][1]
            mm = self.K.nc.tensor.matmul(self.sim(g)[:, h, 0:tiles * P], qk[0], qk[1], start=True, stop=True)
        mm.then_inc(self.sim_ready, 1)

    def turn(self, pe, base, g):
        pe.wait_ge(self.p_ready, base + (g + 1))
        tiles = self.groups[g][1]
        for h in range(self.G):
            for kt in range(tiles):
                mm = self.K.nc.tensor.transpose(self.moved(g)[:, toks(h * tiles + kt, P)],
                                                self.s[:, g % 3, h, toks(kt, P)], self.K.ident)
        mm.then_inc(self.pt_ready, 1)

    def values(self, pe, base, g):
        pe.wait_ge(self.pt_copied, base + (g + 1))
        tiles, v = self.groups[g][1], self.groups[g][3]
        for h in range(self.G):
            for kt in range(tiles):
                mm = self.K.nc.tensor.matmul(self.K.ps[:, self.o_bank(g), h * self.dv:(h + 1) * self.dv],
                                             self.pt[:, g % 2, toks(h * tiles + kt, P)], v[h][kt],
                                             start=(kt == 0), stop=(kt == tiles - 1))
        mm.then_inc(self.o_ready, 1)

    def exps(self, act, base, g):
        act.wait_ge(self.max_ready, base + (g + 1))
        n = self.groups[g][1] * P
        for h in range(self.G):
            a = self.K.nc.scalar.activation(self.s[:, g % 3, h, 0:n], self.s[:, g % 3, h, 0:n], ACT.Exp,
                                            bias=self.stat[:, g % 4, 0, h:h + 1],
                                            accum_out=self.stat[:, g % 4, 1, h:h + 1])
        a.then_inc(self.p_ready, 1)

    def copy(self, act, base, g):
        act.wait_ge(self.pt_ready, base + (g + 1))
        if g >= 2:
            act.wait_ge(self.o_ready, base + (g - 1))
        m = self.moved(g)
        self.K.nc.scalar.activation(self.pt[:, g % 2, 0:m.shape[1]], m, ACT.Copy).then_inc(self.pt_copied, 1)

    def mask_and_max(self, dve, base, g):
        nc = self.K.nc
        dve.wait_ge(self.sim_ready, base + (g + 1))
        if g >= 3:
            dve.wait_ge(self.pt_ready, base + (g - 2))
        n = self.groups[g][1] * P
        mask = self.groups[g][2].unsqueeze(1).to_broadcast([P, self.G, n])
        nc.vector.scalar_tensor_tensor(self.s[:, g % 3, :, 0:n], self.sim(g)[:, :, 0:n], self.scale, mask,
                                       ALU.mult, ALU.add).then_inc(self.masked, 1)
        dve.wait_ge(self.masked, base + (g + 1))
        nc.vector.tensor_reduce(self.stat[:, g % 4, 0, :], self.s[:, g % 3, :, 0:n], AX, ALU.max, negate=True)\
            .then_inc(self.max_ready, 1)

    def output(self, dve, base, g):
        nc = self.K.nc
        dve.wait_ge(self.p_ready, base + (g + 1))
        nc.vector.reciprocal(self.stat[:, g % 4, 2, :], self.stat[:, g % 4, 1, :]).then_inc(self.recip, 1)
        dve.wait_ge(self.recip, base + (g + 1))
        dve.wait_ge(self.o_ready, base + (g + 1))
        o = self.K.ps[:, self.o_bank(g), 0:self.G * self.dv].rearrange("p (h d) -> p h d", d=self.dv)
        nc.vector.tensor_tensor(self.groups[g][4], o,
                                self.stat[:, g % 4, 2, :].unsqueeze(2).to_broadcast([P, self.G, self.dv]),
                                ALU.mult).then_inc(self.o_copied, 1)

    def pe(self, pe, base, wait_in):
        def ahead(g):
            wait_in(g)
            if g >= 2:
                pe.wait_ge(self.masked, base + (g - 1))
            self.scores(pe, base, g)

        for g in range(min(3, self.n)):
            ahead(g)
        for g in range(self.n):
            self.turn(pe, base, g)
            if g + 3 < self.n:
                ahead(g + 3)
            if g >= 2:
                pe.wait_ge(self.o_copied, base + (g - 1))
            self.values(pe, base, g)

    def act(self, act, base):
        for g in range(min(2, self.n)):
            self.exps(act, base, g)
        for g in range(self.n):
            self.copy(act, base, g)
            if g + 2 < self.n:
                self.exps(act, base, g + 2)

    def dve(self, dve, base):
        for g in range(min(3, self.n)):
            self.mask_and_max(dve, base, g)
        for g in range(self.n):
            if g + 3 < self.n:
                self.mask_and_max(dve, base, g + 3)
            self.output(dve, base, g)


def linear_attention_stage(K, depth=6):
    nc = K.nc
    HD, HEADS, CH = 16, 8, 4
    st = Stage(nc, "linattn")
    (st.wa_ready, st.wb_ready, st.q_ready, st.q_max, st.q_shift, st.q_exp, st.q_sum, st.q_rsum, st.q_soft,
     st.q_moved, st.k_ready, st.k_max, st.k_exp, st.k_rsum, st.k_moved, st.k_copied, st.v_ready,
     st.v_copied, st.q_copied, st.ctx_ready, st.ctx_masked, st.cw_ready, st.cw_copied,
     st.proj_ready, st.y_attn, st.hid_ready, st.hid_leak, st.hid_act, st.mlp_ready, st.y_ready,
     st.x_done) = st.signals(
        "wa_ready wb_ready q_ready q_max q_shift q_exp q_sum q_rsum q_soft q_moved k_ready k_max k_exp k_rsum "
        "k_moved k_copied v_ready v_copied q_copied ctx_ready ctx_masked cw_ready cw_copied "
        "proj_ready y_attn hid_ready hid_leak hid_act mlp_ready y_ready x_done")
    outer = LayerNorm(K, st, "outer_")
    inner = LayerNorm(K, st, "inner_", affine=True)
    wa = st.sb("wa", [P, K.d["linattn_wa"].shape[2]])
    wb = st.sb("wb", [P, K.d["linattn_wb"].shape[2]])
    wq, wk, wv, wo = (wa[:, toks(i, P)] for i in range(4))
    ln1w, ln1b, bo = (wa[:, 512 + i:513 + i] for i in range(3))
    w1 = [wb[:, toks(c, P)] for c in range(CH)]
    w2 = [wb[:, toks(CH + c, P)] for c in range(CH)]
    ln2w, ln2b = (wb[:, 2 * CH * P + i:2 * CH * P + i + 1] for i in range(2))
    y, h = K.y, K.h
    qs = st.sb("qs", [P, TOK])
    qst = st.sb("qst", [P, NJ, 64])
    ke = st.sb("ke", [P, TOK])
    kst = st.sb("kst", [P, NJ, 3, SPW])
    kt = st.sb("kt", [P, TOK])
    vt = st.sb("vt", [P, TOK])
    qt = st.sb("qt", [P, TOK])
    ctx = st.sb("ctx", [P, NJ, SPW, P])
    cw = st.sb("cw", [P, NJ, SPW, P])
    hid = st.sb("hid", [P, CH, TOK])
    leak = st.sb("leak", [P, TOK])
    heads = TPW * HEADS

    def grouped(ap):
        return ap.rearrange("p (g f) -> p g f", f=HD)

    with nc.Block() as block:
        @block.sync
        def _(sp):
            def load(what, to, l, done):
                sp.dma_start(to[:, :], K.d[what][bass.ds(l, 1), :, :].rearrange("a p n -> (a p) n")).then_inc(done, 16)

            load("linattn_wa", wa, 0, st.wa_ready)
            load("linattn_wb", wb, 0, st.wb_ready)
            with sp.Fori(0, depth - 1) as l:
                sp.wait_ge(st.y_attn, (l + 1) * NJ)
                load("linattn_wa", wa, l + 1, st.wa_ready)
                sp.wait_ge(st.y_ready, (l + 2) * NJ)
                load("linattn_wb", wb, l + 1, st.wb_ready)

        @block.tensor
        def _(pe):
            outer.pe(pe, 0, K.x, lambda j: None)
            with pe.Fori(0, depth) as l:
                inner.pe(pe, 2 * l, y, lambda j: pe.wait_ge(st.y_ready, at(l, j)))
                pe.wait_ge(st.wa_ready, 16 * l + 16)
                for j in range(NJ):
                    pe.wait_ge(inner.norm_ready, at(2 * l, j))
                    for t in range(TPW):
                        mm = nc.tensor.matmul(K.ps[:, j, toks(t, P)], h[:, toks(TPW * j + t, P)], wq,
                                              start=True, stop=True)
                    mm.then_inc(st.q_ready, 1)
                for j in range(NJ):
                    nc.tensor.matmul(K.ps[:, 4 + j, :], wk, h[:, toks(j)], start=True, stop=True)\
                        .then_inc(st.k_ready, 1)
                for j in range(NJ):
                    pe.wait_ge(st.q_shift, at(l, j))
                    for t in range(TPW):
                        mm = nc.tensor.matmul(K.ps[:, j, toks(t, P)], h[:, toks(TPW * j + t, P)], wv,
                                              start=True, stop=True)
                    mm.then_inc(st.v_ready, 1)
                for j in range(NJ):
                    pe.wait_ge(st.k_exp, at(l, j))
                    for t in range(TPW):
                        mm = nc.tensor.transpose(K.ps[:, 4 + j, toks(t, P)], ke[:, toks(TPW * j + t, P)], K.ident)
                    mm.then_inc(st.k_moved, 1)
                for j in range(NJ):
                    pe.wait_ge(st.q_soft, at(l, j))
                    pe.wait_ge(st.v_copied, at(l, j))
                    for t in range(TPW):
                        mm = nc.tensor.transpose(K.ps[:, j, toks(t, P)], qs[:, toks(TPW * j + t, P)], K.ident)
                    mm.then_inc(st.q_moved, 1)
                for j in range(NJ):
                    pe.wait_ge(st.k_copied, at(l, j))
                    for s in range(SPW):
                        for t in range(2):
                            tile = toks(TPW * j + 2 * s + t, P)
                            mm = nc.tensor.matmul(K.ps[:, 4 + j, toks(s, P)], vt[:, tile], kt[:, tile],
                                                  start=(t == 0), stop=(t == 1))
                    mm.then_inc(st.ctx_ready, 1)
                for j in range(NJ):
                    pe.wait_ge(st.ctx_masked, at(l, j))
                    pe.wait_ge(st.q_copied, at(l, j))
                    for s in range(SPW):
                        mm = nc.tensor.matmul(K.ps[:, j, toks(s, P)], ctx[:, j, s, :], wo, start=True, stop=True)
                    mm.then_inc(st.cw_ready, 1)
                for j in range(NJ):
                    pe.wait_ge(st.cw_copied, at(l, j))
                    for s in range(SPW):
                        mm = nc.tensor.matmul(K.ps[:, 4 + j, toks(s, LEN)], cw[:, j, s, :],
                                              qt[:, toks(SPW * j + s, LEN)], start=True, stop=True)
                    mm.then_inc(st.proj_ready, 1)
                inner.pe(pe, 2 * l + 1, y, lambda j: pe.wait_ge(st.y_attn, at(l, j)))
                pe.wait_ge(st.wb_ready, 16 * l + 16)
                for c in range(CH + 1):
                    for j in range(NJ):
                        if c < CH:
                            if c == 0:
                                pe.wait_ge(inner.norm_ready, at(2 * l + 1, j))
                            else:
                                pe.wait_ge(st.hid_act, at(CH * l + c - 1, j))
                            nc.tensor.matmul(K.ps[:, j, :], w1[c], h[:, toks(j)], start=True, stop=True)\
                                .then_inc(st.hid_ready, 1)
                        if c > 0:
                            if c == CH:
                                pe.wait_ge(st.hid_act, at(CH * l + c - 1, j))
                            mm = nc.tensor.matmul(K.ps[:, 4 + j, :], w2[c - 1], hid[:, c - 1, toks(j)],
                                                  start=(c == 1), stop=(c == CH))
                            if c == CH:
                                mm.then_inc(st.mlp_ready, 1)

        @block.scalar
        def _(act):
            nc.scalar.preload_act_table_set("natural_log_exp_and_others")
            outer.act(act, 0)
            with act.Fori(0, depth) as l:
                inner.act(act, 2 * l)
                for j in range(NJ):
                    act.wait_ge(st.k_max, at(l, j))
                    for s in range(SPW):
                        a = nc.scalar.activation(ke[:, toks(SPW * j + s, LEN)], K.ps[:, 4 + j, toks(s, LEN)], ACT.Exp,
                                                 bias=kst[:, j, 0, s:s + 1], accum_out=kst[:, j, 1, s:s + 1])
                    a.then_inc(st.k_exp, 1)
                    act.wait_ge(st.q_shift, at(l, j))
                    nc.scalar.activation(qs[:, toks(j)], qs[:, toks(j)], ACT.Exp).then_inc(st.q_exp, 1)
                for j in range(NJ):
                    act.wait_ge(st.v_ready, at(l, j))
                    nc.scalar.activation(vt[:, toks(j)], K.ps[:, j, :], ACT.Copy).then_inc(st.v_copied, 1)
                for j in range(NJ):
                    act.wait_ge(st.q_moved, at(l, j))
                    nc.scalar.activation(qt[:, toks(j)], K.ps[:, j, :], ACT.Copy).then_inc(st.q_copied, 1)
                for j in range(NJ):
                    act.wait_ge(st.cw_ready, at(l, j))
                    act.wait_ge(st.k_rsum, at(l, j))
                    for s in range(SPW):
                        a = nc.scalar.activation(cw[:, j, s, :], K.ps[:, j, toks(s, P)], ACT.Identity,
                                                 scale=kst[:, j, 2, s:s + 1])
                    a.then_inc(st.cw_copied, 1)
                inner.act(act, 2 * l + 1)
                for c in range(CH):
                    for j in range(NJ):
                        act.wait_ge(st.hid_ready, at(CH * l + c, j))
                        nc.scalar.activation(leak[:, toks(j)], K.ps[:, j, :], ACT.Copy, scale=0.01)\
                            .then_inc(st.hid_leak, 1)

        @block.vector
        def _(dve):
            outer.dve(dve, 0, K.x, y)
            dve.wait_ge(outer.norm_ready, NJ)
            dve.sem_inc(st.y_ready, NJ)
            with dve.Fori(0, depth) as l:
                dve.wait_ge(st.wa_ready, 16 * l + 16)
                inner.dve(dve, 2 * l, y, h, ln1w, ln1b)
                for j in range(NJ):
                    dve.wait_ge(st.q_ready, at(l, j))
                    nc.vector.tensor_reduce(qst[:, j, 0:heads], grouped(K.ps[:, j, :]), AX, ALU.max)\
                        .then_inc(st.q_max, 1)
                    dve.wait_ge(st.q_max, at(l, j))
                    nc.vector.tensor_tensor(grouped(qs[:, toks(j)]), grouped(K.ps[:, j, :]),
                                            qst[:, j, 0:heads].unsqueeze(2).to_broadcast([P, heads, HD]),
                                            ALU.subtract).then_inc(st.q_shift, 1)
                for j in range(NJ):
                    dve.wait_ge(st.k_ready, at(l, j))
                    nc.vector.tensor_reduce(kst[:, j, 0, :], K.ps[:, 4 + j, :].rearrange("p (s n) -> p s n", n=LEN),
                                            AX, ALU.max, negate=True).then_inc(st.k_max, 1)
                for j in range(NJ):
                    dve.wait_ge(st.q_exp, at(l, j))
                    nc.vector.tensor_reduce(qst[:, j, 32:32 + heads], grouped(qs[:, toks(j)]), AX, ALU.add)\
                        .then_inc(st.q_sum, 1)
                for j in range(NJ):
                    dve.wait_ge(st.q_sum, at(l, j))
                    nc.vector.reciprocal(qst[:, j, 0:heads], qst[:, j, 32:32 + heads]).then_inc(st.q_rsum, 1)
                for j in range(NJ):
                    dve.wait_ge(st.q_rsum, at(l, j))
                    nc.vector.tensor_tensor(grouped(qs[:, toks(j)]), grouped(qs[:, toks(j)]),
                                            qst[:, j, 0:heads].unsqueeze(2).to_broadcast([P, heads, HD]),
                                            ALU.mult).then_inc(st.q_soft, 1)
                for j in range(NJ):
                    dve.wait_ge(st.k_exp, at(l, j))
                    nc.vector.reciprocal(kst[:, j, 2, :], kst[:, j, 1, :]).then_inc(st.k_rsum, 1)
                for j in range(NJ):
                    dve.wait_ge(st.k_moved, at(l, j))
                    nc.vector.tensor_copy(kt[:, toks(j)], K.ps[:, 4 + j, :]).then_inc(st.k_copied, 1)
                for j in range(NJ):
                    dve.wait_ge(st.ctx_ready, at(l, j))
                    nc.vector.tensor_tensor(ctx[:, j], K.ps[:, 4 + j, 0:SPW * P].rearrange("p (s f) -> p s f", f=P),
                                            K.head_mask16.unsqueeze(1).to_broadcast([P, SPW, P]), ALU.mult)\
                        .then_inc(st.ctx_masked, 1)
                for j in range(NJ):
                    dve.wait_ge(st.proj_ready, at(l, j))
                    nc.vector.scalar_tensor_tensor(y[:, toks(j)], K.ps[:, 4 + j, :], bo, y[:, toks(j)],
                                                   ALU.add, ALU.add).then_inc(st.y_attn, 1)
                dve.wait_ge(st.wb_ready, 16 * l + 16)
                inner.dve(dve, 2 * l + 1, y, h, ln2w, ln2b)
                for c in range(CH):
                    for j in range(NJ):
                        dve.wait_ge(st.hid_leak, at(CH * l + c, j))
                        nc.vector.tensor_tensor(hid[:, c, toks(j)], K.ps[:, j, :], leak[:, toks(j)], ALU.max)\
                            .then_inc(st.hid_act, 1)
                for j in range(NJ):
                    dve.wait_ge(st.mlp_ready, at(l, j))
                    nc.vector.tensor_tensor(y[:, toks(j)], K.ps[:, 4 + j, :], y[:, toks(j)], ALU.add)\
                        .then_inc(st.y_ready, 1)
            for j in range(NJ):
                dve.wait_ge(st.y_ready, at(depth, j))
                nc.vector.tensor_tensor(K.x[:, toks(j)], K.x[:, toks(j)], y[:, toks(j)], ALU.add)\
                    .then_inc(st.x_done, 1)
    st.end()


def window_attention_stage(K, tag):
    nc = K.nc
    DEPTH, DH, GH, QC = 2, 64, 4, 4
    NB = 4
    LAG = 2
    HID = 341
    HC = [(0, 128), (128, 128), (256, HID - 256)]
    st = Stage(nc, f"window{tag}")
    (st.tabs_ready, st.wa_ready, st.wb_ready, st.tab_ready, st.edge, st.y_ready, st.sh_low, st.sh_high,
     st.lin_ready, st.sq_ready, st.lin_read, st.rot_read, st.ss_ready, st.ss_safe, st.ss_log, st.rn_ready,
     st.turned, st.qk_done, st.v_ready, st.v_copied, st.o_turned, st.o_moved, st.proj_ready, st.y_attn,
     st.sh2_low, st.sh2_high, st.hid_a, st.hid_g, st.gelu_done, st.hid_done, st.mlp_ready, st.x_done) = st.signals(
        "tabs_ready wa_ready wb_ready tab_ready edge y_ready sh_low sh_high lin_ready sq_ready "
        "lin_read rot_read ss_ready ss_safe ss_log rn_ready turned qk_done v_ready v_copied "
        "o_turned o_moved proj_ready y_attn sh2_low sh2_high hid_a hid_g gelu_done hid_done "
        "mlp_ready x_done")
    outer = LayerNorm(K, st, "outer_")
    inner = LayerNorm(K, st, "inner_", affine=True)
    wa = st.sb("wa", [P, K.d["window_wa"].shape[2]])
    wb = st.sb("wb", [P, K.d["window_wb"].shape[2]])
    tabs = st.sb("tabs", [P, 4, LEN])
    wqk = []
    for i in range(2 * QC):
        wqk.append((wa[:, toks(2 * i, P)], wa[:, toks(2 * i + 1, P)]))
    o = 4 * QC * P
    wv = wa[:, o:o + 512]
    o += 512
    wo = [wa[:, o + c * P:o + (c + 1) * P] for c in range(QC)]
    o += 512
    scales = [wa[:, o + i:o + i + 1] for i in range(4)]
    w1a = [wb[:, a:a + n] for a, n in HC]
    w1g = [wb[:, HID + a:HID + a + n] for a, n in HC]
    o = 2 * HID
    w2 = [wb[0:n, o + c * P:o + (c + 1) * P] for c, (a, n) in enumerate(HC)]
    o += 3 * P
    ln_w, ln_b, b2 = (wb[:, o + i:o + i + 1] for i in range(3))
    b1a = [wb[0:n, o + 3 + c:o + 4 + c] for c, (a, n) in enumerate(HC)]
    b1g = [wb[0:n, o + 6 + c:o + 7 + c] for c, (a, n) in enumerate(HC)]

    y = K.y
    sh = st.sb("sh", [P, W])
    tab = st.sb("tab", [P, 4, LEN])
    sq = st.sb("sq", [P, NB, W])
    part = st.sb("part", [P, NB, 2, W])
    qk = st.sb("qk", [P, 2 * 2 * QC, W])
    vt = st.sb("vt", [P, TPW, W])
    ot = st.sb("ot", [P, TPW, W])
    of = st.sb("of", [P, QC, W])
    ya = K.h
    sh2 = st.sb("sh2", [P, TOK])
    hn = K.ln_xc
    gl, hid = qk[:, 0:3, :], [qk[:, 3:6, :], qk[:, 6:9, :]]
    seqs = lambda ap: ap.rearrange("p (s n) -> p s n", n=LEN)

    groups = []
    for n in range(NJ):
        q, k = qk[:, 8 * (n % 2):8 * (n % 2) + 4, :], qk[:, 8 * (n % 2) + 4:8 * (n % 2) + 8, :]
        for s, t in ((0, 0), (0, 1), (1, 1), (1, 0)):
            for hg in range(2):
                ops, vs = [], []
                for h in range(hg, 2 * GH, 2):
                    rows = slice(DH * (h % 2), DH * (h % 2) + DH)
                    ops.append((q[rows, h // 2, s * LEN + t * P:s * LEN + (t + 1) * P],
                                k[rows, h // 2, s * LEN:s * LEN + (t + 1) * P]))
                    vs.append([vt[:, 2 * s + kt, DH * h:DH * (h + 1)] for kt in range(t + 1)])
                groups.append((ops, t + 1, K.banded[:, LEN * t:LEN * t + (t + 1) * P], vs,
                               ot[:, 2 * s + t, :].rearrange("p (h a d) -> p a h d", a=2, d=DH)[:, hg]))
    GP = len(groups) // NJ
    LAST = GP * (NJ - 1)
    alone = lambda g: g >= LAST and g % 2 == 1
    att = Attention(K, st, groups, GH, DH, 8.0, sim_banks=lambda g: 5 if alone(g) else 0, moved_banks=2,
                    o_bank=lambda g: 7 if alone(g) else 4)
    lin_bank = lambda n, i: 5 if n else 2 * (i % 2)
    ss_bank = lambda n, i: 7 if n else 4 + i % 2
    depth = lambda n: 1 if n else 2
    v_bank = lambda n, t: (5, 6, 4, 5)[t] if n else (6, 7, 0, 1)[t]

    def tokens(ap, n, first=0, size=W):
        return ap[:, n * W + first:n * W + first + size]

    with nc.Block() as block:
        @block.sync
        def _(sp):
            def load(what, to, l, done):
                sp.dma_start(to[:, :], K.d[what][bass.ds(l, 1), :, :].rearrange("a p n -> (a p) n")).then_inc(done, 16)

            load("window_wa", wa, 0, st.wa_ready)
            sp.dma_start(tabs[:, :, :].rearrange("p a n -> p (a n)"), K.d["window_tabs"]).then_inc(st.tabs_ready, 16)
            load("window_wb", wb, 0, st.wb_ready)
            with sp.Fori(0, DEPTH - 1) as l:
                sp.wait_ge(st.tab_ready, l + 1)
                sp.wait_ge(st.proj_ready, (l + 1) * NJ)
                load("window_wa", wa, l + 1, st.wa_ready)
                sp.wait_ge(st.y_ready, (l + 2) * NJ)
                load("window_wb", wb, l + 1, st.wb_ready)

        @block.tensor
        def _(pe):
            outer.pe(pe, 0, K.x, lambda j: None)
            with pe.Fori(0, DEPTH) as l:
                base, pair = l * att.n, lambda n: l * NJ + n

                def lin(n, i):
                    k = pair(n)
                    if i == 0:
                        pe.wait_ge(st.sh_low, k + 1)
                        pe.wait_ge(st.sh_high, k + 1)
                    if i >= depth(n):
                        pe.wait_ge(st.lin_read, k * 8 + (i + 1 - depth(n)))
                        pe.wait_ge(st.rot_read, k * 8 + (i + 1 - depth(n)))
                    for a in range(2):
                        mm = nc.tensor.matmul(K.ps[:, lin_bank(n, i) + a, :], wqk[i][a], sh[:, :],
                                              start=True, stop=True)
                    mm.then_inc(st.lin_ready, 1)

                def norm(n, i):
                    k = pair(n)
                    pe.wait_ge(st.sq_ready, k * 8 + (i + 1))
                    if i >= depth(n):
                        pe.wait_ge(st.ss_safe, k * 8 + (i + 1 - depth(n)))
                    if i == 0 and n >= 2:
                        pe.wait_ge(st.y_attn, k - 1)
                    nc.tensor.matmul(K.ps[:, ss_bank(n, i), :], K.half_ones, sq[:, i % NB, :], start=True, stop=True)\
                        .then_inc(st.ss_ready, 1)

                def v(n, t):
                    nc.tensor.matmul(K.ps[:, v_bank(n, t), :], sh[:, toks(t, P)], wv, start=True, stop=True)\
                        .then_inc(st.v_ready, 1)

                def turn_output(n):
                    pe.wait_ge(att.o_copied, base + GP * (n + 1))
                    for c in range(QC):
                        for t in range(TPW):
                            mm = nc.tensor.transpose(K.ps[:, c, toks(t, P)], ot[:, t, toks(c, P)], K.ident)
                        mm.then_inc(st.o_turned, 1)

                def project(n):
                    for c in range(QC):
                        pe.wait_ge(st.o_moved, pair(n) * QC + (c + 1))
                        mm = nc.tensor.matmul(K.ps[:, 7, :], wo[c], of[:, c, :], start=(c == 0), stop=(c == QC - 1))
                    mm.then_inc(st.proj_ready, 1)

                pe.wait_ge(st.wa_ready, 16 * l + 16)
                pe.wait_ge(st.y_ready, (l + 1) * NJ)
                for i in range(2 * QC):
                    lin(0, i)
                    if i >= 1:
                        norm(0, i - 1)
                norm(0, 2 * QC - 1)
                for t in range(TPW):
                    if t == 2:
                        pe.wait_ge(st.lin_read, pair(0) * 8 + 7)
                        pe.wait_ge(st.rot_read, pair(0) * 8 + 7)
                    v(0, t)
                pe.wait_ge(st.v_copied, pair(0) * TPW + TPW)
                pe.wait_ge(st.qk_done, pair(0) * 8 + 8)
                att.scores(pe, base, 0)
                for n in range(NJ - 1):
                    for i in range(GP):
                        g = GP * n + i
                        lin(n + 1, i)
                        if i < GP - 1:
                            pe.wait_ge(att.masked, base + (g + 1))
                            att.scores(pe, base, g + 1)
                        att.turn(pe, base, g)
                        if i >= 1:
                            norm(n + 1, i - 1)
                            pe.wait_ge(att.o_copied, base + g)
                        att.values(pe, base, g)
                    norm(n + 1, GP - 1)
                    pe.wait_ge(st.lin_read, pair(n + 1) * 8 + 8)
                    pe.wait_ge(st.rot_read, pair(n + 1) * 8 + 8)
                    v(n + 1, 0)
                    v(n + 1, 1)
                    turn_output(n)
                    v(n + 1, 2)
                    pe.wait_ge(st.v_copied, pair(n + 1) * TPW + 1)
                    v(n + 1, 3)
                    pe.wait_ge(st.qk_done, pair(n + 1) * 8 + 8)
                    pe.wait_ge(st.o_moved, pair(n) * QC + 2)
                    att.scores(pe, base, GP * (n + 1))
                    pe.wait_ge(st.ss_safe, pair(n + 1) * 8 + 8)
                    project(n)
                    pe.wait_ge(st.v_copied, pair(n + 1) * TPW + TPW)
                att.scores(pe, base, LAST + 1)
                pe.wait_ge(att.masked, base + (LAST + 1))
                att.scores(pe, base, LAST + 2)
                for g in range(LAST, LAST + GP):
                    att.turn(pe, base, g)
                    if g + 3 < LAST + GP:
                        pe.wait_ge(att.masked, base + (g + 2))
                        att.scores(pe, base, g + 3)
                    if g == LAST + 1:
                        pe.wait_ge(st.y_attn, pair(NJ - 2) + 1)
                    if g >= LAST + 2:
                        pe.wait_ge(att.o_copied, base + (g - 1))
                    att.values(pe, base, g)
                turn_output(NJ - 1)
                project(NJ - 1)
                inner.pe(pe, l, sh2, lambda j: (pe.wait_ge(st.sh2_low, at(l, j)), pe.wait_ge(st.sh2_high, at(l, j))))
                pe.wait_ge(st.wb_ready, 16 * l + 16)
                for j in range(NJ + 1):
                    k = l * NJ + j
                    if j < NJ:
                        pe.wait_ge(inner.norm_ready, at(l, j))
                        for c, (a, m) in enumerate(HC):
                            if j >= 1:
                                pe.wait_ge(st.hid_done, k * 3 + (c - 2))
                            nc.tensor.matmul(K.ps[0:m, c, :], w1g[c], hn[:, toks(j)], start=True, stop=True)\
                                .then_inc(st.hid_g, 1)
                            nc.tensor.matmul(K.ps[0:m, 3 + c, :], w1a[c], hn[:, toks(j)], start=True, stop=True)\
                                .then_inc(st.hid_a, 1)
                    if j >= 1:
                        if j >= 3:
                            pe.wait_ge(st.y_ready, (l + 1) * NJ + j - 2)
                        for c, (a, m) in enumerate(HC):
                            pe.wait_ge(st.hid_done, k * 3 + (c - 2))
                            mm = nc.tensor.matmul(K.ps[:, 6 + (j - 1) % 2, :], w2[c], hid[(j - 1) % 2][0:m, c, :],
                                                  start=(c == 0), stop=(c == 2))
                        mm.then_inc(st.mlp_ready, 1)

        @block.scalar
        def _(act):
            nc.scalar.preload_act_table_set("natural_log_exp_and_others")
            outer.act(act, 0)
            with act.Fori(0, DEPTH) as l:
                nc.scalar.preload_act_table_set("natural_log_exp_and_others")
                base, pair = l * att.n, lambda n: l * NJ + n

                def shift_low(n):
                    act.wait_ge(st.y_ready, pair(n) + 1)
                    nc.scalar.activation(sh[0:64, :], tokens(y[0:64], n), ACT.Copy).then_inc(st.sh_low, 1)

                def shift2_low(n):
                    act.wait_ge(st.y_attn, pair(n) + 1)
                    nc.scalar.activation(tokens(sh2[0:64], n), tokens(ya[0:64], n), ACT.Copy).then_inc(st.sh2_low, 1)

                def square(n, i):
                    act.wait_ge(st.lin_ready, pair(n) * 8 + (i + 1))
                    if i >= NB:
                        act.wait_ge(st.qk_done, pair(n) * 8 + (i + 1 - NB))
                    nc.scalar.activation(sq[:, i % NB, :], K.ps[:, lin_bank(n, i), :], ACT.Square)\
                        .then_inc(st.sq_ready, 1)

                def inverse(n, i):
                    act.wait_ge(st.ss_safe, pair(n) * 8 + (i + 1))
                    r = sq[:, i % NB, :]
                    nc.scalar.activation(r, r, ACT.Ln, scale=float(2 ** 20)).then_inc(st.ss_log, 1)
                    act.wait_ge(st.ss_log, pair(n) * 8 + (i + 1))
                    nc.scalar.activation(r, r, ACT.Exp, scale=-0.5, bias=K.ln_shift).then_inc(st.rn_ready, 1)

                def copy_v(n, t):
                    act.wait_ge(st.v_ready, pair(n) * TPW + (t + 1))
                    nc.scalar.activation(vt[:, t, :], K.ps[:, v_bank(n, t), :], ACT.Copy).then_inc(st.v_copied, 1)

                def copy_output(n):
                    for c in range(QC):
                        act.wait_ge(st.o_turned, pair(n) * QC + (c + 1))
                        nc.scalar.activation(of[:, c, :], K.ps[:, c, :], ACT.Copy).then_inc(st.o_moved, 1)

                shift_low(0)
                for i in range(2 * QC + LAG):
                    if i < 2 * QC:
                        square(0, i)
                    if i >= LAG:
                        inverse(0, i - LAG)
                for t in range(TPW):
                    copy_v(0, t)
                shift_low(1)
                att.exps(act, base, 0)
                for n in range(NJ - 1):
                    for i in range(GP):
                        square(n + 1, i)
                        att.copy(act, base, GP * n + i)
                        if i >= LAG:
                            inverse(n + 1, i - LAG)
                        if i < GP - 1:
                            att.exps(act, base, GP * n + i + 1)
                    inverse(n + 1, GP - 2)
                    copy_v(n + 1, 0)
                    copy_v(n + 1, 1)
                    inverse(n + 1, GP - 1)
                    copy_output(n)
                    copy_v(n + 1, 2)
                    copy_v(n + 1, 3)
                    if n + 2 < NJ:
                        shift_low(n + 2)
                    att.exps(act, base, GP * (n + 1))
                    shift2_low(n)
                att.exps(act, base, LAST + 1)
                for g in range(LAST, LAST + GP):
                    att.copy(act, base, g)
                    if g + 2 < LAST + GP:
                        att.exps(act, base, g + 2)
                copy_output(NJ - 1)
                shift2_low(NJ - 1)
                act.wait_ge(st.wb_ready, 16 * l + 16)
                inner.act(act, l)
                for j in range(NJ):
                    for c, (a, m) in enumerate(HC):
                        act.wait_ge(st.hid_g, (l * NJ + j) * 3 + (c + 1))
                        if j >= 1:
                            act.wait_ge(st.hid_done, (l * NJ + j) * 3 + (c - 2))
                        nc.scalar.activation(gl[0:m, c, :], K.ps[0:m, c, :], ACT.Gelu, bias=b1g[c])\
                            .then_inc(st.gelu_done, 1)

        @block.gpsimd
        def _(pool):
            nc.gpsimd.memset(sh[64:128, :], 0.0)
            nc.gpsimd.memset(sh2[64:128, :], 0.0).then_inc(st.edge, 1)
            with pool.Fori(0, DEPTH * NJ // 2) as m:
                for u in range(2):
                    k = m * 2 + u
                    for i in range(2 * QC + LAG):
                        if i < 2 * QC:
                            a = part[:, i % NB, 0, :]
                            pool.wait_ge(st.lin_read, k * 8 + (i + 1))
                            nc.gpsimd.tensor_tensor(a, a, part[:, i % NB, 1, :], ALU.add).then_inc(st.turned, 1)
                        if i >= LAG:
                            c = i - LAG
                            pool.wait_ge(st.turned, k * 8 + (c + 1))
                            pool.wait_ge(st.rn_ready, k * 8 + (c + 1))
                            nc.gpsimd.tensor_tensor(qk[:, 8 * u + c, :], part[:, c % NB, 0, :], sq[:, c % NB, :],
                                                    ALU.mult).then_inc(st.qk_done, 1)

        @block.vector
        def _(dve):
            outer.dve(dve, 0, K.x, y)
            dve.wait_ge(outer.norm_ready, NJ)
            dve.sem_inc(st.y_ready, NJ)
            dve.wait_ge(st.edge, 1)
            dve.wait_ge(st.tabs_ready, 16)
            with dve.Fori(0, DEPTH) as l:
                dve.wait_ge(st.wa_ready, 16 * l + 16)
                for i in range(4):
                    v = nc.vector.tensor_scalar(tab[:, i, :], tabs[:, i, :], scales[i], None, ALU.mult)
                v.then_inc(st.tab_ready, 1)
                base, pair = l * att.n, lambda n: l * NJ + n

                def shift_high(n):
                    dve.wait_ge(st.y_ready, pair(n) + 1)
                    if n:
                        dve.wait_ge(st.v_ready, pair(n) * TPW)
                    for s in range(SPW):
                        v = nc.vector.tensor_copy(sh[64:128, s * LEN + 1:(s + 1) * LEN],
                                                  tokens(y[64:128], n, s * LEN, LEN - 1))
                    v.then_inc(st.sh_high, 1)

                def rotate(n, i):
                    k, b, kind = pair(n), lin_bank(n, i), 2 * (i // QC)
                    table = lambda a: tab[:, kind + a, :].unsqueeze(1).to_broadcast([P, SPW, LEN])
                    dve.wait_ge(st.tab_ready, l + 1)
                    dve.wait_ge(st.lin_ready, k * 8 + (i + 1))
                    if i >= NB:
                        dve.wait_ge(st.qk_done, k * 8 + (i + 1 - NB))
                    nc.vector.tensor_tensor(seqs(part[:, i % NB, 1, :]), seqs(K.ps[:, b + 1, :]), table(1),
                                            ALU.mult).then_inc(st.rot_read, 1)
                    dve.wait_ge(st.sq_ready, k * 8 + (i + 1))
                    nc.vector.tensor_tensor(seqs(part[:, i % NB, 0, :]), seqs(K.ps[:, b, :]), table(0),
                                            ALU.mult).then_inc(st.lin_read, 1)

                def guard(n, i):
                    dve.wait_ge(st.ss_ready, pair(n) * 8 + (i + 1))
                    nc.vector.tensor_scalar(sq[:, i % NB, :], K.ps[:, ss_bank(n, i), :], 1e-24, None, ALU.max)\
                        .then_inc(st.ss_safe, 1)

                def attended(n):
                    k = pair(n)
                    dve.wait_ge(st.proj_ready, k + 1)
                    nc.vector.tensor_tensor(tokens(ya, n), K.ps[:, 7, :], tokens(y, n), ALU.add).then_inc(st.y_attn, 1)
                    dve.wait_ge(st.y_attn, k + 1)
                    for s in range(SPW):
                        v = nc.vector.tensor_copy(tokens(sh2[64:128], n, s * LEN + 1, LEN - 1),
                                                  tokens(ya[64:128], n, s * LEN, LEN - 1))
                    v.then_inc(st.sh2_high, 1)

                shift_high(0)
                for i in range(2 * QC + 1):
                    if i < 2 * QC:
                        rotate(0, i)
                    if i >= 1:
                        guard(0, i - 1)
                shift_high(1)
                att.mask_and_max(dve, base, 0)
                for n in range(NJ - 1):
                    for i in range(GP):
                        rotate(n + 1, i)
                        if i < GP - 1:
                            att.mask_and_max(dve, base, GP * n + i + 1)
                        if i >= 1:
                            guard(n + 1, i - 1)
                        att.output(dve, base, GP * n + i)
                    guard(n + 1, GP - 1)
                    if n + 2 < NJ:
                        shift_high(n + 2)
                    att.mask_and_max(dve, base, GP * (n + 1))
                    attended(n)
                att.mask_and_max(dve, base, LAST + 1)
                att.mask_and_max(dve, base, LAST + 2)
                for g in range(LAST, LAST + GP):
                    if g + 3 < LAST + GP:
                        att.mask_and_max(dve, base, g + 3)
                    att.output(dve, base, g)
                attended(NJ - 1)
                dve.wait_ge(st.wb_ready, 16 * l + 16)
                inner.dve(dve, l, sh2, hn, ln_w, ln_b)
                for j in range(NJ + 1):
                    k = l * NJ + j
                    if j < NJ:
                        for c, (a, m) in enumerate(HC):
                            dve.wait_ge(st.gelu_done, k * 3 + (c + 1))
                            dve.wait_ge(st.hid_a, k * 3 + (c + 1))
                            if j >= 2:
                                dve.wait_ge(st.mlp_ready, k - 1)
                            nc.vector.scalar_tensor_tensor(hid[j % 2][0:m, c, :], K.ps[0:m, 3 + c, :], b1a[c],
                                                           gl[0:m, c, :], ALU.add, ALU.mult).then_inc(st.hid_done, 1)
                    if j >= 1:
                        dve.wait_ge(st.mlp_ready, k)
                        nc.vector.scalar_tensor_tensor(y[:, toks(j - 1)], K.ps[:, 6 + (j - 1) % 2, :], b2,
                                                       ya[:, toks(j - 1)], ALU.add, ALU.add).then_inc(st.y_ready, 1)
            for j in range(NJ):
                dve.wait_ge(st.y_ready, NJ * DEPTH + at(0, j))
                nc.vector.tensor_tensor(K.x[:, toks(j)], K.x[:, toks(j)], y[:, toks(j)], ALU.add)\
                    .then_inc(st.x_done, 1)
    st.end()


def window_attention_first(K):
    window_attention_stage(K, 0)


def window_attention_second(K):
    window_attention_stage(K, 1)


def retention_stage(K):
    nc = K.nc
    st = Stage(nc, "retention")
    (st.w_ready, st.k_ready, st.k_decayed, st.v_ready, st.v_copied, st.q_ready, st.q_copied,
     st.ctx_ready, st.ctx_copied, st.ret_ready, st.ret_decayed, st.stats, st.mean_var, st.gn_log,
     st.gn_rstd, st.shift_a, st.shift_b, st.gate_ready, st.gate_done, st.gn_done, st.gated,
     st.out_ready, st.x_done) = st.signals(
        "w_ready k_ready k_decayed v_ready v_copied q_ready q_copied ctx_ready ctx_copied ret_ready "
        "ret_decayed stats mean_var gn_log gn_rstd shift_a shift_b gate_ready gate_done gn_done "
        "gated out_ready x_done")
    outer = LayerNorm(K, st, "outer_")
    wt = st.sb("wt", [P, K.d["retention_w"].shape[1]])
    wq, wk, wv, wg, wo = (wt[:, toks(i, P)] for i in range(5))
    gn_g, gn_b = wt[:, 640:641], wt[:, 641:642]
    kt, vt, qf, gate, ret = (st.sb(n, [P, TOK]) for n in ("kt", "vt", "qf", "gate", "ret"))
    ctx = st.sb("ctx", [P, SEQS, P])
    bn = st.sb("bn", [P, SEQS, 6])
    mv = st.sb("mv", [P, SEQS, 2])
    co = st.sb("co", [P, 3, SEQS])
    with nc.Block() as block:
        @block.sync
        def _(sp):
            sp.dma_start(wt[:, :], K.d["retention_w"]).then_inc(st.w_ready, 16)

        @block.tensor
        def _(pe):
            outer.pe(pe, 0, K.x, lambda j: None)
            pe.wait_ge(st.w_ready, 16)
            for j in range(NJ):
                pe.wait_ge(outer.norm_ready, at(0, j))
                for t in range(TPW):
                    mm = nc.tensor.matmul(K.ps[:, j, toks(t, P)], K.h[:, toks(TPW * j + t, P)], wk,
                                          start=True, stop=True)
                mm.then_inc(st.k_ready, 1)
            for j in range(NJ):
                for t in range(TPW):
                    mm = nc.tensor.matmul(K.ps[:, 4 + j, toks(t, P)], K.h[:, toks(TPW * j + t, P)], wv,
                                          start=True, stop=True)
                mm.then_inc(st.v_ready, 1)
            for j in range(NJ):
                pe.wait_ge(st.k_decayed, j + 1)
                nc.tensor.matmul(K.ps[:, j, :], wq, K.h[:, toks(j)], start=True, stop=True).then_inc(st.q_ready, 1)
            for j in range(NJ):
                pe.wait_ge(st.v_copied, j + 1)
                for s in range(SPW):
                    for t in range(2):
                        tile = toks(TPW * j + 2 * s + t, P)
                        mm = nc.tensor.matmul(K.ps[:, 4 + j, toks(s, P)], kt[:, tile], vt[:, tile],
                                              start=(t == 0), stop=(t == 1))
                mm.then_inc(st.ctx_ready, 1)
            for j in range(NJ):
                pe.wait_ge(st.q_copied, j + 1)
                pe.wait_ge(st.ctx_copied, j + 1)
                for s in range(SPW):
                    mm = nc.tensor.matmul(K.ps[:, j, toks(s, LEN)], ctx[:, SPW * j + s, :],
                                          qf[:, toks(SPW * j + s, LEN)], start=True, stop=True)
                mm.then_inc(st.ret_ready, 1)
            for j in range(NJ):
                nc.tensor.matmul(K.ps[:, 4 + j, :], wg, K.h[:, toks(j)], start=True, stop=True)\
                    .then_inc(st.gate_ready, 1)
            for j in range(NJ):
                pe.wait_ge(st.gated, j + 1)
                nc.tensor.matmul(K.ps[:, j, :], wo, ret[:, toks(j)], start=True, stop=True).then_inc(st.out_ready, 1)

        @block.scalar
        def _(act):
            nc.scalar.preload_act_table_set("natural_log_exp_and_others")
            outer.act(act, 0)
            for j in range(NJ):
                act.wait_ge(st.v_ready, j + 1)
                nc.scalar.activation(vt[:, toks(j)], K.ps[:, 4 + j, :], ACT.Copy).then_inc(st.v_copied, 1)
            for j in range(NJ):
                act.wait_ge(st.q_ready, j + 1)
                nc.scalar.activation(qf[:, toks(j)], K.ps[:, j, :], ACT.Copy).then_inc(st.q_copied, 1)
            for j in range(NJ):
                act.wait_ge(st.gate_ready, j + 1)
                nc.scalar.activation(gate[:, toks(j)], K.ps[:, 4 + j, :], ACT.Relu).then_inc(st.gate_done, 1)
            act.wait_ge(st.mean_var, SEQS)
            nc.scalar.activation(co[:, 0, :], mv[:, :, 1], ACT.Ln, bias=K.eps_gn).then_inc(st.gn_log, 1)
            act.wait_ge(st.gn_log, 1)
            nc.scalar.activation(co[:, 0, :], co[:, 0, :], ACT.Exp, scale=-0.5).then_inc(st.gn_rstd, 1)
            act.wait_ge(st.shift_b, 2)
            for s in range(SEQS):
                act.wait_ge(st.gate_done, s // SPW + 1)
                seq = toks(s, LEN)
                nc.scalar.activation(ret[:, seq], ret[:, seq], ACT.Identity, scale=co[:, 1, s:s + 1],
                                     bias=co[:, 2, s:s + 1]).then_inc(st.gn_done, 1)

        @block.vector
        def _(dve):
            outer.dve(dve, 0, K.x, K.h)
            for j in range(NJ):
                dve.wait_ge(st.k_ready, j + 1)
                for t in range(TPW):
                    v = nc.vector.tensor_scalar(kt[:, toks(TPW * j + t, P)], K.ps[:, j, toks(t, P)],
                                                K.gamma_col[:, t % 2:t % 2 + 1], None, ALU.mult)
                v.then_inc(st.k_decayed, 1)
            for j in range(NJ):
                dve.wait_ge(st.ctx_ready, j + 1)
                nc.vector.tensor_copy(ctx[:, SPW * j:SPW * (j + 1), :].rearrange("p s n -> p (s n)"),
                                      K.ps[:, 4 + j, 0:SPW * P]).then_inc(st.ctx_copied, 1)
            for j in range(NJ):
                dve.wait_ge(st.ret_ready, j + 1)
                seqs = lambda ap: ap.rearrange("p (s n) -> p s n", n=LEN)
                nc.vector.tensor_tensor(seqs(ret[:, toks(j)]), seqs(K.ps[:, j, :]),
                                        K.gamma_row.unsqueeze(1).to_broadcast([P, SPW, LEN]), ALU.mult)\
                    .then_inc(st.ret_decayed, 1)
            for s in range(SEQS):
                dve.wait_ge(st.ret_decayed, s // SPW + 1)
                nc.vector.bn_stats(bn[:, s, :], ret[:, toks(s, LEN)]).then_inc(st.stats, 1)
            for s in range(SEQS):
                dve.wait_ge(st.stats, s + 1)
                nc.vector.bn_aggr(mv[:, s, :], bn[:, s, :]).then_inc(st.mean_var, 1)
            dve.wait_ge(st.w_ready, 16)
            dve.wait_ge(st.gn_rstd, 1)
            nc.vector.tensor_scalar(co[:, 1, :], co[:, 0, :], gn_g, None, ALU.mult).then_inc(st.shift_a, 1)
            dve.wait_ge(st.shift_a, 1)
            dve.wait_ge(st.mean_var, SEQS)
            nc.vector.tensor_tensor(co[:, 2, :], mv[:, :, 0], co[:, 1, :], ALU.mult).then_inc(st.shift_b, 1)
            dve.wait_ge(st.shift_b, 1)
            nc.vector.tensor_scalar(co[:, 2, :], co[:, 2, :], -1.0, gn_b, ALU.mult, ALU.add).then_inc(st.shift_b, 1)
            for j in range(NJ):
                dve.wait_ge(st.gn_done, SPW * (j + 1))
                nc.vector.tensor_tensor(ret[:, toks(j)], ret[:, toks(j)], gate[:, toks(j)], ALU.mult)\
                    .then_inc(st.gated, 1)
            for j in range(NJ):
                dve.wait_ge(st.out_ready, j + 1)
                nc.vector.tensor_tensor(K.x[:, toks(j)], K.x[:, toks(j)], K.ps[:, j, :], ALU.add)\
                    .then_inc(st.x_done, 1)
    st.end()


def gated_delta_stage(K):
    nc = K.nc
    H, KD, VD, CC, PAD = 4, 32, 64, 2, 3
    NT = TOK // P
    NH = NT * H
    LEVELS = 7
    st = Stage(nc, "delta")
    (st.w_ready, st.c_ready, st.rms_sq, st.rms_ready, st.rms_log, st.rms_rstd, st.h_ready,
     st.in_ready, st.x_in, st.edge, st.conv, st.conved, st.silu_done, st.l2_sq, st.l2_ready,
     st.l2_log, st.l2_rstd, st.l2_done, st.ab_ready, st.ab_copied, st.sp_in, st.sp_n, st.sp_abs,
     st.sp_e, st.sp_d, st.sp_r, st.sp_s, st.sp_z, st.sp_h, st.sp_done, st.ea, st.beta_done,
     st.g_done, st.csum_ready, st.decay_exp, st.beta_decay, st.v_turned, st.v_done, st.k_turned,
     st.k_done, st.rep_done, st.bb_ready, st.kb_done, st.gb_ready, st.gb_exp, st.qg_done,
     st.copies, st.small, st.gl_done, st.lg_ready, st.kk_ready, st.gam_exp, st.gam_masked,
     st.nt_done, st.pt_done, st.bm_done, st.y_ready, st.y_copied, st.xx_ready, st.x_new,
     st.xt_ready, st.xt_new, st.d_ready, st.d_copied, st.s_ready, st.s_done, st.ks_ready,
     st.ks_decay, st.r_done, st.o_ready, st.o_copied, st.on_sq, st.on_ready, st.on_log,
     st.on_rstd, st.on_done, st.gate_ready, st.gate_done, st.gated, st.enc_ready, st.y_enc,
     st.w2_ready, st.gelu, st.x_sum, st.x_done) = st.signals(
        "w_ready c_ready rms_sq rms_ready rms_log rms_rstd h_ready in_ready x_in edge conv conved "
        "silu_done l2_sq l2_ready l2_log l2_rstd l2_done ab_ready ab_copied sp_in sp_n sp_abs sp_e "
        "sp_d sp_r sp_s sp_z sp_h sp_done ea beta_done g_done csum_ready decay_exp beta_decay "
        "v_turned v_done k_turned k_done rep_done bb_ready kb_done gb_ready gb_exp qg_done copies "
        "small gl_done lg_ready kk_ready gam_exp gam_masked nt_done pt_done bm_done y_ready "
        "y_copied xx_ready x_new xt_ready xt_new d_ready d_copied s_ready s_done ks_ready ks_decay "
        "r_done o_ready o_copied on_sq on_ready on_log on_rstd on_done gate_ready gate_done gated "
        "enc_ready y_enc w2_ready gelu x_sum x_done")
    outer = LayerNorm(K, st, "outer_")
    inner = LayerNorm(K, st, "inner_", affine=True)
    wt = st.sb("wt", [P, K.d["delta_w"].shape[1]])
    ct = st.sb("ct", [P, K.d["delta_c"].shape[1]])
    w_in = [wt[:, toks(i, P)] for i in range(4)]
    wg = [wt[:, toks(4 + i, P)] for i in range(2)]
    wo = [wt[:, toks(6 + i, P)] for i in range(2)]
    w2 = wt[:, toks(8, P)]
    o = 9 * P
    wab, dtb, alog = wt[:, o:o + 8], wt[:, o + 8:o + 12], wt[:, o + 12:o + 16]
    o += 16
    conv_w = [[wt[:, o + 4 * c + k:o + 4 * c + k + 1] for k in range(4)] for c in range(4)]
    o += 16
    ln1g, ln1b, ln2g, ln2b, rms_w, b2, onw = (wt[:, o + i:o + i + 1] for i in range(7))
    upto, after = ct[:, 0:P], ct[:, P:2 * P]
    level_mask = [ct[:, toks(2 + i, P)] for i in range(LEVELS)]
    head32 = ct[:, toks(9, P)]
    s_mask = ct[:, 10 * P:12 * P]

    y, h = K.y, K.h
    qf, kf, kb, qg = (st.sb(n, [P, TOK]) for n in ("qf", "kf", "kb", "qg"))
    xi = [st.sb(f"xi{i}", [P, SEQS, LEN + PAD]) for i in range(2)]
    o_f = st.sb("o_f", [P, CC, TOK])
    v_tm = st.sb("v_tm", [P, NT, H * VD])
    k_tm = st.sb("k_tm", [P, NT, P])
    sm = st.sb("sm", [P, 12, NH])
    ea = st.sb("ea", [P, H])
    z_, n_, e_, d_, s_, hh, g, beta, eg, er, bg, _ = (sm[:, i, :] for i in range(12))
    ab2 = st.sb("ab2", [P, NT, 8])
    rep_b, rep_g = K.ln_xc, K.ln_sq
    ks, kbs, qs = (st.sb(n, [P, LEN]) for n in ("ks", "kbs", "qs"))
    kts = st.sb("kts", [P, P])
    small = st.sb("small", [P, 2, 2, H])
    gl = st.sb("gl", [P, 2, H, P])
    gam, nt, pt, xm, xt, ym = (st.sb(n, [P, 2, H, P]) for n in ("gam", "nt", "pt", "xm", "xt", "ym"))
    bm = st.sb("bm", [P, 2, 2, H, P])
    dl = st.sb("dl", [P, 2, H * VD])
    state = st.sb("state", [P, H * VD])
    ksd, rr = st.sb("ksd", [P, H * VD]), st.sb("rr", [P, H * VD])
    seqs = lambda ap: ap.rearrange("p (s n) -> p s n", n=LEN)
    heads = lambda ap: ap.unsqueeze(1).to_broadcast([P, H, P])
    hv = lambda ap: ap.rearrange("p (h v) -> p h v", h=H)
    bank4 = lambda ap: ap.rearrange("p (h n) -> p h n", h=H)
    tile_h = lambda ap: ap.rearrange("p (n h) -> p n h", h=H)
    cv = [qf[:, :], kf[:, :], o_f[:, 0, :], o_f[:, 1, :]]

    with nc.Block() as block:
        @block.sync
        def _(sp):
            sp.dma_start(wt[:, :], K.d["delta_w"]).then_inc(st.w_ready, 16)
            sp.dma_start(ct[:, :], K.d["delta_c"]).then_inc(st.c_ready, 16)

        @block.tensor
        def _(pe):
            outer.pe(pe, 0, K.x, lambda j: None)
            inner.pe(pe, 0, y, lambda j: pe.wait_ge(outer.norm_ready, at(0, j)))
            for j in range(NJ):
                pe.wait_ge(st.rms_sq, j + 1)
                nc.tensor.matmul(K.ps[:, j, :], K.mean_mat, K.ln_sq[:, toks(j)], start=True, stop=True)\
                    .then_inc(st.rms_ready, 1)
            pe.wait_ge(st.w_ready, 16)
            pe.wait_ge(st.c_ready, 16)
            for i in range(4):
                for j in range(NJ):
                    if i == 0:
                        pe.wait_ge(st.h_ready, j + 1)
                    if i >= 2:
                        pe.wait_ge(st.x_in, at(i - 2, j))
                    if i == 1:
                        pe.wait_ge(st.rms_log, NJ)
                    nc.tensor.matmul(K.ps[:, 4 * ((i + 1) % 2) + j, :], w_in[i], h[:, toks(j)], start=True, stop=True)\
                        .then_inc(st.in_ready, 1)
            pe.wait_ge(st.x_in, 4 * NJ)
            for n in range(NT):
                mm = nc.tensor.matmul(K.ps[:, 7, 8 * n:8 * n + 8], h[:, toks(n, P)], wab, start=True, stop=True)
            mm.then_inc(st.ab_ready, 1)
            for i in range(2):
                for j in range(NJ):
                    pe.wait_ge(st.l2_sq, at(i, j))
                    if i == 1:
                        pe.wait_ge(st.l2_log, j + 1)
                    nc.tensor.matmul(K.ps[:, j, :], head32, (K.ln_xc, K.ln_sq)[i][:, toks(j)], start=True, stop=True)\
                        .then_inc(st.l2_ready, 1)
            pe.wait_ge(st.g_done, 1)
            nc.tensor.matmul(K.ps[:, 4, 0:NH], upto, g, start=True, stop=True)
            nc.tensor.matmul(K.ps[:, 4, NH:2 * NH], after, g, start=True, stop=True).then_inc(st.csum_ready, 1)
            for m in range(NT // 2):
                pe.wait_ge(st.silu_done, 4)
                if m >= 2:
                    pe.wait_ge(st.v_done, m - 1)
                for n in range(2 * m, 2 * m + 2):
                    for c in range(CC):
                        mm = nc.tensor.transpose(K.ps[:, 5 + m % 2, toks(2 * (n % 2) + c, P)], o_f[:, c, toks(n, P)],
                                                 K.ident)
                mm.then_inc(st.v_turned, 1)
            for j in range(NJ):
                pe.wait_ge(st.l2_done, at(1, j))
                pe.wait_ge(st.l2_log, 2 * NJ)
                for t in range(TPW):
                    mm = nc.tensor.transpose(K.ps[:, j, toks(t, P)], kf[:, toks(TPW * j + t, P)], K.ident)
                mm.then_inc(st.k_turned, 1)
            for j in range(NJ):
                pe.wait_ge(st.rep_done, 2)
                pe.wait_ge(st.k_done, j + 1)
                for t in range(TPW):
                    mm = nc.tensor.transpose(K.ps[:, j, toks(t, P)], rep_b[:, toks(TPW * j + t, P)], K.ident)
                mm.then_inc(st.bb_ready, 1)
            for j in range(NJ):
                pe.wait_ge(st.decay_exp, 1)
                pe.wait_ge(st.v_done, NT // 2)
                for t in range(TPW):
                    mm = nc.tensor.matmul(K.ps[:, 4 + j, toks(t, P)], rep_g[:, toks(TPW * j + t, P)], upto,
                                          start=True, stop=True)
                mm.then_inc(st.gb_ready, 1)
            pe.wait_ge(st.gb_exp, NJ)
            pe.wait_ge(st.kb_done, NJ)
            pe.wait_ge(st.qg_done, NJ)
            with pe.Fori(0, SEQS) as b:
                for u in range(2):
                    pe.wait_ge(st.gl_done, b * 2 + (u + 1))
                    for i in range(H):
                        mm = nc.tensor.matmul(K.ps[:, u, toks(i, P)], gl[:, u, i, :], upto, start=True, stop=True)
                    mm.then_inc(st.lg_ready, 1)
                pe.wait_ge(st.copies, b + 1)
                for u in range(2):
                    for a in range(2):
                        for i in range(H):
                            rows = slice(KD * i, KD * i + KD)
                            mm = nc.tensor.matmul(K.ps[:, 4 + i, toks(2 * u + a, P)], ks[rows, toks(u, P)],
                                                  (kbs, qs)[a][rows, toks(u, P)], start=True, stop=True)
                            if u == 1 and a == 1:
                                mm.then_inc(st.kk_ready, 1)
                for lv in range(LEVELS):
                    for u in range(2):
                        pe.wait_ge(st.bm_done, b * (2 * LEVELS) + (2 * lv + u + 1))
                        if lv == 0:
                            pe.wait_ge(st.gam_exp, b * 2 + (u + 1))
                        else:
                            pe.wait_ge(st.x_new, b * (2 * LEVELS - 2) + (2 * (lv - 1) + u + 1))
                        for i in range(H):
                            mm = nc.tensor.matmul(K.ps[:, u, toks(i, P)], bm[:, lv % 2, u, i, :],
                                                  K.ident if lv == 0 else xm[:, u, i, :], start=True, stop=True)
                        mm.then_inc(st.y_ready, 1)
                    if lv == 0:
                        continue
                    for u in range(2):
                        pe.wait_ge(st.y_copied, b * (2 * LEVELS - 2) + (2 * (lv - 1) + u + 1))
                        pe.wait_ge(st.xt_new, b * (2 * LEVELS) + (2 * (lv - 1) + u + 1))
                        if lv == 1:
                            pe.wait_ge(st.pt_done, b * 2 + 2)
                        for i in range(H):
                            mm = nc.tensor.matmul(K.ps[:, 4 + u, toks(i, P)], ym[:, u, i, :], xt[:, u, i, :],
                                                  start=True, stop=True)
                        mm.then_inc(st.xt_ready, 1)
                        if lv < LEVELS - 1:
                            for i in range(H):
                                mm = nc.tensor.matmul(K.ps[:, 2 + u, toks(i, P)], xt[:, u, i, :], ym[:, u, i, :],
                                                      start=True, stop=True)
                            mm.then_inc(st.xx_ready, 1)
                pe.wait_ge(st.xt_new, b * (2 * LEVELS) + 2 * LEVELS)
                for i in range(H):
                    mm = nc.tensor.matmul(K.ps[:, 6, i * VD:(i + 1) * VD], xt[:, 0, i, :],
                                          v_tm[:, bass.ds(b * 2, 1), i * VD:(i + 1) * VD].rearrange("p a v -> p (a v)"),
                                          start=True, stop=True)
                mm.then_inc(st.d_ready, 1)
                pe.wait_ge(st.d_copied, b * 2 + 1)
                nc.tensor.matmul(K.ps[:, 7, 0:H * VD], kts[:, :], dl[:, 0, :], start=True, stop=True)\
                    .then_inc(st.s_ready, 1)
                for i in range(H):
                    mm = nc.tensor.matmul(K.ps[VD * (i % 2):VD * (i % 2) + VD, 2, toks(i // 2, P)],
                                          dl[:, 0, i * VD:(i + 1) * VD], pt[:, 0, i, :], start=True, stop=True)
                mm.then_inc(st.o_ready, 1)
                pe.wait_ge(st.s_done, b + 1)
                nc.tensor.matmul(K.ps[:, 0, 0:H * VD], ks[:, P:2 * P], state[:, :], start=True, stop=True)\
                    .then_inc(st.ks_ready, 1)
                pe.wait_ge(st.r_done, b + 1)
                for i in range(H):
                    mm = nc.tensor.matmul(K.ps[:, 1, i * VD:(i + 1) * VD], xt[:, 1, i, :], rr[:, i * VD:(i + 1) * VD],
                                          start=True, stop=True)
                mm.then_inc(st.d_ready, 1)
                pe.wait_ge(st.d_copied, b * 2 + 2)
                for c in range(CC):
                    nc.tensor.matmul(K.ps[:, 3, toks(c, P)], state[:, toks(c, P)], qg[:, bass.ds(b * LEN + P, P)],
                                     start=True, stop=False)
                    for i in (2 * c, 2 * c + 1):
                        mm = nc.tensor.matmul(K.ps[VD * (i % 2):VD * (i % 2) + VD, 3, toks(c, P)],
                                              dl[:, 1, i * VD:(i + 1) * VD], pt[:, 1, i, :], start=False, stop=True)
                mm.then_inc(st.o_ready, 1)
            pe.wait_ge(st.o_copied, 2 * SEQS)
            for c in range(CC):
                for j in range(NJ):
                    pe.wait_ge(st.on_sq, at(c, j))
                    nc.tensor.matmul(K.ps[:, 4 * c + j, :], K.half_ones, (K.ln_xc, K.ln_sq)[c][:, toks(j)],
                                     start=True, stop=True).then_inc(st.on_ready, 1)
            for c in range(CC):
                for j in range(NJ):
                    pe.wait_ge(st.on_log, at(c, j))
                    nc.tensor.matmul(K.ps[:, 4 * c + j, :], wg[c], h[:, toks(j)], start=True, stop=True)\
                        .then_inc(st.gate_ready, 1)
            for j in range(NJ):
                pe.wait_ge(st.gated, at(1, j))
                pe.wait_ge(st.gate_done, 2 * NJ)
                for c in range(CC):
                    mm = nc.tensor.matmul(K.ps[:, j, :], wo[c], o_f[:, c, toks(j)], start=(c == 0), stop=(c == 1))
                mm.then_inc(st.enc_ready, 1)
            inner.pe(pe, 1, y, lambda j: pe.wait_ge(st.y_enc, j + 1))
            for j in range(NJ):
                pe.wait_ge(inner.norm_ready, at(1, j))
                nc.tensor.matmul(K.ps[:, j, :], w2, h[:, toks(j)], start=True, stop=True).then_inc(st.w2_ready, 1)

        @block.scalar
        def _(act):
            nc.scalar.preload_act_table_set("natural_log_exp_and_others")
            outer.act(act, 0)
            act.wait_ge(st.w_ready, 16)
            inner.act(act, 0)
            for j in range(NJ):
                act.wait_ge(inner.norm_ready, at(0, j))
                nc.scalar.activation(K.ln_sq[:, toks(j)], h[:, toks(j)], ACT.Square).then_inc(st.rms_sq, 1)
            for j in range(NJ):
                act.wait_ge(st.rms_ready, j + 1)
                nc.scalar.activation(K.ln_sq[:, toks(j)], K.ps[:, j, :], ACT.Ln, bias=K.eps_rms).then_inc(st.rms_log, 1)
            for j in range(NJ):
                act.wait_ge(st.rms_log, j + 1)
                nc.scalar.activation(K.ln_sq[:, toks(j)], K.ln_sq[:, toks(j)], ACT.Exp, scale=-0.5)\
                    .then_inc(st.rms_rstd, 1)
            nc.scalar.activation(ea[:, :], alog, ACT.Exp).then_inc(st.ea, 1)
            act.wait_ge(st.edge, 1)
            for i in range(4):
                for j in range(NJ):
                    act.wait_ge(st.in_ready, at(i, j))
                    if i >= 2:
                        act.wait_ge(st.conved, i - 1)
                    nc.scalar.activation(xi[i % 2][:, SPW * j:SPW * (j + 1), PAD:],
                                         seqs(K.ps[:, 4 * ((i + 1) % 2) + j, :]), ACT.Copy).then_inc(st.x_in, 1)
            for i in range(4):
                act.wait_ge(st.conved, i + 1)
                nc.scalar.activation(cv[i], cv[i], ACT.Silu).then_inc(st.silu_done, 1)
            act.wait_ge(st.ab_copied, 1)
            nc.scalar.activation(tile_h(beta), ab2[:, :, 4:8], ACT.Sigmoid).then_inc(st.beta_done, 1)
            act.wait_ge(st.h_ready, NJ)
            for i in range(2):
                for j in range(NJ):
                    act.wait_ge(st.silu_done, i + 1)
                    nc.scalar.activation((K.ln_xc, K.ln_sq)[i][:, toks(j)], cv[i][:, toks(j)], ACT.Square)\
                        .then_inc(st.l2_sq, 1)
            for i in range(2):
                for j in range(NJ):
                    act.wait_ge(st.l2_ready, at(i, j))
                    nc.scalar.activation((K.ln_xc, K.ln_sq)[i][:, toks(j)], K.ps[:, j, :], ACT.Ln, bias=K.eps_rms)\
                        .then_inc(st.l2_log, 1)
            for i in range(2):
                for j in range(NJ):
                    act.wait_ge(st.l2_log, at(i, j))
                    r = (K.ln_xc, K.ln_sq)[i][:, toks(j)]
                    nc.scalar.activation(r, r, ACT.Exp, scale=-0.5).then_inc(st.l2_rstd, 1)
            act.wait_ge(st.sp_abs, 1)
            nc.scalar.activation(e_, e_, ACT.Exp, scale=-1.0).then_inc(st.sp_e, 1)
            act.wait_ge(st.csum_ready, 1)
            nc.scalar.activation(sm[:, 8:10, :].rearrange("p a n -> p (a n)"), K.ps[:, 4, 0:2 * NH], ACT.Exp)\
                .then_inc(st.decay_exp, 1)
            for j in range(NJ):
                act.wait_ge(st.gb_ready, j + 1)
                nc.scalar.activation(qg[:, toks(j)], K.ps[:, 4 + j, :], ACT.Exp).then_inc(st.gb_exp, 1)
            act.wait_ge(st.kb_done, NJ)
            act.wait_ge(st.k_done, NJ)
            act.wait_ge(st.l2_done, 2 * NJ)
            with act.Fori(0, SEQS) as b:
                seq = bass.ds(b * LEN, LEN)
                nc.scalar.activation(ks[:, :], kf[:, seq], ACT.Copy)
                nc.scalar.activation(kbs[:, :], kb[:, seq], ACT.Copy)
                nc.scalar.activation(qs[:, :], qf[:, seq], ACT.Copy)
                nc.scalar.activation(kts[:, :], k_tm[:, bass.ds(b * 2, 1), :].rearrange("p a n -> p (a n)"), ACT.Copy)\
                    .then_inc(st.copies, 1)
                for u in range(2):
                    act.wait_ge(st.lg_ready, b * 2 + (u + 1))
                    nc.scalar.activation(gam[:, u], bank4(K.ps[:, u, :]), ACT.Exp).then_inc(st.gam_exp, 1)
                for lv in range(1, LEVELS):
                    for u in range(2):
                        act.wait_ge(st.y_ready, b * (2 * LEVELS) + (2 * lv + u + 1))
                        nc.scalar.activation(ym[:, u], bank4(K.ps[:, u, :]), ACT.Copy).then_inc(st.y_copied, 1)
                for u in range(2):
                    act.wait_ge(st.d_ready, b * 2 + (u + 1))
                    nc.scalar.activation(dl[:, u, :], K.ps[:, (6, 1)[u], 0:H * VD], ACT.Copy).then_inc(st.d_copied, 1)
                for u in range(2):
                    act.wait_ge(st.o_ready, b * 2 + (u + 1))
                    nc.scalar.activation(o_f[:, :, bass.ds(b * LEN + u * P, P)],
                                         K.ps[:, 2 + u, 0:CC * P].rearrange("p (c n) -> p c n", c=CC), ACT.Copy)\
                        .then_inc(st.o_copied, 1)
            act.wait_ge(st.o_copied, 2 * SEQS)
            for c in range(CC):
                for j in range(NJ):
                    nc.scalar.activation((K.ln_xc, K.ln_sq)[c][:, toks(j)], o_f[:, c, toks(j)], ACT.Square)\
                        .then_inc(st.on_sq, 1)
            for c in range(CC):
                for j in range(NJ):
                    act.wait_ge(st.on_ready, at(c, j))
                    nc.scalar.activation((K.ln_xc, K.ln_sq)[c][:, toks(j)], K.ps[:, 4 * c + j, :], ACT.Ln,
                                         scale=1.0 / VD, bias=K.eps_rms).then_inc(st.on_log, 1)
            for c in range(CC):
                for j in range(NJ):
                    act.wait_ge(st.on_log, at(c, j))
                    r = (K.ln_xc, K.ln_sq)[c][:, toks(j)]
                    nc.scalar.activation(r, r, ACT.Exp, scale=-0.5).then_inc(st.on_rstd, 1)
            for c in range(CC):
                for j in range(NJ):
                    act.wait_ge(st.gate_ready, at(c, j))
                    nc.scalar.activation((kb, qg)[c][:, toks(j)], K.ps[:, 4 * c + j, :], ACT.Silu)\
                        .then_inc(st.gate_done, 1)
            act.wait_ge(st.on_done, 2 * NJ)
            inner.act(act, 1)
            for j in range(NJ):
                act.wait_ge(st.w2_ready, j + 1)
                nc.scalar.activation(kf[:, toks(j)], K.ps[:, j, :], ACT.Gelu, bias=b2).then_inc(st.gelu, 1)

        @block.gpsimd
        def _(pool):
            for i in range(2):
                p = nc.gpsimd.memset(xi[i][:, :, 0:PAD], 0.0)
            p.then_inc(st.edge, 1)
            pool.wait_ge(st.c_ready, 16)
            with pool.Fori(0, SEQS) as b:
                for u in range(2):
                    pool.wait_ge(st.small, b + 1)
                    nc.gpsimd.tensor_tensor(gl[:, u], heads(after), small[:, 0, u, :].unsqueeze(2).to_broadcast([P, H, P]),
                                            ALU.mult).then_inc(st.gl_done, 1)
                for u in range(2):
                    pool.wait_ge(st.gam_exp, b * 2 + (u + 1))
                    nc.gpsimd.tensor_tensor(gam[:, u], gam[:, u], heads(upto), ALU.mult).then_inc(st.gam_masked, 1)
                for lv in range(LEVELS):
                    for u in range(2):
                        pool.wait_ge(st.nt_done, b * 2 + (u + 1))
                        if lv >= 2:
                            pool.wait_ge(st.y_ready, b * (2 * LEVELS) + (2 * (lv - 2) + u + 1))
                        if lv == 2:
                            pool.wait_ge(st.xt_new, b * (2 * LEVELS) + (u + 1))
                        nc.gpsimd.tensor_tensor(bm[:, lv % 2, u], nt[:, u], heads(level_mask[lv]), ALU.mult)\
                            .then_inc(st.bm_done, 1)

        @block.vector
        def _(dve):
            outer.dve(dve, 0, K.x, y)
            for j in range(NJ):
                dve.wait_ge(outer.norm_ready, at(0, j))
            dve.wait_ge(st.w_ready, 16)
            inner.dve(dve, 0, y, h, ln1g, ln1b)
            for j in range(NJ):
                dve.wait_ge(st.rms_rstd, j + 1)
                nc.vector.scalar_tensor_tensor(h[:, toks(j)], h[:, toks(j)], rms_w, K.ln_sq[:, toks(j)],
                                               ALU.mult, ALU.mult).then_inc(st.h_ready, 1)
            for i in range(4):
                dve.wait_ge(st.x_in, at(i, NJ - 1))
                dve.wait_ge(st.edge, 1)
                nc.vector.tensor_scalar(seqs(cv[i]), xi[i % 2][:, :, 3:3 + LEN], conv_w[i][3], None, ALU.mult)\
                    .then_inc(st.conv, 1)
                for k in (2, 1, 0):
                    dve.wait_ge(st.conv, 3 * i + 3 - k)
                    nc.vector.scalar_tensor_tensor(seqs(cv[i]), xi[i % 2][:, :, k:k + LEN], conv_w[i][k], seqs(cv[i]),
                                                   ALU.mult, ALU.add).then_inc(st.conved if k == 0 else st.conv, 1)
            dve.wait_ge(st.ab_ready, 1)
            nc.vector.tensor_copy(ab2[:, :, :], K.ps[:, 7, 0:8 * NT].rearrange("p (n a) -> p n a", a=8))\
                .then_inc(st.ab_copied, 1)
            dve.wait_ge(st.ab_copied, 1)
            nc.vector.tensor_tensor(tile_h(z_), ab2[:, :, 0:4], dtb.unsqueeze(1).to_broadcast([P, NT, H]), ALU.add)\
                .then_inc(st.sp_in, 1)
            dve.wait_ge(st.sp_in, 1)
            nc.vector.tensor_scalar(n_, z_, -1.0, None, ALU.mult).then_inc(st.sp_n, 1)
            dve.wait_ge(st.sp_n, 1)
            nc.vector.tensor_tensor(e_, z_, n_, ALU.max).then_inc(st.sp_abs, 1)
            dve.wait_ge(st.sp_e, 1)
            nc.vector.tensor_scalar(d_, e_, 2.0, None, ALU.add).then_inc(st.sp_d, 1)
            dve.wait_ge(st.sp_d, 1)
            nc.vector.reciprocal(d_, d_).then_inc(st.sp_r, 1)
            dve.wait_ge(st.sp_r, 1)
            nc.vector.tensor_tensor(s_, e_, d_, ALU.mult).then_inc(st.sp_s, 1)
            dve.wait_ge(st.sp_s, 1)
            nc.vector.tensor_tensor(d_, s_, s_, ALU.mult).then_inc(st.sp_z, 1)
            dve.wait_ge(st.sp_z, 1)
            nc.vector.tensor_scalar(hh, d_, ATANH[0], None, ALU.mult).then_inc(st.sp_h, 1)
            for n, cf in enumerate(ATANH[1:-1]):
                dve.wait_ge(st.sp_h, n + 1)
                nc.vector.scalar_tensor_tensor(hh, hh, cf, d_, ALU.add, ALU.mult).then_inc(st.sp_h, 1)
            n = len(ATANH) - 1
            dve.wait_ge(st.sp_h, n)
            nc.vector.scalar_tensor_tensor(hh, hh, ATANH[-1], s_, ALU.add, ALU.mult).then_inc(st.sp_h, 1)
            dve.wait_ge(st.sp_h, n + 1)
            nc.vector.scalar_tensor_tensor(z_, z_, 0.0, hh, ALU.max, ALU.add).then_inc(st.sp_done, 1)
            dve.wait_ge(st.sp_done, 1)
            dve.wait_ge(st.ea, 1)
            nc.vector.scalar_tensor_tensor(tile_h(g), tile_h(z_), -1.0, ea[:, :].unsqueeze(1).to_broadcast([P, NT, H]),
                                           ALU.mult, ALU.mult).then_inc(st.g_done, 1)
            for i in range(2):
                for j in range(NJ):
                    dve.wait_ge(st.l2_rstd, at(i, j))
                    nc.vector.scalar_tensor_tensor(cv[i][:, toks(j)], cv[i][:, toks(j)], (KD ** -0.5, 1.0)[i],
                                                   (K.ln_xc, K.ln_sq)[i][:, toks(j)], ALU.mult, ALU.mult)\
                        .then_inc(st.l2_done, 1)
            dve.wait_ge(st.decay_exp, 1)
            dve.wait_ge(st.beta_done, 1)
            nc.vector.tensor_tensor(bg, beta, eg, ALU.mult).then_inc(st.beta_decay, 1)
            for m in range(NT // 2):
                dve.wait_ge(st.v_turned, m + 1)
                nc.vector.tensor_tensor(v_tm[:, 2 * m:2 * m + 2, :].rearrange("p n (h v) -> p (n h) v", v=VD),
                                        K.ps[:, 5 + m % 2, :].rearrange("p (n v) -> p n v", v=VD),
                                        beta[:, 2 * H * m:2 * H * (m + 1)].unsqueeze(2).to_broadcast([P, 2 * H, VD]),
                                        ALU.mult).then_inc(st.v_done, 1)
            for j in range(NJ):
                dve.wait_ge(st.k_turned, j + 1)
                nc.vector.tensor_tensor(k_tm[:, TPW * j:TPW * (j + 1), :].rearrange("p n (h k) -> p (n h) k", k=KD),
                                        K.ps[:, j, :].rearrange("p (n k) -> p n k", k=KD),
                                        er[:, 16 * j:16 * (j + 1)].unsqueeze(2).to_broadcast([P, 16, KD]),
                                        ALU.mult).then_inc(st.k_done, 1)
            dve.wait_ge(st.l2_done, 2 * NJ)
            for rep, src in ((rep_b, beta), (rep_g, g)):
                nc.vector.tensor_copy(rep[:, :].rearrange("p (n k) -> p n k", k=KD),
                                      src.unsqueeze(2).to_broadcast([P, NH, KD])).then_inc(st.rep_done, 1)
            for j in range(NJ):
                dve.wait_ge(st.bb_ready, j + 1)
                nc.vector.tensor_tensor(kb[:, toks(j)], kf[:, toks(j)], K.ps[:, j, :], ALU.mult).then_inc(st.kb_done, 1)
            for j in range(NJ):
                dve.wait_ge(st.gb_exp, j + 1)
                nc.vector.tensor_tensor(qg[:, toks(j)], qg[:, toks(j)], qf[:, toks(j)], ALU.mult)\
                    .then_inc(st.qg_done, 1)
            dve.wait_ge(st.beta_decay, 1)
            dve.wait_ge(st.v_done, NT // 2)
            with dve.Fori(0, SEQS) as b:
                nc.vector.tensor_copy(small[:, 0].rearrange("p u h -> p (u h)"), g[:, bass.ds(b * (2 * H), 2 * H)])
                nc.vector.tensor_copy(small[:, 1].rearrange("p u h -> p (u h)"), bg[:, bass.ds(b * (2 * H), 2 * H)])\
                    .then_inc(st.small, 1)
                for u in range(2):
                    dve.wait_ge(st.kk_ready, b * H + H)
                    dve.wait_ge(st.gam_masked, b * 2 + (u + 1))
                    for a, dst, done in ((0, nt, st.nt_done), (1, pt, st.pt_done)):
                        nc.vector.tensor_tensor(dst[:, u], K.ps[:, 4:8, toks(2 * u + a, P)], gam[:, u], ALU.mult)\
                            .then_inc(done, 1)
                for u in range(2):
                    dve.wait_ge(st.bm_done, b * (2 * LEVELS) + (u + 1))
                    nc.vector.tensor_tensor(xt[:, u], heads(K.ident), bm[:, 0, u], ALU.subtract).then_inc(st.xt_new, 1)
                    dve.wait_ge(st.y_ready, b * (2 * LEVELS) + (u + 1))
                    nc.vector.tensor_tensor(xm[:, u], heads(K.ident), bank4(K.ps[:, u, :]), ALU.subtract)\
                        .then_inc(st.x_new, 1)
                for lv in range(1, LEVELS):
                    for u in range(2):
                        dve.wait_ge(st.xt_ready, b * (2 * LEVELS - 2) + (2 * (lv - 1) + u + 1))
                        dve.wait_ge(st.xt_new, b * (2 * LEVELS) + (2 * (lv - 1) + u + 1))
                        if lv < LEVELS - 1:
                            dve.wait_ge(st.xx_ready, b * (2 * LEVELS - 4) + (2 * (lv - 1) + u + 1))
                        nc.vector.tensor_tensor(xt[:, u], xt[:, u], bank4(K.ps[:, 4 + u, :]), ALU.subtract)\
                            .then_inc(st.xt_new, 1)
                        if lv < LEVELS - 1:
                            dve.wait_ge(st.x_new, b * (2 * LEVELS - 2) + (2 * (lv - 1) + u + 1))
                            nc.vector.tensor_tensor(xm[:, u], xm[:, u], bank4(K.ps[:, 2 + u, :]), ALU.subtract)\
                                .then_inc(st.x_new, 1)
                dve.wait_ge(st.s_ready, b + 1)
                nc.vector.tensor_tensor(state[:, :], K.ps[:, 7, 0:H * VD], s_mask, ALU.mult).then_inc(st.s_done, 1)
                dve.wait_ge(st.small, b + 1)
                dve.wait_ge(st.ks_ready, b + 1)
                nc.vector.tensor_tensor(hv(ksd[:, :]), hv(K.ps[:, 0, 0:H * VD]),
                                        small[:, 1, 1, :].unsqueeze(2).to_broadcast([P, H, VD]), ALU.mult)\
                    .then_inc(st.ks_decay, 1)
                dve.wait_ge(st.ks_decay, b + 1)
                nc.vector.tensor_tensor(rr[:, :], v_tm[:, bass.ds(b * 2 + 1, 1), :].rearrange("p a v -> p (a v)"),
                                        ksd[:, :], ALU.subtract).then_inc(st.r_done, 1)
            for c in range(CC):
                for j in range(NJ):
                    dve.wait_ge(st.on_rstd, at(c, j))
                    nc.vector.scalar_tensor_tensor(o_f[:, c, toks(j)], o_f[:, c, toks(j)], onw,
                                                   (K.ln_xc, K.ln_sq)[c][:, toks(j)], ALU.mult, ALU.mult)\
                        .then_inc(st.on_done, 1)
            for c in range(CC):
                for j in range(NJ):
                    dve.wait_ge(st.gate_done, at(c, j))
                    dve.wait_ge(st.on_done, at(c, j))
                    nc.vector.tensor_tensor(o_f[:, c, toks(j)], o_f[:, c, toks(j)], (kb, qg)[c][:, toks(j)], ALU.mult)\
                        .then_inc(st.gated, 1)
            for j in range(NJ):
                dve.wait_ge(st.enc_ready, j + 1)
                nc.vector.tensor_tensor(y[:, toks(j)], y[:, toks(j)], K.ps[:, j, :], ALU.add).then_inc(st.y_enc, 1)
            for j in range(NJ):
                dve.wait_ge(st.y_enc, j + 1)
                nc.vector.tensor_tensor(K.x[:, toks(j)], K.x[:, toks(j)], y[:, toks(j)], ALU.add).then_inc(st.x_sum, 1)
            inner.dve(dve, 1, y, h, ln2g, ln2b)
            for j in range(NJ):
                dve.wait_ge(st.gelu, j + 1)
                dve.wait_ge(st.x_sum, j + 1)
                nc.vector.tensor_tensor(K.x[:, toks(j)], K.x[:, toks(j)], kf[:, toks(j)], ALU.add)\
                    .then_inc(st.x_done, 1)
    st.end()


def lora_linear_stage(K, tag):
    nc = K.nc
    st = Stage(nc, f"lora{tag}")
    (st.w_ready, st.t1_ready, st.t1_copied, st.t2_ready, st.t2_copied, st.delta_ready,
     st.weff_ready, st.out_ready, st.x_done) = st.signals(
        "w_ready t1_ready t1_copied t2_ready t2_copied delta_ready weff_ready out_ready x_done")
    outer = LayerNorm(K, st, "outer_")
    wt = st.sb("wt", [P, K.d["lora_w"].shape[1]])
    w_t, down_t, down_aux, up_t, upaux_t, bias = (
        wt[:, 0:128], wt[0:100, 128:132], wt[0:100, 132:260], wt[0:4, 260:310], wt[0:50, 310:438], wt[:, 438:439])
    t1 = st.sb("t1", [4, P])
    t2 = st.sb("t2", [50, P])
    weff = st.sb("weff", [P, P])
    with nc.Block() as block:
        @block.sync
        def _(sp):
            sp.dma_start(wt[:, :], K.d["lora_w"]).then_inc(st.w_ready, 16)

        @block.tensor
        def _(pe):
            pe.wait_ge(st.w_ready, 16)
            outer.pe(pe, 0, K.x, lambda j: None)
            pe.wait_ge(outer.centered, at(0, NJ - 1))
            nc.tensor.matmul(K.ps[0:4, 0, 0:128], down_t, down_aux, start=True, stop=True).then_inc(st.t1_ready, 1)
            pe.wait_ge(st.t1_copied, 1)
            nc.tensor.matmul(K.ps[0:50, 1, 0:128], up_t, t1[:, :], start=True, stop=True).then_inc(st.t2_ready, 1)
            pe.wait_ge(st.t2_copied, 1)
            nc.tensor.matmul(K.ps[:, 2, 0:128], t2[:, :], upaux_t, start=True, stop=True).then_inc(st.delta_ready, 1)
            pe.wait_ge(st.weff_ready, 1)
            for j in range(NJ):
                pe.wait_ge(outer.norm_ready, at(0, j))
                nc.tensor.matmul(K.ps[:, j, :], weff[:, :], K.h[:, toks(j)], start=True, stop=True)\
                    .then_inc(st.out_ready, 1)

        @block.scalar
        def _(act):
            nc.scalar.preload_act_table_set("natural_log_exp_and_others")
            outer.act(act, 0)

        @block.vector
        def _(dve):
            outer.dve(dve, 0, K.x, K.h)
            dve.wait_ge(st.t1_ready, 1)
            nc.vector.tensor_copy(t1[:, :], K.ps[0:4, 0, 0:128]).then_inc(st.t1_copied, 1)
            dve.wait_ge(st.t2_ready, 1)
            nc.vector.tensor_copy(t2[:, :], K.ps[0:50, 1, 0:128]).then_inc(st.t2_copied, 1)
            dve.wait_ge(st.w_ready, 16)
            dve.wait_ge(st.delta_ready, 1)
            nc.vector.tensor_tensor(weff[:, :], K.ps[:, 2, 0:128], w_t, ALU.add).then_inc(st.weff_ready, 1)
            for j in range(NJ):
                dve.wait_ge(st.out_ready, j + 1)
                nc.vector.scalar_tensor_tensor(K.x[:, toks(j)], K.ps[:, j, :], bias, K.x[:, toks(j)],
                                               ALU.add, ALU.add).then_inc(st.x_done, 1)
    st.end()


def lora_linear_first(K):
    lora_linear_stage(K, 0)


def lora_linear_second(K):
    lora_linear_stage(K, 1)


def lstm_stage(K):
    nc = K.nc
    st = Stage(nc, "lstm")
    (st.w_ready, st.gates_ready, st.gates_done, st.tanh_done, st.c_part, st.c_new, st.c_tanh,
     st.h_ready) = st.signals(
        "w_ready gates_ready gates_done tanh_done c_part c_new c_tanh h_ready")
    outer = LayerNorm(K, st, "outer_")
    wt = st.sb("wt", [P, K.d["lstm_w"].shape[1]])
    w = [wt[:, toks(g, P)] for g in range(4)]
    u = [wt[:, 512 + P * g:512 + P * (g + 1)] for g in range(4)]
    bias = [wt[:, 1024 + g:1025 + g] for g in range(4)]
    gate = st.sb("gate", [P, 4, LEN])
    part = st.sb("part", [P, LEN])
    c = st.sb("c", [P, LEN])
    tc = st.sb("tc", [P, LEN])
    hs = st.sb("hs", [P, SEQS, LEN])
    with nc.Block() as block:
        @block.sync
        def _(sp):
            sp.dma_start(wt[:, :], K.d["lstm_w"]).then_inc(st.w_ready, 16)

        @block.tensor
        def _(pe):
            pe.wait_ge(st.w_ready, 16)
            outer.pe(pe, 0, K.x, lambda j: None)
            for s in range(SEQS):
                if s < 2:
                    pe.wait_ge(outer.log_ready, at(0, NJ - 1))
                else:
                    pe.wait_ge(st.gates_done, 4 * (s - 1))
                pe.wait_ge(outer.norm_ready, at(0, s // SPW))
                for g in range(4):
                    mm = nc.tensor.matmul(K.ps[:, 4 * (s % 2) + g, 0:LEN], w[g], K.h[:, toks(s, LEN)],
                                          start=True, stop=(s == 0))
                    if s == 0:
                        mm.then_inc(st.gates_ready, 1)
                if s > 0:
                    pe.wait_ge(st.h_ready, s)
                    for g in range(4):
                        nc.tensor.matmul(K.ps[:, 4 * (s % 2) + g, 0:LEN], u[g], hs[:, s - 1, :],
                                         start=False, stop=True).then_inc(st.gates_ready, 1)

        @block.scalar
        def _(act):
            nc.scalar.preload_act_table_set("natural_log_exp_and_others")
            outer.act(act, 0)
            act.wait_ge(st.w_ready, 16)
            for s in range(SEQS):
                for g, f in ((0, ACT.Sigmoid), (1, ACT.Sigmoid), (2, ACT.Sigmoid), (3, ACT.Tanh)):
                    act.wait_ge(st.gates_ready, 4 * s + g + 1)
                    if g == 0 and s > 0:
                        act.wait_ge(st.h_ready, s)
                    nc.scalar.activation(gate[:, g, :], K.ps[:, 4 * (s % 2) + g, 0:LEN], f, bias=bias[g])\
                        .then_inc(st.gates_done, 1)
                act.wait_ge(st.c_new, s + 1)
                nc.scalar.activation(tc[:, :], c[:, :], ACT.Tanh).then_inc(st.c_tanh, 1)

        @block.vector
        def _(dve):
            outer.dve(dve, 0, K.x, K.h)
            for s in range(SEQS):
                dve.wait_ge(st.gates_done, 4 * s + 4)
                if s == 0:
                    nc.vector.tensor_tensor(c[:, :], gate[:, 0, :], gate[:, 3, :], ALU.mult).then_inc(st.c_new, 1)
                else:
                    nc.vector.tensor_tensor(part[:, :], gate[:, 0, :], gate[:, 3, :], ALU.mult)\
                        .then_inc(st.c_part, 1)
                    nc.vector.tensor_tensor(c[:, :], gate[:, 1, :], c[:, :], ALU.mult).then_inc(st.c_part, 1)
                    dve.wait_ge(st.c_part, 2 * s)
                    nc.vector.tensor_tensor(c[:, :], c[:, :], part[:, :], ALU.add).then_inc(st.c_new, 1)
                dve.wait_ge(st.c_tanh, s + 1)
                nc.vector.tensor_tensor(hs[:, s, :], gate[:, 2, :], tc[:, :], ALU.mult).then_inc(st.h_ready, 1)
            dve.wait_ge(st.h_ready, SEQS)
            nc.vector.tensor_tensor(K.x[:, :], K.x[:, :], hs[:, :, :].rearrange("p s n -> p (s n)"), ALU.add)
    st.end()


TWO_PI_HI = float(np.float32(6.28125))
TWO_PI_LO = float(np.float32(2 * np.pi - 6.28125))
ROUND = float(1.5 * 2 ** 23)


def lru_stage(K):
    nc = K.nc
    st = Stage(nc, "lru")
    (st.w_ready, st.sp_e, st.sp_d, st.sp_r, st.sp_s, st.sp_z, st.sp_h, st.decay_col, st.xh_ready,
     st.xh_done, st.gate_ready, st.gate_done, st.xg, st.logr_done, st.r_done, st.e2, st.om,
     st.norm_log, st.norm_done, st.masked, st.theta, st.phi, st.turn0, st.turn1, st.turn2,
     st.turn3, st.half, st.sin_done, st.cos_sq, st.cos_done, st.xn, st.rot_a, st.rot_b, st.rot_c,
     st.rot_d, st.rotated, st.scanned, st.out_ready, st.x_done, st.hrot_done) = st.signals(
        "w_ready sp_e sp_d sp_r sp_s sp_z sp_h decay_col xh_ready xh_done gate_ready gate_done xg "
        "logr_done r_done e2 om norm_log norm_done masked theta phi turn0 turn1 turn2 turn3 half "
        "sin_done cos_sq cos_done xn rot_a rot_b rot_c rot_d rotated scanned out_ready x_done "
        "hrot_done")
    outer = LayerNorm(K, st, "outer_")
    wt = st.sb("wt", [P, K.d["lru_w"].shape[1]])
    win = [wt[:, 0:128], wt[:, 128:256]]
    gates_w = [[wt[:, 256 + 128 * (2 * g + c):384 + 128 * (2 * g + c)] for c in range(2)] for g in range(2)]
    wout = [wt[:, 768:896], wt[:, 896:1024]]
    b_in = [wt[:, 1024:1025], wt[:, 1025:1026]]
    b_gate = [wt[:, 1026:1027], wt[:, 1027:1028]]
    a_real, a_imag, b_out = wt[:, 1028:1029], wt[:, 1029:1030], wt[:, 1030:1031]
    col = st.sb("col", [P, 12])
    xh = st.sb("xh", [P, 2, TOK])
    gx = st.sb("gx", [P, TOK])
    ga = st.sb("ga", [P, TOK])
    r = st.sb("r", [P, TOK])
    nrm = st.sb("nrm", [P, TOK])
    ph = st.sb("ph", [P, TOK])
    tn = st.sb("tn", [P, TOK])
    sn = st.sb("sn", [P, TOK])
    cs = st.sb("cs", [P, TOK])
    seq = lambda ap: ap.rearrange("p (s n) -> p s n", n=LEN)
    e, d2, rc, s_, z, hh, sp_, decay, decay2 = (col[:, i:i + 1] for i in range(9))
    ta, tb = K.ln_xc, K.ln_sq
    with nc.Block() as block:
        @block.sync
        def _(sp):
            sp.dma_start(wt[:, :], K.d["lru_w"]).then_inc(st.w_ready, 16)

        @block.tensor
        def _(pe):
            outer.pe(pe, 0, K.x, lambda j: None)
            pe.wait_ge(st.w_ready, 16)
            for j in range(NJ):
                pe.wait_ge(outer.norm_ready, at(0, j))
                for c in range(2):
                    nc.tensor.matmul(K.ps[:, 4 * c + j, :], win[c], K.h[:, toks(j)], start=True, stop=True)\
                        .then_inc(st.xh_ready, 1)
            for j in range(NJ):
                pe.wait_ge(st.xh_done, 2 * j + 2)
                for g in range(2):
                    for c in range(2):
                        mm = nc.tensor.matmul(K.ps[:, 4 * g + j, :], gates_w[g][c], xh[:, c, toks(j)],
                                              start=(c == 0), stop=(c == 1))
                    mm.then_inc(st.gate_ready, 1)
            for j in range(NJ):
                pe.wait_ge(st.gate_done, 2 * j + 2)
                pe.wait_ge(st.hrot_done, 2)
                for c in range(2):
                    mm = nc.tensor.matmul(K.ps[:, j, :], wout[c], xh[:, c, toks(j)], start=(c == 0), stop=(c == 1))
                mm.then_inc(st.out_ready, 1)

        @block.scalar
        def _(act):
            nc.scalar.preload_act_table_set("natural_log_exp_and_others")
            outer.act(act, 0)
            act.wait_ge(st.w_ready, 16)
            act.wait_ge(st.sp_z, 1)
            nc.scalar.activation(e, z, ACT.Exp, scale=-1.0).then_inc(st.sp_e, 1)
            for j in range(NJ):
                for c in range(2):
                    act.wait_ge(st.xh_ready, 2 * j + c + 1)
                    nc.scalar.activation(xh[:, c, toks(j)], K.ps[:, 4 * c + j, :], ACT.Identity, bias=b_in[c])\
                        .then_inc(st.xh_done, 1)
            for j in range(NJ):
                for g in range(2):
                    act.wait_ge(st.gate_ready, 2 * j + g + 1)
                    nc.scalar.activation((gx, ga)[g][:, toks(j)], K.ps[:, 4 * g + j, :], ACT.Sigmoid, bias=b_gate[g])\
                        .then_inc(st.gate_done, 1)
            act.wait_ge(st.gate_done, 2 * NJ)
            act.wait_ge(st.decay_col, 2)
            nc.scalar.activation(r[:, :], ga[:, :], ACT.Exp, scale=decay).then_inc(st.r_done, 1)
            nc.scalar.activation(nrm[:, :], ga[:, :], ACT.Exp, scale=decay2).then_inc(st.e2, 1)
            act.wait_ge(st.om, 2)
            nc.scalar.activation(nrm[:, :], nrm[:, :], ACT.Ln).then_inc(st.norm_log, 1)
            act.wait_ge(st.norm_log, 1)
            nc.scalar.activation(nrm[:, :], nrm[:, :], ACT.Exp, scale=0.5).then_inc(st.norm_done, 1)
            act.wait_ge(st.turn3, 1)
            nc.scalar.activation(cs[:, :], ph[:, :], ACT.Sin, scale=0.5).then_inc(st.half, 1)
            nc.scalar.activation(sn[:, :], ph[:, :], ACT.Sin).then_inc(st.sin_done, 1)
            act.wait_ge(st.half, 1)
            nc.scalar.activation(cs[:, :], cs[:, :], ACT.Square).then_inc(st.cos_sq, 1)

        @block.vector
        def _(dve):
            dve.wait_ge(st.w_ready, 16)
            nc.vector.tensor_scalar(s_, a_real, -1.0, None, ALU.mult).then_inc(st.sp_s, 1)
            dve.wait_ge(st.sp_s, 1)
            nc.vector.tensor_tensor(z, a_real, s_, ALU.max).then_inc(st.sp_z, 1)
            outer.dve(dve, 0, K.x, K.h)
            dve.wait_ge(st.sp_e, 1)
            nc.vector.tensor_scalar(d2, e, 2.0, None, ALU.add).then_inc(st.sp_d, 1)
            dve.wait_ge(st.sp_d, 1)
            nc.vector.reciprocal(rc, d2).then_inc(st.sp_r, 1)
            dve.wait_ge(st.sp_r, 1)
            nc.vector.tensor_tensor(s_, e, rc, ALU.mult).then_inc(st.sp_s, 1)
            dve.wait_ge(st.sp_s, 2)
            nc.vector.tensor_tensor(z, s_, s_, ALU.mult).then_inc(st.sp_z, 1)
            dve.wait_ge(st.sp_z, 2)
            nc.vector.tensor_scalar(hh, z, ATANH[0], None, ALU.mult).then_inc(st.sp_h, 1)
            for n, cf in enumerate(ATANH[1:-1]):
                dve.wait_ge(st.sp_h, n + 1)
                nc.vector.scalar_tensor_tensor(hh, hh, cf, z, ALU.add, ALU.mult).then_inc(st.sp_h, 1)
            n = len(ATANH) - 1
            dve.wait_ge(st.sp_h, n)
            nc.vector.scalar_tensor_tensor(hh, hh, ATANH[-1], s_, ALU.add, ALU.mult).then_inc(st.sp_h, 1)
            dve.wait_ge(st.sp_h, n + 1)
            nc.vector.scalar_tensor_tensor(sp_, a_real, 0.0, hh, ALU.max, ALU.add).then_inc(st.sp_h, 1)
            dve.wait_ge(st.sp_h, n + 2)
            nc.vector.tensor_scalar(decay, sp_, -8.0, None, ALU.mult).then_inc(st.decay_col, 1)
            nc.vector.tensor_scalar(decay2, sp_, -16.0, None, ALU.mult).then_inc(st.decay_col, 1)
            dve.wait_ge(st.gate_done, 2 * NJ)
            nc.vector.tensor_scalar(tn[:, :], ga[:, :], a_imag, None, ALU.mult).then_inc(st.theta, 1)
            dve.wait_ge(st.theta, 1)
            for s in range(SEQS):
                nc.vector.tensor_tensor_scan(ph[:, toks(s, LEN)], K.one.to_broadcast([P, LEN]),
                                             tn[:, toks(s, LEN)], 0.0, ALU.mult, ALU.add).then_inc(st.phi, 1)
            dve.wait_ge(st.phi, SEQS)
            nc.vector.tensor_scalar(tn[:, :], ph[:, :], 1.0 / (2 * np.pi), ROUND, ALU.mult, ALU.add)\
                .then_inc(st.turn0, 1)
            dve.wait_ge(st.turn0, 1)
            nc.vector.tensor_scalar(tn[:, :], tn[:, :], ROUND, None, ALU.subtract).then_inc(st.turn1, 1)
            dve.wait_ge(st.turn1, 1)
            nc.vector.scalar_tensor_tensor(ph[:, :], tn[:, :], -TWO_PI_HI, ph[:, :], ALU.mult, ALU.add)\
                .then_inc(st.turn2, 1)
            dve.wait_ge(st.turn2, 1)
            nc.vector.scalar_tensor_tensor(ph[:, :], tn[:, :], -TWO_PI_LO, ph[:, :], ALU.mult, ALU.add)\
                .then_inc(st.turn2, 1)
            dve.wait_ge(st.turn2, 2)
            nc.vector.tensor_scalar(ph[:, :], ph[:, :], PI_IN, -PI_IN, ALU.min, ALU.max).then_inc(st.turn3, 1)
            dve.wait_ge(st.e2, 1)
            nc.vector.tensor_scalar(nrm[:, :], nrm[:, :], -1.0, 1.0, ALU.mult, ALU.add).then_inc(st.om, 1)
            dve.wait_ge(st.om, 1)
            nc.vector.tensor_scalar(nrm[:, :], nrm[:, :], 1e-6, None, ALU.max).then_inc(st.om, 1)
            dve.wait_ge(st.r_done, 1)
            nc.vector.memset(seq(r[:, :])[:, :, 0:1], 0.0).then_inc(st.masked, 1)
            dve.wait_ge(st.norm_done, 1)
            nc.vector.tensor_tensor(gx[:, :], gx[:, :], nrm[:, :], ALU.mult).then_inc(st.xg, 1)
            dve.wait_ge(st.xg, 1)
            for c in range(2):
                nc.vector.tensor_tensor(xh[:, c, :], xh[:, c, :], gx[:, :], ALU.mult).then_inc(st.xn, 1)
            dve.wait_ge(st.cos_sq, 1)
            nc.vector.tensor_scalar(cs[:, :], cs[:, :], -2.0, 1.0, ALU.mult, ALU.add).then_inc(st.cos_done, 1)
            dve.wait_ge(st.cos_done, 1)
            dve.wait_ge(st.sin_done, 1)
            dve.wait_ge(st.xn, 2)
            dve.wait_ge(outer.norm_ready, NJ)
            nc.vector.tensor_tensor(ta[:, :], cs[:, :], xh[:, 0, :], ALU.mult).then_inc(st.rot_a, 1)
            nc.vector.tensor_tensor(tb[:, :], sn[:, :], xh[:, 1, :], ALU.mult).then_inc(st.rot_b, 1)
            nc.vector.tensor_tensor(gx[:, :], cs[:, :], xh[:, 1, :], ALU.mult).then_inc(st.rot_c, 1)
            nc.vector.tensor_tensor(tn[:, :], sn[:, :], xh[:, 0, :], ALU.mult).then_inc(st.rot_d, 1)
            dve.wait_ge(st.rot_b, 1)
            nc.vector.tensor_tensor(nrm[:, :], ta[:, :], tb[:, :], ALU.add).then_inc(st.rotated, 1)
            dve.wait_ge(st.rot_d, 1)
            nc.vector.tensor_tensor(gx[:, :], gx[:, :], tn[:, :], ALU.subtract).then_inc(st.rotated, 1)
            dve.wait_ge(st.rotated, 2)
            dve.wait_ge(st.masked, 1)
            nc.vector.tensor_tensor_scan(ta[:, :], r[:, :], nrm[:, :], 0.0, ALU.mult, ALU.add).then_inc(st.scanned, 1)
            nc.vector.tensor_tensor_scan(tb[:, :], r[:, :], gx[:, :], 0.0, ALU.mult, ALU.add).then_inc(st.scanned, 1)
            dve.wait_ge(st.scanned, 2)
            nc.vector.tensor_tensor(nrm[:, :], cs[:, :], ta[:, :], ALU.mult).then_inc(st.rot_a, 1)
            nc.vector.tensor_tensor(gx[:, :], sn[:, :], tb[:, :], ALU.mult).then_inc(st.rot_b, 1)
            nc.vector.tensor_tensor(tn[:, :], sn[:, :], ta[:, :], ALU.mult).then_inc(st.rot_c, 1)
            nc.vector.tensor_tensor(ph[:, :], cs[:, :], tb[:, :], ALU.mult).then_inc(st.rot_d, 1)
            dve.wait_ge(st.rot_b, 2)
            nc.vector.tensor_tensor(xh[:, 0, :], nrm[:, :], gx[:, :], ALU.subtract).then_inc(st.hrot_done, 1)
            dve.wait_ge(st.rot_d, 2)
            nc.vector.tensor_tensor(xh[:, 1, :], tn[:, :], ph[:, :], ALU.add).then_inc(st.hrot_done, 1)
            for j in range(NJ):
                dve.wait_ge(st.out_ready, j + 1)
                nc.vector.scalar_tensor_tensor(K.x[:, toks(j)], K.ps[:, j, :], b_out, K.x[:, toks(j)],
                                               ALU.add, ALU.add).then_inc(st.x_done, 1)
    st.end()


def channel_mix_stage(K, tag):
    nc = K.nc
    st = Stage(nc, f"chmix{tag}")
    (st.w_ready, st.omm_ready, st.prev_ready, st.prev_edge, st.mixed, st.r_ready, st.r_gate,
     st.k_ready, st.k_relu, st.k_sq, st.v_ready, st.out_gated, st.x_done) = st.signals(
        "w_ready omm_ready prev_ready prev_edge mixed r_ready r_gate k_ready k_relu k_sq v_ready "
        "out_gated x_done")
    outer = LayerNorm(K, st, "outer_")
    wt = st.sb("wt", [P, K.d["chmix_w"].shape[1]])
    wr, wk, wv = (wt[:, toks(i, P)] for i in range(3))
    mu = [wt[:, 384:385], wt[:, 385:386]]
    omm = st.sb("omm", [P, 2])
    prev = st.sb("prev", [P, 2, TOK])
    mix = st.sb("mix", [P, 2, TOK])
    r = st.sb("r", [P, TOK])
    ka = st.sb("ka", [P, TOK])
    h = K.h
    with nc.Block() as block:
        @block.sync
        def _(sp):
            sp.dma_start(wt[:, :], K.d["chmix_w"]).then_inc(st.w_ready, 16)

        @block.tensor
        def _(pe):
            outer.pe(pe, 0, K.x, lambda j: None)
            pe.wait_ge(st.w_ready, 16)
            for j in range(NJ):
                pe.wait_ge(st.mixed, 2 * j + 1)
                nc.tensor.matmul(K.ps[:, j, :], wr, mix[:, 0, toks(j)], start=True, stop=True).then_inc(st.r_ready, 1)
                pe.wait_ge(st.mixed, 2 * j + 2)
                nc.tensor.matmul(K.ps[:, 4 + j, :], wk, mix[:, 1, toks(j)], start=True, stop=True)\
                    .then_inc(st.k_ready, 1)
            for j in range(NJ):
                pe.wait_ge(st.k_sq, j + 1)
                nc.tensor.matmul(K.ps[:, 4 + j, :], wv, ka[:, toks(j)], start=True, stop=True).then_inc(st.v_ready, 1)

        @block.scalar
        def _(act):
            nc.scalar.preload_act_table_set("natural_log_exp_and_others")
            outer.act(act, 0)
            act.wait_ge(st.omm_ready, 1)
            for j in range(NJ):
                for i in range(2):
                    act.wait_ge(outer.norm_ready, at(0, j))
                    seqs = h[:, toks(j)].rearrange("p (s n) -> p s n", n=LEN)
                    dst = prev[:, i, toks(j)].rearrange("p (s n) -> p s n", n=LEN)
                    act.wait_ge(st.prev_edge, 1)
                    nc.scalar.activation(dst[:, :, 1:LEN], seqs[:, :, 0:LEN - 1], ACT.Copy, scale=omm[:, i:i + 1])\
                        .then_inc(st.prev_ready, 1)
            for j in range(NJ):
                act.wait_ge(st.k_ready, j + 1)
                nc.scalar.activation(ka[:, toks(j)], K.ps[:, 4 + j, :], ACT.Relu).then_inc(st.k_relu, 1)
            for j in range(NJ):
                act.wait_ge(st.k_relu, j + 1)
                nc.scalar.activation(ka[:, toks(j)], ka[:, toks(j)], ACT.Square).then_inc(st.k_sq, 1)
            for j in range(NJ):
                act.wait_ge(st.r_ready, j + 1)
                nc.scalar.activation(r[:, toks(j)], K.ps[:, j, :], ACT.Sigmoid).then_inc(st.r_gate, 1)

        @block.vector
        def _(dve):
            nc.vector.memset(prev[:, :, :].rearrange("p i (s n) -> p (i s) n", n=LEN)[:, :, 0:1], 0.0)\
                .then_inc(st.prev_edge, 1)
            dve.wait_ge(st.w_ready, 16)
            nc.vector.tensor_scalar(omm[:, :], wt[:, 384:386], -1.0, 1.0, ALU.mult, ALU.add).then_inc(st.omm_ready, 1)
            outer.dve(dve, 0, K.x, h)
            dve.wait_ge(st.prev_edge, 1)
            for j in range(NJ):
                dve.wait_ge(outer.norm_ready, at(0, j))
                for i in range(2):
                    dve.wait_ge(st.prev_ready, 2 * j + i + 1)
                    nc.vector.scalar_tensor_tensor(mix[:, i, toks(j)], h[:, toks(j)], mu[i], prev[:, i, toks(j)],
                                                   ALU.mult, ALU.add).then_inc(st.mixed, 1)
            for j in range(NJ):
                dve.wait_ge(st.v_ready, j + 1)
                dve.wait_ge(st.r_gate, j + 1)
                nc.vector.tensor_tensor(r[:, toks(j)], K.ps[:, 4 + j, :], r[:, toks(j)], ALU.mult)\
                    .then_inc(st.out_gated, 1)
            for j in range(NJ):
                dve.wait_ge(st.out_gated, j + 1)
                nc.vector.tensor_tensor(K.x[:, toks(j)], K.x[:, toks(j)], r[:, toks(j)], ALU.add)\
                    .then_inc(st.x_done, 1)
    st.end()


def channel_mix_first(K):
    channel_mix_stage(K, 0)


def channel_mix_second(K):
    channel_mix_stage(K, 1)


def causal_attention_stage(K):
    nc = K.nc
    st = Stage(nc, "causal")
    (st.w_ready, st.qk_ready, st.qk_done, st.v_ready, st.v_copied, st.o_turned, st.x_done) = st.signals(
        "w_ready qk_ready qk_done v_ready v_copied o_turned x_done")
    outer = LayerNorm(K, st, "outer_")
    wt = st.sb("wt", [P, K.d["causal_w"].shape[1]])
    wq, wk, wv = (wt[:, toks(i, P)] for i in range(3))
    bias = [wt[:, 384 + i:385 + i] for i in range(3)]
    qk = st.sb("qk", [P, 2, TOK])
    vt = st.sb("vt", [P, TOK])
    o = st.sb("o", [P, TOK])
    groups = []
    for s in range(SEQS):
        for t in range(2):
            q = qk[:, 0, s * LEN + t * P:s * LEN + (t + 1) * P]
            k = qk[:, 1, s * LEN:s * LEN + (t + 1) * P]
            v = [[vt[:, toks(2 * s + kt, P)] for kt in range(t + 1)]]
            groups.append(([(q, k)], t + 1, K.causal[:, LEN * t:LEN * t + (t + 1) * P], v,
                           o[:, toks(2 * s + t, P)].unsqueeze(1)))
    att = Attention(K, st, groups, 1, P, float(P) ** -0.5)
    with nc.Block() as block:
        @block.sync
        def _(sp):
            sp.dma_start(wt[:, :], K.d["causal_w"]).then_inc(st.w_ready, 16)

        @block.tensor
        def _(pe):
            outer.pe(pe, 0, K.x, lambda j: None)
            pe.wait_ge(st.w_ready, 16)
            for i, w in enumerate((wq, wk)):
                for j in range(NJ):
                    pe.wait_ge(outer.norm_ready, at(0, j))
                    nc.tensor.matmul(K.ps[:, 4 * i + j, :], w, K.h[:, toks(j)], start=True, stop=True)\
                        .then_inc(st.qk_ready, 1)
            for j in range(NJ):
                pe.wait_ge(st.qk_done, at(0, j))
                for t in range(TPW):
                    mm = nc.tensor.matmul(K.ps[:, j, toks(t, P)], K.h[:, toks(TPW * j + t, P)], wv,
                                          start=True, stop=True)
                mm.then_inc(st.v_ready, 1)
            pe.wait_ge(st.qk_done, 2 * NJ)
            pe.wait_ge(st.v_copied, NJ)
            att.pe(pe, 0, lambda g: None)
            pe.wait_ge(att.o_copied, att.n)
            for j in range(NJ):
                for t in range(TPW):
                    mm = nc.tensor.transpose(K.ps[:, j, toks(t, P)], o[:, toks(TPW * j + t, P)], K.ident)
                mm.then_inc(st.o_turned, 1)

        @block.scalar
        def _(act):
            nc.scalar.preload_act_table_set("natural_log_exp_and_others")
            outer.act(act, 0)
            act.wait_ge(st.w_ready, 16)
            for i in range(2):
                for j in range(NJ):
                    act.wait_ge(st.qk_ready, at(i, j))
                    nc.scalar.activation(qk[:, i, toks(j)], K.ps[:, 4 * i + j, :], ACT.Identity, bias=bias[i])\
                        .then_inc(st.qk_done, 1)
            for j in range(NJ):
                act.wait_ge(st.v_ready, j + 1)
                nc.scalar.activation(vt[:, toks(j)], K.ps[:, j, :], ACT.Copy).then_inc(st.v_copied, 1)
            att.act(act, 0)

        @block.vector
        def _(dve):
            outer.dve(dve, 0, K.x, K.h)
            att.dve(dve, 0)
            dve.wait_ge(st.w_ready, 16)
            for j in range(NJ):
                dve.wait_ge(st.o_turned, j + 1)
                nc.vector.scalar_tensor_tensor(K.x[:, toks(j)], K.ps[:, j, :], bias[2], K.x[:, toks(j)],
                                               ALU.add, ALU.add).then_inc(st.x_done, 1)
    st.end()


def mamba_stage(K):
    nc = K.nc
    NS, DTR, CC, PAD = 16, 64, 2, 3
    st = Stage(nc, "mamba")
    (st.w_ready, st.in_ready, st.x_in, st.edge, st.z_done, st.conv, st.conved, st.silu_done,
     st.xdbl_ready, st.xdbl_copied, st.dt_ready, st.dt_biased, st.dt_abs, st.dt_exp, st.sp_w,
     st.sp_rest, st.sp_most, st.sp_log, st.dt_done, st.a_exp, st.a_neg, st.a_tiny, st.a_keep,
     st.a_safe, st.a_inv, st.picked, st.bc_ready, st.abar_done, st.less_one, st.bx_done, st.bx1_done, st.b_used, st.cut,
     st.scanned, st.c_used, st.summed, st.y_d, st.y_gated, st.out_ready, st.x_done, st.zeroed) = st.signals(
        "w_ready in_ready x_in edge z_done conv conved silu_done xdbl_ready xdbl_copied dt_ready "
        "dt_biased dt_abs dt_exp sp_w sp_rest sp_most sp_log dt_done a_exp a_neg a_tiny a_keep a_safe "
        "a_inv picked bc_ready abar_done less_one bx_done bx1_done b_used cut scanned c_used summed y_d y_gated "
        "out_ready x_done zeroed")
    outer = LayerNorm(K, st, "outer_")
    wt = st.sb("wt", [P, K.d["mamba_w"].shape[1]])
    o = 0
    win = [wt[:, toks(i, P)] for i in range(4)]
    o += 512
    wx = [wt[:, o + 96 * c:o + 96 * (c + 1)] for c in range(CC)]
    o += 192
    wdt = [wt[0:DTR, o + P * c:o + P * (c + 1)] for c in range(CC)]
    o += 256
    wo = [wt[:, o + P * c:o + P * (c + 1)] for c in range(CC)]
    o += 256
    a_log = wt[:, o:o + CC * NS]
    o += CC * NS
    conv_w = [[wt[:, o + 4 * c + k:o + 4 * c + k + 1] for k in range(4)] for c in range(CC)]
    o += 8
    in_b = [wt[:, o + i:o + i + 1] for i in range(4)]
    conv_b, d_skip, dt_b = ([wt[:, o + 4 + 2 * i + c:o + 5 + 2 * i + c] for c in range(CC)] for i in range(3))
    out_b = wt[:, o + 10:o + 11]
    xi = st.sb("xi", [P, CC, SEQS, LEN + PAD])
    xc = st.sb("xc", [P, CC, TOK])
    xd = st.sb("xd", [96, TOK])
    dt = st.sb("dt", [P, CC, TOK])
    ab = st.sb("ab", [P, CC, TOK])
    bx = st.sb("bx", [P, CC, TOK])
    yy = st.sb("yy", [P, CC, TOK])
    a2 = st.sb("a2", [P, 3, CC, NS])
    acol = st.sb("acol", [P, 2, 2, CC])
    selb = st.sb("selb", [96, 2, 2, P])
    z = [K.y, st.sb("z1", [P, TOK])]
    ab1 = st.sb("ab1", [P, TOK])
    hs = [[K.ln_xc, K.ln_sq], [K.h, st.sb("h1", [P, TOK])]]
    flat = lambda ap: ap.rearrange("p c n -> p (c n)")
    seqs = lambda ap: ap.rearrange("p (s n) -> p s n", n=LEN)
    with nc.Block() as block:
        @block.sync
        def _(sp):
            sp.dma_start(wt[:, :], K.d["mamba_w"]).then_inc(st.w_ready, 16)

        @block.tensor
        def _(pe):
            outer.pe(pe, 0, K.x, lambda j: None)
            pe.wait_ge(st.w_ready, 16)
            pe.wait_ge(outer.log_ready, NJ)
            for j in range(NJ):
                pe.wait_ge(outer.norm_ready, at(0, j))
                for i in range(4):
                    b = 4 * (j % 2) + i
                    if j >= 2:
                        pe.wait_ge(st.x_in, 2 * (j - 1))
                        pe.wait_ge(st.z_done, 2 * (j - 1))
                    nc.tensor.matmul(K.ps[:, b, :], win[i], K.h[:, toks(j)], start=True, stop=True)\
                        .then_inc(st.in_ready, 1)
            pe.wait_ge(st.x_in, 2 * NJ)
            pe.wait_ge(st.z_done, 2 * NJ)
            pe.wait_ge(st.silu_done, 2)
            for j in range(NJ):
                for c in range(CC):
                    mm = nc.tensor.matmul(K.ps[0:96, j, :], wx[c], xc[:, c, toks(j)], start=(c == 0), stop=(c == 1))
                mm.then_inc(st.xdbl_ready, 1)
            for j in range(NJ):
                pe.wait_ge(st.xdbl_copied, j + 1)
                for c in range(CC):
                    b = 4 + (2 * j + c) % 4
                    if j >= 2:
                        pe.wait_ge(st.dt_biased, 2 * j + c - 3)
                    nc.tensor.matmul(K.ps[:, b, :], wdt[c], xd[0:DTR, toks(j)], start=True, stop=True)\
                        .then_inc(st.dt_ready, 1)
            pe.wait_ge(st.dt_biased, 2 * NJ)
            with pe.Fori(0, NS // 2) as m:
                for u in range(2):
                    k = m * 2 + u
                    pe.wait_ge(st.picked, k + 1)
                    for i in range(2):
                        pe.wait_ge((st.b_used, st.c_used)[i], k * CC + CC)
                        for j in range(NJ):
                            mm = nc.tensor.matmul(K.ps[:, 4 * i + j, :], selb[:, u, i, :], xd[:, toks(j)],
                                                  start=True, stop=True)
                        mm.then_inc(st.bc_ready, 1)
            for j in range(NJ):
                pe.wait_ge(st.y_gated, CC)
                for c in range(CC):
                    mm = nc.tensor.matmul(K.ps[:, j, :], wo[c], yy[:, c, toks(j)], start=(c == 0), stop=(c == 1))
                mm.then_inc(st.out_ready, 1)

        @block.scalar
        def _(act):
            nc.scalar.preload_act_table_set("natural_log_exp_and_others")
            outer.act(act, 0)
            act.wait_ge(st.w_ready, 16)
            nc.scalar.activation(flat(a2[:, 0]), a_log, ACT.Exp).then_inc(st.a_exp, 1)
            act.wait_ge(outer.norm_ready, NJ)
            for j in range(NJ):
                for c in range(CC):
                    act.wait_ge(st.in_ready, 4 * j + 3 + c)
                    nc.scalar.activation(z[c][:, toks(j)], K.ps[:, 4 * (j % 2) + 2 + c, :], ACT.Silu,
                                         bias=in_b[2 + c]).then_inc(st.z_done, 1)
            for c in range(CC):
                act.wait_ge(st.conved, c + 1)
                nc.scalar.activation(xc[:, c, :], xc[:, c, :], ACT.Silu).then_inc(st.silu_done, 1)
            for j in range(NJ):
                act.wait_ge(st.xdbl_ready, j + 1)
                nc.scalar.activation(xd[:, toks(j)], K.ps[0:96, j, :], ACT.Copy).then_inc(st.xdbl_copied, 1)
            for j in range(NJ):
                for c in range(CC):
                    act.wait_ge(st.dt_ready, 2 * j + c + 1)
                    nc.scalar.activation(dt[:, c, toks(j)], K.ps[:, 4 + (2 * j + c) % 4, :], ACT.Identity,
                                         bias=dt_b[c]).then_inc(st.dt_biased, 1)
            nc.scalar.preload_act_table_set("natural_log_exp_and_others")
            act.wait_ge(st.dt_biased, 2 * NJ)
            for c in range(CC):
                nc.scalar.activation(ab[:, c, :], dt[:, c, :], ACT.Abs).then_inc(st.dt_abs, 1)
                act.wait_ge(st.dt_abs, c + 1)
                nc.scalar.activation(ab[:, c, :], ab[:, c, :], ACT.Exp, scale=-1.0).then_inc(st.dt_exp, 1)
            for c in range(CC):
                act.wait_ge(st.sp_rest, c + 1)
                nc.scalar.activation(bx[:, c, :], bx[:, c, :], ACT.Ln).then_inc(st.sp_log, 1)
            act.wait_ge(st.dt_done, CC)
            with act.Fori(0, NS // 2) as m:
                for u in range(2):
                    k = m * 2 + u
                    for c in range(CC):
                        act.wait_ge(st.picked, k + 1)
                        act.wait_ge(st.scanned, k * CC + c + 1)
                        nc.scalar.activation(ab[:, c, :], dt[:, c, :], ACT.Exp, scale=acol[:, u, 0, c:c + 1])\
                            .then_inc(st.abar_done, 1)
                    act.wait_ge(st.abar_done, k * CC + CC)
                    act.wait_ge(st.bx1_done, k + 1)
                    nc.scalar.activation(ab1[:, :], ab[:, 1, :], ACT.Copy, bias=-1.0).then_inc(st.less_one, 1)

        @block.gpsimd
        def _(pool):
            nc.gpsimd.memset(xi[:, :, :, 0:PAD], 0.0).then_inc(st.edge, 1)
            pool.wait_ge(st.a_inv, 1)
            pool.wait_ge(st.dt_done, CC)
            pool.wait_ge(st.zeroed, 1)

            def pick(k, u):
                for i in range(2):
                    nc.gpsimd.tensor_copy(selb[:, u, i, :],
                                          K.ident[0:96, bass.ds(k + (DTR + NS * i), 1)].to_broadcast([96, P]))
                    p = nc.gpsimd.tensor_copy(acol[:, u, i, :].unsqueeze(2), a2[:, 2 * i, :, bass.ds(k, 1)])
                p.then_inc(st.picked, 1)

            def grow(k):
                pool.wait_ge(st.less_one, k + 1)
                pool.wait_ge(st.b_used, k * CC + (CC + 1))
                nc.gpsimd.tensor_tensor(bx[:, 1, :], bx[:, 1, :], ab1[:, :], ALU.mult).then_inc(st.bx1_done, 1)

            def add_to_y(k, u):
                for c in range(CC):
                    pool.wait_ge(st.c_used, k * CC + CC + (c + 1))
                    pool.wait_ge(st.summed, k * CC + CC + (c + 1))
                    nc.gpsimd.tensor_tensor(yy[:, c, :], yy[:, c, :], hs[u][c][:, :], ALU.add).then_inc(st.summed, 1)

            pool.sem_inc(st.bx1_done, 1)
            pick(0, 0)
            pick(1, 1)
            grow(0)
            with pool.Fori(0, NS // 2 - 1) as m:
                for u in range(2):
                    k = m * 2 + (u + 1)
                    pool.wait_ge(st.c_used, k * CC + CC)
                    pick(k + 1, u)
                    grow(k)
                    add_to_y(m * 2 + u, u)
            grow(NS - 1)
            add_to_y(NS - 2, 0)
            add_to_y(NS - 1, 1)

        @block.vector
        def _(dve):
            outer.dve(dve, 0, K.x, K.h)
            dve.wait_ge(st.w_ready, 16)
            dve.wait_ge(st.a_exp, 1)
            nc.vector.tensor_scalar(flat(a2[:, 0]), flat(a2[:, 0]), -1.0, None, ALU.mult).then_inc(st.a_neg, 1)
            dve.wait_ge(st.a_neg, 1)
            nc.vector.tensor_scalar(flat(a2[:, 1]), flat(a2[:, 0]), -1e-6, None, ALU.is_gt).then_inc(st.a_tiny, 1)
            dve.wait_ge(st.a_tiny, 1)
            nc.vector.tensor_scalar(flat(a2[:, 2]), flat(a2[:, 1]), -1.0, 1.0, ALU.mult, ALU.add).then_inc(st.a_keep, 1)
            dve.wait_ge(st.a_keep, 1)
            nc.vector.tensor_tensor(flat(a2[:, 2]), flat(a2[:, 2]), flat(a2[:, 0]), ALU.mult).then_inc(st.a_keep, 1)
            dve.wait_ge(st.a_keep, 2)
            nc.vector.tensor_tensor(flat(a2[:, 2]), flat(a2[:, 2]), flat(a2[:, 1]), ALU.add).then_inc(st.a_safe, 1)
            dve.wait_ge(st.a_safe, 1)
            nc.vector.reciprocal(flat(a2[:, 2]), flat(a2[:, 2])).then_inc(st.a_inv, 1)
            dve.wait_ge(outer.norm_ready, NJ)
            for j in range(NJ):
                for c in range(CC):
                    dve.wait_ge(st.in_ready, 4 * j + c + 1)
                    nc.vector.tensor_scalar(xi[:, c, SPW * j:SPW * (j + 1), PAD:], seqs(K.ps[:, 4 * (j % 2) + c, :]),
                                            in_b[c], None, ALU.add).then_inc(st.x_in, 1)
            dve.wait_ge(st.x_in, 2 * NJ)
            dve.wait_ge(st.edge, 1)
            for c in range(CC):
                nc.vector.tensor_scalar(seqs(xc[:, c, :]), xi[:, c, :, 3:3 + LEN], conv_w[c][3], conv_b[c],
                                        ALU.mult, ALU.add).then_inc(st.conv, 1)
            for k in (2, 1, 0):
                for c in range(CC):
                    dve.wait_ge(st.conv, 2 * (3 - k) + c - 1)
                    v = nc.vector.scalar_tensor_tensor(seqs(xc[:, c, :]), xi[:, c, :, k:k + LEN], conv_w[c][k],
                                                       seqs(xc[:, c, :]), ALU.mult, ALU.add)
                    v.then_inc(st.conved if k == 0 else st.conv, 1)
            for c in range(CC):
                dve.wait_ge(st.dt_exp, c + 1)
                nc.vector.tensor_scalar(bx[:, c, :], ab[:, c, :], 1.0, None, ALU.add).then_inc(st.sp_w, 1)
                dve.wait_ge(st.sp_w, c + 1)
                nc.vector.scalar_tensor_tensor(ab[:, c, :], bx[:, c, :], 1.0, ab[:, c, :],
                                               ALU.subtract, ALU.subtract).then_inc(st.sp_rest, 1)
            for c in range(CC):
                dve.wait_ge(st.sp_rest, c + 1)
                nc.vector.scalar_tensor_tensor(dt[:, c, :], dt[:, c, :], 0.0, ab[:, c, :],
                                               ALU.max, ALU.subtract).then_inc(st.sp_most, 1)
            for c in range(CC):
                dve.wait_ge(st.sp_most, c + 1)
                dve.wait_ge(st.sp_log, c + 1)
                nc.vector.tensor_tensor(dt[:, c, :], dt[:, c, :], bx[:, c, :], ALU.add).then_inc(st.dt_done, 1)
            dve.wait_ge(st.dt_done, CC)
            for c in range(CC):
                nc.vector.tensor_scalar(yy[:, c, :], xc[:, c, :], d_skip[c], None, ALU.mult).then_inc(st.scanned, 1)
            dve.wait_ge(st.scanned, CC)
            dve.sem_inc(st.zeroed, 1)
            dve.sem_inc(st.b_used, CC)
            dve.sem_inc(st.c_used, CC)
            dve.sem_inc(st.summed, 2 * CC)
            with dve.Fori(0, NS // 2) as m:
                for u in range(2):
                    k = m * 2 + u
                    for c in (1, 0):
                        dve.wait_ge(st.bc_ready, k * 2 + 1)
                        dve.wait_ge(st.picked, k + 1)
                        nc.vector.scalar_tensor_tensor(bx[:, c, :], K.ps[:, 0:4, :].rearrange("p b n -> p (b n)"),
                                                       acol[:, u, 1, c:c + 1], xc[:, c, :], ALU.mult, ALU.mult)\
                            .then_inc(st.b_used, 1)
                    dve.wait_ge(st.b_used, k * CC + 2 * CC)
                    dve.wait_ge(st.abar_done, k * CC + 1)
                    nc.vector.scalar_tensor_tensor(bx[:, 0, :], ab[:, 0, :], 1.0, bx[:, 0, :],
                                                   ALU.subtract, ALU.mult).then_inc(st.bx_done, 1)
                    dve.wait_ge(st.bx_done, k + 1)
                    nc.vector.memset(seqs(ab[:, 0, :])[:, :, 0:1], 0.0).then_inc(st.cut, 1)
                    dve.wait_ge(st.less_one, k + 1)
                    nc.vector.memset(seqs(ab[:, 1, :])[:, :, 0:1], 0.0).then_inc(st.cut, 1)
                    for c in range(CC):
                        h = hs[u][c]
                        dve.wait_ge(st.cut, k * CC + (c + 1))
                        dve.wait_ge(st.summed, k * CC + (c + 1))
                        if c == 1:
                            dve.wait_ge(st.bx1_done, k + 2)
                        nc.vector.tensor_tensor_scan(h[:, :], ab[:, c, :], bx[:, c, :], 0.0, ALU.mult, ALU.add)\
                            .then_inc(st.scanned, 1)
                        dve.wait_ge(st.bc_ready, k * 2 + 2)
                        dve.wait_ge(st.scanned, k * CC + CC + (c + 1))
                        nc.vector.tensor_tensor(h[:, :], h[:, :], K.ps[:, 4:8, :].rearrange("p b n -> p (b n)"),
                                                ALU.mult).then_inc(st.c_used, 1)
            for c in range(CC):
                dve.wait_ge(st.summed, CC * NS + 2 * CC)
                dve.wait_ge(st.z_done, CC * NJ)
                nc.vector.tensor_tensor(yy[:, c, :], yy[:, c, :], z[c][:, :], ALU.mult).then_inc(st.y_gated, 1)
            for j in range(NJ):
                dve.wait_ge(st.out_ready, j + 1)
                nc.vector.scalar_tensor_tensor(K.x[:, toks(j)], K.ps[:, j, :], out_b, K.x[:, toks(j)],
                                               ALU.add, ALU.add).then_inc(st.x_done, 1)
    st.end()


def rope_attention_stage(K):
    nc = K.nc
    HEADS, DH, GH = 16, 8, 4
    ROUNDS = 2
    st = Stage(nc, "rope")
    (st.w_ready, st.lin_ready, st.rot_cos, st.rot_sin, st.rotated, st.v_ready, st.v_copied,
     st.q_copied, st.q_head, st.o_turned, st.o_moved, st.proj_ready, st.x_done, st.heads_read,
     st.first_kv) = st.signals(
        "w_ready lin_ready rot_cos rot_sin rotated v_ready v_copied q_copied q_head o_turned "
        "o_moved proj_ready x_done heads_read first_kv")
    outer = LayerNorm(K, st, "outer_")
    wt = st.sb("wt", [P, K.d["rope_w"].shape[1]])
    wqk = [[wt[:, toks(i, P)] for i in (0, 1)], [wt[:, toks(i, P)] for i in (2, 3)]]
    wv, wo = wt[:, 512:640], wt[:, 640:768]
    cos, sin = wt[:, 768:1024], wt[:, 1024:1280]
    sel = wt[:, 1280:1296]
    qk = st.sb("qk", [P, 2, TOK])
    part = st.sb("part", [P, 2, W])
    vt = st.sb("vt", [P, TOK])
    qm = st.sb("qm", [P, 2, HEADS, LEN])
    o = st.sb("o", [P, TOK])
    ot = K.h
    qst, kst, vst, ost = (st.sb(n, [P, 2, LEN]) for n in ("qs", "ks", "vs", "os"))
    groups = []
    for s, t in ROUNDS * ((0, 0), (0, 1), (1, 1), (1, 0)):
        for hg in range(HEADS // GH):
            heads = range(GH * hg, GH * (hg + 1))
            groups.append(([(qm[:, s, h, toks(t, P)], kst[:, s, 0:(t + 1) * P]) for h in heads], t + 1,
                           K.causal[:, LEN * t:LEN * t + (t + 1) * P],
                           [[vst[:, s, P * kt + DH * h:P * kt + DH * (h + 1)] for kt in range(t + 1)] for h in heads],
                           ost[:, s, P * t + DH * GH * hg:P * t + DH * GH * (hg + 1)]
                           .rearrange("p (h d) -> p h d", d=DH)))
    att = Attention(K, st, groups, GH, DH, float(DH) ** -0.5)
    N = att.n // ROUNDS
    with nc.Block() as block:
        @block.sync
        def _(sp):
            sp.dma_start(wt[:, :], K.d["rope_w"]).then_inc(st.w_ready, 16)

        @block.tensor
        def _(pe):
            outer.pe(pe, 0, K.x, lambda j: None)
            pe.wait_ge(st.w_ready, 16)
            for i in range(2):
                for j in range(NJ):
                    pe.wait_ge(outer.norm_ready, at(0, j))
                    b = (NJ * i + j) % 2
                    if NJ * i + j >= 2:
                        pe.wait_ge(st.rot_sin, at(i, j) - 2)
                    for a in range(2):
                        mm = nc.tensor.matmul(K.ps[:, 2 * b + a, :], wqk[i][a], K.h[:, toks(j)], start=True, stop=True)
                    mm.then_inc(st.lin_ready, 1)
            for j in range(NJ):
                for t in range(TPW):
                    mm = nc.tensor.matmul(K.ps[:, 4 + j, toks(t, P)], K.h[:, toks(TPW * j + t, P)], wv,
                                          start=True, stop=True)
                mm.then_inc(st.v_ready, 1)
            pe.wait_ge(st.rot_sin, 2 * NJ)
            pe.wait_ge(st.v_copied, NJ)
            pe.wait_ge(st.first_kv, 1)
            with pe.Fori(0, NJ // ROUNDS) as m:
                att.pe(pe, m * att.n, lambda g: pe.wait_ge(st.q_head, m * (2 * ROUNDS) + (g // (N // 2) + 1)))
            for j in range(NJ):
                pe.wait_ge(st.heads_read, 2 * j + 2)
                for t in range(TPW):
                    mm = nc.tensor.transpose(K.ps[:, j, toks(t, P)], o[:, toks(TPW * j + t, P)], K.ident)
                mm.then_inc(st.o_turned, 1)
            for j in range(NJ):
                pe.wait_ge(st.o_moved, j + 1)
                nc.tensor.matmul(K.ps[:, 4 + j, :], wo, ot[:, toks(j)], start=True, stop=True)\
                    .then_inc(st.proj_ready, 1)

        @block.scalar
        def _(act):
            nc.scalar.preload_act_table_set("natural_log_exp_and_others")
            outer.act(act, 0)
            for j in range(NJ):
                act.wait_ge(st.v_ready, j + 1)
                nc.scalar.activation(vt[:, toks(j)], K.ps[:, 4 + j, :], ACT.Copy).then_inc(st.v_copied, 1)
            act.wait_ge(st.rotated, 2 * NJ)
            act.wait_ge(st.v_copied, NJ)
            nc.scalar.activation(kst[:, :, :].rearrange("p s n -> p (s n)"), qk[:, 1, 0:2 * LEN], ACT.Copy)
            nc.scalar.activation(vst[:, :, :].rearrange("p s n -> p (s n)"), vt[:, 0:2 * LEN], ACT.Copy)\
                .then_inc(st.first_kv, 1)
            with act.Fori(0, NJ // ROUNDS) as m:
                att.act(act, m * att.n)
            for j in range(NJ):
                act.wait_ge(st.o_turned, j + 1)
                nc.scalar.activation(ot[:, toks(j)], K.ps[:, j, :], ACT.Copy).then_inc(st.o_moved, 1)

        @block.gpsimd
        def _(pool):
            pool.wait_ge(st.w_ready, 16)
            pool.wait_ge(st.rotated, 2 * NJ)
            pool.wait_ge(st.v_copied, NJ)

            def queries(m, s):
                seq = bass.ds(m * (2 * LEN) + s * LEN, LEN)
                nc.gpsimd.tensor_copy(qst[:, s, :], qk[:, 0, seq]).then_inc(st.q_copied, 1)
                pool.wait_ge(st.q_copied, m * 2 + (s - 1))
                nc.gpsimd.tensor_copy(kst[:, s, :], qk[:, 1, seq])
                for h in range(HEADS):
                    nc.gpsimd.tensor_scalar(qm[:, s, h, :], qst[:, s, :], sel[:, h:h + 1], None, ALU.mult)

            def values(m, s):
                seq = bass.ds(m * (2 * LEN) + s * LEN, LEN)
                nc.gpsimd.tensor_copy(vst[:, s, :], vt[:, seq]).then_inc(st.q_head, 1)

            def take(m, s):
                pool.wait_ge(att.o_copied, m * N + N // 2 * (s + 1))
                seq = bass.ds(m * (2 * LEN) + s * LEN, LEN)
                nc.gpsimd.tensor_copy(o[:, seq], ost[:, s, :]).then_inc(st.heads_read, 1)

            with pool.Fori(0, NJ - 1) as m:
                for s in range(2):
                    pool.wait_ge(att.sim_ready, m * N + N // 2 * (s + 1))
                    queries(m + 1, s)
                    take(m, s)
                    values(m + 1, s)
            for s in range(2):
                take(NJ - 1, s)

        @block.vector
        def _(dve):
            outer.dve(dve, 0, K.x, K.h)
            dve.wait_ge(st.w_ready, 16)
            for i in range(2):
                for j in range(NJ):
                    b = (NJ * i + j) % 2
                    n = NJ * i + j
                    seqs = lambda ap: ap.rearrange("p (s n) -> p s n", n=LEN)
                    both = lambda ap: ap.unsqueeze(1).to_broadcast([P, SPW, LEN])
                    dve.wait_ge(st.lin_ready, n + 1)
                    if n:
                        dve.wait_ge(st.rotated, n)
                    nc.vector.tensor_tensor(seqs(part[:, 0, :]), seqs(K.ps[:, 2 * b, :]), both(cos), ALU.mult)\
                        .then_inc(st.rot_cos, 1)
                    nc.vector.tensor_tensor(seqs(part[:, 1, :]), seqs(K.ps[:, 2 * b + 1, :]), both(sin), ALU.mult)\
                        .then_inc(st.rot_sin, 1)
                    dve.wait_ge(st.rot_sin, n + 1)
                    nc.vector.tensor_tensor(qk[:, i, toks(j)], part[:, 0, :], part[:, 1, :], ALU.add)\
                        .then_inc(st.rotated, 1)
            for s in range(2):
                dve.wait_ge(st.rotated, 2 * NJ)
                for h in range(HEADS):
                    v = nc.vector.tensor_scalar(qm[:, s, h, :], qk[:, 0, toks(s, LEN)], sel[:, h:h + 1], None, ALU.mult)
                v.then_inc(st.q_head, 1)
            with dve.Fori(0, NJ // ROUNDS) as m:
                att.dve(dve, m * att.n)
            for j in range(NJ):
                dve.wait_ge(st.proj_ready, j + 1)
                nc.vector.tensor_tensor(K.x[:, toks(j)], K.x[:, toks(j)], K.ps[:, 4 + j, :], ALU.add)\
                    .then_inc(st.x_done, 1)
    st.end()


def switch_stage(K, tag):
    nc = K.nc
    GT = 32
    NG = TOK // GT
    ES = P
    NQ = ES // 4
    NT = TOK // P
    st = Stage(nc, f"switch{tag}")
    (st.w_ready, st.w2_ready, st.logit_ready, st.biased, st.logits, st.maxima, st.chosen,
     st.chosen_tm, st.chosen_copied, st.x_tm, st.x_copied, st.picked, st.picked_copied,
     st.h1_ready, st.h1_biased, st.h1_done, st.h2_ready, st.h2_copied, st.turned, st.result_ready,
     st.y_ready, st.x_done) = st.signals(
        "w_ready w2_ready logit_ready biased logits maxima chosen chosen_tm chosen_copied x_tm "
        "x_copied picked picked_copied h1_ready h1_biased h1_done h2_ready h2_copied turned "
        "result_ready y_ready x_done")
    outer = LayerNorm(K, st, "outer_")
    wt = st.sb("wt", [P, K.d["switch_w"].shape[1]])
    w1 = st.sb("w1", [P, ES, GT])
    w2 = st.sb("w2", [P, NQ, P])
    wc, b2, b1, bc, tie = wt[:, 0:128], wt[:, 128:256], wt[:, 256:288], wt[:, 288:289], wt[:, 289:321]
    h = K.h
    logit = K.y
    top = st.sb("top", [P, NG])
    perm = st.sb("perm", [P, TOK])
    perm_tm = K.ln_xc
    h_tm = K.ln_sq
    z = st.sb("z", [P, ES, NG])
    hid = st.sb("hid", [P, NQ, NG])
    res = z
    resm = st.sb("resm", [P, NG, P])
    with nc.Block() as block:
        scalar_copy, vector_copy = nc.scalar.activation, nc.vector.tensor_copy

        def picked_copy(copy, eng, n):
            eng.wait_ge(st.picked, n + 1)
            if n:
                eng.wait_ge(st.picked_copied, n)
            j, g = n // 4, n % 4
            dst = z[:, :, :].rearrange("p e (j t g) -> p j g t e", j=NJ, g=4)[:, j, g]
            src = K.ps[:, (4 + n) % 8, :].rearrange("p (g e) -> p g e", e=P)
            args = (ACT.Copy,) if copy is scalar_copy else ()
            copy(dst, src, *args).then_inc(st.picked_copied, 1)

        def result_copy(copy, eng, n):
            eng.wait_ge(st.h2_ready, n + 1)
            if n:
                eng.wait_ge(st.h2_copied, n)
            args = (ACT.Copy,) if copy is scalar_copy else ()
            copy(res[:, :, :].rearrange("p (c q r) g -> p c r q g", c=4, r=4)[:, n // 4, n % 4],
                 K.ps[:, (4 + n) % 8, :].rearrange("p (q g) -> p q g", g=NG), *args)\
                .then_inc(st.h2_copied, 1)

        @block.sync
        def _(sp):
            sp.dma_start(wt[:, :], K.d["switch_w"]).then_inc(st.w_ready, 16)
            sp.dma_start(w1[:, :, :].rearrange("p a b -> p (a b)"), K.d["switch_w1"]).then_inc(st.w2_ready, 16)
            sp.dma_start(w2[:, :, :].rearrange("p a b -> p (a b)"), K.d["switch_w2"]).then_inc(st.w2_ready, 16)

        @block.tensor
        def _(pe):
            outer.pe(pe, 0, K.x, lambda j: None)
            pe.wait_ge(st.w_ready, 16)
            for j in range(NJ):
                pe.wait_ge(outer.norm_ready, at(0, j))
                nc.tensor.matmul(K.ps[:, j, :], wc, h[:, toks(j)], start=True, stop=True).then_inc(st.logit_ready, 1)
            for j in range(NJ):
                for t in range(TPW):
                    mm = nc.tensor.transpose(K.ps[:, 4 + j, toks(t, P)], h[:, toks(TPW * j + t, P)], K.ident)
                mm.then_inc(st.x_tm, 1)
            for j in range(NJ):
                pe.wait_ge(st.chosen, j + 1)
                for t in range(TPW):
                    mm = nc.tensor.transpose(K.ps[:, j, toks(t, P)], perm[:, toks(TPW * j + t, P)], K.ident)
                mm.then_inc(st.chosen_tm, 1)
            for j in range(NJ):
                pe.wait_ge(st.chosen_copied, j + 1 if j == 0 else NJ)
                pe.wait_ge(st.x_copied, NJ)
                if j >= 2:
                    pe.wait_ge(st.picked_copied, 4 * (j - 1))
                for t in range(TPW):
                    for g in range(4):
                        rows, tile = slice(32 * g, 32 * g + 32), toks(TPW * j + t, P)
                        mm = nc.tensor.matmul(K.ps[:, (4 * (j + 1) + g) % 8, toks(t, P)], h_tm[rows, tile],
                                              perm_tm[rows, tile], start=True, stop=True)
                        if t == TPW - 1:
                            mm.then_inc(st.picked, 1)
            pe.wait_ge(st.w2_ready, 32)
            pe.wait_ge(st.picked_copied, NT)
            for q in range(NQ):
                for r in range(4):
                    mm = nc.tensor.matmul(K.ps[32 * r:32 * r + 32, q // 8, toks(q % 8, NG)], w1[:, 4 * q + r, :],
                                          z[:, 4 * q + r, :], start=True, stop=True)
                if q % 8 == 7:
                    mm.then_inc(st.h1_ready, 1)
            for c in range(4):
                pe.wait_ge(st.h1_done, c + 1 if c == 0 else 4)
                if c >= 2:
                    pe.wait_ge(st.h2_copied, 4 * (c - 1))
                for q in range(8):
                    for r in range(4):
                        rows = slice(32 * r, 32 * r + 32)
                        mm = nc.tensor.matmul(K.ps[:, (4 * (c + 1) + r) % 8, toks(q, NG)], w2[rows, 8 * c + q, :],
                                              hid[rows, 8 * c + q, :], start=True, stop=True)
                        if q == 7:
                            mm.then_inc(st.h2_ready, 1)
            for n in range(NT):
                b = (4 + n) % 8
                pe.wait_ge(st.h2_copied, ES // 8)
                if n >= 8:
                    pe.wait_ge(st.result_ready, n - 7)
                for g in range(4 * n, 4 * n + 4):
                    mm = nc.tensor.transpose(K.ps[:, b, toks(g % 4, P)], res[:, :, g], K.ident)
                mm.then_inc(st.turned, 1)
            for j in range(NJ):
                pe.wait_ge(st.result_ready, min(4 * j + 4 + 8, NT))
                for g in range(16 * j, 16 * j + 16):
                    mm = nc.tensor.matmul(K.ps[:, 4 + j, toks(g % 16, GT)], resm[:, g, :], perm[:, toks(g, GT)],
                                          start=True, stop=True)
                mm.then_inc(st.y_ready, 1)

        @block.scalar
        def _(act):
            nc.scalar.preload_act_table_set("natural_log_exp_and_others")
            outer.act(act, 0)
            act.wait_ge(st.w_ready, 16)
            for j in range(NJ):
                act.wait_ge(st.logit_ready, j + 1)
                nc.scalar.activation(logit[:, toks(j)], K.ps[:, j, :], ACT.Identity, bias=bc).then_inc(st.biased, 1)
            act.wait_ge(outer.norm_ready, NJ)
            for j in range(NJ):
                act.wait_ge(st.x_tm, j + 1)
                nc.scalar.activation(h_tm[:, toks(j)], K.ps[:, 4 + j, :], ACT.Copy).then_inc(st.x_copied, 1)
            for n in range(0, NT, 2):
                picked_copy(scalar_copy, act, n)
            for n in range(0, ES // 8, 2):
                result_copy(scalar_copy, act, n)

        @block.vector
        def _(dve):
            outer.dve(dve, 0, K.x, h)
            dve.wait_ge(st.w_ready, 16)
            grouped = lambda ap: ap.rearrange("p (g t) -> p g t", t=GT)
            for j in range(NJ):
                gs = slice(16 * j, 16 * j + 16)
                dve.wait_ge(st.biased, j + 1)
                nc.vector.tensor_tensor(grouped(logit[:, toks(j)]), grouped(logit[:, toks(j)]),
                                        tie.unsqueeze(1).to_broadcast([P, 16, GT]), ALU.add).then_inc(st.logits, 1)
                dve.wait_ge(st.logits, j + 1)
                nc.vector.tensor_reduce(top[:, gs], grouped(logit[:, toks(j)]), AX, ALU.max).then_inc(st.maxima, 1)
                dve.wait_ge(st.maxima, j + 1)
                nc.vector.tensor_tensor(grouped(perm[:, toks(j)]), grouped(logit[:, toks(j)]),
                                        top[:, gs].unsqueeze(2).to_broadcast([P, 16, GT]), ALU.is_equal)\
                    .then_inc(st.chosen, 1)
            dve.wait_ge(outer.norm_ready, NJ)
            for j in range(NJ):
                dve.wait_ge(st.chosen_tm, j + 1)
                nc.vector.tensor_copy(perm_tm[:, toks(j)], K.ps[:, j, :]).then_inc(st.chosen_copied, 1)
            for n in range(1, NT, 2):
                picked_copy(vector_copy, dve, n)
            for c in range(4):
                part = hid[:, 8 * c:8 * c + 8, :]
                dve.wait_ge(st.h1_ready, c + 1)
                nc.vector.tensor_tensor(part, K.ps[:, c, :].rearrange("p (q g) -> p q g", g=NG),
                                        b1[:, 8 * c:8 * c + 8].unsqueeze(2).to_broadcast([P, 8, NG]), ALU.add)\
                    .then_inc(st.h1_biased, 1)
                dve.wait_ge(st.h1_biased, c + 1)
                nc.vector.tensor_scalar(part, part, 0.0, None, ALU.max).then_inc(st.h1_done, 1)
            for n in range(1, ES // 8, 2):
                result_copy(vector_copy, dve, n)
            for n in range(NT):
                dve.wait_ge(st.turned, n + 1)
                nc.vector.tensor_tensor(resm[:, 4 * n:4 * n + 4, :],
                                        K.ps[:, (4 + n) % 8, :].rearrange("p (g d) -> p g d", d=P),
                                        b2.unsqueeze(1).to_broadcast([P, 4, P]), ALU.add).then_inc(st.result_ready, 1)
            for j in range(NJ):
                dve.wait_ge(st.y_ready, j + 1)
                nc.vector.tensor_tensor(K.x[:, toks(j)], K.x[:, toks(j)], K.ps[:, 4 + j, :], ALU.add)\
                    .then_inc(st.x_done, 1)
    st.end()


def switch_first(K):
    switch_stage(K, 0)


def switch_second(K):
    switch_stage(K, 1)


class Kernel:
    pass


def build(nc, d, out):
    K = Kernel()
    K.nc, K.d = nc, d
    stored = nc.alloc_semaphore("output_stored")
    with ExitStack() as ctx:
        def sb(name, shape):
            return ctx.enter_context(nc.sbuf_tensor(name, shape, F32))

        K.ps = ctx.enter_context(nc.psum_tensor("ps", [P, 8, W], F32))
        K.x = sb("x", [P, TOK])
        K.y = sb("y", [P, TOK])
        K.h = sb("h", [P, TOK])
        K.ln_xc = sb("ln_xc", [P, TOK])
        K.ln_sq = sb("ln_sq", [P, TOK])
        consts = sb("consts", [P, d["consts"].shape[1]])
        K.mean_mat = consts[:, 0:128]
        K.ident = consts[:, 128:256]
        K.head_mask16 = consts[:, 256:384]
        K.half_ones = consts[:, 384:512]
        K.causal = consts[:, 512:1024]
        K.banded = consts[:, 1024:1536]
        K.gamma_row = consts[:, 1536:1792]
        K.gamma_col = consts[:, 1792:1794]
        K.eps_ln = consts[:, 1794:1795]
        K.eps_gn = consts[:, 1795:1796]
        K.eps_rms = consts[:, 1796:1797]
        K.ln_shift = consts[:, 1797:1798]
        K.one = consts[:, 1798:1799]

        st = Stage(nc, "load")
        (st.loaded, st.moved, st.copied) = st.signals(
            "loaded moved copied")
        with nc.Block() as block:
            tm = K.y

            @block.sync
            def _(sp):
                sp.dma_start(consts[:, :], d["consts"]).then_inc(st.loaded, 16)
                sp.dma_start(tm[:, :].rearrange("p (t f) -> p t f", f=P),
                             d["x"].rearrange("(t p) f -> p t f", p=P)).then_inc(st.loaded, 16)

            @block.tensor
            def _(pe):
                pe.wait_ge(st.loaded, 32)
                for j in range(NJ):
                    for t in range(TPW):
                        mm = nc.tensor.transpose(K.ps[:, j, toks(t, P)], tm[:, toks(TPW * j + t, P)], K.ident)
                    mm.then_inc(st.moved, 1)

            @block.vector
            def _(dve):
                for j in range(NJ):
                    dve.wait_ge(st.moved, j + 1)
                    nc.vector.tensor_copy(K.x[:, toks(j)], K.ps[:, j, :]).then_inc(st.copied, 1)
        st.end()

        for stage in STAGES:
            stage(K)

        st = Stage(nc, "store")
        (st.moved, st.copied) = st.signals(
            "moved copied")
        with nc.Block() as block:
            tm = K.y

            @block.tensor
            def _(pe):
                for j in range(NJ):
                    for t in range(TPW):
                        mm = nc.tensor.transpose(K.ps[:, j, toks(t, P)], K.x[:, toks(TPW * j + t, P)], K.ident)
                    mm.then_inc(st.moved, 1)

            @block.vector
            def _(dve):
                for j in range(NJ):
                    dve.wait_ge(st.moved, j + 1)
                    nc.vector.tensor_copy(tm[:, toks(j)], K.ps[:, j, :]).then_inc(st.copied, 1)

            @block.sync
            def _(sp):
                for j in range(NJ):
                    sp.wait_ge(st.copied, j + 1)
                    sp.dma_start(out.rearrange("b (t p) f -> p (b t) f", p=P)[:, TPW * j:TPW * (j + 1), :],
                                 tm[:, toks(j)].rearrange("p (t f) -> p t f", f=P)).then_inc(stored, 16)
                sp.wait_ge(stored, 16 * NJ)
        st.end()


STAGES = [
    linear_attention_stage,
    window_attention_first,
    retention_stage,
    window_attention_second,
    gated_delta_stage,
    lora_linear_first,
    lstm_stage,
    lora_linear_second,
    lru_stage,
    channel_mix_first,
    causal_attention_stage,
    channel_mix_second,
    mamba_stage,
    switch_first,
    rope_attention_stage,
    switch_second,
]


def _constants():
    ar = np.arange(P)
    cols = [
        np.full((P, P), 1.0 / P),
        np.eye(P),
        (ar[:, None] // 16 == ar[None, :] // 16),
        (ar[:, None] // 64 == ar[None, :] // 64),
    ]
    key = np.arange(LEN)
    for t in range(2):
        cols.append(np.where(key[None, :] <= (ar + P * t)[:, None], 0.0, -1e30))
    for t in range(2):
        back = (ar + P * t)[:, None] - key[None, :]
        cols.append(np.where((back >= 0) & (back <= 64), 0.0, -1e30))
    gamma = 1.0 - 2.0 ** -5.0
    cols.append(np.broadcast_to(gamma ** np.arange(LEN, dtype=np.float64), (P, LEN)))
    cols.append(np.stack([gamma ** -(ar + P * t).astype(np.float64) for t in range(2)], 1))
    for v in (LN_EPS, 1e-3, 1e-6, 10 * np.log(2.0), 1.0):
        cols.append(np.full((P, 1), v))
    return np.ascontiguousarray(np.concatenate(cols, 1).astype(np.float32))


def _columns(*vectors):
    return np.concatenate([v.reshape(-1, P).T for v in vectors], 1)


def _chunks(w):
    return np.concatenate(list(w.reshape(-1, P, w.shape[1])), 1)


def _block_diagonal(blocks):
    n, a, b = blocks.shape
    full = np.zeros((n * a, n * b), blocks.dtype)
    for i in range(n):
        full[i * a:(i + 1) * a, i * b:(i + 1) * b] = blocks[i]
    return full


def _pad_rows(w, n):
    return np.concatenate([w, np.zeros((n - len(w),) + w.shape[1:], w.dtype)])


def _xpos_tables():
    f32 = np.float32
    half = np.arange(0, 64, 2, dtype=f32)
    inv = f32(1.0) / (f32(10000.0) ** (half / f32(64))).astype(f32)
    t = np.arange(LEN, dtype=f32)
    angle = (t[:, None] * inv[None, :]).astype(f32)
    base = (half + f32(25.6)) / f32(89.6)
    scale = (base[None, :] ** ((t - f32(LEN // 2)) / f32(32))[:, None]).astype(f32)
    angle, scale = (np.tile(z, (1, 4)).T for z in (angle, scale))
    sign = np.where(np.arange(P) % 64 < 32, -1.0, 1.0)[:, None]
    cos, sin = np.cos(angle), sign * np.sin(angle)
    return np.concatenate([cos * scale, sin * scale, cos / scale, sin / scale], 1).astype(f32)


def _delta_constants():
    r, c = np.arange(P)[:, None], np.arange(P)[None, :]
    cols = [r <= c, r > c]
    for m in (1, 2, 4, 8, 16, 32, 64):
        cols.append((r // (2 * m) == c // (2 * m)) & (r % (2 * m) < m) & (c % (2 * m) >= m))
    cols.append(r // 32 == c // 32)
    cols.append(r // 32 == np.arange(256)[None, :] // 64)
    return np.concatenate(cols, 1).astype(np.float32)


def _rope_tables():
    dh = 8
    f = np.arange(P)
    theta = (np.float32(10000.0) ** (np.float32(-2.0) * np.arange(dh // 2, dtype=np.float32) / np.float32(dh)))
    angle = np.arange(LEN, dtype=np.float32)[None, :] * theta.astype(np.float32)[(f % dh) // 2][:, None]
    sign = np.where(f % 2 == 0, -1.0, 1.0)[:, None]
    heads = f[:, None] // dh == np.arange(P // dh)[None, :]
    return np.concatenate([np.cos(angle), sign * np.sin(angle), heads], 1).astype(np.float32)


def _arrays(v):
    a = {"consts": _constants(), "x": v["L0_attn_a_x"].reshape(TOK, P)}
    g = lambda n: v["L0_attn_a_" + n]
    a["linattn_wa"] = np.stack([
        np.concatenate([g("wq")[l], g("wk")[l], g("wv")[l], g("wo")[l],
                        _columns(g("ln1_w")[l], g("ln1_b")[l], g("bo")[l])], 1) for l in range(6)])
    a["linattn_wb"] = np.stack([
        np.concatenate([g("w1")[l], _chunks(g("w2")[l]), _columns(g("ln2_w")[l], g("ln2_b")[l])], 1)
        for l in range(6)])
    g = lambda n: v["L0_ffn_" + n]
    half = np.arange(512) ^ 32
    a["window_tabs"] = _xpos_tables()
    layers, mlps = [], []
    for l in range(2):
        wqkv = g("wqkv")[l]
        cols = []
        for i in range(2):
            w = wqkv[:, 512 * i:512 * (i + 1)]
            for c in range(4):
                cols += [w[:, toks(c, P)], w[:, half][:, toks(c, P)]]
        cols += [wqkv[:, 1024:1536], _chunks(g("wo")[l])]
        for name in ("q_scale", "k_scale"):
            scale = np.tile(g(name)[l], 8)
            cols += [_columns(scale[:P]), _columns(scale[half][:P])]
        layers.append(np.concatenate(cols, 1))
        cols = [g("w1")[l], _chunks(_pad_rows(g("w2")[l], 384)), _columns(g("ln_g")[l], g("ln_b")[l], g("b2")[l])]
        for part in (g("b1")[l][:341], g("b1")[l][341:]):
            cols += [_pad_rows(part[:, None], 384).reshape(3, P).T]
        mlps.append(np.concatenate(cols, 1))
    a["window_wa"], a["window_wb"] = np.stack(layers), np.stack(mlps)
    g = lambda n: v["L0_attn_b_" + n]
    a["retention_w"] = np.concatenate([g("Wq")[0], g("Wk")[0], g("Wv")[0], g("Wg"), g("Wo"),
                                       _columns(g("gn_gamma"), g("gn_beta"))], 1)
    g = lambda n: v["L1_attn_a_" + n]
    rows = lambda w: np.broadcast_to(w[None, :], (P, len(w)))
    a["delta_w"] = np.concatenate([
        g("Wq"), g("Wk"), g("Wv"), g("Wg"), _chunks(g("Wo")), g("W2"), g("Wa"), g("Wb"), rows(g("dt_bias")),
        rows(g("A_log")), g("conv_q_w"), g("conv_k_w"), _chunks(g("conv_v_w")),
        _columns(g("ln1_g"), g("ln1_b"), g("ln2_g"), g("ln2_b"), g("rms_in_w"), g("b2")),
        np.tile(g("o_norm_w"), 2)[:, None]], 1)
    a["delta_c"] = _delta_constants()
    g = lambda n: v["L1_ffn_" + n]
    lora = np.zeros((P, 439), np.float32)
    lora[:, 0:128] = g("W").T
    lora[:100, 128:132] = g("lora_down").T
    lora[:100, 132:260] = g("down_aux")
    lora[:4, 260:310] = g("lora_up").T
    lora[:50, 310:438] = g("up_aux").T
    lora[:, 438] = g("b")
    a["lora_w"] = lora
    g = lambda n: v["L1_attn_b_" + n]
    a["lstm_w"] = np.concatenate([g("w"), g("u"), _columns(g("bias"))], 1)
    g = lambda n: v["L2_ffn_" + n]
    a["chmix_w"] = np.concatenate([g("W_r").T, g("W_k").T, g("W_v").T, _columns(g("mu_r"), g("mu_k"))], 1)
    g = lambda n: v["L2_attn_a_" + n]
    a["lru_w"] = np.concatenate([
        g("w_in"), _chunks(_block_diagonal(g("w_gx"))), _chunks(_block_diagonal(g("w_ga"))), _chunks(g("w_out")),
        _columns(g("b_in"), g("b_gx"), g("b_ga"), g("a_real_param"), g("a_imag_param"), g("b_out"))], 1)
    g = lambda n: v["L2_attn_b_" + n]
    a["causal_w"] = np.concatenate([g("W_qkv").T, _columns(g("b_qkv"))], 1)
    g = lambda n: v["L3_attn_b_" + n]
    swap = np.arange(P) ^ 1
    a["rope_w"] = np.concatenate([g("W_q").T, g("W_q").T[:, swap], g("W_k").T, g("W_k").T[:, swap],
                                  g("W_v").T, g("W_o").T, _rope_tables()], 1)
    g = lambda n: v["L3_attn_a_" + n]
    a["mamba_w"] = np.concatenate([
        g("in_proj_w").T, _chunks(g("x_proj_w").T), _pad_rows(g("dt_proj_w").T, P), _chunks(g("out_proj_w").T),
        _chunks(g("A_log").T), _chunks(g("conv_w")),
        _columns(g("in_proj_b"), g("conv_b"), g("D"), g("dt_proj_b"), g("out_proj_b"))], 1)
    g = lambda n: v["L3_ffn_" + n]
    b1 = g("b1").reshape(32, 4, 32).transpose(1, 2, 0).reshape(P, 32)
    tie = np.broadcast_to(np.linspace(0.0, 1e-6, 32, dtype=np.float32), (P, 32))
    a["switch_w"] = np.concatenate([g("Wc").reshape(P, P), g("b2").reshape(P, P), b1, _columns(g("bc").reshape(P)), tie],
                                   1)
    a["switch_w1"] = g("W1").transpose(2, 0, 1, 3).reshape(P, -1)
    a["switch_w2"] = g("W2").reshape(32, 4, P, 32).transpose(1, 3, 0, 2).reshape(P, -1)
    return {n: np.ascontiguousarray(x) for n, x in a.items()}


def kernel(**inputs):
    import concourse.bacc as _bacc
    from concourse.bass_utils import run_bass_kernel_spmd as _run

    nc = _bacc.Bacc("TRN2", target_bir_lowering=False, num_devices=1)
    arrays = _arrays({n: np.asarray(a) for n, a in inputs.items()})
    d = {n: nc.dram_tensor(f"in_{n}", a.shape, mybir.dt.from_np(a.dtype), kind="ExternalInput").ap()
         for n, a in arrays.items()}
    out = nc.dram_tensor("out", (SEQS, LEN, P), F32, kind="ExternalOutput").ap()
    build(nc, d, out)
    r = _run(nc, [{f"in_{n}": a for n, a in arrays.items()}], core_ids=[0])
    return r.results[0]["out"]
```
